# Optimizing a Trainium2 kernel written in Bass

```python
import numpy as np
import jax
import jax.numpy as jnp

def _softmax(x, axis=-1):
    return jax.nn.softmax(x, axis=axis)

def _gelu(x):
    return jax.nn.gelu(x, approximate=True)

def _silu(x):
    return jax.nn.silu(x)

def _sigmoid(x):
    return jax.nn.sigmoid(x)

def _layernorm(x, axis=-1, eps=1e-05):
    m = jnp.mean(x, axis=axis, keepdims=True)
    v = jnp.var(x, axis=axis, keepdims=True)
    return (x - m) / jnp.sqrt(v + eps)

def _scatter_add(tgt, idx, src, axis=0):
    return tgt.at[idx].add(src)

def _segment_sum(src, seg, n):
    return jax.ops.segment_sum(src, seg, n)
kernel_name = 'mk_gps_d4_gnn_r16_6a2144'

def setup_inputs(seed: int=0):
    np.random.seed(seed)
    _w = jnp.asarray

    def _rec_inputs():
        import jax
        import jax.numpy as jnp
        _gk = jax.random.key(seed)
        x = -0.0002117 + 1 * jax.random.normal(jax.random.fold_in(_gk, 1), (3125, 256), jnp.float32)
        src = jax.random.randint(jax.random.fold_in(_gk, 2), (100000,), 0, 3125, jnp.int32)
        dst = jax.random.randint(jax.random.fold_in(_gk, 3), (100000,), 0, 3125, jnp.int32)
        _o = jnp.argsort(dst, stable=True)
        src = src[_o]
        dst = dst[_o]
        edge_type_7 = jax.random.randint(jax.random.fold_in(_gk, 13), (100000,), 0, 7, jnp.int32)
        edge_weight = jax.random.uniform(jax.random.fold_in(_gk, 14), (100000,), jnp.float32, 0.0, 0.999998)
        edge_weight1 = 0.000747931 + 0.998196 * jax.random.normal(jax.random.fold_in(_gk, 15), (100000, 1), jnp.float32)
        return (x, src, dst, edge_type_7, edge_weight, edge_weight1)
    x, src, dst, edge_type_7, edge_weight, edge_weight1 = _rec_inputs()

    def _L0_gnn_setup():
        import jax, jax.numpy as jnp
        import numpy as np
        N_NODES = 6250
        N_EDGES = 18750
        D_IN = 256
        D_OUT = 256
        NEG_SLOPE = 0.2
        key = jax.random.key(seed)
        ks = jax.random.split(key, 6)
        feat = jax.random.normal(ks[0], (N_NODES, D_IN), dtype=jnp.float32)
        scale = (2.0 / (D_IN + D_OUT)) ** 0.5
        W_src = jax.random.normal(ks[1], (D_IN, D_OUT), dtype=jnp.float32) * scale
        b_src = jnp.zeros((D_OUT,), dtype=jnp.float32)
        W_dst = jax.random.normal(ks[2], (D_IN, D_OUT), dtype=jnp.float32) * scale
        b_dst = jnp.zeros((D_OUT,), dtype=jnp.float32)
        attn = jax.random.normal(ks[3], (D_OUT,), dtype=jnp.float32) * scale
        src = jax.random.randint(ks[4], (N_EDGES,), 0, N_NODES, dtype=jnp.int32)
        dst = jax.random.randint(ks[5], (N_EDGES,), 0, N_NODES, dtype=jnp.int32)
        return {'feat': feat, 'W_src': W_src, 'b_src': b_src, 'W_dst': W_dst, 'b_dst': b_dst, 'attn': attn, 'src': src, 'dst': dst}
    _L0_gnn_all = _L0_gnn_setup()
    _L0_gnn_in = {k: v for k, v in _L0_gnn_all.items() if k in ('W_src', 'b_src', 'W_dst', 'b_dst', 'attn')}
    del _L0_gnn_all

    def _L0_mix_setup():
        import jax, jax.numpy as jnp
        import numpy as np
        MIDC = 256
        HEADS = 8
        HEADC = MIDC // HEADS
        EPS = 1e-05

        def _ln(x, gamma, beta):
            mu = jnp.mean(x, axis=-1, keepdims=True)
            var = jnp.var(x, axis=-1, keepdims=True)
            return (x - mu) * jax.lax.rsqrt(var + EPS) * gamma + beta
        key = jax.random.key(seed)
        ks = jax.random.split(key, 8)
        B, HW, C = (8, 256, MIDC)
        s = 1.0 / np.sqrt(C)
        return {'x': jax.random.normal(ks[0], (B, HW, C), jnp.float32), 'w_qkv': jax.random.normal(ks[1], (C, 3 * C), jnp.float32) * s, 'b_qkv': jnp.zeros((3 * C,), jnp.float32), 'kln_g': jnp.ones((HEADC,), jnp.float32), 'kln_b': jnp.zeros((HEADC,), jnp.float32), 'vln_g': jnp.ones((HEADC,), jnp.float32), 'vln_b': jnp.zeros((HEADC,), jnp.float32), 'w1': jax.random.normal(ks[2], (C, C), jnp.float32) * s, 'b1': jnp.zeros((C,), jnp.float32), 'w2': jax.random.normal(ks[3], (C, C), jnp.float32) * s, 'b2': jnp.zeros((C,), jnp.float32)}
    _L0_mix_all = _L0_mix_setup()
    _L0_mix_in = {k: v for k, v in _L0_mix_all.items() if k in ('w_qkv', 'b_qkv', 'kln_g', 'kln_b', 'vln_g', 'vln_b', 'w1', 'b1', 'w2', 'b2')}
    del _L0_mix_all

    def _L0_ffn_setup():
        import jax, jax.numpy as jnp
        import numpy as np
        B, A = (256, 8)
        IN, OUT = (256, 256)
        SH1, SH2 = (256, 128)
        EH1, EH2 = (128, 64)
        E, TOPK = (4, 2)

        def _shared_mlp(x, W1, b1, W2, b2, W3, b3):
            h = jax.nn.relu(x @ W1 + b1)
            h = jax.nn.relu(h @ W2 + b2)
            return h @ W3 + b3

        def _experts_mlp(x, eW1, eb1, eW2, eb2, eW3, eb3):
            h = jax.nn.relu(jnp.einsum('baf,efh->ebah', x, eW1) + eb1[:, None, None, :])
            h = jax.nn.relu(jnp.einsum('ebah,ehg->ebag', h, eW2) + eb2[:, None, None, :])
            o = jnp.einsum('ebag,ego->ebao', h, eW3) + eb3[:, None, None, :]
            return jnp.moveaxis(o, 0, -1)
        key = jax.random.key(seed)
        ks = jax.random.split(key, 16)
        s = 0.05
        return {'x': jax.random.normal(ks[0], (B, A, IN), jnp.float32), 'sW1': jax.random.normal(ks[1], (IN, SH1), jnp.float32) * s, 'sb1': jnp.zeros((SH1,), jnp.float32), 'sW2': jax.random.normal(ks[2], (SH1, SH2), jnp.float32) * s, 'sb2': jnp.zeros((SH2,), jnp.float32), 'sW3': jax.random.normal(ks[3], (SH2, OUT), jnp.float32) * s, 'sb3': jnp.zeros((OUT,), jnp.float32), 'eW1': jax.random.normal(ks[4], (E, IN, EH1), jnp.float32) * s, 'eb1': jnp.zeros((E, EH1), jnp.float32), 'eW2': jax.random.normal(ks[5], (E, EH1, EH2), jnp.float32) * s, 'eb2': jnp.zeros((E, EH2), jnp.float32), 'eW3': jax.random.normal(ks[6], (E, EH2, OUT), jnp.float32) * s, 'eb3': jnp.zeros((E, OUT), jnp.float32), 'gW': jax.random.normal(ks[7], (IN, E), jnp.float32) * s, 'gb': jnp.zeros((E,), jnp.float32)}
    _L0_ffn_all = _L0_ffn_setup()
    _L0_ffn_in = {k: v for k, v in _L0_ffn_all.items() if k in ('sW1', 'sb1', 'sW2', 'sb2', 'sW3', 'sb3', 'eW1', 'eb1', 'eW2', 'eb2', 'eW3', 'eb3', 'gW', 'gb')}
    del _L0_ffn_all

    def _L1_gnn_setup():
        import jax, jax.numpy as jnp
        import numpy as np
        N = 3125
        E = 21875
        IN_C = 256
        OUT_C = 256
        N_EDGE_TYPE = 7
        key = jax.random.key(seed)
        k1, k2, k3, k4 = jax.random.split(key, 4)
        x = jax.random.normal(k1, (N, IN_C), dtype=jnp.float32)
        edge_index = jax.random.randint(k2, (2, E), 0, N, dtype=jnp.int64)
        edge_type = jax.random.randint(k3, (E,), 0, N_EDGE_TYPE, dtype=jnp.int64)
        avg_degree = 7
        std = np.sqrt(2.0 / float(avg_degree * IN_C + avg_degree * OUT_C))
        a = np.sqrt(3.0) * std
        weights = jax.random.uniform(k4, (N_EDGE_TYPE * IN_C, OUT_C), dtype=jnp.float32, minval=-a, maxval=a)
        return {'x': x, 'edge_index': edge_index, 'edge_type': edge_type, 'weights': weights}
    _L1_gnn_all = _L1_gnn_setup()
    _L1_gnn_in = {k: v for k, v in _L1_gnn_all.items() if k in ('weights',)}
    del _L1_gnn_all

    def _L1_mix_setup():
        import jax, jax.numpy as jnp
        import numpy as np
        EPS = 1e-05

        def _layernorm(x, weight, bias):
            mean = jnp.mean(x, axis=-1, keepdims=True)
            std = jnp.std(x, axis=-1, keepdims=True, ddof=1)
            out = (x - mean) / (std + EPS)
            return weight * out + bias
        key = jax.random.key(seed)
        B, N, C = (4, 2048, 256)
        H, hc = (8, C // 8)
        kx, = jax.random.split(key, 1)
        x = jax.random.normal(kx, (B, N, C), dtype=jnp.float32)
        return {'x': x, 'kln_weight': jnp.ones((H, 1, hc), dtype=jnp.float32), 'kln_bias': jnp.zeros((H, 1, hc), dtype=jnp.float32), 'vln_weight': jnp.ones((H, 1, hc), dtype=jnp.float32), 'vln_bias': jnp.zeros((H, 1, hc), dtype=jnp.float32)}
    _L1_mix_all = _L1_mix_setup()
    _L1_mix_in = {k: v for k, v in _L1_mix_all.items() if k in ('kln_weight', 'kln_bias', 'vln_weight', 'vln_bias')}
    del _L1_mix_all

    def _L1_ffn_setup():
        import math
        import jax, jax.numpy as jnp
        import numpy as np
        CAPACITY_FACTOR = 1.25
        TOP_K = 2
        LN_EPS = 1e-05

        def _layer_norm(x, gamma, beta):
            mu = jnp.mean(x, axis=-1, keepdims=True)
            var = jnp.var(x, axis=-1, keepdims=True)
            return (x - mu) * jax.lax.rsqrt(var + LN_EPS) * gamma + beta
        key = jax.random.key(seed)
        ks = jax.random.split(key, 4)
        B, S, D, F, E = (8, 256, 256, 512, 8)
        x = jax.random.normal(ks[0], (B, S, D), dtype=jnp.float32)
        Wr = jax.random.normal(ks[1], (D, E), dtype=jnp.float32) / np.sqrt(D)
        br = jnp.zeros((E,), jnp.float32)
        W1 = jax.random.normal(ks[2], (E, D, F), dtype=jnp.float32) / np.sqrt(D)
        b1 = jnp.zeros((E, F), jnp.float32)
        W2 = jax.random.normal(ks[3], (E, F, D), dtype=jnp.float32) / np.sqrt(F)
        b2 = jnp.zeros((E, D), jnp.float32)
        gamma = jnp.ones((D,), jnp.float32)
        beta = jnp.zeros((D,), jnp.float32)
        return {'x': x, 'Wr': Wr, 'br': br, 'W1': W1, 'b1': b1, 'W2': W2, 'b2': b2, 'gamma': gamma, 'beta': beta}
    _L1_ffn_all = _L1_ffn_setup()
    _L1_ffn_in = {k: v for k, v in _L1_ffn_all.items() if k in ('Wr', 'br', 'W1', 'b1', 'W2', 'b2', 'gamma', 'beta')}
    del _L1_ffn_all

    def _L2_gnn_setup():
        import jax, jax.numpy as jnp
        import numpy as np
        N_NODES = 3125
        N_EDGES = 50000
        D = 256

        def _gcn_forward(x, edge_index, edge_weight, W, bias, gamma, beta):
            N = x.shape[0]
            h = x @ W
            self_idx = jnp.arange(N, dtype=edge_index.dtype)
            row = jnp.concatenate([edge_index[0], self_idx])
            col = jnp.concatenate([edge_index[1], self_idx])
            ew = jnp.concatenate([edge_weight, jnp.ones((N,), dtype=x.dtype)])
            deg = jax.ops.segment_sum(ew, col, num_segments=N)
            dinv = jnp.where(deg > 0, jax.lax.rsqrt(deg), 0.0)
            norm = dinv[row] * ew * dinv[col]
            msgs = h[row] * norm[:, None]
            out = jax.ops.segment_sum(msgs, col, num_segments=N) + bias
            out = out + x
            mu = jnp.mean(out, axis=-1, keepdims=True)
            var = jnp.mean(jnp.square(out - mu), axis=-1, keepdims=True)
            out = (out - mu) * jax.lax.rsqrt(var + 1e-05) * gamma + beta
            return out
        key = jax.random.key(seed)
        ks = jax.random.split(key, 6)
        x = jax.random.normal(ks[0], (N_NODES, D), dtype=jnp.float32)
        edge_index = jax.random.randint(ks[1], (2, N_EDGES), 0, N_NODES, dtype=jnp.int64)
        edge_weight = jax.random.uniform(ks[2], (N_EDGES,), dtype=jnp.float32)
        W = jax.random.normal(ks[3], (D, D), dtype=jnp.float32) * (1.0 / np.sqrt(D))
        bias = jax.random.normal(ks[4], (D,), dtype=jnp.float32) * 0.02
        gamma = jnp.ones((D,), dtype=jnp.float32)
        beta = jnp.zeros((D,), dtype=jnp.float32)
        return {'x': x, 'edge_index': edge_index, 'edge_weight': edge_weight, 'W': W, 'bias': bias, 'gamma': gamma, 'beta': beta}
    _L2_gnn_all = _L2_gnn_setup()
    _L2_gnn_in = {k: v for k, v in _L2_gnn_all.items() if k in ('W', 'bias', 'gamma', 'beta')}
    del _L2_gnn_all

    def _L2_mix_setup():
        import jax, jax.numpy as jnp
        import numpy as np
        N, F, C, H = (32, 256, 256, 8)
        D = C // H
        EPS_ATTN = 1e-06
        EPS_LN = 1e-05

        def layer_norm(x, g, b):
            mu = jnp.mean(x, axis=-1, keepdims=True)
            var = jnp.var(x, axis=-1, keepdims=True)
            return (x - mu) * jax.lax.rsqrt(var + EPS_LN) * g + b
        key = jax.random.key(seed)
        ks = jax.random.split(key, 8)
        s = 1.0 / np.sqrt(C)
        return {'x': jax.random.normal(ks[0], (N, F, C), jnp.float32), 'Wqkv': jax.random.uniform(ks[1], (3 * C, C), jnp.float32, -s, s), 'ln1_g': jnp.ones((C,), jnp.float32), 'ln1_b': jnp.zeros((C,), jnp.float32), 'W1': jax.random.uniform(ks[2], (C, C), jnp.float32, -s, s), 'b1': jax.random.uniform(ks[3], (C,), jnp.float32, -s, s), 'W2': jax.random.uniform(ks[4], (C, C), jnp.float32, -s, s), 'b2': jax.random.uniform(ks[5], (C,), jnp.float32, -s, s), 'ln2_g': jnp.ones((C,), jnp.float32), 'ln2_b': jnp.zeros((C,), jnp.float32)}
    _L2_mix_all = _L2_mix_setup()
    _L2_mix_in = {k: v for k, v in _L2_mix_all.items() if k in ('Wqkv', 'ln1_g', 'ln1_b', 'W1', 'b1', 'W2', 'b2', 'ln2_g', 'ln2_b')}
    del _L2_mix_all

    def _L2_ffn_setup():
        import jax, jax.numpy as jnp
        import numpy as np
        TOP_K = 2
        LN_EPS = 1e-05
        key = jax.random.key(seed)
        ks = jax.random.split(key, 8)
        B, S, D, E, H = (16, 1024, 256, 8, 1024)
        x = jax.random.normal(ks[0], (B, S, D), dtype=jnp.float32)
        Wr = jax.random.normal(ks[1], (D, E), dtype=jnp.float32) * 0.1
        br = jnp.zeros((E,), dtype=jnp.float32)
        ln_g = jnp.ones((E, D), dtype=jnp.float32)
        ln_b = jnp.zeros((E, D), dtype=jnp.float32)
        W1 = jax.random.normal(ks[2], (E, D, H), dtype=jnp.float32) * (1.0 / np.sqrt(D))
        b1 = jnp.zeros((E, H), dtype=jnp.float32)
        W2 = jax.random.normal(ks[3], (E, H, D), dtype=jnp.float32) * (1.0 / np.sqrt(H))
        b2 = jnp.zeros((E, D), dtype=jnp.float32)
        return {'x': x, 'Wr': Wr, 'br': br, 'ln_g': ln_g, 'ln_b': ln_b, 'W1': W1, 'b1': b1, 'W2': W2, 'b2': b2}
    _L2_ffn_all = _L2_ffn_setup()
    _L2_ffn_in = {k: v for k, v in _L2_ffn_all.items() if k in ('Wr', 'br', 'ln_g', 'ln_b', 'W1', 'b1', 'W2', 'b2')}
    del _L2_ffn_all

    def _L3_gnn_setup():
        import jax, jax.numpy as jnp
        import numpy as np
        NEG_SLOPE = 0.2
        EPS = 1e-16
        LN_EPS = 1e-05

        def _gat_layer(x, edge_index, edge_attr, W, att_src, att_dst, We, att_edge, bias, gamma, beta):
            N, HID = x.shape
            H, C = att_src.shape
            src, dst = (edge_index[0], edge_index[1])
            ones = jnp.ones((src.shape[0],), x.dtype)
            deg = jax.ops.segment_sum(ones, dst, num_segments=N)
            loop_attr = jax.ops.segment_sum(edge_attr, dst, num_segments=N) / jnp.maximum(deg, 1.0)[:, None]
            loop_idx = jnp.arange(N, dtype=src.dtype)
            src = jnp.concatenate([src, loop_idx])
            dst = jnp.concatenate([dst, loop_idx])
            e_attr = jnp.concatenate([edge_attr, loop_attr], axis=0)
            xp = (x @ W).reshape(N, H, C)
            a_s = jnp.einsum('nhc,hc->nh', xp, att_src)
            a_d = jnp.einsum('nhc,hc->nh', xp, att_dst)
            ep = (e_attr @ We).reshape(-1, H, C)
            a_e = jnp.einsum('ehc,hc->eh', ep, att_edge)
            logits = a_s[src] + a_d[dst] + a_e
            logits = jax.nn.leaky_relu(logits, NEG_SLOPE)
            m = jax.ops.segment_max(logits, dst, num_segments=N)
            p = jnp.exp(logits - m[dst])
            z = jax.ops.segment_sum(p, dst, num_segments=N)
            alpha = p / (z[dst] + EPS)
            msg = xp[src] * alpha[:, :, None]
            out = jax.ops.segment_sum(msg, dst, num_segments=N)
            out = out.reshape(N, H * C) + bias
            mu = jnp.mean(out, axis=-1, keepdims=True)
            var = jnp.var(out, axis=-1, keepdims=True)
            h = (out - mu) * jax.lax.rsqrt(var + LN_EPS) * gamma + beta
            return jax.nn.relu(h + x)
        key = jax.random.key(seed)
        ks = jax.random.split(key, 12)
        N, E, HID, H = (625, 20000, 256, 4)
        C = HID // H
        s = 1.0 / np.sqrt(HID)
        x = jax.random.normal(ks[0], (N, HID), jnp.float32)
        src = jax.random.randint(ks[1], (E,), 0, N, dtype=jnp.int32)
        dst = jax.random.randint(ks[2], (E,), 0, N, dtype=jnp.int32)
        edge_index = jnp.stack([src, dst])
        edge_attr = jax.random.normal(ks[3], (E, 1), jnp.float32)
        W = jax.random.normal(ks[4], (HID, HID), jnp.float32) * s
        att_src = jax.random.normal(ks[5], (H, C), jnp.float32) * s
        att_dst = jax.random.normal(ks[6], (H, C), jnp.float32) * s
        We = jax.random.normal(ks[7], (1, HID), jnp.float32) * s
        att_edge = jax.random.normal(ks[8], (H, C), jnp.float32) * s
        bias = jnp.zeros((HID,), jnp.float32)
        gamma = jnp.ones((HID,), jnp.float32)
        beta = jnp.zeros((HID,), jnp.float32)
        return {'x': x, 'edge_index': edge_index, 'edge_attr': edge_attr, 'W': W, 'att_src': att_src, 'att_dst': att_dst, 'We': We, 'att_edge': att_edge, 'bias': bias, 'gamma': gamma, 'beta': beta}
    _L3_gnn_all = _L3_gnn_setup()
    _L3_gnn_in = {k: v for k, v in _L3_gnn_all.items() if k in ('W', 'att_src', 'att_dst', 'We', 'att_edge', 'bias', 'gamma', 'beta')}
    del _L3_gnn_all

    def _L3_mix_setup():
        import jax, jax.numpy as jnp
        import numpy as np
        B, N, C, H = (8, 1024, 256, 8)
        D = C // H
        GH = C // 4
        key = jax.random.key(seed)
        ks = jax.random.split(key, 6)
        s = 0.02
        return {'x': jax.random.normal(ks[0], (B, N, C), dtype=jnp.float32), 'Wqkv': jax.random.normal(ks[1], (C, 3 * C), dtype=jnp.float32) * s, 'Wproj': jax.random.normal(ks[2], (C, C), dtype=jnp.float32) * s, 'bproj': jnp.zeros((C,), dtype=jnp.float32), 'ln_g': jnp.ones((C,), dtype=jnp.float32), 'ln_b': jnp.zeros((C,), dtype=jnp.float32), 'Wg1': jax.random.normal(ks[3], (C, GH), dtype=jnp.float32) * s, 'bg1': jnp.zeros((GH,), dtype=jnp.float32), 'Wg2': jax.random.normal(ks[4], (GH, C), dtype=jnp.float32) * s, 'bg2': jnp.zeros((C,), dtype=jnp.float32)}
    _L3_mix_all = _L3_mix_setup()
    _L3_mix_in = {k: v for k, v in _L3_mix_all.items() if k in ('Wqkv', 'Wproj', 'bproj', 'ln_g', 'ln_b', 'Wg1', 'bg1', 'Wg2', 'bg2')}
    del _L3_mix_all

    def _L3_ffn_setup():
        import jax, jax.numpy as jnp
        import numpy as np
        BN_EPS = 0.001

        def _bn(h, g, b, m, v):
            return g * (h - m) * jax.lax.rsqrt(v + BN_EPS) + b
        key = jax.random.key(seed)
        ks = jax.random.split(key, 8)
        B, F, Df = (256, 64, 256)
        E, H, D = (8, 256, 256)
        s1 = 1.0 / np.sqrt(Df)
        s2 = 1.0 / np.sqrt(H)
        return {'x': jax.random.normal(ks[0], (B, F, Df), jnp.float32), 'Wr': jax.random.normal(ks[1], (Df, E), jnp.float32) * s1, 'br': jnp.zeros((E,), jnp.float32), 'W1': jax.random.normal(ks[2], (E, Df, H), jnp.float32) * s1, 'b1': jnp.zeros((E, H), jnp.float32), 'g1': jnp.ones((E, H), jnp.float32), 'be1': jnp.zeros((E, H), jnp.float32), 'm1': jnp.zeros((E, H), jnp.float32), 'v1': jnp.ones((E, H), jnp.float32), 'W2': jax.random.normal(ks[3], (E, H, H), jnp.float32) * s2, 'b2': jnp.zeros((E, H), jnp.float32), 'g2': jnp.ones((E, H), jnp.float32), 'be2': jnp.zeros((E, H), jnp.float32), 'm2': jnp.zeros((E, H), jnp.float32), 'v2': jnp.ones((E, H), jnp.float32), 'Wo': jax.random.normal(ks[4], (E, H, D), jnp.float32) * s2, 'bo': jnp.zeros((E, D), jnp.float32)}
    _L3_ffn_all = _L3_ffn_setup()
    _L3_ffn_in = {k: v for k, v in _L3_ffn_all.items() if k in ('Wr', 'br', 'W1', 'b1', 'g1', 'be1', 'm1', 'v1', 'W2', 'b2', 'g2', 'be2', 'm2', 'v2', 'Wo', 'bo')}
    del _L3_ffn_all
    return {'x': x, 'src': src, 'dst': dst, 'edge_type_7': edge_type_7, 'edge_weight': edge_weight, 'edge_weight1': edge_weight1, 'L0_gnn_W_src': _L0_gnn_in['W_src'], 'L0_gnn_b_src': _L0_gnn_in['b_src'], 'L0_gnn_W_dst': _L0_gnn_in['W_dst'], 'L0_gnn_b_dst': _L0_gnn_in['b_dst'], 'L0_gnn_attn': _L0_gnn_in['attn'], 'L0_mix_w_qkv': _L0_mix_in['w_qkv'], 'L0_mix_b_qkv': _L0_mix_in['b_qkv'], 'L0_mix_kln_g': _L0_mix_in['kln_g'], 'L0_mix_kln_b': _L0_mix_in['kln_b'], 'L0_mix_vln_g': _L0_mix_in['vln_g'], 'L0_mix_vln_b': _L0_mix_in['vln_b'], 'L0_mix_w1': _L0_mix_in['w1'], 'L0_mix_b1': _L0_mix_in['b1'], 'L0_mix_w2': _L0_mix_in['w2'], 'L0_mix_b2': _L0_mix_in['b2'], 'L0_ffn_sW1': _L0_ffn_in['sW1'], 'L0_ffn_sb1': _L0_ffn_in['sb1'], 'L0_ffn_sW2': _L0_ffn_in['sW2'], 'L0_ffn_sb2': _L0_ffn_in['sb2'], 'L0_ffn_sW3': _L0_ffn_in['sW3'], 'L0_ffn_sb3': _L0_ffn_in['sb3'], 'L0_ffn_eW1': _L0_ffn_in['eW1'], 'L0_ffn_eb1': _L0_ffn_in['eb1'], 'L0_ffn_eW2': _L0_ffn_in['eW2'], 'L0_ffn_eb2': _L0_ffn_in['eb2'], 'L0_ffn_eW3': _L0_ffn_in['eW3'], 'L0_ffn_eb3': _L0_ffn_in['eb3'], 'L0_ffn_gW': _L0_ffn_in['gW'], 'L0_ffn_gb': _L0_ffn_in['gb'], 'L1_gnn_weights': _L1_gnn_in['weights'], 'L1_mix_kln_weight': _L1_mix_in['kln_weight'], 'L1_mix_kln_bias': _L1_mix_in['kln_bias'], 'L1_mix_vln_weight': _L1_mix_in['vln_weight'], 'L1_mix_vln_bias': _L1_mix_in['vln_bias'], 'L1_ffn_Wr': _L1_ffn_in['Wr'], 'L1_ffn_br': _L1_ffn_in['br'], 'L1_ffn_W1': _L1_ffn_in['W1'], 'L1_ffn_b1': _L1_ffn_in['b1'], 'L1_ffn_W2': _L1_ffn_in['W2'], 'L1_ffn_b2': _L1_ffn_in['b2'], 'L1_ffn_gamma': _L1_ffn_in['gamma'], 'L1_ffn_beta': _L1_ffn_in['beta'], 'L2_gnn_W': _L2_gnn_in['W'], 'L2_gnn_bias': _L2_gnn_in['bias'], 'L2_gnn_gamma': _L2_gnn_in['gamma'], 'L2_gnn_beta': _L2_gnn_in['beta'], 'L2_mix_Wqkv': _L2_mix_in['Wqkv'], 'L2_mix_ln1_g': _L2_mix_in['ln1_g'], 'L2_mix_ln1_b': _L2_mix_in['ln1_b'], 'L2_mix_W1': _L2_mix_in['W1'], 'L2_mix_b1': _L2_mix_in['b1'], 'L2_mix_W2': _L2_mix_in['W2'], 'L2_mix_b2': _L2_mix_in['b2'], 'L2_mix_ln2_g': _L2_mix_in['ln2_g'], 'L2_mix_ln2_b': _L2_mix_in['ln2_b'], 'L2_ffn_Wr': _L2_ffn_in['Wr'], 'L2_ffn_br': _L2_ffn_in['br'], 'L2_ffn_ln_g': _L2_ffn_in['ln_g'], 'L2_ffn_ln_b': _L2_ffn_in['ln_b'], 'L2_ffn_W1': _L2_ffn_in['W1'], 'L2_ffn_b1': _L2_ffn_in['b1'], 'L2_ffn_W2': _L2_ffn_in['W2'], 'L2_ffn_b2': _L2_ffn_in['b2'], 'L3_gnn_W': _L3_gnn_in['W'], 'L3_gnn_att_src': _L3_gnn_in['att_src'], 'L3_gnn_att_dst': _L3_gnn_in['att_dst'], 'L3_gnn_We': _L3_gnn_in['We'], 'L3_gnn_att_edge': _L3_gnn_in['att_edge'], 'L3_gnn_bias': _L3_gnn_in['bias'], 'L3_gnn_gamma': _L3_gnn_in['gamma'], 'L3_gnn_beta': _L3_gnn_in['beta'], 'L3_mix_Wqkv': _L3_mix_in['Wqkv'], 'L3_mix_Wproj': _L3_mix_in['Wproj'], 'L3_mix_bproj': _L3_mix_in['bproj'], 'L3_mix_ln_g': _L3_mix_in['ln_g'], 'L3_mix_ln_b': _L3_mix_in['ln_b'], 'L3_mix_Wg1': _L3_mix_in['Wg1'], 'L3_mix_bg1': _L3_mix_in['bg1'], 'L3_mix_Wg2': _L3_mix_in['Wg2'], 'L3_mix_bg2': _L3_mix_in['bg2'], 'L3_ffn_Wr': _L3_ffn_in['Wr'], 'L3_ffn_br': _L3_ffn_in['br'], 'L3_ffn_W1': _L3_ffn_in['W1'], 'L3_ffn_b1': _L3_ffn_in['b1'], 'L3_ffn_g1': _L3_ffn_in['g1'], 'L3_ffn_be1': _L3_ffn_in['be1'], 'L3_ffn_m1': _L3_ffn_in['m1'], 'L3_ffn_v1': _L3_ffn_in['v1'], 'L3_ffn_W2': _L3_ffn_in['W2'], 'L3_ffn_b2': _L3_ffn_in['b2'], 'L3_ffn_g2': _L3_ffn_in['g2'], 'L3_ffn_be2': _L3_ffn_in['be2'], 'L3_ffn_m2': _L3_ffn_in['m2'], 'L3_ffn_v2': _L3_ffn_in['v2'], 'L3_ffn_Wo': _L3_ffn_in['Wo'], 'L3_ffn_bo': _L3_ffn_in['bo']}

def reference(x, src, dst, edge_type_7, edge_weight, edge_weight1, L0_gnn_W_src, L0_gnn_b_src, L0_gnn_W_dst, L0_gnn_b_dst, L0_gnn_attn, L0_mix_w_qkv, L0_mix_b_qkv, L0_mix_kln_g, L0_mix_kln_b, L0_mix_vln_g, L0_mix_vln_b, L0_mix_w1, L0_mix_b1, L0_mix_w2, L0_mix_b2, L0_ffn_sW1, L0_ffn_sb1, L0_ffn_sW2, L0_ffn_sb2, L0_ffn_sW3, L0_ffn_sb3, L0_ffn_eW1, L0_ffn_eb1, L0_ffn_eW2, L0_ffn_eb2, L0_ffn_eW3, L0_ffn_eb3, L0_ffn_gW, L0_ffn_gb, L1_gnn_weights, L1_mix_kln_weight, L1_mix_kln_bias, L1_mix_vln_weight, L1_mix_vln_bias, L1_ffn_Wr, L1_ffn_br, L1_ffn_W1, L1_ffn_b1, L1_ffn_W2, L1_ffn_b2, L1_ffn_gamma, L1_ffn_beta, L2_gnn_W, L2_gnn_bias, L2_gnn_gamma, L2_gnn_beta, L2_mix_Wqkv, L2_mix_ln1_g, L2_mix_ln1_b, L2_mix_W1, L2_mix_b1, L2_mix_W2, L2_mix_b2, L2_mix_ln2_g, L2_mix_ln2_b, L2_ffn_Wr, L2_ffn_br, L2_ffn_ln_g, L2_ffn_ln_b, L2_ffn_W1, L2_ffn_b1, L2_ffn_W2, L2_ffn_b2, L3_gnn_W, L3_gnn_att_src, L3_gnn_att_dst, L3_gnn_We, L3_gnn_att_edge, L3_gnn_bias, L3_gnn_gamma, L3_gnn_beta, L3_mix_Wqkv, L3_mix_Wproj, L3_mix_bproj, L3_mix_ln_g, L3_mix_ln_b, L3_mix_Wg1, L3_mix_bg1, L3_mix_Wg2, L3_mix_bg2, L3_ffn_Wr, L3_ffn_br, L3_ffn_W1, L3_ffn_b1, L3_ffn_g1, L3_ffn_be1, L3_ffn_m1, L3_ffn_v1, L3_ffn_W2, L3_ffn_b2, L3_ffn_g2, L3_ffn_be2, L3_ffn_m2, L3_ffn_v2, L3_ffn_Wo, L3_ffn_bo):
    import jax
    import jax.numpy as jnp

    def _L0_gnn_ref(feat, W_src, b_src, W_dst, b_dst, attn, src, dst):
        import jax, jax.numpy as jnp
        import numpy as np
        N_NODES = 6250
        N_EDGES = 18750
        D_IN = 256
        D_OUT = 256
        NEG_SLOPE = 0.2
        N = feat.shape[0]
        el = feat @ W_src + b_src
        er = feat @ W_dst + b_dst
        e = jax.nn.leaky_relu(el[src] + er[dst], NEG_SLOPE)
        score = e @ attn
        smax = jax.ops.segment_max(score, dst, num_segments=N)
        ex = jnp.exp(score - smax[dst])
        ssum = jax.ops.segment_sum(ex, dst, num_segments=N)
        a = ex / ssum[dst]
        out = jax.ops.segment_sum(el[src] * a[:, None], dst, num_segments=N)
        return out

    def _L0_mix_ref(x, w_qkv, b_qkv, kln_g, kln_b, vln_g, vln_b, w1, b1, w2, b2):
        import jax, jax.numpy as jnp
        import numpy as np
        MIDC = 256
        HEADS = 8
        HEADC = MIDC // HEADS
        EPS = 1e-05

        def _ln(x, gamma, beta):
            mu = jnp.mean(x, axis=-1, keepdims=True)
            var = jnp.var(x, axis=-1, keepdims=True)
            return (x - mu) * jax.lax.rsqrt(var + EPS) * gamma + beta
        B, HW, C = x.shape
        bias = x
        qkv = (x @ w_qkv + b_qkv).reshape(B, HW, HEADS, 3 * HEADC)
        qkv = qkv.transpose(0, 2, 1, 3)
        q, k, v = jnp.split(qkv, 3, axis=-1)
        k = _ln(k, kln_g, kln_b)
        v = _ln(v, vln_g, vln_b)
        kv = jnp.einsum('bhnd,bhne->bhde', k, v) / HW
        out = jnp.einsum('bhnd,bhde->bhne', q, kv)
        out = out.transpose(0, 2, 1, 3).reshape(B, HW, C)
        ret = out + bias
        h = jax.nn.gelu(ret @ w1 + b1, approximate=False)
        return h @ w2 + b2 + bias

    def _L0_ffn_ref(x, sW1, sb1, sW2, sb2, sW3, sb3, eW1, eb1, eW2, eb2, eW3, eb3, gW, gb):
        import jax, jax.numpy as jnp
        import numpy as np
        B, A = (256, 8)
        IN, OUT = (256, 256)
        SH1, SH2 = (256, 128)
        EH1, EH2 = (128, 64)
        E, TOPK = (4, 2)

        def _shared_mlp(x, W1, b1, W2, b2, W3, b3):
            h = jax.nn.relu(x @ W1 + b1)
            h = jax.nn.relu(h @ W2 + b2)
            return h @ W3 + b3

        def _experts_mlp(x, eW1, eb1, eW2, eb2, eW3, eb3):
            h = jax.nn.relu(jnp.einsum('baf,efh->ebah', x, eW1) + eb1[:, None, None, :])
            h = jax.nn.relu(jnp.einsum('ebah,ehg->ebag', h, eW2) + eb2[:, None, None, :])
            o = jnp.einsum('ebag,ego->ebao', h, eW3) + eb3[:, None, None, :]
            return jnp.moveaxis(o, 0, -1)
        all_out = _experts_mlp(x, eW1, eb1, eW2, eb2, eW3, eb3)
        shared = _shared_mlp(x, sW1, sb1, sW2, sb2, sW3, sb3)
        gates = jax.nn.softmax(x @ gW + gb, axis=-1)
        topv, topi = jax.lax.top_k(gates, TOPK)
        topw = jax.nn.softmax(topv, axis=-1)
        sel = jnp.take_along_axis(all_out, topi[:, :, None, :], axis=-1)
        gated = jnp.sum(sel * topw[:, :, None, :], axis=-1)
        return shared + gated

    def _L1_gnn_ref(x, edge_index, edge_type, weights):
        import jax, jax.numpy as jnp
        import numpy as np
        N = 3125
        E = 21875
        IN_C = 256
        OUT_C = 256
        N_EDGE_TYPE = 7
        n = x.shape[0]
        row, col = (edge_index[0], edge_index[1])
        index = row * N_EDGE_TYPE + edge_type
        num_seg = n * N_EDGE_TYPE
        gathered = x[col]
        sums = jax.ops.segment_sum(gathered, index, num_segments=num_seg)
        cnt = jax.ops.segment_sum(jnp.ones((index.shape[0],), x.dtype), index, num_segments=num_seg)
        mean = sums / jnp.maximum(cnt, 1.0)[:, None]
        return mean.reshape(n, -1) @ weights

    def _L1_mix_ref(x, kln_weight, kln_bias, vln_weight, vln_bias):
        import jax, jax.numpy as jnp
        import numpy as np
        EPS = 1e-05

        def _layernorm(x, weight, bias):
            mean = jnp.mean(x, axis=-1, keepdims=True)
            std = jnp.std(x, axis=-1, keepdims=True, ddof=1)
            out = (x - mean) / (std + EPS)
            return weight * out + bias
        B, N, C = x.shape
        H = kln_weight.shape[0]
        hc = C // H
        qkv = x.reshape(B, N, H, hc).transpose(0, 2, 1, 3)
        q = qkv
        k = _layernorm(qkv, kln_weight, kln_bias)
        v = _layernorm(qkv, vln_weight, vln_bias)
        kv = jnp.einsum('bhnd,bhne->bhde', k, v) / N
        out = jnp.einsum('bhnd,bhde->bhne', q, kv)
        out = out.transpose(0, 2, 1, 3).reshape(B, N, C)
        return out + x

    def _L1_ffn_ref(x, Wr, br, W1, b1, W2, b2, gamma, beta):
        import math
        import jax, jax.numpy as jnp
        import numpy as np
        CAPACITY_FACTOR = 1.25
        TOP_K = 2
        LN_EPS = 1e-05

        def _layer_norm(x, gamma, beta):
            mu = jnp.mean(x, axis=-1, keepdims=True)
            var = jnp.var(x, axis=-1, keepdims=True)
            return (x - mu) * jax.lax.rsqrt(var + LN_EPS) * gamma + beta
        B, S, D = x.shape
        E = Wr.shape[1]
        N = B * S
        K = TOP_K
        logits = jnp.mean(x, axis=1) @ Wr + br
        routing_weights = jax.nn.softmax(logits, axis=-1)
        capacity = float(math.ceil(N * CAPACITY_FACTOR / E))
        expected_loads = routing_weights.sum(axis=0) * (N / B)
        scale = jnp.where(expected_loads > capacity, capacity / expected_loads, 1.0)
        routing_weights = jax.nn.softmax(routing_weights * scale, axis=-1)
        rw_tok = jnp.broadcast_to(routing_weights[:, None, :], (B, S, E)).reshape(N, E)
        top_w, top_i = jax.lax.top_k(rw_tok, K)
        top_w = jax.nn.softmax(top_w, axis=-1)
        xf = x.reshape(N, D)
        h = jax.nn.gelu(jnp.einsum('nd,edf->enf', xf, W1) + b1[:, None, :], approximate=False)
        y = jnp.einsum('enf,efd->end', h, W2) + b2[:, None, :]
        w_dense = jnp.zeros((N, E), x.dtype).at[jnp.arange(N)[:, None], top_i].add(top_w)
        out = jnp.einsum('ne,end->nd', w_dense, y).reshape(B, S, D)
        out = _layer_norm(out + x, gamma, beta)
        return out

    def _L2_gnn_ref(x, edge_index, edge_weight, W, bias, gamma, beta):
        import jax, jax.numpy as jnp
        import numpy as np
        N_NODES = 3125
        N_EDGES = 50000
        D = 256

        def _gcn_forward(x, edge_index, edge_weight, W, bias, gamma, beta):
            N = x.shape[0]
            h = x @ W
            self_idx = jnp.arange(N, dtype=edge_index.dtype)
            row = jnp.concatenate([edge_index[0], self_idx])
            col = jnp.concatenate([edge_index[1], self_idx])
            ew = jnp.concatenate([edge_weight, jnp.ones((N,), dtype=x.dtype)])
            deg = jax.ops.segment_sum(ew, col, num_segments=N)
            dinv = jnp.where(deg > 0, jax.lax.rsqrt(deg), 0.0)
            norm = dinv[row] * ew * dinv[col]
            msgs = h[row] * norm[:, None]
            out = jax.ops.segment_sum(msgs, col, num_segments=N) + bias
            out = out + x
            mu = jnp.mean(out, axis=-1, keepdims=True)
            var = jnp.mean(jnp.square(out - mu), axis=-1, keepdims=True)
            out = (out - mu) * jax.lax.rsqrt(var + 1e-05) * gamma + beta
            return out
        return _gcn_forward(x, edge_index, edge_weight, W, bias, gamma, beta)

    def _L2_mix_ref(x, Wqkv, ln1_g, ln1_b, W1, b1, W2, b2, ln2_g, ln2_b):
        import jax, jax.numpy as jnp
        import numpy as np
        N, F, C, H = (32, 256, 256, 8)
        D = C // H
        EPS_ATTN = 1e-06
        EPS_LN = 1e-05

        def layer_norm(x, g, b):
            mu = jnp.mean(x, axis=-1, keepdims=True)
            var = jnp.var(x, axis=-1, keepdims=True)
            return (x - mu) * jax.lax.rsqrt(var + EPS_LN) * g + b
        n, f, c = x.shape
        qkv = jnp.einsum('nfc,oc->nfo', x, Wqkv)
        q, k, v = jnp.split(qkv, 3, axis=-1)
        q = q.reshape(n, f, H, D)
        k = k.reshape(n, f, H, D)
        v = v.reshape(n, f, H, D)
        q = jax.nn.elu(q) + 1.0
        k = jax.nn.elu(k) + 1.0
        kv = jnp.einsum('nshd,nshm->nhmd', k, v)
        ksum = jnp.sum(k, axis=1)
        z = 1.0 / (jnp.einsum('nlhd,nhd->nlh', q, ksum) + EPS_ATTN)
        t = jnp.einsum('nlhd,nhmd,nlh->nlhm', q, kv, z)
        t = t.reshape(n, f, c)
        x1 = layer_norm(t + x, ln1_g, ln1_b)
        h = jax.nn.gelu(jnp.einsum('nfc,oc->nfo', x1, W1) + b1, approximate=False)
        y = jnp.einsum('nfc,oc->nfo', h, W2) + b2
        return layer_norm(y + x1, ln2_g, ln2_b)

    def _L2_ffn_ref(x, Wr, br, ln_g, ln_b, W1, b1, W2, b2):
        import jax, jax.numpy as jnp
        import numpy as np
        TOP_K = 2
        LN_EPS = 1e-05
        B, S, D = x.shape
        N = B * S
        xt = x.reshape(N, D)
        logits = xt @ Wr + br
        probs = jax.nn.softmax(logits, axis=-1)
        top_p, top_idx = jax.lax.top_k(probs, TOP_K)
        weights = top_p / top_p.sum(axis=-1, keepdims=True)
        mu = xt.mean(axis=-1, keepdims=True)
        var = ((xt - mu) ** 2).mean(axis=-1, keepdims=True)
        xn = (xt - mu) * jax.lax.rsqrt(var + LN_EPS)
        xe = xn[None, :, :] * ln_g[:, None, :] + ln_b[:, None, :]
        h = jax.nn.gelu(jnp.einsum('end,edh->enh', xe, W1) + b1[:, None, :], approximate=False)
        y = jnp.einsum('enh,ehd->end', h, W2) + b2[:, None, :]
        y_tok = jnp.transpose(y, (1, 0, 2))
        sel = jnp.take_along_axis(y_tok, top_idx[:, :, None], axis=1)
        out = (weights[:, :, None] * sel).sum(axis=1)
        return out.reshape(B, S, D)

    def _L3_gnn_ref(x, edge_index, edge_attr, W, att_src, att_dst, We, att_edge, bias, gamma, beta):
        import jax, jax.numpy as jnp
        import numpy as np
        NEG_SLOPE = 0.2
        EPS = 1e-16
        LN_EPS = 1e-05

        def _gat_layer(x, edge_index, edge_attr, W, att_src, att_dst, We, att_edge, bias, gamma, beta):
            N, HID = x.shape
            H, C = att_src.shape
            src, dst = (edge_index[0], edge_index[1])
            ones = jnp.ones((src.shape[0],), x.dtype)
            deg = jax.ops.segment_sum(ones, dst, num_segments=N)
            loop_attr = jax.ops.segment_sum(edge_attr, dst, num_segments=N) / jnp.maximum(deg, 1.0)[:, None]
            loop_idx = jnp.arange(N, dtype=src.dtype)
            src = jnp.concatenate([src, loop_idx])
            dst = jnp.concatenate([dst, loop_idx])
            e_attr = jnp.concatenate([edge_attr, loop_attr], axis=0)
            xp = (x @ W).reshape(N, H, C)
            a_s = jnp.einsum('nhc,hc->nh', xp, att_src)
            a_d = jnp.einsum('nhc,hc->nh', xp, att_dst)
            ep = (e_attr @ We).reshape(-1, H, C)
            a_e = jnp.einsum('ehc,hc->eh', ep, att_edge)
            logits = a_s[src] + a_d[dst] + a_e
            logits = jax.nn.leaky_relu(logits, NEG_SLOPE)
            m = jax.ops.segment_max(logits, dst, num_segments=N)
            p = jnp.exp(logits - m[dst])
            z = jax.ops.segment_sum(p, dst, num_segments=N)
            alpha = p / (z[dst] + EPS)
            msg = xp[src] * alpha[:, :, None]
            out = jax.ops.segment_sum(msg, dst, num_segments=N)
            out = out.reshape(N, H * C) + bias
            mu = jnp.mean(out, axis=-1, keepdims=True)
            var = jnp.var(out, axis=-1, keepdims=True)
            h = (out - mu) * jax.lax.rsqrt(var + LN_EPS) * gamma + beta
            return jax.nn.relu(h + x)
        return _gat_layer(x, edge_index, edge_attr, W, att_src, att_dst, We, att_edge, bias, gamma, beta)

    def _L3_mix_ref(x, Wqkv, Wproj, bproj, ln_g, ln_b, Wg1, bg1, Wg2, bg2):
        import jax, jax.numpy as jnp
        import numpy as np
        B, N, C, H = (8, 1024, 256, 8)
        D = C // H
        GH = C // 4
        b, n, c = x.shape
        h, d = (H, D)
        qkv = (x @ Wqkv).reshape(b, n, 3, h, d)
        q, k, v = (qkv[:, :, 0], qkv[:, :, 1], qkv[:, :, 2])
        k = jax.nn.softmax(k, axis=1)
        context = jnp.einsum('bnhd,bnhv->bhdv', k, v)
        out = jnp.einsum('bnhd,bhdv->bnhv', q, context).reshape(b, n, c)
        mu = jnp.mean(x, axis=-1, keepdims=True)
        var = jnp.var(x, axis=-1, keepdims=True)
        xn = (x - mu) * jax.lax.rsqrt(var + 1e-05) * ln_g + ln_b
        hgate = jax.nn.gelu(xn @ Wg1 + bg1, approximate=False)
        gate = jax.nn.sigmoid(hgate @ Wg2 + bg2)
        return out * gate @ Wproj + bproj

    def _L3_ffn_ref(x, Wr, br, W1, b1, g1, be1, m1, v1, W2, b2, g2, be2, m2, v2, Wo, bo):
        import jax, jax.numpy as jnp
        import numpy as np
        BN_EPS = 0.001

        def _bn(h, g, b, m, v):
            return g * (h - m) * jax.lax.rsqrt(v + BN_EPS) + b
        feat = jnp.mean(x, axis=0)
        w = jax.nn.softmax(feat @ Wr + br, axis=-1)
        h = jnp.einsum('bfd,edh->bfeh', x, W1) + b1
        h = jax.nn.relu(_bn(h, g1, be1, m1, v1))
        h = jnp.einsum('bfeh,ehk->bfek', h, W2) + b2
        h = jax.nn.relu(_bn(h, g2, be2, m2, v2))
        y = jnp.einsum('bfeh,ehd->bfed', h, Wo) + bo
        return jnp.einsum('bfed,fe->bfd', y, w)
    edge_index = jnp.stack([src, dst])
    xn = _layernorm(x, axis=-1)
    x = x + _L0_gnn_ref(xn, L0_gnn_W_src, L0_gnn_b_src, L0_gnn_W_dst, L0_gnn_b_dst, L0_gnn_attn, src, dst) + _L0_mix_ref(xn[None], L0_mix_w_qkv, L0_mix_b_qkv, L0_mix_kln_g, L0_mix_kln_b, L0_mix_vln_g, L0_mix_vln_b, L0_mix_w1, L0_mix_b1, L0_mix_w2, L0_mix_b2)[0]
    x = x + _L0_ffn_ref(_layernorm(x, axis=-1)[None], L0_ffn_sW1, L0_ffn_sb1, L0_ffn_sW2, L0_ffn_sb2, L0_ffn_sW3, L0_ffn_sb3, L0_ffn_eW1, L0_ffn_eb1, L0_ffn_eW2, L0_ffn_eb2, L0_ffn_eW3, L0_ffn_eb3, L0_ffn_gW, L0_ffn_gb)[0]
    xn = _layernorm(x, axis=-1)
    x = x + _L1_gnn_ref(xn, edge_index, edge_type_7, L1_gnn_weights) + _L1_mix_ref(xn[None], L1_mix_kln_weight, L1_mix_kln_bias, L1_mix_vln_weight, L1_mix_vln_bias)[0]
    x = x + _L1_ffn_ref(_layernorm(x, axis=-1)[None], L1_ffn_Wr, L1_ffn_br, L1_ffn_W1, L1_ffn_b1, L1_ffn_W2, L1_ffn_b2, L1_ffn_gamma, L1_ffn_beta)[0]
    xn = _layernorm(x, axis=-1)
    x = x + _L2_gnn_ref(xn, edge_index, edge_weight, L2_gnn_W, L2_gnn_bias, L2_gnn_gamma, L2_gnn_beta) + _L2_mix_ref(xn[None], L2_mix_Wqkv, L2_mix_ln1_g, L2_mix_ln1_b, L2_mix_W1, L2_mix_b1, L2_mix_W2, L2_mix_b2, L2_mix_ln2_g, L2_mix_ln2_b)[0]
    x = x + _L2_ffn_ref(_layernorm(x, axis=-1)[None], L2_ffn_Wr, L2_ffn_br, L2_ffn_ln_g, L2_ffn_ln_b, L2_ffn_W1, L2_ffn_b1, L2_ffn_W2, L2_ffn_b2)[0]
    xn = _layernorm(x, axis=-1)
    x = x + _L3_gnn_ref(xn, edge_index, edge_weight1, L3_gnn_W, L3_gnn_att_src, L3_gnn_att_dst, L3_gnn_We, L3_gnn_att_edge, L3_gnn_bias, L3_gnn_gamma, L3_gnn_beta) + _L3_mix_ref(xn[None], L3_mix_Wqkv, L3_mix_Wproj, L3_mix_bproj, L3_mix_ln_g, L3_mix_ln_b, L3_mix_Wg1, L3_mix_bg1, L3_mix_Wg2, L3_mix_bg2)[0]
    x = x + _L3_ffn_ref(_layernorm(x, axis=-1)[None], L3_ffn_Wr, L3_ffn_br, L3_ffn_W1, L3_ffn_b1, L3_ffn_g1, L3_ffn_be1, L3_ffn_m1, L3_ffn_v1, L3_ffn_W2, L3_ffn_b2, L3_ffn_g2, L3_ffn_be2, L3_ffn_m2, L3_ffn_v2, L3_ffn_Wo, L3_ffn_bo)[0]
    return x

_drawn_inputs = setup_inputs


def setup_inputs(seed=0):
    import zlib

    import numpy as np

    out = dict(_drawn_inputs(seed))
    spreads = {'L0_gnn_b_src': (0.0, 0.1),
     'L0_gnn_b_dst': (0.0, 0.8),
     'L0_mix_b_qkv': (0.0, 0.1),
     'L0_mix_kln_g': (1.0, 0.6),
     'L0_mix_kln_b': (0.0, 0.42),
     'L0_mix_vln_g': (1.0, 0.552),
     'L0_mix_vln_b': (0.0, 0.374),
     'L0_mix_b1': (0.0, 0.1),
     'L0_mix_b2': (0.0, 0.1),
     'L0_ffn_sb1': (0.0, 0.663),
     'L0_ffn_sb2': (0.0, 0.305),
     'L0_ffn_sb3': (0.0, 0.1),
     'L0_ffn_eb1': (0.0, 0.8),
     'L0_ffn_eb2': (0.0, 0.8),
     'L0_ffn_eb3': (0.0, 0.1),
     'L0_ffn_gb': (0.0, 0.766),
     'L1_mix_kln_weight': (1.0, 0.2),
     'L1_mix_kln_bias': (0.0, 0.271),
     'L1_mix_vln_weight': (1.0, 0.2),
     'L1_mix_vln_bias': (0.0, 0.1),
     'L1_ffn_br': (0.0, 0.1),
     'L1_ffn_b1': (0.0, 0.8),
     'L1_ffn_b2': (0.0, 0.645),
     'L1_ffn_gamma': (1.0, 0.2),
     'L1_ffn_beta': (0.0, 0.42),
     'L2_gnn_gamma': (1.0, 0.2),
     'L2_gnn_beta': (0.0, 0.515),
     'L2_mix_ln1_g': (1.0, 0.569),
     'L2_mix_ln1_b': (0.0, 0.503),
     'L2_mix_ln2_g': (1.0, 0.6),
     'L2_mix_ln2_b': (0.0, 0.496),
     'L2_ffn_br': (0.0, 0.715),
     'L2_ffn_ln_g': (1.0, 0.6),
     'L2_ffn_ln_b': (0.0, 0.8),
     'L2_ffn_b1': (0.0, 0.8),
     'L2_ffn_b2': (0.0, 0.723),
     'L3_gnn_bias': (0.0, 2.0),
     'L3_gnn_gamma': (1.0, 0.6),
     'L3_gnn_beta': (0.0, 2.0),
     'L3_mix_bproj': (0.0, 2.0),
     'L3_mix_ln_g': (1.0, 0.6),
     'L3_mix_ln_b': (0.0, 0.8),
     'L3_mix_bg1': (0.0, 0.8),
     'L3_mix_bg2': (0.0, 0.8),
     'L3_ffn_br': (0.0, 2.0),
     'L3_ffn_b1': (0.0, 2.0),
     'L3_ffn_g1': (1.0, 0.6),
     'L3_ffn_be1': (0.0, 2.0),
     'L3_ffn_m1': (0.0, 2.0),
     'L3_ffn_v1': (1.0, 0.6),
     'L3_ffn_b2': (0.0, 2.0),
     'L3_ffn_g2': (1.0, 0.6),
     'L3_ffn_be2': (0.0, 2.0),
     'L3_ffn_m2': (0.0, 2.0),
     'L3_ffn_v2': (1.0, 0.6),
     'L3_ffn_bo': (0.0, 2.0)}
    factors = {'edge_weight': 31.794,
     'edge_weight1': 33.29,
     'L0_ffn_eW1': 2.775,
     'L2_gnn_bias': 8.0,
     'L2_mix_b1': 8.0,
     'L2_mix_b2': 8.0,
     'L3_gnn_att_dst': 200.0,
     'L3_gnn_We': 131.056,
     'L3_gnn_att_edge': 200.0,
     'L3_mix_Wqkv': 8.0,
     'L3_mix_Wproj': 8.0,
     'L3_mix_Wg1': 8.0,
     'L3_mix_Wg2': 8.0,
     'L3_gnn_att_src': 64.0,
     'L3_ffn_W1': 3.252,
     'L3_gnn_W': 3.65}
    for name, (base, spread) in spreads.items():
        noise = np.random.default_rng([zlib.crc32(name.encode()), seed]).standard_normal(out[name].shape)
        drawn = base * np.exp(spread * noise) if base else spread * noise
        out[name] = jnp.asarray(drawn.astype(out[name].dtype))
    for name, factor in factors.items():
        out[name] = (out[name] * factor).astype(out[name].dtype)
    return out
```

```python
from contextlib import ExitStack, contextmanager

import concourse.bass as bass
from concourse import mybir

F32 = mybir.dt.float32
I32 = mybir.dt.int32
ALU = mybir.AluOpType
ACT = mybir.ActivationFunctionType
AX = mybir.AxisListType.X

NODES, EDGES, D = 3125, 100000, 256
R = 125
TILES = NODES // R
CHUNKS = EDGES // R
G = 4
LANES = 2
UNIT = G * LANES
TURNS = CHUNKS // UNIT
GT = 5
GROUPS = TILES // GT
GN = GT * R
KB = D // 128
HUGE = 3.0e38
TYPES = 7
ACCS = G


class Chain:

    def __init__(self, eng, sem, turn=None, per_turn=0, before=0):
        self.eng, self.sem, self.turn, self.per_turn, self.before, self.n = eng, sem, turn, per_turn, before, 0

    def __call__(self, ins):
        self.n += 1
        ins.then_inc(self.sem, 1)
        n = self.before + self.n
        self.eng.wait_ge(self.sem, n if self.turn is None else self.turn * self.per_turn + n)

    def pause(self, passed):
        self.eng.sem_inc(passed, 1)

    def end(self):
        assert self.turn is None or self.n == self.per_turn, f"this loop's turn has {self.n} steps"


class Steps:

    def __init__(self, sem, names, before=0):
        self.sem, self.names, self.before, self.order = sem, names, before, {n: k for k, n in enumerate(names)}
        assert len(self.order) == len(names)

    def at(self, name, turn=None):
        k = self.before + self.order[name] + 1
        return k if turn is None else turn * len(self.names) + k


@contextmanager
def phase(nc, tag, *names):
    sems = {n: nc.alloc_semaphore(f"{tag}_{n}") for n in names}
    yield sems
    nc.clear_and_free_semaphores(list(sems.values()))
    nc.all_engine_barrier()


def row_of(ap, k):
    return ap.unsqueeze(1).to_broadcast([ap.shape[0], k, ap.shape[1]])


def col_of(ap, n):
    return ap.unsqueeze(2).to_broadcast([ap.shape[0], ap.shape[1], n])


def build_constants(nc, c):
    with phase(nc, "constants", "pool_made", "made", "chain") as s:
        with nc.Block() as block:
            @block.gpsimd
            def _(pool):
                own = Chain(pool, s["pool_made"])
                own(nc.gpsimd.iota(c["iota_i"][:], [[1, 256]], base=0, channel_multiplier=0))
                own(nc.gpsimd.iota(c["part_i"][:], [[0, 1]], base=0, channel_multiplier=1))

            @block.vector
            def _(dve):
                own = Chain(dve, s["chain"])
                dve.wait_ge(s["pool_made"], 2)
                own(nc.vector.tensor_copy(c["iota"][:], c["iota_i"][:]))
                own(nc.vector.tensor_copy(c["part"][:], c["part_i"][:]))
                own(nc.vector.memset(c["ones"][:], 1.0))
                own(nc.vector.memset(c["zeros"][:], 0.0))
                own(nc.vector.tensor_scalar(c["ident"][:], c["iota"][:, 0:128], c["part"][:], None, ALU.is_equal))
                own(nc.vector.tensor_scalar(c["lower"][:], c["iota"][:, 0:128], c["part"][:], None, ALU.is_lt))
                for h in range(4):
                    own(nc.vector.tensor_scalar(c["block4"][:, h:h + 1], c["part"][:], h * 32 - 0.5, None, ALU.is_gt))
                    own(nc.vector.tensor_scalar(c["tmp1"][:], c["part"][:], h * 32 + 31.5, None, ALU.is_lt))
                    own(nc.vector.tensor_tensor(c["block4"][:, h:h + 1], c["block4"][:, h:h + 1], c["tmp1"][:], ALU.mult))
                own(nc.vector.tensor_copy(c["block"][:].rearrange("p (h x) -> p h x", x=32), col_of(c["block4"][:], 32)))


def build_edge_numbers(nc, c, e, src, dst, edge_type, edge_weight, edge_attr):
    with phase(nc, "numbers", "edges_in", "chain") as s, nc.Block() as block:
        @block.sync
        def _(sp):
            for to, frm in ((e["src_i"], src), (e["dst_i"], dst), (e["typ_i"], edge_type)):
                sp.dma_start(to[:], frm.rearrange("(p c) -> p c", p=R)).then_inc(s["edges_in"], 16)
            sp.dma_start(e["weight"][:], edge_weight.rearrange("(p c) -> p c", p=R)).then_inc(s["edges_in"], 16)
            sp.dma_start(e["attr"][:], edge_attr.rearrange("(p c) k -> p (c k)", p=R)).then_inc(s["edges_in"], 16)

        @block.vector
        def _(dve):
            own = Chain(dve, s["chain"])
            dve.wait_ge(s["edges_in"], 80)
            v = nc.vector
            for side in ("src", "dst"):
                ids, lo, hi, cmp, it = e[side][:], e[side + "_lo"][:], e[side + "_hi"][:], e["tmp"][:], e["tmp_i"][:]
                own(v.tensor_copy(ids, e[side + "_i"][:]))
                own(v.tensor_scalar(hi, ids, 1.0 / R, None, ALU.mult))
                own(v.tensor_copy(it, hi))
                own(v.tensor_copy(hi, it))
                own(v.scalar_tensor_tensor(lo, hi, -float(R), ids, ALU.mult, ALU.add))
                own(v.tensor_scalar(cmp, lo, 0.0, None, ALU.is_lt))
                own(v.scalar_tensor_tensor(lo, cmp, float(R), lo, ALU.mult, ALU.add))
                own(v.scalar_tensor_tensor(hi, cmp, -1.0, hi, ALU.mult, ALU.add))
                own(v.tensor_scalar(cmp, lo, float(R), None, ALU.is_ge))
                own(v.scalar_tensor_tensor(lo, cmp, -float(R), lo, ALU.mult, ALU.add))
                own(v.tensor_tensor(hi, cmp, hi, ALU.add))
            own(v.tensor_copy(e["tmp"][:], e["typ_i"][:]))
            own(v.scalar_tensor_tensor(e["slot"][:], e["src_hi"][:], float(TYPES), e["tmp"][:], ALU.mult, ALU.add))
            own(v.scalar_tensor_tensor(e["tmp"][:], e["dst"][:], float(TYPES), e["tmp"][:], ALU.mult, ALU.add))
            own(v.tensor_copy(e["rel_i"][:], e["tmp"][:]))


def build_scatter_rows(nc, c, e, dram):
    sides = ("src", "dst")
    with ExitStack() as ctx:
        sb = lambda n, sh, d=F32: ctx.enter_context(nc.sbuf_tensor(n, sh, d))
        diag = [sb(f"diag{k}", [R, G * R]) for k in range(2)]
        same = [sb(f"same{k}", [R, G * R]) for k in range(2)]
        rowp = [ctx.enter_context(nc.psum_tensor(f"rowp{k}", [R, 512], F32)) for k in range(2)]
        with phase(nc, "scatter_rows", "diag_ready", "row_ready", "chain", "stored") as s, nc.Block() as block:
            @block.vector
            def _(dve):
                v = nc.vector
                with dve.Fori(0, CHUNKS // G) as i:
                    own = Chain(dve, s["chain"], i, 6)
                    for k, side in enumerate(sides):
                        v.tensor_tensor(diag[k][:].rearrange("p (g j) -> p g j", g=G), row_of(c["ident"][0:R, 0:R], G),
                                        col_of(e[side][:, bass.ds(i * G, G)], R), ALU.mult).then_inc(s["diag_ready"], 1)
                    for k, side in enumerate(sides):
                        same3 = same[k][:].rearrange("p (g j) -> p g j", g=G)
                        dve.wait_ge(s["row_ready"], i * 2 + k + 1)
                        own(v.tensor_tensor(same3, rowp[k][:, 0:G * R].rearrange("p (g j) -> p g j", g=G),
                                            col_of(e[side][:, bass.ds(i * G, G)], R), ALU.is_equal))
                        own(v.tensor_tensor(same3, same3, row_of(c["lower"][0:R, 0:R], G), ALU.mult))
                        own(v.tensor_reduce(e[side + "_dup"][:, bass.ds(i * G, G)], same3, AX, ALU.max))
                    own.end()
                after = Chain(dve, s["chain"], before=6 * (CHUNKS // G))
                for side in sides:
                    dup, t = e[side + "_dup"][:], e["tmp"][:]
                    after(v.tensor_scalar(t, e[side][:], c["part"][0:R, :], -float(NODES), ALU.subtract, ALU.add))
                    after(v.tensor_tensor(t, t, dup, ALU.mult))
                    after(v.tensor_tensor(t, e[side][:], t, ALU.subtract))
                    after(v.tensor_copy(e["tmp_i"][:] if side == "src" else e["typ_i"][:], t))
                    after(v.tensor_scalar(dup, dup, -1.0, 1.0, ALU.mult, ALU.add))

            @block.tensor
            def _(pe):
                with pe.Fori(0, CHUNKS // G) as i:
                    for k in range(2):
                        pe.wait_ge(s["diag_ready"], i * 2 + k + 1)
                        nc.tensor.matmul(rowp[k][:, 0:G * R], c["ones"][0:R, 0:R], diag[k][:], start=True, stop=True).then_inc(s["row_ready"], 1)

            @block.sync
            def _(sp):
                sp.wait_ge(s["chain"], 6 * (CHUNKS // G) + 10)
                sp.dma_start(dram["src_row"], e["tmp_i"][:]).then_inc(s["stored"], 16)
                sp.dma_start(dram["dst_row"], e["typ_i"][:]).then_inc(s["stored"], 16)
                sp.dma_start(dram["rel"], e["rel_i"][:]).then_inc(s["stored"], 16)
                sp.wait_ge(s["stored"], 48)


def build_degrees(nc, c, e, deg3, relcnt):
    KD, KT = 3 * TILES, TILES * TYPES
    with ExitStack() as ctx:
        sb = lambda n, sh, d=F32: ctx.enter_context(nc.sbuf_tensor(n, sh, d))
        hot_d, hot_s = [[sb(f"hot_{n}{l}", [R, G, R]) for l in range(LANES)] for n in "ds"]
        pay_d = [sb(f"pay_d{l}", [R, G, 3, TILES]) for l in range(LANES)]
        pay_s = [sb(f"pay_s{l}", [R, G, KT]) for l in range(LANES)]
        acc_d = ctx.enter_context(nc.psum_tensor("acc_d", [R, KD], F32))
        acc_s = ctx.enter_context(nc.psum_tensor("acc_s", [R, KT], F32))
        with phase(nc, "degrees", "hots_ready", "summed", "chain") as s, nc.Block() as block:
            @block.vector
            def _(dve):
                v = nc.vector
                with dve.Fori(0, TURNS) as i:
                    own = Chain(dve, s["chain"], i, LANES)
                    for l in range(LANES):
                        cs = bass.ds(i * UNIT + l * G, G)
                        dve.wait_ge(s["summed"], i * LANES + l + 1)
                        v.tensor_tensor(hot_d[l][:], row_of(c["iota"][0:R, 0:R], G), col_of(e["dst_lo"][:, cs], R), ALU.is_equal)
                        v.tensor_tensor(hot_s[l][:], row_of(c["iota"][0:R, 0:R], G), col_of(e["src_lo"][:, cs], R), ALU.is_equal)
                        v.tensor_tensor(pay_s[l][:], row_of(c["iota"][0:R, 0:KT], G), col_of(e["slot"][:, cs], KT), ALU.is_equal)
                        own(v.tensor_tensor(pay_d[l][:, :, 0, :], row_of(c["iota"][0:R, 0:TILES], G),
                                            col_of(e["dst_hi"][:, cs], TILES), ALU.is_equal))
                        v.tensor_tensor(pay_d[l][:, :, 1, :], pay_d[l][:, :, 0, :], col_of(e["weight"][:, cs], TILES), ALU.mult)
                        v.tensor_tensor(pay_d[l][:, :, 2, :], pay_d[l][:, :, 0, :],
                                        col_of(e["attr"][:, cs], TILES), ALU.mult).then_inc(s["hots_ready"], 1)
                    own.end()
                dve.wait_ge(s["summed"], LANES * (TURNS + 1) + 1)
                v.tensor_copy(deg3, acc_d[:])
                v.tensor_copy(relcnt, acc_s[:])

            @block.tensor
            def _(pe):
                t = nc.tensor
                t.matmul(acc_d[:], c["zeros"][0:R, 0:R], c["zeros"][0:R, 0:KD], start=True, stop=False, skip_group_check=True)
                t.matmul(acc_s[:], c["zeros"][0:R, 0:R], c["zeros"][0:R, 0:KT], start=True, stop=False,
                         skip_group_check=True).then_inc(s["summed"], LANES)
                with pe.Fori(0, TURNS) as i:
                    for l in range(LANES):
                        pe.wait_ge(s["hots_ready"], i * LANES + l + 1)
                        for g in range(G):
                            t.matmul(acc_d[:], hot_d[l][:, g, :], pay_d[l][:, g].rearrange("p k t -> p (k t)"),
                                     start=False, stop=False, skip_group_check=True)
                            last = t.matmul(acc_s[:], hot_s[l][:, g, :], pay_s[l][:, g, :],
                                            start=False, stop=False, skip_group_check=True)
                        last.then_inc(s["summed"], 1)
                t.matmul(acc_d[:], c["zeros"][0:R, 0:R], c["zeros"][0:R, 0:KD], start=False, stop=True, skip_group_check=True)
                t.matmul(acc_s[:], c["zeros"][0:R, 0:R], c["zeros"][0:R, 0:KT], start=False, stop=True,
                         skip_group_check=True).then_inc(s["summed"], 1)


def build_node_gather(nc, c, tag, table, keys_lo, keys_slot, slots, heads, out):
    K = slots * heads
    with ExitStack() as ctx:
        sb = lambda n, sh, d=F32: ctx.enter_context(nc.sbuf_tensor(f"{tag}_{n}", sh, d))
        ps = lambda n, sh: ctx.enter_context(nc.psum_tensor(f"{tag}_{n}", sh, F32))
        diag = [sb(f"diag{l}", [R, G, R]) for l in range(LANES)]
        hot = [sb(f"hot{l}", [R, G, R]) for l in range(LANES)]
        mask = [sb(f"mask{l}", [R, G, slots]) for l in range(LANES)]
        picked = [sb(f"picked{l}", [R, G, slots, heads]) for l in range(LANES)]
        rowp = [ps(f"rowp{l}", [R, 512]) for l in range(LANES)]
        rows = [ps(f"rows{l}", [R, G, 256]) for l in range(LANES)]
        with phase(nc, tag, "diag_ready", "row_ready", "hot_ready", "rows_ready", "chain") as s, nc.Block() as block:
            @block.vector
            def _(dve):
                v = nc.vector
                with dve.Fori(0, TURNS) as i:
                    own = Chain(dve, s["chain"], i, 3 * LANES)
                    cs = [bass.ds(i * UNIT + l * G, G) for l in range(LANES)]
                    for l in range(LANES):
                        v.tensor_tensor(diag[l][:], row_of(c["ident"][0:R, 0:R], G), col_of(keys_lo[:, cs[l]], R),
                                        ALU.mult).then_inc(s["diag_ready"], 1)
                    for l in range(LANES):
                        dve.wait_ge(s["row_ready"], i * LANES + l + 1)
                        v.tensor_scalar(hot[l][:].rearrange("p g j -> p (g j)"), rowp[l][:, 0:G * R], c["part"][0:R, :],
                                        None, ALU.is_equal).then_inc(s["hot_ready"], 1)
                        own(v.tensor_tensor(mask[l][:], row_of(c["iota"][0:R, 0:slots], G), col_of(keys_slot[:, cs[l]], slots),
                                            ALU.is_equal))
                    for l in range(LANES):
                        dve.wait_ge(s["rows_ready"], i * LANES + l + 1)
                        own(v.tensor_tensor(picked[l][:], rows[l][:, :, 0:K].rearrange("p g (k h) -> p g k h", h=heads),
                                            mask[l][:].unsqueeze(3).to_broadcast([R, G, slots, heads]), ALU.mult))
                        own(v.tensor_reduce(out[:, cs[l], :], picked[l][:].rearrange("p g k h -> p g h k"), AX, ALU.add))
                    own.end()

            @block.tensor
            def _(pe):
                with pe.Fori(0, TURNS) as i:
                    for l in range(LANES):
                        pe.wait_ge(s["diag_ready"], i * LANES + l + 1)
                        nc.tensor.matmul(rowp[l][:, 0:G * R], c["ones"][0:R, 0:R], diag[l][:].rearrange("p g j -> p (g j)"),
                                         start=True, stop=True).then_inc(s["row_ready"], 1)
                    for l in range(LANES):
                        pe.wait_ge(s["hot_ready"], i * LANES + l + 1)
                        for g in range(G):
                            last = nc.tensor.matmul(rows[l][:, g, 0:K], hot[l][:, g, :], table, start=True, stop=True)
                        last.then_inc(s["rows_ready"], 1)


def build_segment_max(nc, c, e, tag, score, heads, top):
    H1 = heads + 1
    with ExitStack() as ctx:
        sb = lambda n, sh, d=F32: ctx.enter_context(nc.sbuf_tensor(f"{tag}_{n}", sh, d))
        ps = lambda n, sh: ctx.enter_context(nc.psum_tensor(f"{tag}_{n}", sh, F32))
        diag = [[sb(f"diag{l}_{h}", [R, G, R]) for h in range(H1)] for l in range(LANES)]
        other = [sb(f"other{l}", [R, G, R]) for l in range(LANES)]
        masked = [sb(f"masked{l}", [R, G, R]) for l in range(LANES)]
        hot = [sb(f"hot{l}", [R, G, R]) for l in range(LANES)]
        best = [sb(f"best{l}", [R, heads, G]) for l in range(LANES)]
        pay = [sb(f"pay{l}", [R, G, H1, TILES]) for l in range(LANES)]
        cand = [sb(f"cand{l}", [R, G, H1, TILES]) for l in range(LANES)]
        most = [sb(f"most{l}", [R, heads, TILES]) for l in range(LANES)]
        rowp = [ps(f"rowp{l}", [R, 512]) for l in range(LANES)]
        scorep = [ps(f"scorep{l}", [R, 512]) for l in range(LANES)]
        placed = [ps(f"placed{l}", [R, G, 128]) for l in range(LANES)]
        SIG = H1 * LANES
        with phase(nc, tag, "diag_ready", "row_ready", "score_free", "pay_ready", "placed_ready", "chain") as s, nc.Block() as block:
            @block.vector
            def _(dve):
                v = nc.vector
                before = Chain(dve, s["chain"])
                before(v.memset(top, -HUGE))
                PER = LANES * (2 * heads + 7)
                with dve.Fori(0, TURNS) as i:
                    own = Chain(dve, s["chain"], i, PER, before=1)
                    cs = [bass.ds(i * UNIT + l * G, G) for l in range(LANES)]
                    for l in range(LANES):
                        v.tensor_tensor(diag[l][0][:], row_of(c["ident"][0:R, 0:R], G), col_of(e["dst"][:, cs[l]], R),
                                        ALU.mult).then_inc(s["diag_ready"], 1)
                        for h in range(heads):
                            v.tensor_tensor(diag[l][1 + h][:], row_of(c["ident"][0:R, 0:R], G), col_of(score[:, cs[l], h], R),
                                            ALU.mult).then_inc(s["diag_ready"], 1)
                    for l in range(LANES):
                        dve.wait_ge(s["row_ready"], i * SIG + l * H1 + 1)
                        own(v.tensor_tensor(other[l][:], rowp[l][:, 0:G * R].rearrange("p (g j) -> p g j", g=G),
                                            col_of(e["dst"][:, cs[l]], R), ALU.not_equal))
                        for h in range(heads):
                            dve.wait_ge(s["row_ready"], i * SIG + l * H1 + 2 + h)
                            v.scalar_tensor_tensor(masked[l][:].rearrange("p g j -> p (g j)"), other[l][:].rearrange("p g j -> p (g j)"),
                                                   -HUGE, scorep[l][:, 0:G * R], ALU.mult, ALU.add).then_inc(s["score_free"], 1)
                            dve.wait_ge(s["score_free"], (i * LANES + l) * heads + h + 1)
                            own(v.tensor_reduce(best[l][:, h, :], masked[l][:], AX, ALU.max))
                        own(v.tensor_tensor(hot[l][:], row_of(c["iota"][0:R, 0:R], G), col_of(e["dst_lo"][:, cs[l]], R), ALU.is_equal))
                        own(v.tensor_tensor(cand[l][:, :, heads, :], row_of(c["iota"][0:R, 0:TILES], G),
                                            col_of(e["dst_hi"][:, cs[l]], TILES), ALU.is_equal))
                        own(v.tensor_tensor(pay[l][:, :, heads, :], cand[l][:, :, heads, :], col_of(e["dst_dup"][:, cs[l]], TILES), ALU.mult))
                        for h in range(heads):
                            last = v.tensor_tensor(pay[l][:, :, h, :], pay[l][:, :, heads, :], col_of(best[l][:, h, :], TILES), ALU.mult)
                            if h < heads - 1:
                                own(last)
                        last.then_inc(s["pay_ready"], 1)
                    for l in range(LANES):
                        dve.wait_ge(s["placed_ready"], i * LANES + l + 1)
                        there = cand[l][:, :, heads, :]
                        own(v.tensor_scalar(there, placed[l][:, :, heads * TILES:H1 * TILES], 1.0, HUGE, ALU.subtract, ALU.mult))
                        own(v.tensor_tensor(cand[l][:, :, 0:heads, :], placed[l][:, :, 0:heads * TILES].rearrange("p g (h t) -> p g h t", h=heads),
                                            there.unsqueeze(2).to_broadcast([R, G, heads, TILES]), ALU.add))
                        own(v.tensor_reduce(most[l][:], cand[l][:, :, 0:heads, :].rearrange("p g h t -> p h t g"), AX, ALU.max))
                        own(v.tensor_tensor(top, top, most[l][:], ALU.max))
                    own.end()

            @block.tensor
            def _(pe):
                t = nc.tensor
                with pe.Fori(0, TURNS) as i:
                    for l in range(LANES):
                        for h in range(H1):
                            pe.wait_ge(s["diag_ready"], i * SIG + l * H1 + h + 1)
                            if h >= 2:
                                pe.wait_ge(s["score_free"], (i * LANES + l) * heads + h - 1)
                            to = rowp[l] if h == 0 else scorep[l]
                            t.matmul(to[:, 0:G * R], c["ones"][0:R, 0:R], diag[l][h][:].rearrange("p g j -> p (g j)"),
                                     start=True, stop=True).then_inc(s["row_ready"], 1)
                    for l in range(LANES):
                        pe.wait_ge(s["pay_ready"], i * LANES + l + 1)
                        for g in range(G):
                            last = t.matmul(placed[l][:, g, 0:H1 * TILES], hot[l][:, g, :], pay[l][:, g].rearrange("p h t -> p (h t)"),
                                            start=True, stop=True)
                        last.then_inc(s["placed_ready"], 1)


def build_messages(nc, c, e, tag, table, take, put, node, weight, heads, acc):
    W = D + heads
    C = D // heads
    with ExitStack() as ctx:
        sb = lambda n, sh, d=F32: ctx.enter_context(nc.sbuf_tensor(f"{tag}_{n}", sh, d))
        take_b = [sb(f"take{l}", [R, G], I32) for l in range(LANES)]
        put_b = [sb(f"put{l}", [R, G], I32) for l in range(LANES)]
        rows = [sb(f"rows{l}", [R, G, W]) for l in range(LANES)]
        zrow = sb("zrow", [R, (NODES + R) // 2 // R * W])
        sent = [sb(f"sent{l}", [R, G, W]) for l in range(LANES)]
        diag = [sb(f"diag{l}", [R, G, R]) for l in range(LANES)]
        same = [sb(f"same{l}", [R, G, R]) for l in range(LANES)]
        rowp = [ctx.enter_context(nc.psum_tensor(f"{tag}_rowp{l}", [R, 512], F32)) for l in range(LANES)]
        sum_p = [ctx.enter_context(nc.psum_tensor(f"{tag}_sum{g}", [R, 512], F32)) for g in range(G)]
        names = ([f"take_in{l}" for l in range(LANES)] + [f"put_in{l}" for l in range(LANES)] + [f"rows_in{l}" for l in range(LANES)]
                 + [f"acc_done{g}" for g in range(G)] + ["made", "zeroed", "diag_ready", "row_ready", "same_ready", "scaled", "summed", "moved", "pool_at"])
        with phase(nc, tag, *names) as s, nc.Block() as block:
            @block.sync
            def _(sp):
                sp.wait_ge(s["made"], 1)
                half = (NODES + R) // 2
                for k in range(ACCS):
                    for part in range(2):
                        sp.dma_start(acc[k][part * half:(part + 1) * half].rearrange("(p n) d -> p (n d)", p=R),
                                     zrow[:]).then_inc(s["zeroed"], 16)

                def loads(i, first=False):
                    for l in range(LANES):
                        cs = bass.ds(i * UNIT + l * G, G)
                        if not first:
                            sp.wait_ge(s[f"rows_in{l}"], i * (16 * G))
                        sp.dma_start(take_b[l][:], take[:, cs]).then_inc(s[f"take_in{l}"], 16)
                        if not first:
                            for g in range(G):
                                sp.wait_ge(s[f"acc_done{g}"], i * (16 * LANES) + 16 * (l - LANES + 1))
                        sp.dma_start(put_b[l][:], put[:, cs]).then_inc(s[f"put_in{l}"], 16)
                loads(0, first=True)
                with sp.Fori(1, TURNS) as i:
                    loads(i)

            @block.vector
            def _(dve):
                v = nc.vector
                with dve.Fori(0, TURNS) as i:
                    cs = [bass.ds(i * UNIT + l * G, G) for l in range(LANES)]
                    for l in range(LANES):
                        v.tensor_tensor(diag[l][:], row_of(c["ident"][0:R, 0:R], G), col_of(node[:, cs[l]], R),
                                        ALU.mult).then_inc(s["diag_ready"], 1)
                    for l in range(LANES):
                        dve.wait_ge(s["row_ready"], i * LANES + l + 1)
                        v.tensor_tensor(same[l][:], rowp[l][:, 0:G * R].rearrange("p (g j) -> p g j", g=G),
                                        col_of(node[:, cs[l]], R), ALU.is_equal).then_inc(s["same_ready"], 1)
                    for l in range(LANES):
                        dve.wait_ge(s[f"rows_in{l}"], i * (16 * G) + 16 * G)
                        v.tensor_copy(rows[l][:, :, D:W], weight[:, cs[l], :])
                        vw = rows[l][:, :, 0:D].rearrange("p g (h x) -> p g h x", h=heads)
                        v.tensor_tensor(vw, vw, weight[:, cs[l], :].unsqueeze(3).to_broadcast([R, G, heads, C]),
                                        ALU.mult).then_inc(s["scaled"], 1)

            @block.tensor
            def _(pe):
                t = nc.tensor
                pe.sem_inc(s["summed"], G)
                with pe.Fori(0, TURNS) as i:
                    for l in range(LANES):
                        pe.wait_ge(s["diag_ready"], i * LANES + l + 1)
                        t.matmul(rowp[l][:, 0:G * R], c["ones"][0:R, 0:R], diag[l][:].rearrange("p g j -> p (g j)"),
                                 start=True, stop=True).then_inc(s["row_ready"], 1)
                    for l in range(LANES):
                        pe.wait_ge(s["same_ready"], i * LANES + l + 1)
                        pe.wait_ge(s["scaled"], i * LANES + l + 1)
                        for g in range(G):
                            pe.wait_ge(s["moved"], i * UNIT + l * G + g + 1)
                            t.matmul(sum_p[g][:, 0:W], same[l][:, g, :], rows[l][:, g, :], start=True, stop=True).then_inc(s["summed"], 1)

            @block.scalar
            def _(act):
                act.sem_inc(s["moved"], G)

                def move(i, first=False):
                    for l in range(LANES):
                        for g in range(G):
                            act.wait_ge(s["summed"], i * UNIT + (l + 1) * G + g + 1)
                            if not first:
                                act.wait_ge(s[f"acc_done{g}"], i * (16 * LANES))
                            nc.scalar.copy(sent[l][:, g, :], sum_p[g][:, 0:W]).then_inc(s["moved"], 1)

                move(0, first=True)
                with act.Fori(1, TURNS) as i:
                    move(i)

            @block.gpsimd
            def _(pool):
                nc.gpsimd.memset(zrow[:], 0.0).then_inc(s["made"], 1)

                def gather(i, l, first=False):
                    pool.wait_ge(s[f"take_in{l}"], i * 16 + 16)
                    if l or not first:
                        pool.wait_ge(s["summed"], i * UNIT + l * G)
                    pool.sem_inc(s["pool_at"], 1)
                    for g in range(G):
                        nc.gpsimd.indirect_dma_start(rows[l][:, g, 0:D], None, table, bass.IndirectOffsetOnAxis(ap=take_b[l][:, g:g + 1], axis=0)
                                                     ).then_inc(s[f"rows_in{l}"], 16)

                def scatter(i, l, first=False):
                    pool.wait_ge(s[f"put_in{l}"], i * 16 + 16)
                    for g in range(G):
                        pool.wait_ge(s["moved"], i * UNIT + (l + 1) * G + g + 1)
                        if not first:
                            pool.wait_ge(s[f"acc_done{g}"], i * (16 * LANES) + 16 * l)
                        pool.sem_inc(s["pool_at"], 1)
                        nc.gpsimd.indirect_dma_start(acc[g], bass.IndirectOffsetOnAxis(ap=put_b[l][:, g:g + 1], axis=0), sent[l][:, g, :], None,
                                                     compute_op=ALU.add).then_inc(s[f"acc_done{g}"], 16)

                gather(0, 0, first=True)
                gather(0, 1)
                pool.wait_ge(s["zeroed"], 16 * 2 * ACCS)
                scatter(0, 0, first=True)
                gather(1, 0)
                scatter(0, 1)
                with pool.Fori(1, TURNS - 1) as i:
                    gather(i, 1)
                    scatter(i, 0)
                    gather(i + 1, 0)
                    scatter(i, 1)
                gather(TURNS - 1, 1)
                scatter(TURNS - 1, 0)
                scatter(TURNS - 1, 1)
                for g in range(G):
                    pool.wait_ge(s[f"acc_done{g}"], 16 * LANES * TURNS)



def until(eng, steps, name, turn=None):
    eng.wait_ge(steps.sem, steps.at(name, turn))


def mark(ins, steps):
    ins.then_inc(steps.sem, 1)


def by_tile(ap):
    return ap.rearrange("(t r) w -> r t w", r=R)


def slices(ap):
    return ap[:, 0:GT * 128].rearrange("p (s x) -> p s x", x=128)[:, :, 0:R]


def dense(ap):
    return ap.rearrange("p (s x) -> p s x", x=R)


def turn_tiles(nc, c, to, tile, blocks=KB):
    for k in range(blocks):
        for j in range(GT):
            q = k * GT + j
            last = nc.tensor.transpose(to[:, q * 128:q * 128 + R], tile[:, j, k * 128:(k + 1) * 128], c["ident"][0:R, 0:R])
    return last


def turned(ap, blocks=KB):
    return ap[:, 0:blocks * GT * 128].rearrange("p (q x) -> p q x", x=128)[:, :, 0:R]


def product_t(nc, to, m, pairs):
    first, second = to[0:m, 0:512].rearrange("p (s x) -> p s x", x=128)[:, :, 0:R], to[0:m, 512:512 + R]
    n = len(pairs)
    for a, (w, f) in enumerate(pairs):
        nc.tensor.matmul(first, w, f[:, 0:4 * R].rearrange("p (s x) -> p s x", x=R), start=(a == 0), stop=(a == n - 1))
    for a, (w, f) in enumerate(pairs):
        last = nc.tensor.matmul(second, w, f[:, 4 * R:GN], start=(a == 0), stop=(a == n - 1))
    return last


def product_rows(nc, to, pairs):
    n = len(pairs)
    for j in range(GT):
        for a, (f, w) in enumerate(pairs):
            last = nc.tensor.matmul(to[:, j, :], f[:, j * R:(j + 1) * R], w, start=(a == 0), stop=(a == n - 1))
    return last


def variance(v, own, x, b, eps, passed):
    for j in range(GT):
        last = v.bn_stats(b["stats"][:, j, :], x[:, j, :])
    own(last)
    own.pause(passed)
    for j in range(GT):
        last = v.bn_aggr(b["mv"][:, j, :], b["stats"][:, j, :])
    own(last)
    return v.tensor_scalar(b["var"][:], b["mv"][:, :, 1], eps, None, ALU.add)


VARIANCE_STEPS = 2


def standardize(v, own, x, out, b):
    own(v.reciprocal(b["rstd"][:], b["std"][:]))
    for j in range(GT):
        last = v.tensor_scalar(out[:, j, :], x[:, j, :], b["mv"][:, j, 0:1], b["rstd"][:, j:j + 1], ALU.subtract, ALU.mult)
    return last


STANDARDIZE_STEPS = 1


def norm_buffers(sb):
    return {"stats": sb("stats", [R, GT, 6]), "mv": sb("mv", [R, GT, 2]), "var": sb("var", [R, GT]),
            "std": sb("std", [R, GT]), "rstd": sb("rstd", [R, GT])}


def build_open(nc, c, layer, X, XN, XNT, loads, units, post, stores, kv, kv_cols, per_turn, hand=()):
    tag = f"open{layer}"
    NU = len(units(None))
    UNITS = [f"u{n}" for n in range(NU * GT)]
    with ExitStack() as ctx:
        sb = lambda n, sh, d=F32: ctx.enter_context(nc.sbuf_tensor(f"{tag}_{n}", sh, d))
        ps = lambda n, sh: ctx.enter_context(nc.psum_tensor(f"{tag}_{n}", sh, F32))
        b = norm_buffers(sb)
        xn_s, xT = sb("xn_s", [R, GT, D]), sb("xT", [128, KB, GN])
        st = sb("st", [R, GT, max(sum(n for _, n in units(None)), 1)])
        b["st"], b["xn_s"] = st, xn_s
        wide, unit_p, kv_p = ps("wide", [128, 1536]), [ps(f"unit{n}", [R, 512]) for n in range(4)], ps("kv_p", [128, KB, 256])
        w, w_loads = loads(sb)
        b.update(w)
        with phase(nc, tag, "loaded", "pe", "dve", "act", "stored", "chain", "passed", "sp_passed") as s, nc.Block() as block:
            PE = Steps(s["pe"], ["turn"] + UNITS + ["kv_added"])
            HANDS = [f"hand{n}" for n in range(len(hand))]
            DV = Steps(s["dve"], ["var", "xn"] + HANDS + ["post"])
            AC = Steps(s["act"], ["std", "keep", "turned", "all_turned"] + UNITS + HANDS)
            NS = stores(None, b, None)

            @block.sync
            def _(sp):
                for to, frm in w_loads:
                    sp.dma_start(to, frm).then_inc(s["loaded"], 16)
                with sp.Fori(0, GROUPS) as i:
                    until(sp, DV, "post", i)
                    sp.sem_inc(s["sp_passed"], 1)
                    if NS:
                        stores(sp, b, i, s["stored"])
                if NS:
                    sp.wait_ge(s["stored"], 16 * NS * GROUPS)

            @block.vector
            def _(dve):
                v = nc.vector
                dve.wait_ge(s["loaded"], 16 * len(w_loads))
                with dve.Fori(0, GROUPS) as i:
                    own = Chain(dve, s["chain"], i, VARIANCE_STEPS + STANDARDIZE_STEPS + per_turn)
                    grp = bass.ds(i * GT, GT)
                    mark(variance(v, own, X[:, grp, :], b, 1e-5, s["passed"]), DV)
                    until(dve, AC, "std", i)
                    mark(standardize(v, own, X[:, grp, :], xn_s, b), DV)
                    until(dve, DV, "xn", i)
                    until(dve, AC, (UNITS or ["all_turned"])[-1], i)
                    handed = iter(HANDS)

                    def hand_over(ins):
                        mark(ins, DV)
                        until(dve, AC, next(handed), i)

                    mark(post(v, own, hand_over, b, grp), DV)
                    own.end()
                    until(dve, PE, "kv_added", i)
                    until(dve, AC, "all_turned", i)
                    if NS:
                        dve.wait_ge(s["stored"], i * (16 * NS) + 16 * NS)

            @block.scalar
            def _(act):
                a = nc.scalar
                with act.Fori(0, GROUPS) as i:
                    grp = bass.ds(i * GT, GT)
                    until(act, DV, "var", i)
                    mark(a.activation(b["std"][:], b["var"][:], ACT.Sqrt), AC)
                    until(act, DV, "xn", i)
                    mark(a.copy(XN[:, grp, :], xn_s[:]), AC)
                    until(act, PE, "turn", i)
                    mark(a.copy(xT[:].rearrange("p k (j x) -> p (k j) x", x=R), turned(wide[:])), AC)
                    until(act, AC, "turned", i)
                    mark(a.copy(XNT[:, :, bass.ds(i * GN, GN)], xT[:]), AC)
                    at = 0
                    for u, name in enumerate(UNITS):
                        n = units(None)[u % NU][1]
                        until(act, PE, name, i)
                        mark(a.copy(st[:, u // NU, at:at + n], unit_p[u % 4][:, 0:n]), AC)
                        at = (at + n) % st.shape[2]
                    for n, name in enumerate(HANDS):
                        until(act, DV, name, i)
                        mark(a.activation(b["hand_out"], b["hand_in"], hand[n]), AC)
                    until(act, DV, "post", i)
                    until(act, PE, "kv_added", i)
                    if NS:
                        act.wait_ge(s["stored"], i * (16 * NS) + 16 * NS)

            @block.tensor
            def _(pe):
                t = nc.tensor
                pe.wait_ge(s["loaded"], 16 * len(w_loads))
                for k in range(KB):
                    t.matmul(kv_p[:, k, :], c["zeros"][:, 0:128], c["zeros"][:, 0:256], start=(k == 0), stop=False, skip_group_check=True)
                with pe.Fori(0, GROUPS) as i:
                    until(pe, DV, "xn", i)
                    mark(turn_tiles(nc, c, wide, xn_s), PE)
                    until(pe, AC, "turned", i)
                    for u, name in enumerate(UNITS):
                        if u >= 4:
                            until(pe, AC, UNITS[u - 4], i)
                        j, (wk, n) = u // NU, units(w)[u % NU]
                        for k in range(KB):
                            last = t.matmul(unit_p[u % 4][:, 0:n], xT[:, k, j * R:(j + 1) * R], wk[k], start=(k == 0), stop=(k == KB - 1))
                        mark(last, PE)
                    until(pe, DV, "post", i)
                    if kv is None:
                        mark(t.matmul(kv_p[:, 0, :], c["zeros"][:, 0:128], c["zeros"][:, 0:256], start=False, stop=False, skip_group_check=True), PE)
                    else:
                        mark(kv(t, kv_p, b), PE)
                for k in range(KB):
                    last = t.matmul(kv_p[:, k, :], c["zeros"][:, 0:128], c["zeros"][:, 0:256], start=False, stop=True, skip_group_check=True)
        if kv_cols is None:
            return
        with phase(nc, tag + "_end", "chain") as s, nc.Block() as block:
            @block.vector
            def _(dve):
                v = nc.vector
                own = Chain(dve, s["chain"])
                kv_cols(v, own, kv_p, b)


def blocked(w, k):
    return w[k * 128:(k + 1) * 128]


def everywhere(vec, p=R):
    return vec.partition_broadcast(p)


def center_heads(v, own, x3, b, div, eps):
    n = x3.shape[1]
    own(v.tensor_reduce(b["hm"][:, 0:n], x3, AX, ALU.add))
    own(v.tensor_scalar(b["hm"][:, 0:n], b["hm"][:, 0:n], 1.0 / 32, None, ALU.mult))
    own(v.tensor_tensor(x3, x3, col_of(b["hm"][:, 0:n], 32), ALU.subtract))
    own(v.tensor_tensor(b["sq"][:, 0:n, :], x3, x3, ALU.mult))
    own(v.tensor_reduce(b["hm"][:, 0:n], b["sq"][:, 0:n, :], AX, ALU.add))
    return v.tensor_scalar(b["hand_in"], b["hm"][:, 0:n], 1.0 / div, eps, ALU.mult, ALU.add)


CENTER_STEPS = 5


def keep_blocks(c, scale, out, ones=False):
    def cols(v, own, kv_p, b):
        for k in range(KB):
            own(v.scalar_tensor_tensor(out[:, k, 0:128], kv_p[:, k, 0:128], scale, c["block"][:], ALU.mult, ALU.mult))
            if ones:
                own(v.tensor_scalar(out[:, k, 128:132], c["block4"][:], kv_p[:, k, 128:129], None, ALU.mult))
    return cols


def open0(nc, c, m, I, dram):
    def loads(sb):
        w = {"el": sb("w_el", [128, KB, 512]), "kv": sb("w_kv", [128, KB, 512]), "bias": sb("bias", [R, 1024]),
             "gain": sb("gain", [R, 512]), "shift": sb("shift", [R, 512]), "hm": sb("hm", [R, 16 * GT]), "sq": sb("sq", [R, 16 * GT, 32]),
             "hv": sb("hv", [R, 16 * GT]), "hs": sb("hs", [R, 16 * GT])}
        w["hand_in"], w["hand_out"] = w["hv"][:], w["hs"][:]
        l = []
        for k in range(KB):
            l += [(w["el"][:, k, 0:D], blocked(I["L0_gnn_W_src"], k)), (w["el"][:, k, D:512], blocked(I["L0_gnn_W_dst"], k)),
                  ] + [(w["kv"][:, k, n * D:(n + 1) * D].rearrange("p (h x) -> p h x", x=32),
                        blocked(I["L0_mix_w_qkv"], k).rearrange("p (h x) -> p h x", x=96)[:, :, 32 * n + 32:32 * n + 64]) for n in range(2)]
        l += [(w["bias"][:, 0:D], everywhere(I["L0_gnn_b_src"])), (w["bias"][:, D:512], everywhere(I["L0_gnn_b_dst"])),
              ] + [(w["bias"][:, 512 + n * D:512 + (n + 1) * D].rearrange("p (h x) -> p h x", x=32),
                    everywhere(I["L0_mix_b_qkv"]).rearrange("p (h x) -> p h x", x=96)[:, :, 32 * n + 32:32 * n + 64]) for n in range(2)]
        for to, kind in (("gain", "g"), ("shift", "b")):
            for n, of in enumerate("kv"):
                l.append((w[to][:, n * D:(n + 1) * D].rearrange("p (h x) -> p h x", x=32),
                          everywhere(I[f"L0_mix_{of}ln_{kind}"]).unsqueeze(1).to_broadcast([R, 8, 32])))
        return w, l

    def units(w):
        return [(w and [w[n][:, k, :] for k in range(KB)], 512) for n in ("el", "kv")]

    def post(v, own, hand_over, b, grp):
        own(v.tensor_tensor(b["st"][:], b["st"][:], row_of(b["bias"][:], GT), ALU.add))
        own(v.tensor_copy(b["sq"][:].rearrange("p (j h) x -> p j (h x)", j=GT), b["st"][:, :, 512:1024]))
        kv3 = b["st"][:, :, 512:1024].rearrange("p j (h x) -> p j h x", x=32)
        sq3, hm3 = b["sq"][:].rearrange("p (j h) x -> p j h x", j=GT), b["hm"][:].rearrange("p (j h) -> p j h", j=GT)
        own(v.tensor_reduce(b["hm"][:], b["sq"][:], AX, ALU.add))
        own(v.tensor_scalar(b["hm"][:], b["hm"][:], 1.0 / 32, None, ALU.mult))
        own(v.tensor_tensor(kv3, kv3, hm3.unsqueeze(3).to_broadcast([R, GT, 16, 32]), ALU.subtract))
        own(v.tensor_tensor(sq3, kv3, kv3, ALU.mult))
        own(v.tensor_reduce(b["hm"][:], b["sq"][:], AX, ALU.add))
        hand_over(v.tensor_scalar(b["hand_in"], b["hm"][:], 1.0 / 32, 1e-5, ALU.mult, ALU.add))
        own(v.reciprocal(b["hm"][:], b["hand_out"]))
        own(v.tensor_tensor(kv3, kv3, hm3.unsqueeze(3).to_broadcast([R, GT, 16, 32]), ALU.mult))
        own(v.tensor_tensor(b["st"][:, :, 512:1024], b["st"][:, :, 512:1024], row_of(b["gain"][:], GT), ALU.mult))
        return v.tensor_tensor(b["st"][:, :, 512:1024], b["st"][:, :, 512:1024], row_of(b["shift"][:], GT), ALU.add)

    def stores(sp, b, i, sem=None):
        if sp is not None:
            grp = bass.ds(i * GT, GT)
            sp.dma_start(by_tile(dram["el"])[:, grp], b["st"][:, :, 0:D]).then_inc(sem, 16)
            sp.dma_start(by_tile(dram["er"])[:, grp], b["st"][:, :, D:512]).then_inc(sem, 16)
        return 2

    def kv(t, kv_p, b):
        for j in range(GT):
            for k in range(KB):
                at = 512 + k * 128
                last = t.matmul(kv_p[:, k, 0:128], b["st"][:, j, at:at + 128], b["st"][:, j, at + D:at + D + 128], start=False, stop=False, skip_group_check=True)
        return last

    build_open(nc, c, 0, m["X"], m["XN"], m["XNT"], loads, units, post, stores, kv, keep_blocks(c, 1.0 / NODES, m["KV"]), 10, hand=(ACT.Sqrt,))


def open1(nc, c, m, I, dram):
    def loads(sb):
        w = {"rel": sb("w_rel", [128, KB, TYPES * D]), "hm": sb("hm", [R, 8 * GT]), "sq": sb("sq", [R, 8 * GT, 32]),
             "hv": sb("hv", [R, 8 * GT]), "hs": sb("hs", [R, 8 * GT]), "val": sb("val", [R, GT, D])}
        w["hand_in"], w["hand_out"] = w["hv"][:], w["hs"][:]
        l = [(w["rel"][:, k, :].rearrange("p (t o) -> p t o", t=TYPES),
              I["L1_gnn_weights"].rearrange("(t k p) o -> k p t o", t=TYPES, k=KB)[k]) for k in range(KB)]
        for n in ("kln_weight", "kln_bias", "vln_weight", "vln_bias"):
            w[n] = sb(n, [R, D])
            l.append((w[n][:], everywhere(I["L1_mix_" + n].rearrange("h o x -> (h o x)"))))
        return w, l

    def units(w):
        at = list(range(0, TYPES * D, 512))
        return [(w and [w["rel"][:, k, a:min(a + 512, TYPES * D)] for k in range(KB)], min(512, TYPES * D - a)) for a in at]

    def post(v, own, hand_over, b, grp):
        heads = b["xn_s"][:].rearrange("p j (h x) -> p (j h) x", x=32)
        hand_over(center_heads(v, own, heads, b, 31.0, 0.0))
        own(v.tensor_scalar(b["hm"][:], b["hand_out"], 1e-5, None, ALU.add))
        own(v.reciprocal(b["hm"][:], b["hm"][:]))
        own(v.tensor_tensor(heads, heads, col_of(b["hm"][:], 32), ALU.mult))
        own(v.tensor_tensor(b["val"][:], b["xn_s"][:], row_of(b["vln_weight"][:], GT), ALU.mult))
        own(v.tensor_tensor(b["val"][:], b["val"][:], row_of(b["vln_bias"][:], GT), ALU.add))
        own(v.tensor_tensor(b["xn_s"][:], b["xn_s"][:], row_of(b["kln_weight"][:], GT), ALU.mult))
        return v.tensor_tensor(b["xn_s"][:], b["xn_s"][:], row_of(b["kln_bias"][:], GT), ALU.add)

    def stores(sp, b, i, sem=None):
        if sp is not None:
            sp.dma_start(dram["rel_table"].rearrange("(t r s) d -> r t (s d)", r=R, s=TYPES)[:, bass.ds(i * GT, GT)], b["st"][:]).then_inc(sem, 16)
        return 1

    def kv(t, kv_p, b):
        for j in range(GT):
            for k in range(KB):
                cs = slice(k * 128, (k + 1) * 128)
                last = t.matmul(kv_p[:, k, 0:128], b["xn_s"][:, j, cs], b["val"][:, j, cs], start=False, stop=False, skip_group_check=True)
        return last

    build_open(nc, c, 1, m["X"], m["XN"], m["XNT"], loads, units, post, stores, kv, keep_blocks(c, 1.0 / NODES, m["KV"]), CENTER_STEPS + 6, hand=(ACT.Sqrt,))


def open2(nc, c, m, I, dram):
    def loads(sb):
        w = {"low": sb("low", [R, GT, D]), "exp": sb("exp", [R, GT, D]), "scaled": sb("scaled", [R, GT, D])}
        w["hand_in"], w["hand_out"] = w["low"][:], w["exp"][:]
        return w, []

    def units(w):
        return [([m["WT"][:, k, D:3 * D] for k in range(KB)], 512)]

    def post(v, own, hand_over, b, grp):
        own(v.tensor_tensor(b["scaled"][:], b["xn_s"][:], col_of(m["dinv"][:, grp], D), ALU.mult))
        hand_over(v.tensor_scalar(b["low"][:], b["st"][:, :, 0:D], 0.0, None, ALU.min))
        own(v.tensor_scalar(b["low"][:], b["st"][:, :, 0:D], 0.0, None, ALU.max))
        return v.tensor_tensor(b["low"][:], b["low"][:], b["exp"][:], ALU.add)

    def stores(sp, b, i, sem=None):
        if sp is not None:
            sp.dma_start(by_tile(dram["el"])[:, bass.ds(i * GT, GT)], b["scaled"][:]).then_inc(sem, 16)
        return 1

    def kv(t, kv_p, b):
        for j in range(GT):
            for k in range(KB):
                key = b["low"][:, j, k * 128:(k + 1) * 128]
                t.matmul(kv_p[:, k, 0:128], key, b["st"][:, j, D + k * 128:D + (k + 1) * 128], start=False, stop=False, skip_group_check=True)
                last = t.matmul(kv_p[:, k, 128:129], key, c["ones"][0:R, 0:1], start=False, stop=False, skip_group_check=True)
        return last

    build_open(nc, c, 2, m["X"], m["XN"], m["XNT"], loads, units, post, stores, kv, keep_blocks(c, 1.0, m["KV"], ones=True), 2, hand=(ACT.Exp,))


def open3(nc, c, m, I, dram):
    def loads(sb):
        w = {"xk": sb("w_xk", [128, KB, 512]), "att_src": sb("att_src", [R, D]), "att_dst": sb("att_dst", [R, D]), "prod": sb("prod", [R, GT, D]),
             "most": sb("most", [R, D])}
        l = []
        for k in range(KB):
            l += [(w["xk"][:, k, 0:D], blocked(I["L3_gnn_W"], k)), (w["xk"][:, k, D:512], blocked(I["L3_mix_Wqkv"], k)[:, D:2 * D])]
        for n in ("att_src", "att_dst"):
            l.append((w[n][:], everywhere(I["L3_gnn_" + n].rearrange("h x -> (h x)"))))
        return w, l

    def units(w):
        return [(w and [w["xk"][:, k, :] for k in range(KB)], 512)]

    def post(v, own, hand_over, b, grp):
        for n in ("src", "dst"):
            own(v.tensor_tensor(b["prod"][:], b["st"][:, :, 0:D], row_of(b["att_" + n][:], GT), ALU.mult))
            own(v.tensor_reduce(m["a_" + n][:, grp, :], b["prod"][:].rearrange("p j (h x) -> p j h x", h=4), AX, ALU.add))
        own(v.tensor_reduce(b["most"][:], b["st"][:, :, D:512].rearrange("p j x -> p x j"), AX, ALU.max))
        return v.tensor_tensor(m["key_top"][:], m["key_top"][:], b["most"][:], ALU.max)

    def stores(sp, b, i, sem=None):
        if sp is not None:
            sp.dma_start(by_tile(dram["el"])[:, bass.ds(i * GT, GT)], b["st"][:, :, 0:D]).then_inc(sem, 16)
        return 1

    build_open(nc, c, 3, m["X"], m["XN"], m["XNT"], loads, units, post, stores, None, None, 5)


def build_score0(nc, c, e, src, dst, el, er, attn, score):
    with ExitStack() as ctx:
        sb = lambda n, sh, d=F32: ctx.enter_context(nc.sbuf_tensor(f"score0_{n}", sh, d))
        ends = ("src", "dst")
        idx = {n: [sb(f"idx_{n}{l}", [R, G], I32) for l in range(LANES)] for n in ends}
        rows = {n: [sb(f"rows_{n}{l}", [R, G, D]) for l in range(LANES)] for n in ends}
        att = sb("att", [R, D])
        names = [f"idx_in{l}" for l in range(LANES)] + [f"rows_in{l}" for l in range(LANES)] + ["loaded", "scored", "chain", "pool_at"]
        with phase(nc, "score0", *names) as s, nc.Block() as block:
            @block.sync
            def _(sp):
                sp.dma_start(att[:], everywhere(attn)).then_inc(s["loaded"], 16)

                def loads(i, first=False):
                    for l in range(LANES):
                        if not first:
                            sp.wait_ge(s[f"rows_in{l}"], i * (2 * 16 * G))
                        for n, frm in (("src", src), ("dst", dst)):
                            sp.dma_start(idx[n][l][:], frm[:, bass.ds(i * UNIT + l * G, G)]).then_inc(s[f"idx_in{l}"], 16)
                loads(0, first=True)
                with sp.Fori(1, TURNS) as i:
                    loads(i)

            @block.gpsimd
            def _(pool):
                def gather(i, first=False):
                    for l in range(LANES):
                        pool.wait_ge(s[f"idx_in{l}"], i * 32 + 32)
                        if not first:
                            pool.wait_ge(s["scored"], i * LANES + l - LANES + 1)
                        pool.sem_inc(s["pool_at"], 1)
                        for g in range(G):
                            for n, table in (("src", el), ("dst", er)):
                                nc.gpsimd.indirect_dma_start(rows[n][l][:, g, :], None, table, bass.IndirectOffsetOnAxis(ap=idx[n][l][:, g:g + 1], axis=0)
                                                             ).then_inc(s[f"rows_in{l}"], 16)
                gather(0, first=True)
                with pool.Fori(1, TURNS) as i:
                    gather(i)

            @block.vector
            def _(dve):
                v = nc.vector
                dve.wait_ge(s["loaded"], 16)
                with dve.Fori(0, TURNS) as i:
                    own = Chain(dve, s["chain"], i, 3 * LANES)
                    for l in range(LANES):
                        a, b = rows["src"][l][:], rows["dst"][l][:]
                        dve.wait_ge(s[f"rows_in{l}"], i * (2 * 16 * G) + 2 * 16 * G)
                        own(v.tensor_tensor(a, a, b, ALU.add))
                        af, bf = a.rearrange("p g d -> p (g d)"), b.rearrange("p g d -> p (g d)")
                        own(v.scalar_tensor_tensor(bf, af, 0.2, af, ALU.mult, ALU.max))
                        own(v.tensor_tensor(b, b, row_of(att[:], G), ALU.mult))
                        v.tensor_reduce(score[:, bass.ds(i * UNIT + l * G, G), 0], b, AX, ALU.add).then_inc(s["scored"], 1)
                    own.end()


def columns(vec, p=128):
    return vec.rearrange("(k p) -> p k", p=p)


def heads_product(nc, to, features, kv, small=None):
    for j in range(GT):
        for k in range(KB):
            f = features[:, k, j * R:(j + 1) * R]
            last = nc.tensor.matmul(to[:, j, k * 128:(k + 1) * 128], f, kv[:, k, 0:128], start=True, stop=True)
            if small is not None:
                last = nc.tensor.matmul(small[:, j, k * 4:(k + 1) * 4], f, kv[:, k, 128:132], start=True, stop=True)
    return last


def sum_accumulators(v, own, b):
    a = b["acc"]
    own(v.tensor_tensor(a[:, 0:2], a[:, 0:2], a[:, 2:4], ALU.add))
    own(v.tensor_tensor(a[:, 0], a[:, 0], a[:, 1], ALU.add))
    return a[:, 0]


def load_accumulators(sp, acc, b, i, sem, extra=()):
    for k in range(ACCS):
        sp.dma_start(b["acc"][:, k], by_tile(acc[k][0:NODES])[:, bass.ds(i * GT, GT)]).then_inc(sem, 16)
    for to, frm in extra:
        sp.dma_start(to[:], by_tile(frm)[:, bass.ds(i * GT, GT)]).then_inc(sem, 16)


def close0(nc, c, m, I, acc):
    tag = "close0"
    with ExitStack() as ctx:
        sb = lambda n, sh, d=F32: ctx.enter_context(nc.sbuf_tensor(f"{tag}_{n}", sh, d))
        ps = lambda n, sh: ctx.enter_context(nc.psum_tensor(f"{tag}_{n}", sh, F32))
        b = {"acc": sb("acc", [R, ACCS, GT, D + 1]), "t": sb("t", [R, GT, D]), "z": sb("z", [R, GT])}
        wq, w1, w2 = sb("wq", [128, KB, D]), sb("w1", [128, KB, D]), sb("w2", [128, KB, D])
        bq, b1, b2 = sb("bq", [128, KB]), sb("b1", [128, KB]), sb("b2", [R, D])
        qT, rT, hT, ret = sb("qT", [128, KB, GN]), sb("rT", [128, KB, GN]), sb("hT", [128, KB, GN]), sb("ret", [R, GT, D])
        wide, fb = ps("wide", [128, 1536]), [ps(f"fb{n}", [128, 1024]) for n in range(2)]
        rows = wide[0:R, 0:GT * D].rearrange("p (j x) -> p j x", j=GT)
        loads = [(b1[:], columns(I["L0_mix_b1"])), (b2[:], everywhere(I["L0_mix_b2"]))]
        for k in range(KB):
            loads += [(wq[:, k, :].rearrange("p (h x) -> p h x", x=32), blocked(I["L0_mix_w_qkv"], k).rearrange("p (h x) -> p h x", x=96)[:, :, 0:32]),
                      (w1[:, k, :], blocked(I["L0_mix_w1"], k)), (w2[:, k, :], blocked(I["L0_mix_w2"], k))]
            for h in range(4):
                at = (k * 4 + h) * 96
                loads.append((bq[h * 32:(h + 1) * 32, k:k + 1], I["L0_mix_b_qkv"][at:at + 32].unsqueeze(1)))
        with phase(nc, tag, "loaded", "acc_in", "sp_passed", "pe", "dve", "act", "chain") as s, nc.Block() as block:
            PE = Steps(s["pe"], ["q0", "q1", "mix", "turn", "h0", "h1", "y"])
            DV = Steps(s["dve"], ["acc_used", "ret", "y"])
            AC = Steps(s["act"], ["q0", "q1", "turn", "h0", "h1"])

            @block.sync
            def _(sp):
                for to, frm in loads:
                    sp.dma_start(to, frm).then_inc(s["loaded"], 16)
                with sp.Fori(0, GROUPS) as i:
                    load_accumulators(sp, acc, b, i, s["acc_in"])
                    until(sp, DV, "acc_used", i)
                    sp.sem_inc(s["sp_passed"], 1)

            @block.tensor
            def _(pe):
                pe.wait_ge(s["loaded"], 16 * len(loads))
                with pe.Fori(0, GROUPS) as i:
                    xt = [m["XNT"][:, k, bass.ds(i * GN, GN)] for k in range(KB)]
                    for g in range(KB):
                        mark(product_t(nc, fb[g], 128, [(wq[:, k, g * 128:(g + 1) * 128], xt[k]) for k in range(KB)]), PE)
                    until(pe, AC, "q1", i)
                    mark(heads_product(nc, rows, qT, m["KV"]), PE)
                    until(pe, DV, "ret", i)
                    mark(turn_tiles(nc, c, wide, ret), PE)
                    until(pe, AC, "turn", i)
                    for g in range(KB):
                        mark(product_t(nc, fb[g], 128, [(w1[:, k, g * 128:(g + 1) * 128], rT[:, k, :]) for k in range(KB)]), PE)
                    until(pe, AC, "h1", i)
                    mark(product_rows(nc, rows, [(hT[:, k, :], w2[:, k, :]) for k in range(KB)]), PE)
                    until(pe, DV, "y", i)

            @block.scalar
            def _(act):
                a = nc.scalar
                act.wait_ge(s["loaded"], 16 * len(loads))
                with act.Fori(0, GROUPS) as i:
                    for g in range(KB):
                        until(act, PE, f"q{g}", i)
                        mark(a.activation(dense(qT[:, g, :]), slices(fb[g]), ACT.Identity, bias=bq[:, g:g + 1]), AC)
                    until(act, PE, "turn", i)
                    mark(a.copy(rT[:].rearrange("p k (j x) -> p (k j) x", x=R), turned(wide[:])), AC)
                    for g in range(KB):
                        until(act, PE, f"h{g}", i)
                        mark(a.activation(dense(hT[:, g, :]), slices(fb[g]), ACT.Gelu, bias=b1[:, g:g + 1]), AC)

            @block.vector
            def _(dve):
                v = nc.vector
                dve.wait_ge(s["loaded"], 16 * len(loads))
                with dve.Fori(0, GROUPS) as i:
                    own = Chain(dve, s["chain"], i, 7)
                    x, xn = m["X"][:, bass.ds(i * GT, GT), :], m["XN"][:, bass.ds(i * GT, GT), :]
                    dve.wait_ge(s["acc_in"], i * (16 * ACCS) + 16 * ACCS)
                    a = sum_accumulators(v, own, b)
                    own(v.tensor_scalar(b["z"][:], a[:, :, D], 0.5, None, ALU.max))
                    own(v.reciprocal(b["z"][:], b["z"][:]))
                    own(v.tensor_tensor(b["t"][:], a[:, :, 0:D], col_of(b["z"][:], D), ALU.mult))
                    own(v.tensor_tensor(b["t"][:], b["t"][:], xn, ALU.add))
                    mark(v.tensor_tensor(x, x, b["t"][:], ALU.add), DV)
                    until(dve, PE, "mix", i)
                    mark(v.tensor_tensor(ret[:], rows, xn, ALU.add), DV)
                    until(dve, PE, "y", i)
                    until(dve, DV, "ret", i)
                    own(v.tensor_tensor(b["t"][:], rows, row_of(b2[:], GT), ALU.add))
                    mark(v.tensor_tensor(x, x, b["t"][:], ALU.add), DV)
                    until(dve, DV, "y", i)
                    own.end()


def close1(nc, c, m, acc):
    tag = "close1"
    with ExitStack() as ctx:
        sb = lambda n, sh, d=F32: ctx.enter_context(nc.sbuf_tensor(f"{tag}_{n}", sh, d))
        b = {"acc": sb("acc", [R, ACCS, GT, D + 1]), "t": sb("t", [R, GT, D])}
        xT = sb("xT", [128, KB, GN])
        wide = ctx.enter_context(nc.psum_tensor(f"{tag}_wide", [128, 1536], F32))
        rows = wide[0:R, 0:GT * D].rearrange("p (j x) -> p j x", j=GT)
        with phase(nc, tag, "acc_in", "sp_passed", "pe", "dve", "act", "chain") as s, nc.Block() as block:
            PE, DV, AC = Steps(s["pe"], ["mix"]), Steps(s["dve"], ["acc_used", "x"]), Steps(s["act"], ["x"])

            @block.sync
            def _(sp):
                with sp.Fori(0, GROUPS) as i:
                    load_accumulators(sp, acc, b, i, s["acc_in"])
                    until(sp, DV, "acc_used", i)
                    sp.sem_inc(s["sp_passed"], 1)

            @block.tensor
            def _(pe):
                with pe.Fori(0, GROUPS) as i:
                    until(pe, AC, "x", i)
                    mark(heads_product(nc, rows, xT, m["KV"]), PE)
                    until(pe, DV, "x", i)

            @block.scalar
            def _(act):
                with act.Fori(0, GROUPS) as i:
                    mark(nc.scalar.copy(xT[:], m["XNT"][:, :, bass.ds(i * GN, GN)]), AC)
                    until(act, PE, "mix", i)

            @block.vector
            def _(dve):
                v = nc.vector
                with dve.Fori(0, GROUPS) as i:
                    own = Chain(dve, s["chain"], i, 3)
                    x, xn = m["X"][:, bass.ds(i * GT, GT), :], m["XN"][:, bass.ds(i * GT, GT), :]
                    dve.wait_ge(s["acc_in"], i * (16 * ACCS) + 16 * ACCS)
                    a = sum_accumulators(v, own, b)
                    own(v.tensor_tensor(x, x, xn, ALU.add))
                    mark(v.tensor_tensor(b["t"][:], a[:, :, 0:D], x, ALU.add), DV)
                    until(dve, DV, "acc_used", i)
                    until(dve, PE, "mix", i)
                    mark(v.tensor_tensor(x, rows, b["t"][:], ALU.add), DV)
                    until(dve, DV, "x", i)
                    own.end()


def build_experts(nc, c, tag, XT, target, table, experts, dims, weights, last_bias, gate, func, layer_bias, layer_scale=None, affine=None):
    L = len(dims) - 1
    blocks = [max(d // 128, 1) for d in dims]
    part = [min(d, 128) for d in dims]
    P = min(experts, 2)
    with ExitStack() as ctx:
        sb = lambda n, sh, d=F32: ctx.enter_context(nc.sbuf_tensor(f"{tag}_{n}", sh, d))
        ps = lambda n, sh: ctx.enter_context(nc.psum_tensor(f"{tag}_{n}", sh, F32))
        wt = [[sb(f"w{l}_{p}", [part[l], blocks[l], dims[l + 1]]) for l in range(L)] for p in range(P)]
        h = [sb(f"h{l}", [part[l], blocks[l], GN]) for l in range(1, L)]
        xe = sb("xe", [128, KB, GN]) if affine else None
        brow, t = sb("brow", [R, experts, D]), sb("t", [R, GT, D])
        wide, fb = ps("wide", [128, 1536]), [ps(f"fb{n}", [128, 1024]) for n in range(2)]
        rows = wide[0:R, 0:GT * D].rearrange("p (j x) -> p j x", j=GT)
        jobs = [(l, g) for l in range(L - 1) for g in range(blocks[l + 1])]
        names = [f"h{l}_{g}" for l, g in jobs]
        NL = sum(blocks[:L])
        with phase(nc, tag, "loaded", "w_in0", "w_in1", "pe", "dve", "act", "chain", "pe_passed", "sp_passed") as s, nc.Block() as block:
            PE = Steps(s["pe"], names + ["rows"])
            AC = Steps(s["act"], (["xe"] if affine else []) + names)
            DV = Steps(s["dve"], ["rows_used", "x"], before=1)

            def each_expert(eng, body):
                if experts <= 2:
                    for e in range(experts):
                        body(e, e, e * GROUPS)
                else:
                    with eng.Fori(0, experts // 2) as n:
                        for p in range(2):
                            body(n * 2 + p, p, (n * 2 + p) * GROUPS)

            @block.sync
            def _(sp):
                sp.dma_start(brow[:], last_bias).then_inc(s["loaded"], 16)

                def load(e, p, first):
                    if not first:
                        until(sp, DV, "x", (e - 1) * GROUPS - 1)
                        sp.sem_inc(s["sp_passed"], 1)
                    for l in range(L):
                        for k in range(blocks[l]):
                            sp.dma_start(wt[p][l][:, k, :], weights[l][bass.ds(e * dims[l] + k * 128, part[l])]).then_inc(s[f"w_in{p}"], 16)
                for p in range(P):
                    load(p, p, True)
                if experts > 2:
                    with sp.Fori(1, experts // 2) as n:
                        for p in range(2):
                            load(n * 2 + p, p, False)

            @block.tensor
            def _(pe):
                def body(e, p, before):
                    pe.wait_ge(s[f"w_in{p}"], (e - p) * (8 * NL) + 16 * NL)
                    pe.sem_inc(s["pe_passed"], 1)
                    with pe.Fori(0, GROUPS) as i:
                        turn = i + before
                        if affine:
                            until(pe, AC, "xe", turn)
                            src = [xe[:, k, :] for k in range(KB)]
                        else:
                            src = [XT[:, k, bass.ds(i * GN, GN)] for k in range(KB)]
                        for n, (l, g) in enumerate(jobs):
                            if n >= 2:
                                until(pe, AC, names[n - 2], turn)
                            if l >= 1 and g == 0:
                                until(pe, AC, names[n - 1], turn)
                            ins = src if l == 0 else [h[l - 1][:, k, :] for k in range(blocks[l])]
                            m_ = part[l + 1]
                            mark(product_t(nc, fb[n % 2], m_, [(wt[p][l][:, k, g * 128:g * 128 + m_], ins[k]) for k in range(blocks[l])]), PE)
                        until(pe, AC, names[-1], turn)
                        until(pe, DV, "x", turn - 1)
                        mark(product_rows(nc, rows, [(h[-1][:, k, :], wt[p][L - 1][:, k, :]) for k in range(blocks[L - 1])]), PE)

                each_expert(pe, body)

            @block.scalar
            def _(act):
                a = nc.scalar

                def body(e, p, before):
                    with act.Fori(0, GROUPS) as i:
                        turn = i + before
                        if affine:
                            for k in range(KB):
                                last = a.activation(xe[:, k, :], XT[:, k, bass.ds(i * GN, GN)], ACT.Identity, bias=affine[1][:, bass.ds(e * KB + k, 1)],
                                                    scale=affine[0][:, bass.ds(e * KB + k, 1)])
                            mark(last, AC)
                        for n, (l, g) in enumerate(jobs):
                            until(act, PE, names[n], turn)
                            at = bass.ds(e * blocks[l + 1] + g, 1)
                            scale = layer_scale[l][0:part[l + 1], at] if layer_scale else 1.0
                            mark(a.activation(dense(h[l][:, g, :]), slices(fb[n % 2][0:part[l + 1], :]), func,
                                              bias=layer_bias[l][0:part[l + 1], at], scale=scale), AC)
                each_expert(act, body)

            @block.vector
            def _(dve):
                v = nc.vector
                dve.wait_ge(s["loaded"], 16)
                dve.sem_inc(s["dve"], 1)

                def body(e, p, before):
                    with dve.Fori(0, GROUPS) as i:
                        turn = i + before
                        own = Chain(dve, s["chain"], turn, 1 if gate is not None else 0)
                        x = target[:, bass.ds(i * GT, GT), :]
                        until(dve, PE, "rows", turn)
                        v.tensor_tensor(t[:], rows, brow[:, bass.ds(e, 1), :].to_broadcast([R, GT, D]), ALU.add).then_inc(s["dve"], 1)
                        until(dve, DV, "rows_used", turn)
                        if gate is not None:
                            own(v.tensor_tensor(t[:], t[:], col_of(gate[:, bass.ds(e * TILES + i * GT, GT)], D), ALU.mult))
                        mark(v.tensor_tensor(x, x, t[:], ALU.add), DV)
                        until(dve, DV, "x", turn)
                        own.end()
                each_expert(dve, body)


def put_in(nc, tag, pairs, fill=()):
    with phase(nc, tag, "loaded") as s, nc.Block() as block:
        @block.sync
        def _(sp):
            for to, frm in pairs:
                sp.dma_start(to, frm).then_inc(s["loaded"], 16)
            if pairs:
                sp.wait_ge(s["loaded"], 16 * len(pairs))

        @block.vector
        def _(dve):
            for to, value in fill:
                nc.vector.memset(to, value)


def top_two(v, own, b, E, n_=GT):
    for n, src in ((1, "g"), (2, "g2")):
        own(v.tensor_reduce(b[f"v{n}"][:], b[src][:], AX, ALU.max))
        own(v.tensor_tensor(b[f"o{n}"][:], b[src][:], col_of(b[f"v{n}"][:], E), ALU.is_equal))
        own(v.tensor_tensor(b["k"][:], b[f"o{n}"][:], row_of(b["rev"][:, 0:E], n_), ALU.mult))
        own(v.tensor_reduce(b["k1"][:], b["k"][:], AX, ALU.max))
        own(v.tensor_tensor(b[f"o{n}"][:], b["k"][:], col_of(b["k1"][:], E), ALU.is_equal))
        if n == 1:
            own(v.scalar_tensor_tensor(b["g2"][:].rearrange("p j e -> p (j e)"), b["o1"][:].rearrange("p j e -> p (j e)"), -4.0,
                                       b["g"][:].rearrange("p j e -> p (j e)"), ALU.mult, ALU.add))


TOP_TWO_STEPS = 11


def gate_buffers(sb, E, n=GT):
    return ({k: sb(k, [R, n, E]) for k in ("g", "g2", "o1", "o2", "k", "ex")} | {k: sb(k, [R, n]) for k in ("v1", "v2", "k1", "r")}
            | {"rev": sb("rev", [R, 8])})


def build_gated_open(nc, c, layer, m, router, router_bias, E, mode):
    def loads(sb):
        w = gate_buffers(sb, E) | {"wr": sb("wr", [128, KB, E]), "br": sb("br", [R, E])}
        w["hand_in"], w["hand_out"] = w["g2"][:], w["ex"][:]
        return w, [(w["wr"][:, k, :], blocked(router, k)) for k in range(KB)] + [(w["br"][:], everywhere(router_bias))]

    def units(w):
        return [(w and [w["wr"][:, k, :] for k in range(KB)], E)]

    def post(v, own, hand_over, b, grp):
        own(v.tensor_scalar(b["rev"][:], c["iota"][0:R, 0:8], -1.0, 8.0, ALU.mult, ALU.add))
        own(v.tensor_tensor(b["g"][:], b["st"][:], row_of(b["br"][:], GT), ALU.add))
        own(v.tensor_reduce(b["r"][:], b["g"][:], AX, ALU.max))
        hand_over(v.tensor_tensor(b["g2"][:], b["g"][:], col_of(b["r"][:], E), ALU.subtract))
        own(v.tensor_reduce(b["r"][:], b["ex"][:], AX, ALU.add))
        own(v.reciprocal(b["r"][:], b["r"][:]))
        own(v.tensor_tensor(b["g"][:], b["ex"][:], col_of(b["r"][:], E), ALU.mult))
        out = m["gate"][:, 0:E * TILES].rearrange("p (e t) -> p t e", e=E)[:, grp, :]
        if mode == "all":
            return v.tensor_copy(out, b["g"][:])
        top_two(v, own, b, E)
        if mode == "top_ratio":
            own(v.tensor_tensor(b["r"][:], b["v1"][:], b["v2"][:], ALU.add))
        else:
            hand_over(v.tensor_tensor(b["g2"][:], b["g"][:], col_of(b["v1"][:], E), ALU.subtract))
            own(v.tensor_tensor(b["k"][:], b["o2"][:], b["ex"][:], ALU.mult))
            own(v.tensor_reduce(b["v2"][:], b["k"][:], AX, ALU.add))
            own(v.tensor_scalar(b["r"][:], b["v2"][:], 1.0, None, ALU.add))
            own(v.memset(b["v1"][:], 1.0))
        own(v.reciprocal(b["r"][:], b["r"][:]))
        own(v.tensor_tensor(b["v1"][:], b["v1"][:], b["r"][:], ALU.mult))
        own(v.tensor_tensor(b["v2"][:], b["v2"][:], b["r"][:], ALU.mult))
        own(v.tensor_tensor(b["o1"][:], b["o1"][:], col_of(b["v1"][:], E), ALU.mult))
        own(v.tensor_tensor(b["o2"][:], b["o2"][:], col_of(b["v2"][:], E), ALU.mult))
        return v.tensor_tensor(out, b["o1"][:], b["o2"][:], ALU.add)

    steps = {"all": 6, "top_ratio": 6 + TOP_TWO_STEPS + 6, "top_softmax": 6 + TOP_TWO_STEPS + 9}[mode]
    hand = (ACT.Exp,) * (2 if mode == "top_softmax" else 1)
    build_open(nc, c, f"{layer}g", m["X"], m["XN"], m["XNT"], loads, units, post, lambda sp, b, i, sem=None: 0, None, None, steps, hand=hand)


def experts0(nc, c, m, I):
    build_gated_open(nc, c, 0, m, I["L0_ffn_gW"], I["L0_ffn_gb"], 4, "top_softmax")
    with ExitStack() as ctx:
        sb = lambda n, sh, d=F32: ctx.enter_context(nc.sbuf_tensor(f"ffn0_{n}", sh, d))
        s1, s2, e1, e2 = sb("s1", [128, 2]), sb("s2", [128, 1]), sb("e1", [128, 4]), sb("e2", [64, 4])
        put_in(nc, "ffn0_in", [(s1[:], columns(I["L0_ffn_sb1"])), (s2[:], columns(I["L0_ffn_sb2"])),
                               (e1[:], I["L0_ffn_eb1"].rearrange("e p -> p e")), (e2[:], I["L0_ffn_eb2"].rearrange("e p -> p e"))])
        flat = lambda n: I[n].rearrange("e r o -> (e r) o")
        build_experts(nc, c, "ffn0s", m["XNT"], m["X"], None, 1, [256, 256, 128, 256], [I["L0_ffn_sW1"], I["L0_ffn_sW2"], I["L0_ffn_sW3"]],
                      everywhere(I["L0_ffn_sb3"]).unsqueeze(1), None, ACT.Relu, [s1, s2])
        build_experts(nc, c, "ffn0e", m["XNT"], m["X"], None, 4, [256, 128, 64, 256], [flat("L0_ffn_eW1"), flat("L0_ffn_eW2"), flat("L0_ffn_eW3")],
                      everywhere(I["L0_ffn_eb3"]), m["gate"], ACT.Relu, [e1, e2])


def experts1(nc, c, m, I):
    ENT = 8
    with ExitStack() as ctx:
        sb = lambda n, sh, d=F32: ctx.enter_context(nc.sbuf_tensor(f"ffn1_{n}", sh, d))
        mean, mean_b, wr, br = sb("mean", [128, KB]), sb("mean_b", [128, KB, R]), sb("wr", [128, KB, ENT]), sb("br", [R, ENT])
        b1 = sb("b1", [128, ENT * 4])

        def add_up(t, kv_p, b):
            for j in range(GT):
                for k in range(KB):
                    last = t.matmul(kv_p[:, k, 0:1], b["xn_s"][:, j, k * 128:(k + 1) * 128], c["ones"][0:R, 0:1], start=False, stop=False, skip_group_check=True)
            return last

        def to_mean(v, own, kv_p, b):
            own(v.tensor_scalar(mean[:], kv_p[:, :, 0], 1.0 / NODES, None, ALU.mult))
            own(v.tensor_copy(mean_b[:], col_of(mean[:], R)))

        build_open(nc, c, "1g", m["X"], m["XN"], m["XNT"], lambda sb: ({}, []), lambda w: [], lambda v, own, hand_over, b, grp: v.memset(b["st"][:], 0.0),
                   lambda sp, b, i, sem=None: 0, add_up, to_mean, 0)
        put_in(nc, "ffn1_in", [(wr[:, k, :], blocked(I["L1_ffn_Wr"], k)) for k in range(KB)] + [(br[:], everywhere(I["L1_ffn_br"]))]
               + [(b1[:, e * 4:(e + 1) * 4], columns(I["L1_ffn_b1"][e])) for e in range(ENT)])
        b = gate_buffers(lambda n, sh: sb("r_" + n, sh), ENT, 1)
        lp = ctx.enter_context(nc.psum_tensor("ffn1_logits", [R, 1, ENT], F32))
        with phase(nc, "route", "pe", "dve", "act", "chain") as s, nc.Block() as block:
            @block.tensor
            def _(pe):
                for k in range(KB):
                    last = nc.tensor.matmul(lp[:, 0, :], mean_b[:, k, :], wr[:, k, :], start=(k == 0), stop=(k == KB - 1))
                last.then_inc(s["pe"], 1)

            @block.scalar
            def _(act):
                for n in range(3):
                    act.wait_ge(s["dve"], n + 1)
                    nc.scalar.activation(b["ex"][:], b["g2"][:], ACT.Exp).then_inc(s["act"], 1)

            @block.vector
            def _(dve):
                v = nc.vector
                own = Chain(dve, s["chain"])
                capacity = float(-(-NODES * 5 // (4 * ENT)))
                exps = iter(range(1, 4))

                def exp(ins):
                    ins.then_inc(s["dve"], 1)
                    dve.wait_ge(s["act"], next(exps))

                def softmax():
                    own(v.tensor_reduce(b["r"][:], b["g"][:], AX, ALU.max))
                    exp(v.tensor_tensor(b["g2"][:], b["g"][:], col_of(b["r"][:], ENT), ALU.subtract))
                    own(v.tensor_reduce(b["r"][:], b["ex"][:], AX, ALU.add))
                    own(v.reciprocal(b["r"][:], b["r"][:]))
                    own(v.tensor_tensor(b["g"][:], b["ex"][:], col_of(b["r"][:], ENT), ALU.mult))

                own(v.tensor_scalar(b["rev"][:], c["iota"][0:R, 0:8], -1.0, 8.0, ALU.mult, ALU.add))
                dve.wait_ge(s["pe"], 1)
                own(v.tensor_tensor(b["g"][:], lp[:], row_of(br[:], 1), ALU.add))
                softmax()
                own(v.tensor_scalar(b["k"][:], b["g"][:], float(NODES), capacity, ALU.mult, ALU.max))
                own(v.reciprocal(b["k"][:], b["k"][:]))
                own(v.tensor_scalar(b["k"][:], b["k"][:], capacity, None, ALU.mult))
                own(v.tensor_tensor(b["g"][:], b["g"][:], b["k"][:], ALU.mult))
                softmax()
                top_two(v, own, b, ENT, 1)
                exp(v.tensor_tensor(b["g2"][:], b["g"][:], col_of(b["v1"][:], ENT), ALU.subtract))
                own(v.tensor_tensor(b["k"][:], b["o2"][:], b["ex"][:], ALU.mult))
                own(v.tensor_reduce(b["r"][:], b["k"][:], AX, ALU.add))
                own(v.tensor_scalar(b["r"][:], b["r"][:], 1.0, None, ALU.add))
                own(v.reciprocal(b["r"][:], b["r"][:]))
                own(v.tensor_tensor(b["k"][:], b["k"][:], b["o1"][:], ALU.add))
                own(v.tensor_tensor(b["k"][:], b["k"][:], col_of(b["r"][:], ENT), ALU.mult))
                own(v.tensor_copy(m["gate"][:].rearrange("p (e t) -> p e t", e=ENT), col_of(b["k"][:, 0, :], TILES)))
        flat = lambda n: I[n].rearrange("e r o -> (e r) o")
        build_experts(nc, c, "ffn1e", m["XNT"], m["XN"], None, ENT, [256, 512, 256], [flat("L1_ffn_W1"), flat("L1_ffn_W2")],
                      everywhere(I["L1_ffn_b2"]), m["gate"], ACT.Gelu, [b1])
    with ExitStack() as ctx:
        sb = lambda n, sh, d=F32: ctx.enter_context(nc.sbuf_tensor(f"norm1_{n}", sh, d))
        b = norm_buffers(sb)
        t, gamma, beta = sb("t", [R, GT, D]), sb("gamma", [R, D]), sb("beta", [R, D])
        put_in(nc, "norm1_in", [(gamma[:], everywhere(I["L1_ffn_gamma"])), (beta[:], everywhere(I["L1_ffn_beta"]))])
        with phase(nc, "norm1", "dve", "act", "chain", "passed") as s, nc.Block() as block:
            DV, AC = Steps(s["dve"], ["var", "x"]), Steps(s["act"], ["std"])

            @block.vector
            def _(dve):
                v = nc.vector
                with dve.Fori(0, GROUPS) as i:
                    own = Chain(dve, s["chain"], i, VARIANCE_STEPS + STANDARDIZE_STEPS + 3)
                    x, y = m["X"][:, bass.ds(i * GT, GT), :], m["XN"][:, bass.ds(i * GT, GT), :]
                    mark(variance(v, own, y, b, 1e-5, s["passed"]), DV)
                    until(dve, AC, "std", i)
                    own(standardize(v, own, y, t, b))
                    own(v.tensor_tensor(t[:], t[:], row_of(gamma[:], GT), ALU.mult))
                    own(v.tensor_tensor(t[:], t[:], row_of(beta[:], GT), ALU.add))
                    mark(v.tensor_tensor(x, x, t[:], ALU.add), DV)
                    until(dve, DV, "x", i)
                    own.end()

            @block.scalar
            def _(act):
                with act.Fori(0, GROUPS) as i:
                    until(act, DV, "var", i)
                    mark(nc.scalar.activation(b["std"][:], b["var"][:], ACT.Sqrt), AC)


def build_transposed(nc, c, tag, parts, out):
    n = sum(w.shape[0] for w in parts) // 128
    with ExitStack() as ctx:
        w = ctx.enter_context(nc.sbuf_tensor(f"{tag}_w", [128, n, D], F32))
        tp = [ctx.enter_context(nc.psum_tensor(f"{tag}_p{q}", [128, KB, 128], F32)) for q in range(2)]
        with phase(nc, tag, "loaded", "pe", "act") as s, nc.Block() as block:
            @block.sync
            def _(sp):
                at = 0
                for part in parts:
                    k = part.shape[0] // 128
                    sp.dma_start(w[:, at:at + k, :], part.rearrange("(b p) x -> p b x", p=128)).then_inc(s["loaded"], 16)
                    at += k

            @block.tensor
            def _(pe):
                pe.wait_ge(s["loaded"], 16 * len(parts))
                for b in range(n):
                    if b >= 2:
                        pe.wait_ge(s["act"], b - 1)
                    for k in range(KB):
                        last = nc.tensor.transpose(tp[b % 2][:, k, :], w[:, b, k * 128:(k + 1) * 128], c["ident"][:])
                    last.then_inc(s["pe"], 1)

            @block.scalar
            def _(act):
                for b in range(n):
                    act.wait_ge(s["pe"], b + 1)
                    nc.scalar.copy(out[:, :, b * 128:(b + 1) * 128], tp[b % 2][:]).then_inc(s["act"], 1)


def close2(nc, c, m, I, acc):
    tag = "close2"
    with ExitStack() as ctx:
        sb = lambda n, sh, d=F32: ctx.enter_context(nc.sbuf_tensor(f"{tag}_{n}", sh, d))
        ps = lambda n, sh: ctx.enter_context(nc.psum_tensor(f"{tag}_{n}", sh, F32))
        b = {"acc": sb("acc", [R, ACCS, GT, D + 1]), "t": sb("t", [R, GT, D]), "u": sb("u", [R, GT, D]), "z": sb("z", [R, GT, 8])} | norm_buffers(sb)
        w = sb("w", [128, KB, D])
        rowv = {n: sb(n, [R, D]) for n in ("bias", "gamma", "beta", "ln1_g", "ln1_b", "b2", "ln2_g", "ln2_b")}
        b1 = sb("b1", [128, KB])
        aT, qT, hT, low, ex = [sb(n, [128, KB, GN]) for n in ("aT", "qT", "hT", "low", "ex")]
        wide, fb = ps("wide", [128, 1536]), [ps(f"fb{n}", [128, 1024]) for n in range(2)]
        small = ps("small", [R, GT, 8])
        rows = wide[0:R, 0:GT * D].rearrange("p (j x) -> p j x", j=GT)
        loads = [(w[:, k, :], blocked(I["L2_gnn_W"], k)) for k in range(KB)] + [(b1[:], columns(I["L2_mix_b1"]))]
        loads += [(rowv[n][:], everywhere(I[("L2_gnn_" if n in ("bias", "gamma", "beta") else "L2_mix_") + n])) for n in rowv]
        W1, W2 = 3 * D, 4 * D
        with phase(nc, tag, "loaded", "acc_in", "sp_passed", "pe", "dve", "act", "chain", "passed") as s, nc.Block() as block:
            PE = Steps(s["pe"], ["agg", "gcn", "q0", "q1", "mix", "x1", "h0", "h1", "y"])
            DV = Steps(s["dve"], ["agg", "gcn_var", "gcn_x", "low0", "low1", "q0", "q1", "x1_var", "x1", "y_var", "x"])
            AC = Steps(s["act"], ["agg", "gcn_std", "ex0", "ex1", "x1_std", "x1", "h0", "h1", "y_std"])

            @block.sync
            def _(sp):
                for to, frm in loads:
                    sp.dma_start(to, frm).then_inc(s["loaded"], 16)
                with sp.Fori(0, GROUPS) as i:
                    load_accumulators(sp, acc, b, i, s["acc_in"])
                    until(sp, DV, "agg", i)
                    sp.sem_inc(s["sp_passed"], 1)

            @block.tensor
            def _(pe):
                pe.wait_ge(s["loaded"], 16 * len(loads))
                with pe.Fori(0, GROUPS) as i:
                    xt = [m["XNT"][:, k, bass.ds(i * GN, GN)] for k in range(KB)]
                    until(pe, DV, "agg", i)
                    mark(turn_tiles(nc, c, wide, b["t"]), PE)
                    until(pe, AC, "agg", i)
                    mark(product_rows(nc, rows, [(aT[:, k, :], w[:, k, :]) for k in range(KB)]), PE)
                    for g in range(KB):
                        mark(product_t(nc, fb[g], 128, [(m["WT"][:, k, g * 128:(g + 1) * 128], xt[k]) for k in range(KB)]), PE)
                    until(pe, DV, "q1", i)
                    until(pe, DV, "gcn_x", i)
                    mark(heads_product(nc, rows, qT, m["KV"], small), PE)
                    until(pe, DV, "x1", i)
                    mark(turn_tiles(nc, c, wide, b["u"]), PE)
                    until(pe, AC, "x1", i)
                    for g in range(KB):
                        mark(product_t(nc, fb[g], 128, [(m["WT"][:, k, W1 + g * 128:W1 + (g + 1) * 128], aT[:, k, :]) for k in range(KB)]), PE)
                    until(pe, AC, "h1", i)
                    mark(product_rows(nc, rows, [(hT[:, k, :], m["WT"][:, k, W2:W2 + D]) for k in range(KB)]), PE)
                    until(pe, DV, "x", i)

            @block.scalar
            def _(act):
                a = nc.scalar
                act.wait_ge(s["loaded"], 16 * len(loads))

                def std(name, i):
                    until(act, DV, name + "_var", i)
                    mark(a.activation(b["std"][:], b["var"][:], ACT.Sqrt), AC)

                def turn(name, i):
                    until(act, PE, name, i)
                    mark(a.copy(aT[:].rearrange("p k (j x) -> p (k j) x", x=R), turned(wide[:])), AC)

                with act.Fori(0, GROUPS) as i:
                    turn("agg", i)
                    std("gcn", i)
                    for g in range(KB):
                        until(act, DV, f"low{g}", i)
                        mark(a.activation(ex[:, g, :], low[:, g, :], ACT.Exp), AC)
                    std("x1", i)
                    turn("x1", i)
                    for g in range(KB):
                        until(act, PE, f"h{g}", i)
                        mark(a.activation(dense(hT[:, g, :]), slices(fb[g]), ACT.Gelu, bias=b1[:, g:g + 1]), AC)
                    std("y", i)

            @block.vector
            def _(dve):
                v = nc.vector
                dve.wait_ge(s["loaded"], 16 * len(loads))
                with dve.Fori(0, GROUPS) as i:
                    own = Chain(dve, s["chain"], i, 29)
                    grp = bass.ds(i * GT, GT)
                    x, xn = m["X"][:, grp, :], m["XN"][:, grp, :]
                    t, u = b["t"][:], b["u"][:]

                    def norm(name, src, gain, shift):
                        mark(variance(v, own, src, b, 1e-5, s["passed"]), DV)
                        until(dve, AC, name + "_std", i)
                        own(standardize(v, own, src, src, b))
                        own(v.tensor_tensor(src, src, row_of(rowv[gain][:], GT), ALU.mult))
                        return v.tensor_tensor(src, src, row_of(rowv[shift][:], GT), ALU.add)

                    dve.wait_ge(s["acc_in"], i * (16 * ACCS) + 16 * ACCS)
                    a = sum_accumulators(v, own, b)
                    own(v.tensor_tensor(u, xn, col_of(m["dinv"][:, grp], D), ALU.mult))
                    own(v.tensor_tensor(u, u, a[:, :, 0:D], ALU.add))
                    mark(v.tensor_tensor(t, u, col_of(m["dinv"][:, grp], D), ALU.mult), DV)
                    until(dve, PE, "gcn", i)
                    own(v.tensor_tensor(u, rows, row_of(rowv["bias"][:], GT), ALU.add))
                    own(v.tensor_tensor(u, u, xn, ALU.add))
                    own(norm("gcn", u, "gamma", "beta"))
                    mark(v.tensor_tensor(x, x, u, ALU.add), DV)
                    for g in range(KB):
                        until(dve, PE, f"q{g}", i)
                        mark(v.tensor_scalar(dense(low[:, g, :]), slices(fb[g]), 0.0, None, ALU.min), DV)
                    for g in range(KB):
                        until(dve, AC, f"ex{g}", i)
                        mark(v.scalar_tensor_tensor(dense(qT[:, g, :]), slices(fb[g]), 0.0, dense(ex[:, g, :]), ALU.max, ALU.add), DV)
                    until(dve, PE, "mix", i)
                    own(v.tensor_scalar(b["z"][:], small[:], 1e-6, None, ALU.add))
                    own(v.reciprocal(b["z"][:], b["z"][:]))
                    u4 = u.rearrange("p j (h x) -> p j h x", x=32)
                    own(v.tensor_tensor(u4, rows.rearrange("p j (h x) -> p j h x", x=32), b["z"][:].unsqueeze(3).to_broadcast([R, GT, 8, 32]), ALU.mult))
                    own(v.tensor_tensor(u, u, xn, ALU.add))
                    mark(norm("x1", u, "ln1_g", "ln1_b"), DV)
                    until(dve, PE, "y", i)
                    own(v.tensor_tensor(t, rows, row_of(rowv["b2"][:], GT), ALU.add))
                    own(v.tensor_tensor(t, t, u, ALU.add))
                    own(norm("y", t, "ln2_g", "ln2_b"))
                    mark(v.tensor_tensor(x, x, t, ALU.add), DV)
                    until(dve, DV, "x", i)
                    own.end()


def build_key_sums(nc, c, m, wkv):
    tag = "keys3"
    with ExitStack() as ctx:
        sb = lambda n, sh, d=F32: ctx.enter_context(nc.sbuf_tensor(f"{tag}_{n}", sh, d))
        ps = lambda n, sh: ctx.enter_context(nc.psum_tensor(f"{tag}_{n}", sh, F32))
        w, xT, st = sb("w", [128, KB, 512]), sb("xT", [128, KB, GN]), sb("st", [R, GT, 512])
        topc, diag, topr, inv = sb("topc", [128, KB]), sb("diag", [128, KB, 128]), sb("topr", [R, D]), sb("inv", [128, KB])
        tp, unit_p, kv_p = ps("tp", [128, KB, 128]), [ps(f"unit{n}", [R, 512]) for n in range(4)], ps("kv_p", [128, KB, 256])
        with phase(nc, tag, "loaded", "pe0", "dve0", "pe", "dve", "act", "chain") as s, nc.Block() as block:
            UNITS = [f"u{j}" for j in range(GT)]
            PE, DV = Steps(s["pe"], UNITS + ["kv"]), Steps(s["dve"], ["low"])
            AC = Steps(s["act"], ["x"] + UNITS + ["exp"])

            @block.sync
            def _(sp):
                for k in range(KB):
                    sp.dma_start(w[:, k, :], blocked(wkv, k)[:, D:3 * D]).then_inc(s["loaded"], 16)

            @block.tensor
            def _(pe):
                t = nc.tensor
                for k in range(KB):
                    last = t.transpose(tp[:, k, 0:R], m["key_top"][:, k * 128:(k + 1) * 128], c["ident"][0:R, 0:R])
                last.then_inc(s["pe0"], 1)
                pe.wait_ge(s["dve0"], 1)
                for k in range(KB):
                    last = t.matmul(tp[0:R, k, :], c["ones"][:, 0:R], diag[:, k, :], start=True, stop=True)
                last.then_inc(s["pe0"], 1)
                for k in range(KB):
                    t.matmul(kv_p[:, k, :], c["zeros"][:, 0:128], c["zeros"][:, 0:256], start=(k == 0), stop=False, skip_group_check=True)
                pe.wait_ge(s["loaded"], 16 * KB)
                with pe.Fori(0, GROUPS) as i:
                    until(pe, AC, "x", i)
                    for j, name in enumerate(UNITS):
                        if j >= 4:
                            until(pe, AC, UNITS[j - 4], i)
                        for k in range(KB):
                            last = t.matmul(unit_p[j % 4][:], xT[:, k, j * R:(j + 1) * R], w[:, k, :], start=(k == 0), stop=(k == KB - 1))
                        mark(last, PE)
                    until(pe, AC, "exp", i)
                    for j in range(GT):
                        for k in range(KB):
                            key = st[:, j, k * 128:(k + 1) * 128]
                            t.matmul(kv_p[:, k, 0:128], key, st[:, j, D + k * 128:D + (k + 1) * 128], start=False, stop=False, skip_group_check=True)
                            last = t.matmul(kv_p[:, k, 128:129], key, c["ones"][0:R, 0:1], start=False, stop=False, skip_group_check=True)
                    mark(last, PE)
                for k in range(KB):
                    last = t.matmul(kv_p[:, k, :], c["zeros"][:, 0:128], c["zeros"][:, 0:256], start=False, stop=True, skip_group_check=True)
                last.then_inc(s["pe0"], 1)

            @block.scalar
            def _(act):
                a = nc.scalar
                with act.Fori(0, GROUPS) as i:
                    mark(a.copy(xT[:], m["XNT"][:, :, bass.ds(i * GN, GN)]), AC)
                    for j, name in enumerate(UNITS):
                        until(act, PE, name, i)
                        mark(a.copy(st[:, j, :], unit_p[j % 4][:]), AC)
                    until(act, DV, "low", i)
                    mark(a.activation(st[:, :, 0:D], st[:, :, 0:D], ACT.Exp), AC)
                    until(act, PE, "kv", i)

            @block.vector
            def _(dve):
                v = nc.vector
                own = Chain(dve, s["chain"])
                dve.wait_ge(s["pe0"], 1)
                own(v.tensor_reduce(topc[:], tp[:, :, 0:R], AX, ALU.max))
                for k in range(KB):
                    last = v.tensor_scalar(diag[:, k, :], c["ident"][:], topc[:, k:k + 1], None, ALU.mult)
                last.then_inc(s["dve0"], 1)
                dve.wait_ge(s["pe0"], 2)
                own(v.tensor_copy(topr[:].rearrange("p (k x) -> p k x", k=KB), tp[0:R, :, :]))
                with dve.Fori(0, GROUPS) as i:
                    until(dve, AC, UNITS[-1], i)
                    mark(v.tensor_tensor(st[:, :, 0:D], st[:, :, 0:D], row_of(topr[:], GT), ALU.subtract), DV)
                dve.wait_ge(s["pe0"], 3)
                own(v.reciprocal(inv[:], kv_p[:, :, 128]))
                for k in range(KB):
                    own(v.scalar_tensor_tensor(m["KV"][:, k, 0:128], kv_p[:, k, 0:128], inv[:, k:k + 1], c["block"][:], ALU.mult, ALU.mult))


def close3(nc, c, m, I, acc, xp_table):
    tag = "close3"
    H, C, GH = 4, D // 4, 64
    with ExitStack() as ctx:
        sb = lambda n, sh, d=F32: ctx.enter_context(nc.sbuf_tensor(f"{tag}_{n}", sh, d))
        ps = lambda n, sh: ctx.enter_context(nc.psum_tensor(f"{tag}_{n}", sh, F32))
        b = {"acc": sb("acc", [R, ACCS, GT, D + H]), "xp": sb("xp", [R, GT, D]), "t": sb("t", [R, GT, D]), "u": sb("u", [R, GT, D]),
             "z": sb("z", [R, GT, H])} | norm_buffers(sb)
        out, gate = sb("out", [R, GT, D]), sb("gate", [R, GT, D])
        wq, wp, wg1, wg2 = sb("wq", [128, KB, D]), sb("wp", [128, KB, D]), sb("wg1", [128, KB, GH]), sb("wg2", [GH, D])
        rowv = {n: sb(n, [R, D]) for n in ("bias", "gamma", "beta", "ln_g", "ln_b", "bg2", "bproj")}
        bg1 = sb("bg1", [GH, 1])
        qT, rT, hT = sb("qT", [128, KB, GN]), sb("rT", [128, KB, GN]), sb("hT", [GH, GN])
        wide, fb = ps("wide", [128, 1536]), [ps(f"fb{n}", [128, 1024]) for n in range(2)]
        rows = wide[0:R, 0:GT * D].rearrange("p (j x) -> p j x", j=GT)
        loads = [(wg2[:], I["L3_mix_Wg2"]), (bg1[:], columns(I["L3_mix_bg1"], GH))]
        for k in range(KB):
            loads += [(wq[:, k, :], blocked(I["L3_mix_Wqkv"], k)[:, 0:D]), (wp[:, k, :], blocked(I["L3_mix_Wproj"], k)), (wg1[:, k, :], blocked(I["L3_mix_Wg1"], k))]
        loads += [(rowv[n][:], everywhere(I[("L3_gnn_" if n in ("bias", "gamma", "beta") else "L3_mix_") + n])) for n in rowv]
        with phase(nc, tag, "loaded", "acc_in", "sp_passed", "pe", "dve", "act", "chain", "passed") as s, nc.Block() as block:
            PE = Steps(s["pe"], ["q0", "q1", "mix", "xg", "h", "gate", "prod", "y"])
            DV = Steps(s["dve"], ["acc_used", "gat_var", "gat_x", "mix", "xg_var", "xg", "pre", "prod", "x"])
            AC = Steps(s["act"], ["q0", "q1", "gat_std", "xg_std", "xg", "h", "gate", "prod"])

            @block.sync
            def _(sp):
                for to, frm in loads:
                    sp.dma_start(to, frm).then_inc(s["loaded"], 16)
                with sp.Fori(0, GROUPS) as i:
                    load_accumulators(sp, acc, b, i, s["acc_in"], [(b["xp"], xp_table)])
                    until(sp, DV, "acc_used", i)
                    sp.sem_inc(s["sp_passed"], 1)

            @block.tensor
            def _(pe):
                pe.wait_ge(s["loaded"], 16 * len(loads))
                with pe.Fori(0, GROUPS) as i:
                    xt = [m["XNT"][:, k, bass.ds(i * GN, GN)] for k in range(KB)]
                    for g in range(KB):
                        mark(product_t(nc, fb[g], 128, [(wq[:, k, g * 128:(g + 1) * 128], xt[k]) for k in range(KB)]), PE)
                    until(pe, AC, "q1", i)
                    mark(heads_product(nc, rows, qT, m["KV"]), PE)
                    until(pe, DV, "xg", i)
                    mark(turn_tiles(nc, c, wide, b["u"]), PE)
                    until(pe, AC, "xg", i)
                    mark(product_t(nc, fb[0], GH, [(wg1[:, k, :], rT[:, k, :]) for k in range(KB)]), PE)
                    until(pe, AC, "h", i)
                    mark(product_rows(nc, rows, [(hT[:], wg2[:])]), PE)
                    until(pe, DV, "prod", i)
                    mark(turn_tiles(nc, c, wide, out), PE)
                    until(pe, AC, "prod", i)
                    mark(product_rows(nc, rows, [(rT[:, k, :], wp[:, k, :]) for k in range(KB)]), PE)
                    until(pe, DV, "x", i)

            @block.scalar
            def _(act):
                a = nc.scalar
                act.wait_ge(s["loaded"], 16 * len(loads))

                def std(name, i):
                    until(act, DV, name + "_var", i)
                    mark(a.activation(b["std"][:], b["var"][:], ACT.Sqrt), AC)

                def turn(name, i):
                    until(act, PE, name, i)
                    mark(a.copy(rT[:].rearrange("p k (j x) -> p (k j) x", x=R), turned(wide[:])), AC)

                with act.Fori(0, GROUPS) as i:
                    for g in range(KB):
                        until(act, PE, f"q{g}", i)
                        mark(a.copy(dense(qT[:, g, :]), slices(fb[g])), AC)
                    std("gat", i)
                    std("xg", i)
                    turn("xg", i)
                    until(act, PE, "h", i)
                    mark(a.activation(dense(hT[:]), slices(fb[0][0:GH, :]), ACT.Gelu, bias=bg1[:]), AC)
                    until(act, DV, "pre", i)
                    mark(a.activation(gate[:], gate[:], ACT.Sigmoid), AC)
                    turn("prod", i)

            @block.vector
            def _(dve):
                v = nc.vector
                dve.wait_ge(s["loaded"], 16 * len(loads))
                with dve.Fori(0, GROUPS) as i:
                    own = Chain(dve, s["chain"], i, 22)
                    grp = bass.ds(i * GT, GT)
                    x, xn = m["X"][:, grp, :], m["XN"][:, grp, :]
                    t, u = b["t"][:], b["u"][:]
                    heads = lambda ap: ap.rearrange("p j (h x) -> p j h x", x=C)
                    each = lambda ap: ap.unsqueeze(3).to_broadcast([R, GT, H, C])
                    dve.wait_ge(s["acc_in"], i * (16 * (ACCS + 1)) + 16 * (ACCS + 1))
                    a = sum_accumulators(v, own, b)
                    own(v.tensor_tensor(heads(t), heads(b["xp"][:]), each(m["p_self"][:, grp, :]), ALU.mult))
                    own(v.tensor_tensor(t, t, a[:, :, 0:D], ALU.add))
                    own(v.tensor_tensor(b["z"][:], a[:, :, D:D + H], m["p_self"][:, grp, :], ALU.add))
                    own(v.tensor_scalar(b["z"][:], b["z"][:], 1e-16, None, ALU.add))
                    own(v.reciprocal(b["z"][:], b["z"][:]))
                    own(v.tensor_tensor(heads(t), heads(t), each(b["z"][:]), ALU.mult))
                    mark(v.tensor_tensor(t, t, row_of(rowv["bias"][:], GT), ALU.add), DV)
                    until(dve, DV, "acc_used", i)
                    mark(variance(v, own, t, b, 1e-5, s["passed"]), DV)
                    until(dve, AC, "gat_std", i)
                    own(standardize(v, own, t, t, b))
                    own(v.tensor_tensor(t, t, row_of(rowv["gamma"][:], GT), ALU.mult))
                    own(v.tensor_tensor(t, t, row_of(rowv["beta"][:], GT), ALU.add))
                    own(v.tensor_tensor(t, t, xn, ALU.add))
                    own(v.tensor_scalar(t, t, 0.0, None, ALU.max))
                    mark(v.tensor_tensor(x, x, t, ALU.add), DV)
                    until(dve, PE, "mix", i)
                    mark(v.tensor_copy(out[:], rows), DV)
                    mark(variance(v, own, xn, b, 1e-5, s["passed"]), DV)
                    until(dve, AC, "xg_std", i)
                    own(standardize(v, own, xn, u, b))
                    own(v.tensor_tensor(u, u, row_of(rowv["ln_g"][:], GT), ALU.mult))
                    mark(v.tensor_tensor(u, u, row_of(rowv["ln_b"][:], GT), ALU.add), DV)
                    until(dve, PE, "gate", i)
                    mark(v.tensor_tensor(gate[:], rows, row_of(rowv["bg2"][:], GT), ALU.add), DV)
                    until(dve, AC, "gate", i)
                    mark(v.tensor_tensor(out[:], out[:], gate[:], ALU.mult), DV)
                    until(dve, PE, "y", i)
                    own(v.tensor_tensor(t, rows, row_of(rowv["bproj"][:], GT), ALU.add))
                    mark(v.tensor_tensor(x, x, t, ALU.add), DV)
                    until(dve, DV, "x", i)
                    own.end()


def alloc_all(nc, ctx, dbg=False):
    sb = lambda n, sh, d=F32: ctx.enter_context(nc.sbuf_tensor(n, sh, d))
    c = {"iota_i": sb("iota_i", [128, 256], I32), "part_i": sb("part_i", [128, 1], I32), "iota": sb("iota", [128, 256]), "part": sb("part", [128, 1]),
         "ones": sb("ones", [128, 128]), "zeros": sb("zeros", [128, 256]), "ident": sb("ident", [128, 128]), "lower": sb("lower", [128, 128]),
         "block": sb("block", [128, 128]), "block4": sb("block4", [128, 4]), "tmp1": sb("tmp1", [128, 1])}
    m = {"X": sb("X", [R, TILES, D]), "XN": sb("XN", [R, TILES, D]), "XNT": sb("XNT", [128, KB, NODES]), "KV": sb("KV", [128, KB, 132]),
         "gate": sb("gate", [R, 8 * TILES]), "deg3": sb("deg3", [R, 3, TILES]), "relcnt": sb("relcnt", [R, TILES * TYPES])}
    e = {n: sb("e_" + n, [R, CHUNKS]) for n in ("src", "dst", "src_lo", "dst_lo", "dst_hi", "slot", "weight", "attr", "dst_dup")}
    return c, m, e


def edge_setup(nc, c, m, e, I, dram):
    build_constants(nc, c)
    with ExitStack() as ctx:
        temps = ("src_i", "dst_i", "typ_i", "rel_i", "tmp_i", "tmp", "src_hi", "src_dup")
        e = e | {n: ctx.enter_context(nc.sbuf_tensor("e_" + n, [R, CHUNKS], I32 if n.endswith("_i") else F32)) for n in temps}
        build_edge_numbers(nc, c, e, I["src"], I["dst"], I["edge_type_7"], I["edge_weight"], I["edge_weight1"])
        build_scatter_rows(nc, c, e, dram)
        build_degrees(nc, c, e, m["deg3"][:].rearrange("p k t -> p (k t)"), m["relcnt"][:])


def as_chunks(v):
    return v.rearrange("(p c) -> p c", p=R)


def bulk(nc, tag, steps):
    with phase(nc, tag, "chain", "dve", "act") as s, nc.Block() as block:
        todo = []

        @block.vector
        def _(dve):
            def act_step(ins, *args, **kw):
                ins.then_inc(s["dve"], 1)
                todo.append((args, kw))
                dve.wait_ge(s["act"], len(todo))
            steps(nc.vector, Chain(dve, s["chain"]), act_step)

        @block.scalar
        def _(act):
            for n, (args, kw) in enumerate(todo):
                act.wait_ge(s["dve"], n + 1)
                nc.scalar.activation(*args, **kw).then_inc(s["act"], 1)


def layer0(nc, c, m, e, I, dram):
    open0(nc, c, m, I, dram)
    src, dst = as_chunks(I["src"]), as_chunks(I["dst"])
    with ExitStack() as ctx:
        sb = lambda n, sh, d=F32: ctx.enter_context(nc.sbuf_tensor(f"gnn0_{n}", sh, d))
        score, top, edge_top = sb("score", [R, CHUNKS, 1]), sb("top", [R, 1, TILES]), sb("edge_top", [R, CHUNKS, 1])
        build_score0(nc, c, e, src, dst, dram["el"], dram["er"], I["L0_gnn_attn"], score)
        build_segment_max(nc, c, e, "max0", score, 1, top[:])
        build_node_gather(nc, c, "top0", top[:, 0, :], e["dst_lo"], e["dst_hi"], TILES, 1, edge_top)

        def exps(v, own, act_step):
            act_step(v.tensor_tensor(score[:], score[:], edge_top[:], ALU.subtract), score[:], score[:], ACT.Exp)
        bulk(nc, "exp0", exps)
        build_messages(nc, c, e, "msg0", dram["el"], src, dram["dst_row"], e["dst"], score, 1, dram["acc"])
    close0(nc, c, m, I, dram["acc"])
    experts0(nc, c, m, I)


def layer1(nc, c, m, e, I, dram):
    open1(nc, c, m, I, dram)
    with ExitStack() as ctx:
        sb = lambda n, sh, d=F32: ctx.enter_context(nc.sbuf_tensor(f"gnn1_{n}", sh, d))
        share = sb("share", [R, CHUNKS, 1])

        def inverse(v, own, act_step):
            own(v.tensor_scalar(m["relcnt"][:], m["relcnt"][:], 1.0, None, ALU.max))
            own(v.reciprocal(m["relcnt"][:], m["relcnt"][:]))
        bulk(nc, "share1", inverse)
        build_node_gather(nc, c, "count1", m["relcnt"][:], e["src_lo"], e["slot"], TILES * TYPES, 1, share)
        build_messages(nc, c, e, "msg1", dram["rel_table"], dram["rel"], dram["src_row"], e["src"], share, 1, dram["acc"])
    close1(nc, c, m, dram["acc"])
    experts1(nc, c, m, I)


def layer2(nc, c, m, e, I, dram):
    with ExitStack() as ctx:
        sb = lambda n, sh, d=F32: ctx.enter_context(nc.sbuf_tensor(f"layer2_{n}", sh, d))
        m["WT"], m["dinv"], live = sb("WT", [128, KB, 5 * D]), sb("dinv", [R, TILES]), sb("live", [R, TILES])
        build_transposed(nc, c, "turn2", [I["L2_mix_Wqkv"], I["L2_mix_W1"], I["L2_mix_W2"]], m["WT"])

        def degree(v, own, act_step):
            d = m["dinv"][:]
            own(v.tensor_scalar(d, m["deg3"][:, 1, :], 1.0, None, ALU.add))
            own(v.tensor_scalar(live[:], d, 0.0, None, ALU.is_gt))
            own(v.tensor_scalar(d, d, 1e-30, None, ALU.max))
            act_step(v.tensor_copy(d, d), d, d, ACT.Sqrt)
            own(v.reciprocal(d, d))
            own(v.tensor_tensor(d, d, live[:], ALU.mult))
        bulk(nc, "degree2", degree)
        open2(nc, c, m, I, dram)
        with ExitStack() as inner:
            weight = e["weight"][:].unsqueeze(2)
            build_messages(nc, c, e, "msg2", dram["el"], as_chunks(I["src"]), dram["dst_row"], e["dst"], weight, 1, dram["acc"])
        close2(nc, c, m, I, dram["acc"])
    experts2(nc, c, m, I)


def experts2(nc, c, m, I):
    ENT, F = 8, 1024
    build_gated_open(nc, c, 2, m, I["L2_ffn_Wr"], I["L2_ffn_br"], ENT, "top_ratio")
    build_open(nc, c, "2n", m["XN"], m["XN"], m["XNT"], lambda sb: ({}, []), lambda w: [], lambda v, own, hand_over, b, grp: v.memset(b["st"][:], 0.0),
               lambda sp, b, i, sem=None: 0, None, None, 0)
    with ExitStack() as ctx:
        sb = lambda n, sh, d=F32: ctx.enter_context(nc.sbuf_tensor(f"ffn2_{n}", sh, d))
        b1, gain, shift = sb("b1", [128, ENT * F // 128]), sb("gain", [128, ENT * KB]), sb("shift", [128, ENT * KB])
        put_in(nc, "ffn2_in", [(b1[:, e * 8:(e + 1) * 8], columns(I["L2_ffn_b1"][e])) for e in range(ENT)]
               + [(t[:, e * KB:(e + 1) * KB], columns(I[n][e])) for t, n in ((gain, "L2_ffn_ln_g"), (shift, "L2_ffn_ln_b")) for e in range(ENT)])
        flat = lambda n: I[n].rearrange("e r o -> (e r) o")
        build_experts(nc, c, "ffn2e", m["XNT"], m["X"], None, ENT, [256, F, 256], [flat("L2_ffn_W1"), flat("L2_ffn_W2")],
                      everywhere(I["L2_ffn_b2"]), m["gate"], ACT.Gelu, [b1], affine=(gain, shift))


def layer3(nc, c, m, e, I, dram):
    H = 4
    with ExitStack() as ctx:
        sb = lambda n, sh, d=F32: ctx.enter_context(nc.sbuf_tensor(f"layer3_{n}", sh, d))
        m["p_self"], top = sb("p_self", [R, TILES, H]), sb("top", [R, H, TILES])
        top_t, self_ = sb("top_t", [R, TILES, H]), sb("self", [R, TILES, H])
        we, att, slope, mean = sb("we", [R, D]), sb("att", [R, D]), sb("slope", [R, H]), sb("mean", [R, TILES])
        m["a_src"], m["a_dst"], m["key_top"] = sb("a_src", [R, TILES, H]), sb("a_dst", [R, TILES, H]), sb("key_top", [R, D])
        put_in(nc, "layer3_in", [(we[:], everywhere(I["L3_gnn_We"].rearrange("o x -> (o x)"))), (att[:], everywhere(I["L3_gnn_att_edge"].rearrange("h x -> (h x)")))],
               [(m["key_top"][:], -HUGE)])
        open3(nc, c, m, I, dram)
        build_key_sums(nc, c, m, I["L3_mix_Wqkv"])

        def own_loops(v, own, act_step):
            own(v.tensor_tensor(we[:], we[:], att[:], ALU.mult))
            own(v.tensor_reduce(slope[:], we[:].rearrange("p (h x) -> p h x", h=H), AX, ALU.add))
            own(v.tensor_scalar(mean[:], m["deg3"][:, 0, :], 1.0, None, ALU.max))
            own(v.reciprocal(mean[:], mean[:]))
            own(v.tensor_tensor(mean[:], mean[:], m["deg3"][:, 2, :], ALU.mult))
            own(v.tensor_tensor(self_[:], col_of(mean[:], H), row_of(slope[:], TILES), ALU.mult))
            own(v.tensor_tensor(self_[:], self_[:], m["a_src"][:], ALU.add))
            own(v.tensor_tensor(self_[:], self_[:], m["a_dst"][:], ALU.add))
            own(leaky(v, self_[:]))
        bulk(nc, "loops3", own_loops)
        with ExitStack() as inner:
            sb = lambda n, sh, d=F32: inner.enter_context(nc.sbuf_tensor(f"gnn3_{n}", sh, d))
            logit, part = sb("logit", [R, CHUNKS, H]), sb("part", [R, CHUNKS, H])
            flat = lambda t: t[:].rearrange("p t h -> p (t h)")
            src_hi = sb("src_hi", [R, CHUNKS])

            def high(v, own, act_step):
                own(v.tensor_tensor(src_hi[:], e["src"][:], e["src_lo"][:], ALU.subtract))
                own(v.tensor_scalar(src_hi[:], src_hi[:], 1.0 / R, None, ALU.mult))
                own(v.tensor_scalar(src_hi[:], src_hi[:], 8388608.0 * 1.5, -8388608.0 * 1.5, ALU.add, ALU.add))
            bulk(nc, "high3", high)
            build_node_gather(nc, c, "asrc3", flat(m["a_src"]), e["src_lo"], src_hi, TILES, H, logit)
            build_node_gather(nc, c, "adst3", flat(m["a_dst"]), e["dst_lo"], e["dst_hi"], TILES, H, part)

            def logits(v, own, act_step):
                own(v.tensor_tensor(logit[:], logit[:], part[:], ALU.add))
                own(v.tensor_tensor(part[:], col_of(e["attr"][:], H), row_of(slope[:], CHUNKS), ALU.mult))
                own(v.tensor_tensor(logit[:], logit[:], part[:], ALU.add))
                own(leaky(v, logit[:]))
            bulk(nc, "logits3", logits)
            build_segment_max(nc, c, e, "max3", logit, H, top[:])

            def with_loops(v, own, act_step):
                own(v.tensor_tensor(top_t[:], top[:].rearrange("p h t -> p t h"), self_[:], ALU.max))
                act_step(v.tensor_tensor(self_[:], self_[:], top_t[:], ALU.subtract), m["p_self"][:], self_[:], ACT.Exp)
            bulk(nc, "tops3", with_loops)
            build_node_gather(nc, c, "top3", flat(top_t), e["dst_lo"], e["dst_hi"], TILES, H, part)

            def exps(v, own, act_step):
                act_step(v.tensor_tensor(logit[:], logit[:], part[:], ALU.subtract), logit[:], logit[:], ACT.Exp)
            bulk(nc, "exp3", exps)
            build_messages(nc, c, e, "msg3", dram["el"], as_chunks(I["src"]), dram["dst_row"], e["dst"], logit, H, dram["acc4"])
        close3(nc, c, m, I, dram["acc4"], dram["el"])
    experts3(nc, c, m, I)


def leaky(v, x):
    flat = x.rearrange("p a b -> p (a b)")
    return v.scalar_tensor_tensor(flat, flat, 0.2, flat, ALU.mult, ALU.max)


def experts3(nc, c, m, I):
    ENT = 8
    build_gated_open(nc, c, 3, m, I["L3_ffn_Wr"], I["L3_ffn_br"], ENT, "all")
    with ExitStack() as ctx:
        sb = lambda n, sh, d=F32: ctx.enter_context(nc.sbuf_tensor(f"ffn3_{n}", sh, d))
        t = {f"{n}{l}": sb(f"{n}{l}", [128, ENT * KB]) for n in ("b", "g", "be", "m", "v") for l in (1, 2)}
        put_in(nc, "ffn3_in", [(t[n][:, e * KB:(e + 1) * KB], columns(I["L3_ffn_" + n][e])) for n in t for e in range(ENT)])

        def fold(v, own, act_step):
            for l in "12":
                own(v.tensor_scalar(t["v" + l][:], t["v" + l][:], 1e-3, None, ALU.add))
                act_step(v.tensor_tensor(t["b" + l][:], t["b" + l][:], t["m" + l][:], ALU.subtract), t["m" + l][:], t["v" + l][:], ACT.Sqrt)
                own(v.reciprocal(t["v" + l][:], t["m" + l][:]))
                own(v.tensor_tensor(t["g" + l][:], t["g" + l][:], t["v" + l][:], ALU.mult))
                own(v.tensor_tensor(t["b" + l][:], t["b" + l][:], t["g" + l][:], ALU.mult))
                own(v.tensor_tensor(t["b" + l][:], t["b" + l][:], t["be" + l][:], ALU.add))
        bulk(nc, "fold3", fold)
        flat = lambda n: I[n].rearrange("e r o -> (e r) o")
        build_experts(nc, c, "ffn3e", m["XNT"], m["X"], None, ENT, [256, 256, 256, 256], [flat("L3_ffn_W1"), flat("L3_ffn_W2"), flat("L3_ffn_Wo")],
                      everywhere(I["L3_ffn_bo"]), m["gate"], ACT.Relu, [t["b1"], t["b2"]], layer_scale=[t["g1"], t["g2"]])


def build(nc, I, out):
    def scratch(name, shape, dt=F32):
        return nc.dram_tensor(name, shape, dt, kind="Internal").ap()

    dram = {"el": scratch("el_table", [NODES, D]), "er": scratch("er_table", [NODES, D]), "rel_table": scratch("rel_table", [NODES * TYPES, D]),
            "acc": [scratch(f"acc{k}", [NODES + R, D + 1]) for k in range(ACCS)], "acc4": [scratch(f"acc_heads{k}", [NODES + R, D + 4]) for k in range(ACCS)],
            "src_row": scratch("src_row", [R, CHUNKS], I32), "dst_row": scratch("dst_row", [R, CHUNKS], I32), "rel": scratch("rel_row", [R, CHUNKS], I32)}
    with ExitStack() as ctx:
        ctx.enter_context(nc.allow_non_contiguous_dma(reason="bias vectors as columns"))
        c, m, e = alloc_all(nc, ctx)
        edge_setup(nc, c, m, e, I, dram)
        put_in(nc, "x_in", [(m["X"][:], by_tile(I["x"]))])
        layer0(nc, c, m, e, I, dram)
        layer1(nc, c, m, e, I, dram)
        layer2(nc, c, m, e, I, dram)
        layer3(nc, c, m, e, I, dram)
        with phase(nc, "x_out", "stored") as s, nc.Block() as block:
            @block.sync
            def _(sp):
                sp.dma_start(by_tile(out), m["X"][:]).then_inc(s["stored"], 16)
                sp.wait_ge(s["stored"], 16)


def kernel(**inputs):
    import numpy as _np
    import concourse.bacc as _bacc
    from concourse import mybir as _mybir
    from concourse.bass_utils import run_bass_kernel_spmd as _run

    nc = _bacc.Bacc("TRN2", target_bir_lowering=False, num_devices=1)
    arrays, aps = {}, {}
    for name, value in inputs.items():
        a = _np.ascontiguousarray(value)
        arrays[f"in_{name}_dram"] = a
        aps[name] = nc.dram_tensor(f"in_{name}_dram", a.shape, _mybir.dt.from_np(a.dtype), kind="ExternalInput").ap()
    out = nc.dram_tensor("out_0_dram", [NODES, D], _mybir.dt.float32, kind="ExternalOutput").ap()
    build(nc, aps, out)
    r = _run(nc, [arrays], core_ids=[0])
    return r.results[0]["out_0_dram"]
```

```python
from contextlib import ExitStack, contextmanager

import concourse.bass as bass
from concourse import mybir

F32 = mybir.dt.float32
I32 = mybir.dt.int32
I16 = mybir.dt.int16
BF16 = mybir.dt.bfloat16
ALU = mybir.AluOpType
ACT = mybir.ActivationFunctionType
AX = mybir.AxisListType.X

NODES, EDGES, D = 3125, 100000, 256
R = 125
TILES = NODES // R
CHUNKS = EDGES // R
G = 4
LANES = 2
UNIT = G * LANES
TURNS = CHUNKS // UNIT
GT = 5
GROUPS = TILES // GT
GN = GT * R
KB = D // 128
HUGE = 3.0e38
TYPES = 7
ACCS = G


class Chain:

    def __init__(self, eng, sem, turn=None, per_turn=0, before=0):
        self.eng, self.sem, self.turn, self.per_turn, self.before, self.n = eng, sem, turn, per_turn, before, 0

    def __call__(self, ins):
        self.n += 1
        ins.then_inc(self.sem, 1)
        n = self.before + self.n
        self.eng.wait_ge(self.sem, n if self.turn is None else self.turn * self.per_turn + n)

    def pause(self, passed):
        self.eng.sem_inc(passed, 1)

    def end(self):
        assert self.turn is None or self.n == self.per_turn, f"this loop's turn has {self.n} steps"


class Steps:

    def __init__(self, sem, names, before=0):
        self.sem, self.names, self.before, self.order = sem, names, before, {n: k for k, n in enumerate(names)}
        assert len(self.order) == len(names)

    def at(self, name, turn=None):
        k = self.before + self.order[name] + 1
        return k if turn is None else turn * len(self.names) + k


@contextmanager
def phase(nc, tag, *names):
    sems = {n: nc.alloc_semaphore(f"{tag}_{n}") for n in names}
    yield sems
    nc.clear_and_free_semaphores(list(sems.values()))
    nc.all_engine_barrier()


def row_of(ap, k):
    return ap.unsqueeze(1).to_broadcast([ap.shape[0], k, ap.shape[1]])


def col_of(ap, n):
    return ap.unsqueeze(2).to_broadcast([ap.shape[0], ap.shape[1], n])


def build_constants(nc, c):
    with phase(nc, "constants", "pool_made", "made", "chain") as s:
        with nc.Block() as block:
            @block.gpsimd
            def _(pool):
                own = Chain(pool, s["pool_made"])
                own(nc.gpsimd.iota(c["iota_i"][:], [[1, 256]], base=0, channel_multiplier=0))
                own(nc.gpsimd.iota(c["part_i"][:], [[0, 1]], base=0, channel_multiplier=1))

            @block.vector
            def _(dve):
                own = Chain(dve, s["chain"])
                dve.wait_ge(s["pool_made"], 2)
                own(nc.vector.tensor_copy(c["iota"][:], c["iota_i"][:]))
                own(nc.vector.tensor_copy(c["part"][:], c["part_i"][:]))
                own(nc.vector.memset(c["ones"][:], 1.0))
                own(nc.vector.memset(c["zeros"][:], 0.0))
                own(nc.vector.tensor_scalar(c["ident"][:], c["iota"][:, 0:128], c["part"][:], None, ALU.is_equal))
                own(nc.vector.tensor_scalar(c["lower"][:], c["iota"][:, 0:128], c["part"][:], None, ALU.is_lt))
                for h in range(4):
                    own(nc.vector.tensor_scalar(c["block4"][:, h:h + 1], c["part"][:], h * 32 - 0.5, None, ALU.is_gt))
                    own(nc.vector.tensor_scalar(c["tmp1"][:], c["part"][:], h * 32 + 31.5, None, ALU.is_lt))
                    own(nc.vector.tensor_tensor(c["block4"][:, h:h + 1], c["block4"][:, h:h + 1], c["tmp1"][:], ALU.mult))
                own(nc.vector.tensor_copy(c["block"][:].rearrange("p (h x) -> p h x", x=32), col_of(c["block4"][:], 32)))


def build_edge_numbers(nc, c, e, src, dst, edge_type, edge_weight, edge_attr):
    with phase(nc, "numbers", "edges_in", "chain") as s, nc.Block() as block:
        @block.sync
        def _(sp):
            for to, frm in ((e["src_i"], src), (e["dst_i"], dst), (e["typ_i"], edge_type)):
                sp.dma_start(to[:], frm.rearrange("(p c) -> p c", p=R)).then_inc(s["edges_in"], 16)
            sp.dma_start(e["weight"][:], edge_weight.rearrange("(p c) -> p c", p=R)).then_inc(s["edges_in"], 16)
            sp.dma_start(e["attr"][:], edge_attr.rearrange("(p c) k -> p (c k)", p=R)).then_inc(s["edges_in"], 16)

        @block.vector
        def _(dve):
            own = Chain(dve, s["chain"])
            dve.wait_ge(s["edges_in"], 80)
            v = nc.vector
            for side in ("src", "dst"):
                ids, lo, hi, cmp, it = e[side][:], e[side + "_lo"][:], e[side + "_hi"][:], e["tmp"][:], e["tmp_i"][:]
                own(v.tensor_copy(ids, e[side + "_i"][:]))
                own(v.tensor_scalar(hi, ids, 1.0 / R, None, ALU.mult))
                own(v.tensor_copy(it, hi))
                own(v.tensor_copy(hi, it))
                own(v.scalar_tensor_tensor(lo, hi, -float(R), ids, ALU.mult, ALU.add))
                own(v.tensor_scalar(cmp, lo, 0.0, None, ALU.is_lt))
                own(v.scalar_tensor_tensor(lo, cmp, float(R), lo, ALU.mult, ALU.add))
                own(v.scalar_tensor_tensor(hi, cmp, -1.0, hi, ALU.mult, ALU.add))
                own(v.tensor_scalar(cmp, lo, float(R), None, ALU.is_ge))
                own(v.scalar_tensor_tensor(lo, cmp, -float(R), lo, ALU.mult, ALU.add))
                own(v.tensor_tensor(hi, cmp, hi, ALU.add))
            own(v.tensor_copy(e["tmp"][:], e["typ_i"][:]))
            own(v.scalar_tensor_tensor(e["slot"][:], e["src_hi"][:], float(TYPES), e["tmp"][:], ALU.mult, ALU.add))
            own(v.scalar_tensor_tensor(e["tmp"][:], e["dst"][:], float(TYPES), e["tmp"][:], ALU.mult, ALU.add))
            own(v.tensor_copy(e["rel_i"][:], e["tmp"][:]))


def build_edge_rows(nc, c, e, dram):
    names = ("src", "dst", "src_lo", "dst_lo")
    B = 100
    with ExitStack() as ctx:
        turned_p = [ctx.enter_context(nc.psum_tensor(f"edge_rows_p{k}", [B, CHUNKS // B, 128], F32)) for k in range(len(names))]
        rows = [ctx.enter_context(nc.sbuf_tensor(f"edge_rows{k}", [B, CHUNKS // B, R], I16)) for k in range(len(names))]
        with phase(nc, "edge_rows", "turned", "copied", "stored") as s, nc.Block() as block:
            @block.tensor
            def _(pe):
                for k, name in enumerate(names):
                    for b in range(CHUNKS // B):
                        last = nc.tensor.transpose(turned_p[k][:, b, 0:R], e[name][:, b * B:(b + 1) * B], c["ident"][0:R, 0:R])
                    last.then_inc(s["turned"], 1)

            @block.scalar
            def _(act):
                for k in range(len(names)):
                    act.wait_ge(s["turned"], k + 1)
                    nc.scalar.copy(rows[k][:], turned_p[k][:, :, 0:R]).then_inc(s["copied"], 1)

            @block.sync
            def _(sp):
                for k, name in enumerate(names):
                    sp.wait_ge(s["copied"], k + 1)
                    sp.dma_start(dram[name + "_ids"].rearrange("(b p r) -> p b r", p=B, r=R), rows[k][:]).then_inc(s["stored"], 16)
                sp.wait_ge(s["stored"], 16 * len(names))


def spread(ids, i, lane):
    return ids[bass.ds((i * UNIT + lane * G) * R, G * R)].partition_broadcast(R)


def flat(t):
    return t.rearrange("p g j -> p (g j)")


def in_chunks(t):
    return t.rearrange("p (g j) -> p g j", g=G)


def build_scatter_rows(nc, c, e, dram):
    sides = ("src", "dst")
    with ExitStack() as ctx:
        ids = {n: [ctx.enter_context(nc.sbuf_tensor(f"ids_{n}{l}", [R, G * R], I16)) for l in range(LANES)] for n in sides}
        earlier = ctx.enter_context(nc.sbuf_tensor("earlier", [R, LANES, G, len(sides), R], F32))
        with phase(nc, "scatter_rows", "ids_in0", "ids_in1", "ids_used", "chain", "stored") as s, nc.Block() as block:
            @block.vector
            def _(dve):
                v = nc.vector
                with dve.Fori(0, TURNS) as i:
                    for l in range(LANES):
                        dve.wait_ge(s[f"ids_in{l}"], i * 32 + 32)
                        for g in range(G):
                            for k, side in enumerate(sides):
                                at = bass.ds(i * UNIT + l * G + g, 1)
                                last = v.scalar_tensor_tensor(earlier[:, l, g, k], ids[side][l][:, g * R:(g + 1) * R], e[side][:, at], c["lower"][0:R, 0:R],
                                                              ALU.is_equal, ALU.mult, accum_out=e[side + "_dup"][:, at])
                        last.then_inc(s["ids_used"], 1)
                    dve.wait_ge(s["ids_used"], (i + 1) * LANES)
                after = Chain(dve, s["chain"])
                for side in sides:
                    dup, t = e[side + "_dup"][:], e["tmp"][:]
                    after(v.tensor_scalar(dup, dup, 1.0, None, ALU.min))
                    after(v.tensor_scalar(t, e[side][:], c["part"][0:R, :], -float(NODES), ALU.subtract, ALU.add))
                    after(v.tensor_tensor(t, t, dup, ALU.mult))
                    after(v.tensor_tensor(t, e[side][:], t, ALU.subtract))
                    after(v.tensor_copy(e["tmp_i"][:] if side == "src" else e["typ_i"][:], t))
                    after(v.tensor_scalar(dup, dup, -1.0, 1.0, ALU.mult, ALU.add))

            @block.sync
            def _(sp):
                def loads(i, first=False):
                    for l in range(LANES):
                        if not first:
                            sp.wait_ge(s["ids_used"], i * LANES + l - LANES + 1)
                        for side in sides:
                            sp.dma_start(ids[side][l][:], spread(dram[side + "_ids"], i, l)).then_inc(s[f"ids_in{l}"], 16)
                loads(0, first=True)
                with sp.Fori(1, TURNS) as i:
                    loads(i)
                sp.wait_ge(s["chain"], 12)
                sp.dma_start(dram["src_row"], e["tmp_i"][:]).then_inc(s["stored"], 16)
                sp.dma_start(dram["dst_row"], e["typ_i"][:]).then_inc(s["stored"], 16)
                sp.dma_start(dram["rel"], e["rel_i"][:]).then_inc(s["stored"], 16)
                sp.wait_ge(s["stored"], 48)


def build_degrees(nc, c, e, deg3, relcnt):
    KD, KT = 3 * TILES, TILES * TYPES
    with ExitStack() as ctx:
        sb = lambda n, sh, d=F32: ctx.enter_context(nc.sbuf_tensor(n, sh, d))
        hot_d = [sb(f"hot_d{l}", [R, G, R]) for l in range(LANES)]
        hot_s = [sb(f"hot_s{l}", [R, G, R], BF16) for l in range(LANES)]
        pay_d = [sb(f"pay_d{l}", [R, G, 3, TILES]) for l in range(LANES)]
        pay_s = [sb(f"pay_s{l}", [R, G, KT], BF16) for l in range(LANES)]
        acc_d = ctx.enter_context(nc.psum_tensor("acc_d", [R, KD], F32))
        acc_s = ctx.enter_context(nc.psum_tensor("acc_s", [R, KT], F32))
        with phase(nc, "degrees", "hots_ready", "summed", "chain") as s, nc.Block() as block:
            @block.vector
            def _(dve):
                v = nc.vector
                with dve.Fori(0, TURNS) as i:
                    own = Chain(dve, s["chain"], i, LANES)
                    for l in range(LANES):
                        cs = bass.ds(i * UNIT + l * G, G)
                        dve.wait_ge(s["summed"], i * LANES + l + 1)
                        v.tensor_tensor(hot_d[l][:], row_of(c["iota"][0:R, 0:R], G), col_of(e["dst_lo"][:, cs], R), ALU.is_equal)
                        v.tensor_tensor(hot_s[l][:], row_of(c["iota"][0:R, 0:R], G), col_of(e["src_lo"][:, cs], R), ALU.is_equal)
                        v.tensor_tensor(pay_s[l][:], row_of(c["iota"][0:R, 0:KT], G), col_of(e["slot"][:, cs], KT), ALU.is_equal)
                        own(v.tensor_tensor(pay_d[l][:, :, 0, :], row_of(c["iota"][0:R, 0:TILES], G),
                                            col_of(e["dst_hi"][:, cs], TILES), ALU.is_equal))
                        v.tensor_tensor(pay_d[l][:, :, 1, :], pay_d[l][:, :, 0, :], col_of(e["weight"][:, cs], TILES), ALU.mult)
                        v.tensor_tensor(pay_d[l][:, :, 2, :], pay_d[l][:, :, 0, :],
                                        col_of(e["attr"][:, cs], TILES), ALU.mult).then_inc(s["hots_ready"], 1)
                    own.end()
                dve.wait_ge(s["summed"], LANES * (TURNS + 1) + 1)
                v.tensor_copy(deg3, acc_d[:])
                v.tensor_copy(relcnt, acc_s[:])

            @block.tensor
            def _(pe):
                t = nc.tensor
                t.matmul(acc_d[:], c["zeros"][0:R, 0:R], c["zeros"][0:R, 0:KD], start=True, stop=False, skip_group_check=True)
                t.matmul(acc_s[:], c["zeros"][0:R, 0:R], c["zeros"][0:R, 0:KT], start=True, stop=False,
                         skip_group_check=True).then_inc(s["summed"], LANES)
                with pe.Fori(0, TURNS) as i:
                    for l in range(LANES):
                        pe.wait_ge(s["hots_ready"], i * LANES + l + 1)
                        for g in range(G):
                            t.matmul(acc_d[:], hot_d[l][:, g, :], pay_d[l][:, g].rearrange("p k t -> p (k t)"),
                                     start=False, stop=False, skip_group_check=True)
                            last = t.matmul(acc_s[:], hot_s[l][:, g, :], pay_s[l][:, g, :],
                                            start=False, stop=False, skip_group_check=True)
                        last.then_inc(s["summed"], 1)
                t.matmul(acc_d[:], c["zeros"][0:R, 0:R], c["zeros"][0:R, 0:KD], start=False, stop=True, skip_group_check=True)
                t.matmul(acc_s[:], c["zeros"][0:R, 0:R], c["zeros"][0:R, 0:KT], start=False, stop=True,
                         skip_group_check=True).then_inc(s["summed"], 1)


class Tops:

    names = ("scores_ready", "spread_ready", "spread_used", "ranking", "pay_ready", "placed_ready")
    STEPS = 6

    def __init__(self, nc, c, e, s, sb, ps, sc, top, heads):
        self.nc, self.c, self.e, self.s, self.sc, self.top, self.heads = nc, c, e, s, sc, top, heads
        lanes = range(LANES)
        self.banks = min(heads, 2)
        self.other = [sb(f"other{l}", [R, G, R]) for l in lanes]
        self.masked = [[sb(f"masked{l}_{k}", [R, G, R]) for k in range(self.banks)] for l in lanes]
        self.hot = [sb(f"place{l}", [R, G, R]) for l in lanes]
        self.best = [sb(f"best{l}", [R, heads, G]) for l in lanes]
        self.pay = [sb(f"pay{l}", [R, G, heads + 1, TILES]) for l in lanes]
        self.cand = [sb(f"cand{l}", [R, G, heads + 1, TILES]) for l in lanes]
        self.most = [sb(f"most{l}", [R, heads, TILES]) for l in lanes]
        self.spread_p = [[ps(f"spread{l}_{k}", [R, 512]) for k in range(self.banks)] for l in lanes]
        self.placed = [ps(f"placed{l}", [R, G, 128]) for l in lanes]

    def prepare(self, v, own, l, i, ids):
        e, c, heads = self.e, self.c, self.heads
        cs = bass.ds(i * UNIT + l * G, G)
        for g in range(G):
            v.tensor_scalar(self.other[l][:, g, :], ids[:, g * R:(g + 1) * R], e["dst"][:, bass.ds(i * UNIT + l * G + g, 1)], -HUGE, ALU.not_equal, ALU.mult)
        v.tensor_tensor(self.hot[l][:], row_of(c["iota"][0:R, 0:R], G), col_of(e["dst_lo"][:, cs], R), ALU.is_equal)
        own(v.tensor_tensor(self.cand[l][:, :, heads, :], row_of(c["iota"][0:R, 0:TILES], G), col_of(e["dst_hi"][:, cs], TILES), ALU.is_equal))
        own(v.tensor_tensor(self.pay[l][:, :, heads, :], self.cand[l][:, :, heads, :], col_of(e["dst_dup"][:, cs], TILES), ALU.mult))

    def rank(self, dve, v, own, l, i):
        s, heads = self.s, self.heads
        for h in range(heads):
            n = (i * LANES + l) * heads + h
            dve.wait_ge(s["spread_ready"], n + 1)
            if h >= 2:
                dve.wait_ge(s["spread_used"], n - 1)
            dve.sem_inc(s["ranking"], 1)
            for g in range(G):
                last = v.tensor_tensor_reduce(self.masked[l][h % 2][:, g, :], self.other[l][:, g, :], self.spread_p[l][h % 2][:, g * R:(g + 1) * R],
                                              1.0, -HUGE, ALU.add, ALU.max, self.best[l][:, h, g:g + 1])
            last.then_inc(s["spread_used"], 1)
        dve.wait_ge(s["spread_used"], (i * LANES + l + 1) * heads)
        v.tensor_tensor(self.pay[l][:, :, 0:heads, :], self.pay[l][:, :, heads, :].unsqueeze(2).to_broadcast([R, G, heads, TILES]),
                        self.best[l][:].rearrange("p h g -> p g h").unsqueeze(3).to_broadcast([R, G, heads, TILES]), ALU.mult).then_inc(s["pay_ready"], 1)

    def raise_tops(self, dve, v, own, l, i):
        heads, cand, placed = self.heads, self.cand, self.placed
        dve.wait_ge(self.s["placed_ready"], i * LANES + l + 1)
        there = cand[l][:, :, heads, :]
        own(v.tensor_scalar(there, placed[l][:, :, heads * TILES:(heads + 1) * TILES], 1.0, HUGE, ALU.subtract, ALU.mult))
        own(v.tensor_tensor(cand[l][:, :, 0:heads, :], placed[l][:, :, 0:heads * TILES].rearrange("p g (h t) -> p g h t", h=heads),
                            there.unsqueeze(2).to_broadcast([R, G, heads, TILES]), ALU.add))
        own(v.tensor_reduce(self.most[l][:], cand[l][:, :, 0:heads, :].rearrange("p g h t -> p h t g"), AX, ALU.max))
        own(v.tensor_tensor(self.top, self.top, self.most[l][:], ALU.max))

    def spread_scores(self, pe, t, l, i):
        s, heads = self.s, self.heads
        pe.wait_ge(s["scores_ready"], i * LANES + l + 1)
        for h in range(heads):
            if h >= 2:
                pe.wait_ge(s["spread_used"], (i * LANES + l) * heads + h - 1)
            for g in range(G):
                last = t.matmul(self.spread_p[l][h % 2][:, g * R:(g + 1) * R], self.sc[l][:, g, h:h + 1].to_broadcast([R, R]),
                                self.c["ident"][0:R, 0:R], start=True, stop=True)
            last.then_inc(s["spread_ready"], 1)

    def place(self, pe, t, l, i):
        pe.wait_ge(self.s["pay_ready"], i * LANES + l + 1)
        for g in range(G):
            last = t.matmul(self.placed[l][:, g, 0:(self.heads + 1) * TILES], self.hot[l][:, g, :], self.pay[l][:, g].rearrange("p h t -> p (h t)"),
                            start=True, stop=True)
        last.then_inc(self.s["placed_ready"], 1)


def build_logits3(nc, c, e, dram, a_src, a_dst, src_hi, slope, logit, top):
    heads = logit.shape[2]
    K = TILES * heads
    with ExitStack() as ctx:
        sb = lambda n, sh, d=F32: ctx.enter_context(nc.sbuf_tensor(f"logits3_{n}", sh, d))
        ps = lambda n, sh: ctx.enter_context(nc.psum_tensor(f"logits3_{n}", sh, F32))
        per_lane = lambda n, sh, d=F32: [sb(f"{n}{l}", sh, d) for l in range(LANES)]
        sides = ("src", "dst")
        table, high = {"src": a_src, "dst": a_dst}, {"src": src_hi, "dst": e["dst_hi"][:]}
        ids = per_lane("ids", [R, G * R], I16)
        lo = {n: per_lane(f"lo_{n}", [R, G * R], I16) for n in sides}
        hot = {n: per_lane(f"hot_{n}", [R, G, R]) for n in sides}
        mask = {n: per_lane(f"mask_{n}", [R, G, TILES]) for n in sides}
        picked = {n: sb(f"picked_{n}", [R, G, TILES, heads]) for n in sides}
        found = {n: ps(f"found_{n}", [R, G, 128]) for n in sides}
        sc, part = per_lane("sc", [R, G, heads]), per_lane("part", [R, G, heads])
        names = ["ids_in0", "ids_in1", "ids_used", "hot_ready", "found_ready", "found_used", "chain", "passed"] + list(Tops.names)
        with phase(nc, "logits3", *names) as s, nc.Block() as block:
            tops = Tops(nc, c, e, s, sb, ps, sc, top, heads)

            @block.sync
            def _(sp):
                def loads(i, first=False):
                    for l in range(LANES):
                        if not first:
                            sp.wait_ge(s["ids_used"], i * LANES + l - LANES + 1)
                        for to, frm in ((ids, "dst"), (lo["src"], "src_lo"), (lo["dst"], "dst_lo")):
                            sp.dma_start(to[l][:], spread(dram[frm + "_ids"], i, l)).then_inc(s[f"ids_in{l}"], 16)
                loads(0, first=True)
                with sp.Fori(1, TURNS) as i:
                    loads(i)

            @block.vector
            def _(dve):
                v = nc.vector
                before = Chain(dve, s["chain"])
                before(v.memset(top, -HUGE))
                with dve.Fori(0, TURNS) as i:
                    own = Chain(dve, s["chain"], i, LANES * (6 + Tops.STEPS), before=1)
                    cs = [bass.ds(i * UNIT + l * G, G) for l in range(LANES)]
                    for l in range(LANES):
                        dve.wait_ge(s[f"ids_in{l}"], i * 48 + 48)
                        for n in sides:
                            v.tensor_scalar(flat(hot[n][l][:]), lo[n][l][:], c["part"][0:R, :], None, ALU.is_equal).then_inc(s["hot_ready"], 1)
                        for n in sides:
                            last = v.tensor_tensor(mask[n][l][:], row_of(c["iota"][0:R, 0:TILES], G), col_of(high[n][:, cs[l]], TILES), ALU.is_equal)
                        own(last)
                        tops.prepare(v, own, l, i, ids[l])
                        v.tensor_tensor(part[l][:], col_of(e["attr"][:, cs[l]], heads), row_of(slope, G), ALU.mult).then_inc(s["ids_used"], 1)
                    for l in range(LANES):
                        for n in sides:
                            dve.wait_ge(s["found_ready"], (i * LANES + l) * 2 + sides.index(n) + 1)
                            v.tensor_tensor(picked[n][:], found[n][:, :, 0:K].rearrange("p g (k h) -> p g k h", h=heads),
                                            mask[n][l][:].unsqueeze(3).to_broadcast([R, G, TILES, heads]), ALU.mult).then_inc(s["found_used"], 1)
                        dve.wait_ge(s["found_used"], (i * LANES + l + 1) * 2)
                        own(v.tensor_tensor(picked["src"][:], picked["src"][:], picked["dst"][:], ALU.add))
                        own(v.tensor_reduce(sc[l][:], picked["src"][:].rearrange("p g k h -> p g h k"), AX, ALU.add))
                        own(v.tensor_tensor(sc[l][:], sc[l][:], part[l][:], ALU.add))
                        own(v.tensor_scalar(part[l][:], sc[l][:], 0.2, None, ALU.mult))
                        last = v.tensor_tensor(sc[l][:], sc[l][:], part[l][:], ALU.max)
                        last.then_inc(s["scores_ready"], 1)
                        dve.wait_ge(s["scores_ready"], i * LANES + l + 1)
                        own(v.tensor_copy(logit[:, cs[l], :], sc[l][:]))
                    for l in range(LANES):
                        tops.rank(dve, v, own, l, i)
                    for l in range(LANES):
                        tops.raise_tops(dve, v, own, l, i)
                    own.end()

            @block.tensor
            def _(pe):
                t = nc.tensor
                with pe.Fori(0, TURNS) as i:
                    for l in range(LANES):
                        for k, n in enumerate(sides):
                            pe.wait_ge(s["hot_ready"], (i * LANES + l) * 2 + k + 1)
                            if l:
                                pe.wait_ge(s["found_used"], (i * LANES + l) * 2 + k - 1)
                            for g in range(G):
                                last = t.matmul(found[n][:, g, 0:K], hot[n][l][:, g, :], table[n], start=True, stop=True)
                            last.then_inc(s["found_ready"], 1)
                    for l in range(LANES):
                        tops.spread_scores(pe, t, l, i)
                    for l in range(LANES):
                        tops.place(pe, t, l, i)


def build_messages(nc, c, e, tag, table, take, put, node, ids, weight, heads, acc, look=None):
    W = D + heads
    C = D // heads
    with ExitStack() as ctx:
        sb = lambda n, sh, d=F32: ctx.enter_context(nc.sbuf_tensor(f"{tag}_{n}", sh, d))
        per_lane = lambda n, sh, d=F32: [sb(f"{n}{l}", sh, d) for l in range(LANES)]
        take_b, put_b = per_lane("take", [R, G], I32), per_lane("put", [R, G], I32)
        rows, sent = per_lane("rows", [R, G, W]), per_lane("sent", [R, G, W])
        zrow = sb("zrow", [R, (NODES + R) // 2 // R * W])
        id_b, same = per_lane("ids", [R, G * R], I16), per_lane("same", [R, G, R])
        sum_p = [ctx.enter_context(nc.psum_tensor(f"{tag}_sum{g}", [R, 512], F32)) for g in range(G)]
        if look:
            slots = look["slots"]
            K = slots * heads
            lo_b, hot, mask = per_lane("lo", [R, G * R], I16), per_lane("hot", [R, G, R]), per_lane("mask", [R, G, slots])
            picked, w = per_lane("picked", [R, G, slots, heads]), per_lane("w", [R, G, heads])
            diff = per_lane("diff", [R, G, heads])
            found = [ctx.enter_context(nc.psum_tensor(f"{tag}_found{l}", [R, G, 128 if K <= 128 else 256], F32)) for l in range(LANES)]
        ids_bytes = 32 if look else 16
        names = ([f"{n}{l}" for n in ("take_in", "put_in", "rows_in", "ids_in") for l in range(LANES)]
                 + [f"acc_done{g}" for g in range(G)]
                 + ["made", "zeroed", "same_ready", "hot_ready", "found_ready", "diff_ready", "exp_ready", "scaled", "summed", "moved", "chain", "pool_at", "sp_at"])
        with phase(nc, tag, *names) as s, nc.Block() as block:
            @block.sync
            def _(sp):
                def load_ids(i, l):
                    sp.dma_start(id_b[l][:], spread(ids, i, l)).then_inc(s[f"ids_in{l}"], 16)
                    if look:
                        sp.dma_start(lo_b[l][:], spread(look["ids"], i, l)).then_inc(s[f"ids_in{l}"], 16)

                def load_numbers(i, l):
                    cs = bass.ds(i * UNIT + l * G, G)
                    sp.dma_start(take_b[l][:], take[:, cs]).then_inc(s[f"take_in{l}"], 16)
                    return cs

                for l in range(LANES):
                    sp.dma_start(put_b[l][:], put[:, load_numbers(0, l)]).then_inc(s[f"put_in{l}"], 16)
                    load_ids(0, l)
                sp.wait_ge(s["made"], 1)
                half = (NODES + R) // 2
                for k in range(ACCS):
                    for part in range(2):
                        sp.dma_start(acc[k][part * half:(part + 1) * half].rearrange("(p n) d -> p (n d)", p=R),
                                     zrow[:]).then_inc(s["zeroed"], 16)
                with sp.Fori(1, TURNS) as i:
                    for l in range(LANES):
                        sp.wait_ge(s["same_ready"], i * LANES + l - LANES + 1)
                        if look:
                            sp.wait_ge(s["hot_ready"], i * LANES + l - LANES + 1)
                        load_ids(i, l)
                    for l in range(LANES):
                        sp.wait_ge(s[f"rows_in{l}"], i * (16 * G))
                        sp.sem_inc(s["sp_at"], 1)
                        cs = load_numbers(i, l)
                        for g in range(G):
                            sp.wait_ge(s[f"acc_done{g}"], i * (16 * LANES) + 16 * (l - LANES + 1))
                        sp.dma_start(put_b[l][:], put[:, cs]).then_inc(s[f"put_in{l}"], 16)

            @block.vector
            def _(dve):
                v = nc.vector
                with dve.Fori(0, TURNS) as i:
                    own = Chain(dve, s["chain"], i, LANES * (2 if weight is None else 3))
                    cs = [bass.ds(i * UNIT + l * G, G) for l in range(LANES)]
                    for l in range(LANES):
                        dve.wait_ge(s[f"ids_in{l}"], i * ids_bytes + ids_bytes)
                        if look:
                            v.tensor_scalar(flat(hot[l][:]), lo_b[l][:], c["part"][0:R, :], None, ALU.is_equal).then_inc(s["hot_ready"], 1)
                            own(v.tensor_tensor(mask[l][:], row_of(c["iota"][0:R, 0:slots], G), col_of(look["slot"][:, cs[l]], slots), ALU.is_equal))
                        dve.wait_ge(s["summed"], i * UNIT + (l + 1) * G)
                        v.tensor_tensor(same[l][:], in_chunks(id_b[l][:]), col_of(node[:, cs[l]], R), ALU.is_equal).then_inc(s["same_ready"], 1)
                    for l in range(LANES if look else 0):
                        dve.wait_ge(s["found_ready"], i * LANES + l + 1)
                        own(v.tensor_tensor(picked[l][:], found[l][:, :, 0:K].rearrange("p g (k h) -> p g k h", h=heads),
                                            mask[l][:].unsqueeze(3).to_broadcast([R, G, slots, heads]), ALU.mult))
                        to = w[l] if weight is None else diff[l]
                        last = v.tensor_reduce(to[:], picked[l][:].rearrange("p g k h -> p g h k"), AX, ALU.add)
                        if weight is None:
                            last.then_inc(s["exp_ready"], 1)
                        else:
                            own(last)
                            v.tensor_tensor(diff[l][:], weight[:, cs[l], :], diff[l][:], ALU.subtract).then_inc(s["diff_ready"], 1)
                    for l in range(LANES):
                        weigh = w[l][:] if look else weight[:, cs[l], :]
                        if look:
                            dve.wait_ge(s["exp_ready"], i * LANES + l + 1)
                        dve.wait_ge(s[f"rows_in{l}"], i * (16 * G) + 16 * G)
                        v.tensor_copy(rows[l][:, :, D:W], weigh)
                        vw = rows[l][:, :, 0:D].rearrange("p g (h x) -> p g h x", h=heads)
                        v.tensor_tensor(vw, vw, weigh.unsqueeze(3).to_broadcast([R, G, heads, C]), ALU.mult).then_inc(s["scaled"], 1)
                    if look:
                        own.end()

            @block.tensor
            def _(pe):
                t = nc.tensor
                pe.sem_inc(s["summed"], UNIT)
                with pe.Fori(0, TURNS) as i:
                    for l in range(LANES if look else 0):
                        pe.wait_ge(s["hot_ready"], i * LANES + l + 1)
                        for g in range(G):
                            last = t.matmul(found[l][:, g, 0:K], hot[l][:, g, :], look["table"], start=True, stop=True)
                        last.then_inc(s["found_ready"], 1)
                    for l in range(LANES):
                        pe.wait_ge(s["same_ready"], i * LANES + l + 1)
                        pe.wait_ge(s["scaled"], i * LANES + l + 1)
                        for g in range(G):
                            pe.wait_ge(s["moved"], i * UNIT + l * G + g + 1)
                            t.matmul(sum_p[g][:, 0:W], same[l][:, g, :], rows[l][:, g, :], start=True, stop=True).then_inc(s["summed"], 1)

            @block.scalar
            def _(act):
                act.sem_inc(s["moved"], G)

                def move(i, first=False):
                    if look and weight is not None:
                        for l in range(LANES):
                            act.wait_ge(s["diff_ready"], i * LANES + l + 1)
                            nc.scalar.activation(w[l][:], diff[l][:], ACT.Exp).then_inc(s["exp_ready"], 1)
                    for l in range(LANES):
                        for g in range(G):
                            act.wait_ge(s["summed"], i * UNIT + UNIT + l * G + g + 1)
                            if not first:
                                act.wait_ge(s[f"acc_done{g}"], i * (16 * LANES))
                            nc.scalar.copy(sent[l][:, g, :], sum_p[g][:, 0:W]).then_inc(s["moved"], 1)

                move(0, first=True)
                with act.Fori(1, TURNS) as i:
                    move(i)

            @block.gpsimd
            def _(pool):
                nc.gpsimd.memset(zrow[:], 0.0).then_inc(s["made"], 1)

                def gather(i, l):
                    pool.wait_ge(s[f"take_in{l}"], i * 16 + 16)
                    pool.wait_ge(s["summed"], i * UNIT + (l + 1) * G)
                    pool.sem_inc(s["pool_at"], 1)
                    for g in range(G):
                        nc.gpsimd.indirect_dma_start(rows[l][:, g, 0:D], None, table, bass.IndirectOffsetOnAxis(ap=take_b[l][:, g:g + 1], axis=0)
                                                     ).then_inc(s[f"rows_in{l}"], 16)

                def scatter(i, l, first=False):
                    pool.wait_ge(s[f"put_in{l}"], i * 16 + 16)
                    for g in range(G):
                        pool.wait_ge(s["moved"], i * UNIT + (l + 1) * G + g + 1)
                        if not first:
                            pool.wait_ge(s[f"acc_done{g}"], i * (16 * LANES) + 16 * l)
                        pool.sem_inc(s["pool_at"], 1)
                        nc.gpsimd.indirect_dma_start(acc[g], bass.IndirectOffsetOnAxis(ap=put_b[l][:, g:g + 1], axis=0), sent[l][:, g, :], None,
                                                     compute_op=ALU.add).then_inc(s[f"acc_done{g}"], 16)

                gather(0, 0)
                gather(0, 1)
                pool.wait_ge(s["zeroed"], 16 * 2 * ACCS)
                scatter(0, 0, first=True)
                gather(1, 0)
                scatter(0, 1)
                with pool.Fori(1, TURNS - 1) as i:
                    gather(i, 1)
                    scatter(i, 0)
                    gather(i + 1, 0)
                    scatter(i, 1)
                gather(TURNS - 1, 1)
                scatter(TURNS - 1, 0)
                scatter(TURNS - 1, 1)
                for g in range(G):
                    pool.wait_ge(s[f"acc_done{g}"], 16 * LANES * TURNS)



def until(eng, steps, name, turn=None):
    eng.wait_ge(steps.sem, steps.at(name, turn))


def mark(ins, steps):
    ins.then_inc(steps.sem, 1)


def by_tile(ap):
    return ap.rearrange("(t r) w -> r t w", r=R)


def slices(ap):
    return ap[:, 0:GT * 128].rearrange("p (s x) -> p s x", x=128)[:, :, 0:R]


def dense(ap):
    return ap.rearrange("p (s x) -> p s x", x=R)


def turn_tiles(nc, c, to, tile, blocks=KB):
    for k in range(blocks):
        for j in range(GT):
            q = k * GT + j
            last = nc.tensor.transpose(to[:, q * 128:q * 128 + R], tile[:, j, k * 128:(k + 1) * 128], c["ident"][0:R, 0:R])
    return last


def turned(ap, blocks=KB):
    return ap[:, 0:blocks * GT * 128].rearrange("p (q x) -> p q x", x=128)[:, :, 0:R]


def product_t(nc, to, m, pairs):
    first, second = to[0:m, 0:512].rearrange("p (s x) -> p s x", x=128)[:, :, 0:R], to[0:m, 512:512 + R]
    n = len(pairs)
    for a, (w, f) in enumerate(pairs):
        nc.tensor.matmul(first, w, f[:, 0:4 * R].rearrange("p (s x) -> p s x", x=R), start=(a == 0), stop=(a == n - 1))
    for a, (w, f) in enumerate(pairs):
        last = nc.tensor.matmul(second, w, f[:, 4 * R:GN], start=(a == 0), stop=(a == n - 1))
    return last


def product_rows(nc, to, pairs):
    n = len(pairs)
    for j in range(GT):
        for a, (f, w) in enumerate(pairs):
            last = nc.tensor.matmul(to[:, j, :], f[:, j * R:(j + 1) * R], w, start=(a == 0), stop=(a == n - 1))
    return last


def variance(v, own, x, b, eps, passed):
    for j in range(GT):
        last = v.bn_stats(b["stats"][:, j, :], x[:, j, :])
    own(last)
    own.pause(passed)
    for j in range(GT):
        last = v.bn_aggr(b["mv"][:, j, :], b["stats"][:, j, :])
    own(last)
    return v.tensor_scalar(b["var"][:], b["mv"][:, :, 1], eps, None, ALU.add)


VARIANCE_STEPS = 2


def standardize(v, own, x, out, b):
    own(v.reciprocal(b["rstd"][:], b["std"][:]))
    for j in range(GT):
        last = v.tensor_scalar(out[:, j, :], x[:, j, :], b["mv"][:, j, 0:1], b["rstd"][:, j:j + 1], ALU.subtract, ALU.mult)
    return last


STANDARDIZE_STEPS = 1


def norm_buffers(sb):
    return {"stats": sb("stats", [R, GT, 6]), "mv": sb("mv", [R, GT, 2]), "var": sb("var", [R, GT]),
            "std": sb("std", [R, GT]), "rstd": sb("rstd", [R, GT])}


def build_open(nc, c, layer, X, XN, XNT, loads, units, post, stores, kv, kv_cols, per_turn, hand=()):
    tag = f"open{layer}"
    NU = len(units(None))
    UNITS = [f"u{n}" for n in range(NU * GT)]
    with ExitStack() as ctx:
        sb = lambda n, sh, d=F32: ctx.enter_context(nc.sbuf_tensor(f"{tag}_{n}", sh, d))
        ps = lambda n, sh: ctx.enter_context(nc.psum_tensor(f"{tag}_{n}", sh, F32))
        b = norm_buffers(sb)
        xn_s, xT = sb("xn_s", [R, GT, D]), sb("xT", [128, KB, GN])
        st = sb("st", [R, GT, max(sum(n for _, n in units(None)), 1)])
        b["st"], b["xn_s"] = st, xn_s
        wide, unit_p, kv_p = ps("wide", [128, 1536]), [ps(f"unit{n}", [R, 512]) for n in range(4)], ps("kv_p", [128, KB, 256])
        w, w_loads = loads(sb)
        b.update(w)
        with phase(nc, tag, "loaded", "pe", "dve", "act", "stored", "chain", "passed", "sp_passed") as s, nc.Block() as block:
            PE = Steps(s["pe"], ["turn"] + UNITS + ["kv_added"])
            HANDS = [f"hand{n}" for n in range(len(hand))]
            DV = Steps(s["dve"], ["var", "xn"] + HANDS + ["post"])
            AC = Steps(s["act"], ["std", "keep", "turned", "all_turned"] + UNITS + HANDS)
            NS = stores(None, b, None)

            @block.sync
            def _(sp):
                for to, frm in w_loads:
                    sp.dma_start(to, frm).then_inc(s["loaded"], 16)
                with sp.Fori(0, GROUPS) as i:
                    until(sp, DV, "post", i)
                    sp.sem_inc(s["sp_passed"], 1)
                    if NS:
                        stores(sp, b, i, s["stored"])
                if NS:
                    sp.wait_ge(s["stored"], 16 * NS * GROUPS)

            @block.vector
            def _(dve):
                v = nc.vector
                dve.wait_ge(s["loaded"], 16 * len(w_loads))
                with dve.Fori(0, GROUPS) as i:
                    own = Chain(dve, s["chain"], i, VARIANCE_STEPS + STANDARDIZE_STEPS + per_turn)
                    grp = bass.ds(i * GT, GT)
                    mark(variance(v, own, X[:, grp, :], b, 1e-5, s["passed"]), DV)
                    until(dve, AC, "std", i)
                    mark(standardize(v, own, X[:, grp, :], xn_s, b), DV)
                    until(dve, DV, "xn", i)
                    until(dve, AC, (UNITS or ["all_turned"])[-1], i)
                    handed = iter(HANDS)

                    def hand_over(ins):
                        mark(ins, DV)
                        until(dve, AC, next(handed), i)

                    mark(post(v, own, hand_over, b, grp), DV)
                    own.end()
                    until(dve, PE, "kv_added", i)
                    until(dve, AC, "all_turned", i)
                    if NS:
                        dve.wait_ge(s["stored"], i * (16 * NS) + 16 * NS)

            @block.scalar
            def _(act):
                a = nc.scalar
                with act.Fori(0, GROUPS) as i:
                    grp = bass.ds(i * GT, GT)
                    until(act, DV, "var", i)
                    mark(a.activation(b["std"][:], b["var"][:], ACT.Sqrt), AC)
                    until(act, DV, "xn", i)
                    mark(a.copy(XN[:, grp, :], xn_s[:]), AC)
                    until(act, PE, "turn", i)
                    mark(a.copy(xT[:].rearrange("p k (j x) -> p (k j) x", x=R), turned(wide[:])), AC)
                    until(act, AC, "turned", i)
                    mark(a.copy(XNT[:, :, bass.ds(i * GN, GN)], xT[:]), AC)
                    at = 0
                    for u, name in enumerate(UNITS):
                        n = units(None)[u % NU][1]
                        until(act, PE, name, i)
                        mark(a.copy(st[:, u // NU, at:at + n], unit_p[u % 4][:, 0:n]), AC)
                        at = (at + n) % st.shape[2]
                    for n, name in enumerate(HANDS):
                        until(act, DV, name, i)
                        mark(a.activation(b["hand_out"], b["hand_in"], hand[n]), AC)
                    until(act, DV, "post", i)
                    until(act, PE, "kv_added", i)
                    if NS:
                        act.wait_ge(s["stored"], i * (16 * NS) + 16 * NS)

            @block.tensor
            def _(pe):
                t = nc.tensor
                pe.wait_ge(s["loaded"], 16 * len(w_loads))
                for k in range(KB):
                    t.matmul(kv_p[:, k, :], c["zeros"][:, 0:128], c["zeros"][:, 0:256], start=(k == 0), stop=False, skip_group_check=True)
                with pe.Fori(0, GROUPS) as i:
                    until(pe, DV, "xn", i)
                    mark(turn_tiles(nc, c, wide, xn_s), PE)
                    until(pe, AC, "turned", i)
                    for u, name in enumerate(UNITS):
                        if u >= 4:
                            until(pe, AC, UNITS[u - 4], i)
                        j, (wk, n) = u // NU, units(w)[u % NU]
                        for k in range(KB):
                            last = t.matmul(unit_p[u % 4][:, 0:n], xT[:, k, j * R:(j + 1) * R], wk[k], start=(k == 0), stop=(k == KB - 1))
                        mark(last, PE)
                    until(pe, DV, "post", i)
                    if kv is None:
                        mark(t.matmul(kv_p[:, 0, :], c["zeros"][:, 0:128], c["zeros"][:, 0:256], start=False, stop=False, skip_group_check=True), PE)
                    else:
                        mark(kv(t, kv_p, b), PE)
                for k in range(KB):
                    last = t.matmul(kv_p[:, k, :], c["zeros"][:, 0:128], c["zeros"][:, 0:256], start=False, stop=True, skip_group_check=True)
        if kv_cols is None:
            return
        with phase(nc, tag + "_end", "chain") as s, nc.Block() as block:
            @block.vector
            def _(dve):
                v = nc.vector
                own = Chain(dve, s["chain"])
                kv_cols(v, own, kv_p, b)


def blocked(w, k):
    return w[k * 128:(k + 1) * 128]


def everywhere(vec, p=R):
    return vec.partition_broadcast(p)


def center_heads(v, own, x3, b, div, eps):
    n = x3.shape[1]
    own(v.tensor_reduce(b["hm"][:, 0:n], x3, AX, ALU.add))
    own(v.tensor_scalar(b["hm"][:, 0:n], b["hm"][:, 0:n], 1.0 / 32, None, ALU.mult))
    own(v.tensor_tensor(x3, x3, col_of(b["hm"][:, 0:n], 32), ALU.subtract))
    own(v.tensor_tensor(b["sq"][:, 0:n, :], x3, x3, ALU.mult))
    own(v.tensor_reduce(b["hm"][:, 0:n], b["sq"][:, 0:n, :], AX, ALU.add))
    return v.tensor_scalar(b["hand_in"], b["hm"][:, 0:n], 1.0 / div, eps, ALU.mult, ALU.add)


CENTER_STEPS = 5


def keep_blocks(c, scale, out, ones=False):
    def cols(v, own, kv_p, b):
        for k in range(KB):
            own(v.scalar_tensor_tensor(out[:, k, 0:128], kv_p[:, k, 0:128], scale, c["block"][:], ALU.mult, ALU.mult))
            if ones:
                own(v.tensor_scalar(out[:, k, 128:132], c["block4"][:], kv_p[:, k, 128:129], None, ALU.mult))
    return cols


def open0(nc, c, m, I, dram):
    def loads(sb):
        w = {"el": sb("w_el", [128, KB, 512]), "kv": sb("w_kv", [128, KB, 512]), "bias": sb("bias", [R, 1024]),
             "gain": sb("gain", [R, 512]), "shift": sb("shift", [R, 512]), "hm": sb("hm", [R, 16 * GT]), "sq": sb("sq", [R, 16 * GT, 32]),
             "hv": sb("hv", [R, 16 * GT]), "hs": sb("hs", [R, 16 * GT])}
        w["hand_in"], w["hand_out"] = w["hv"][:], w["hs"][:]
        l = []
        for k in range(KB):
            l += [(w["el"][:, k, 0:D], blocked(I["L0_gnn_W_src"], k)), (w["el"][:, k, D:512], blocked(I["L0_gnn_W_dst"], k)),
                  ] + [(w["kv"][:, k, n * D:(n + 1) * D].rearrange("p (h x) -> p h x", x=32),
                        blocked(I["L0_mix_w_qkv"], k).rearrange("p (h x) -> p h x", x=96)[:, :, 32 * n + 32:32 * n + 64]) for n in range(2)]
        l += [(w["bias"][:, 0:D], everywhere(I["L0_gnn_b_src"])), (w["bias"][:, D:512], everywhere(I["L0_gnn_b_dst"])),
              ] + [(w["bias"][:, 512 + n * D:512 + (n + 1) * D].rearrange("p (h x) -> p h x", x=32),
                    everywhere(I["L0_mix_b_qkv"]).rearrange("p (h x) -> p h x", x=96)[:, :, 32 * n + 32:32 * n + 64]) for n in range(2)]
        for to, kind in (("gain", "g"), ("shift", "b")):
            for n, of in enumerate("kv"):
                l.append((w[to][:, n * D:(n + 1) * D].rearrange("p (h x) -> p h x", x=32),
                          everywhere(I[f"L0_mix_{of}ln_{kind}"]).unsqueeze(1).to_broadcast([R, 8, 32])))
        return w, l

    def units(w):
        return [(w and [w[n][:, k, :] for k in range(KB)], 512) for n in ("el", "kv")]

    def post(v, own, hand_over, b, grp):
        own(v.tensor_tensor(b["st"][:], b["st"][:], row_of(b["bias"][:], GT), ALU.add))
        own(v.tensor_copy(b["sq"][:].rearrange("p (j h) x -> p j (h x)", j=GT), b["st"][:, :, 512:1024]))
        kv3 = b["st"][:, :, 512:1024].rearrange("p j (h x) -> p j h x", x=32)
        sq3, hm3 = b["sq"][:].rearrange("p (j h) x -> p j h x", j=GT), b["hm"][:].rearrange("p (j h) -> p j h", j=GT)
        own(v.tensor_reduce(b["hm"][:], b["sq"][:], AX, ALU.add))
        own(v.tensor_scalar(b["hm"][:], b["hm"][:], 1.0 / 32, None, ALU.mult))
        own(v.tensor_tensor(kv3, kv3, hm3.unsqueeze(3).to_broadcast([R, GT, 16, 32]), ALU.subtract))
        own(v.tensor_tensor(sq3, kv3, kv3, ALU.mult))
        own(v.tensor_reduce(b["hm"][:], b["sq"][:], AX, ALU.add))
        hand_over(v.tensor_scalar(b["hand_in"], b["hm"][:], 1.0 / 32, 1e-5, ALU.mult, ALU.add))
        own(v.reciprocal(b["hm"][:], b["hand_out"]))
        own(v.tensor_tensor(kv3, kv3, hm3.unsqueeze(3).to_broadcast([R, GT, 16, 32]), ALU.mult))
        own(v.tensor_tensor(b["st"][:, :, 512:1024], b["st"][:, :, 512:1024], row_of(b["gain"][:], GT), ALU.mult))
        return v.tensor_tensor(b["st"][:, :, 512:1024], b["st"][:, :, 512:1024], row_of(b["shift"][:], GT), ALU.add)

    def stores(sp, b, i, sem=None):
        if sp is not None:
            grp = bass.ds(i * GT, GT)
            sp.dma_start(by_tile(dram["el"])[:, grp], b["st"][:, :, 0:D]).then_inc(sem, 16)
            sp.dma_start(by_tile(dram["er"])[:, grp], b["st"][:, :, D:512]).then_inc(sem, 16)
        return 2

    def kv(t, kv_p, b):
        for j in range(GT):
            for k in range(KB):
                at = 512 + k * 128
                last = t.matmul(kv_p[:, k, 0:128], b["st"][:, j, at:at + 128], b["st"][:, j, at + D:at + D + 128], start=False, stop=False, skip_group_check=True)
        return last

    build_open(nc, c, 0, m["X"], m["XN"], m["XNT"], loads, units, post, stores, kv, keep_blocks(c, 1.0 / NODES, m["KV"]), 10, hand=(ACT.Sqrt,))


def open1(nc, c, m, I, dram):
    def loads(sb):
        w = {"rel": sb("w_rel", [128, KB, TYPES * D]), "hm": sb("hm", [R, 8 * GT]), "sq": sb("sq", [R, 8 * GT, 32]),
             "hv": sb("hv", [R, 8 * GT]), "hs": sb("hs", [R, 8 * GT]), "val": sb("val", [R, GT, D])}
        w["hand_in"], w["hand_out"] = w["hv"][:], w["hs"][:]
        l = [(w["rel"][:, k, :].rearrange("p (t o) -> p t o", t=TYPES),
              I["L1_gnn_weights"].rearrange("(t k p) o -> k p t o", t=TYPES, k=KB)[k]) for k in range(KB)]
        for n in ("kln_weight", "kln_bias", "vln_weight", "vln_bias"):
            w[n] = sb(n, [R, D])
            l.append((w[n][:], everywhere(I["L1_mix_" + n].rearrange("h o x -> (h o x)"))))
        return w, l

    def units(w):
        at = list(range(0, TYPES * D, 512))
        return [(w and [w["rel"][:, k, a:min(a + 512, TYPES * D)] for k in range(KB)], min(512, TYPES * D - a)) for a in at]

    def post(v, own, hand_over, b, grp):
        heads = b["xn_s"][:].rearrange("p j (h x) -> p (j h) x", x=32)
        hand_over(center_heads(v, own, heads, b, 31.0, 0.0))
        own(v.tensor_scalar(b["hm"][:], b["hand_out"], 1e-5, None, ALU.add))
        own(v.reciprocal(b["hm"][:], b["hm"][:]))
        own(v.tensor_tensor(heads, heads, col_of(b["hm"][:], 32), ALU.mult))
        own(v.tensor_tensor(b["val"][:], b["xn_s"][:], row_of(b["vln_weight"][:], GT), ALU.mult))
        own(v.tensor_tensor(b["val"][:], b["val"][:], row_of(b["vln_bias"][:], GT), ALU.add))
        own(v.tensor_tensor(b["xn_s"][:], b["xn_s"][:], row_of(b["kln_weight"][:], GT), ALU.mult))
        return v.tensor_tensor(b["xn_s"][:], b["xn_s"][:], row_of(b["kln_bias"][:], GT), ALU.add)

    def stores(sp, b, i, sem=None):
        if sp is not None:
            sp.dma_start(dram["rel_table"].rearrange("(t r s) d -> r t (s d)", r=R, s=TYPES)[:, bass.ds(i * GT, GT)], b["st"][:]).then_inc(sem, 16)
        return 1

    def kv(t, kv_p, b):
        for j in range(GT):
            for k in range(KB):
                cs = slice(k * 128, (k + 1) * 128)
                last = t.matmul(kv_p[:, k, 0:128], b["xn_s"][:, j, cs], b["val"][:, j, cs], start=False, stop=False, skip_group_check=True)
        return last

    build_open(nc, c, 1, m["X"], m["XN"], m["XNT"], loads, units, post, stores, kv, keep_blocks(c, 1.0 / NODES, m["KV"]), CENTER_STEPS + 6, hand=(ACT.Sqrt,))


def open2(nc, c, m, I, dram):
    def loads(sb):
        w = {"low": sb("low", [R, GT, D]), "exp": sb("exp", [R, GT, D]), "scaled": sb("scaled", [R, GT, D])}
        w["hand_in"], w["hand_out"] = w["low"][:], w["exp"][:]
        return w, []

    def units(w):
        return [([m["WT"][:, k, D:3 * D] for k in range(KB)], 512)]

    def post(v, own, hand_over, b, grp):
        own(v.tensor_tensor(b["scaled"][:], b["xn_s"][:], col_of(m["dinv"][:, grp], D), ALU.mult))
        hand_over(v.tensor_scalar(b["low"][:], b["st"][:, :, 0:D], 0.0, None, ALU.min))
        own(v.tensor_scalar(b["low"][:], b["st"][:, :, 0:D], 0.0, None, ALU.max))
        return v.tensor_tensor(b["low"][:], b["low"][:], b["exp"][:], ALU.add)

    def stores(sp, b, i, sem=None):
        if sp is not None:
            sp.dma_start(by_tile(dram["el"])[:, bass.ds(i * GT, GT)], b["scaled"][:]).then_inc(sem, 16)
        return 1

    def kv(t, kv_p, b):
        for j in range(GT):
            for k in range(KB):
                key = b["low"][:, j, k * 128:(k + 1) * 128]
                t.matmul(kv_p[:, k, 0:128], key, b["st"][:, j, D + k * 128:D + (k + 1) * 128], start=False, stop=False, skip_group_check=True)
                last = t.matmul(kv_p[:, k, 128:129], key, c["ones"][0:R, 0:1], start=False, stop=False, skip_group_check=True)
        return last

    build_open(nc, c, 2, m["X"], m["XN"], m["XNT"], loads, units, post, stores, kv, keep_blocks(c, 1.0, m["KV"], ones=True), 2, hand=(ACT.Exp,))


def open3(nc, c, m, I, dram):
    def loads(sb):
        w = {"xk": sb("w_xk", [128, KB, 512]), "att_src": sb("att_src", [R, D]), "att_dst": sb("att_dst", [R, D]), "prod": sb("prod", [R, GT, D]),
             "most": sb("most", [R, D])}
        l = []
        for k in range(KB):
            l += [(w["xk"][:, k, 0:D], blocked(I["L3_gnn_W"], k)), (w["xk"][:, k, D:512], blocked(I["L3_mix_Wqkv"], k)[:, D:2 * D])]
        for n in ("att_src", "att_dst"):
            l.append((w[n][:], everywhere(I["L3_gnn_" + n].rearrange("h x -> (h x)"))))
        return w, l

    def units(w):
        return [(w and [w["xk"][:, k, :] for k in range(KB)], 512)]

    def post(v, own, hand_over, b, grp):
        for n in ("src", "dst"):
            own(v.tensor_tensor(b["prod"][:], b["st"][:, :, 0:D], row_of(b["att_" + n][:], GT), ALU.mult))
            own(v.tensor_reduce(m["a_" + n][:, grp, :], b["prod"][:].rearrange("p j (h x) -> p j h x", h=4), AX, ALU.add))
        own(v.tensor_reduce(b["most"][:], b["st"][:, :, D:512].rearrange("p j x -> p x j"), AX, ALU.max))
        return v.tensor_tensor(m["key_top"][:], m["key_top"][:], b["most"][:], ALU.max)

    def stores(sp, b, i, sem=None):
        if sp is not None:
            sp.dma_start(by_tile(dram["el"])[:, bass.ds(i * GT, GT)], b["st"][:, :, 0:D]).then_inc(sem, 16)
        return 1

    build_open(nc, c, 3, m["X"], m["XN"], m["XNT"], loads, units, post, stores, None, None, 5)


def build_score0(nc, c, e, src, dst, dram, attn, score, top):
    with ExitStack() as ctx:
        sb = lambda n, sh, d=F32: ctx.enter_context(nc.sbuf_tensor(f"score0_{n}", sh, d))
        ps = lambda n, sh: ctx.enter_context(nc.psum_tensor(f"score0_{n}", sh, F32))
        per_lane = lambda n, sh, d=F32: [sb(f"{n}{l}", sh, d) for l in range(LANES)]
        ends = ("src", "dst")
        idx = {n: per_lane(f"idx_{n}", [R, G], I32) for n in ends}
        rows = {n: per_lane(f"rows_{n}", [R, G, D]) for n in ends}
        ids, sc, att = per_lane("ids", [R, G * R], I16), per_lane("sc", [R, G, 1]), sb("att", [R, D])
        names = [f"{n}{l}" for n in ("idx_in", "rows_in", "ids_in") for l in range(LANES)] + ["ids_used", "loaded", "chain", "pool_at", "sp_at"]
        with phase(nc, "score0", *names, *Tops.names) as s, nc.Block() as block:
            tops = Tops(nc, c, e, s, sb, ps, sc, top, 1)

            @block.sync
            def _(sp):
                sp.dma_start(att[:], everywhere(attn)).then_inc(s["loaded"], 16)

                def loads(i, first=False):
                    for l in range(LANES):
                        if not first:
                            sp.wait_ge(s[f"rows_in{l}"], i * (2 * 16 * G))
                            sp.sem_inc(s["sp_at"], 1)
                        for n, frm in (("src", src), ("dst", dst)):
                            sp.dma_start(idx[n][l][:], frm[:, bass.ds(i * UNIT + l * G, G)]).then_inc(s[f"idx_in{l}"], 16)
                        if not first:
                            sp.wait_ge(s["ids_used"], i * LANES + l - LANES + 1)
                            sp.sem_inc(s["sp_at"], 1)
                        sp.dma_start(ids[l][:], spread(dram["dst_ids"], i, l)).then_inc(s[f"ids_in{l}"], 16)
                loads(0, first=True)
                with sp.Fori(1, TURNS) as i:
                    loads(i)

            @block.gpsimd
            def _(pool):
                def gather(i, first=False):
                    for l in range(LANES):
                        pool.wait_ge(s[f"idx_in{l}"], i * 32 + 32)
                        if not first:
                            pool.wait_ge(s["scores_ready"], i * LANES + l - LANES + 1)
                        pool.sem_inc(s["pool_at"], 1)
                        for g in range(G):
                            for n, table in (("src", dram["el"]), ("dst", dram["er"])):
                                nc.gpsimd.indirect_dma_start(rows[n][l][:, g, :], None, table, bass.IndirectOffsetOnAxis(ap=idx[n][l][:, g:g + 1], axis=0)
                                                             ).then_inc(s[f"rows_in{l}"], 16)
                gather(0, first=True)
                with pool.Fori(1, TURNS) as i:
                    gather(i)

            @block.vector
            def _(dve):
                v = nc.vector
                before = Chain(dve, s["chain"])
                before(v.memset(top, -HUGE))
                dve.wait_ge(s["loaded"], 16)
                with dve.Fori(0, TURNS) as i:
                    own = Chain(dve, s["chain"], i, LANES * (2 + Tops.STEPS), before=1)
                    for l in range(LANES):
                        dve.wait_ge(s[f"ids_in{l}"], i * 16 + 16)
                        tops.prepare(v, own, l, i, ids[l])
                        a, b = rows["src"][l], rows["dst"][l]
                        dve.wait_ge(s[f"rows_in{l}"], i * (2 * 16 * G) + 2 * 16 * G)
                        v.tensor_tensor(a[:], a[:], b[:], ALU.add).then_inc(s["ids_used"], 1)
                        dve.wait_ge(s["ids_used"], i * LANES + l + 1)
                        own(v.scalar_tensor_tensor(flat(b[:]), flat(a[:]), 0.2, flat(a[:]), ALU.mult, ALU.max))
                        for g in range(G):
                            last = v.tensor_tensor_reduce(a[:, g, :], b[:, g, :], att[:], 1.0, 0.0, ALU.mult, ALU.add, sc[l][:, g, :])
                        last.then_inc(s["scores_ready"], 1)
                        dve.wait_ge(s["scores_ready"], i * LANES + l + 1)
                        own(v.tensor_copy(score[:, bass.ds(i * UNIT + l * G, G), :], sc[l][:]))
                        if l:
                            tops.rank(dve, v, own, 0, i)
                    tops.rank(dve, v, own, 1, i)
                    for l in range(LANES):
                        tops.raise_tops(dve, v, own, l, i)
                    own.end()

            @block.tensor
            def _(pe):
                t = nc.tensor
                with pe.Fori(0, TURNS) as i:
                    for l in range(LANES):
                        tops.spread_scores(pe, t, l, i)
                    for l in range(LANES):
                        tops.place(pe, t, l, i)


def columns(vec, p=128):
    return vec.rearrange("(k p) -> p k", p=p)


def heads_product(nc, to, features, kv, small=None):
    for j in range(GT):
        for k in range(KB):
            f = features[:, k, j * R:(j + 1) * R]
            last = nc.tensor.matmul(to[:, j, k * 128:(k + 1) * 128], f, kv[:, k, 0:128], start=True, stop=True)
            if small is not None:
                last = nc.tensor.matmul(small[:, j, k * 4:(k + 1) * 4], f, kv[:, k, 128:132], start=True, stop=True)
    return last


def sum_accumulators(v, own, b):
    a = b["acc"]
    own(v.tensor_tensor(a[:, 0:2], a[:, 0:2], a[:, 2:4], ALU.add))
    own(v.tensor_tensor(a[:, 0], a[:, 0], a[:, 1], ALU.add))
    return a[:, 0]


def load_accumulators(sp, acc, b, i, sem, extra=()):
    for k in range(ACCS):
        sp.dma_start(b["acc"][:, k], by_tile(acc[k][0:NODES])[:, bass.ds(i * GT, GT)]).then_inc(sem, 16)
    for to, frm in extra:
        sp.dma_start(to[:], by_tile(frm)[:, bass.ds(i * GT, GT)]).then_inc(sem, 16)


def close0(nc, c, m, I, acc):
    tag = "close0"
    with ExitStack() as ctx:
        sb = lambda n, sh, d=F32: ctx.enter_context(nc.sbuf_tensor(f"{tag}_{n}", sh, d))
        ps = lambda n, sh: ctx.enter_context(nc.psum_tensor(f"{tag}_{n}", sh, F32))
        b = {"acc": sb("acc", [R, ACCS, GT, D + 1]), "t": sb("t", [R, GT, D]), "z": sb("z", [R, GT])}
        wq, w1, w2 = sb("wq", [128, KB, D]), sb("w1", [128, KB, D]), sb("w2", [128, KB, D])
        bq, b1, b2 = sb("bq", [128, KB]), sb("b1", [128, KB]), sb("b2", [R, D])
        qT, rT, hT, ret = sb("qT", [128, KB, GN]), sb("rT", [128, KB, GN]), sb("hT", [128, KB, GN]), sb("ret", [R, GT, D])
        wide, fb = ps("wide", [128, 1536]), [ps(f"fb{n}", [128, 1024]) for n in range(2)]
        rows = wide[0:R, 0:GT * D].rearrange("p (j x) -> p j x", j=GT)
        loads = [(b1[:], columns(I["L0_mix_b1"])), (b2[:], everywhere(I["L0_mix_b2"]))]
        for k in range(KB):
            loads += [(wq[:, k, :].rearrange("p (h x) -> p h x", x=32), blocked(I["L0_mix_w_qkv"], k).rearrange("p (h x) -> p h x", x=96)[:, :, 0:32]),
                      (w1[:, k, :], blocked(I["L0_mix_w1"], k)), (w2[:, k, :], blocked(I["L0_mix_w2"], k))]
            for h in range(4):
                at = (k * 4 + h) * 96
                loads.append((bq[h * 32:(h + 1) * 32, k:k + 1], I["L0_mix_b_qkv"][at:at + 32].unsqueeze(1)))
        with phase(nc, tag, "loaded", "acc_in", "sp_passed", "pe", "dve", "act", "chain") as s, nc.Block() as block:
            PE = Steps(s["pe"], ["q0", "q1", "mix", "turn", "h0", "h1", "y"])
            DV = Steps(s["dve"], ["acc_used", "ret", "y"])
            AC = Steps(s["act"], ["q0", "q1", "turn", "h0", "h1"])

            @block.sync
            def _(sp):
                for to, frm in loads:
                    sp.dma_start(to, frm).then_inc(s["loaded"], 16)
                with sp.Fori(0, GROUPS) as i:
                    load_accumulators(sp, acc, b, i, s["acc_in"])
                    until(sp, DV, "acc_used", i)
                    sp.sem_inc(s["sp_passed"], 1)

            @block.tensor
            def _(pe):
                pe.wait_ge(s["loaded"], 16 * len(loads))
                with pe.Fori(0, GROUPS) as i:
                    xt = [m["XNT"][:, k, bass.ds(i * GN, GN)] for k in range(KB)]
                    for g in range(KB):
                        mark(product_t(nc, fb[g], 128, [(wq[:, k, g * 128:(g + 1) * 128], xt[k]) for k in range(KB)]), PE)
                    until(pe, AC, "q1", i)
                    mark(heads_product(nc, rows, qT, m["KV"]), PE)
                    until(pe, DV, "ret", i)
                    mark(turn_tiles(nc, c, wide, ret), PE)
                    until(pe, AC, "turn", i)
                    for g in range(KB):
                        mark(product_t(nc, fb[g], 128, [(w1[:, k, g * 128:(g + 1) * 128], rT[:, k, :]) for k in range(KB)]), PE)
                    until(pe, AC, "h1", i)
                    mark(product_rows(nc, rows, [(hT[:, k, :], w2[:, k, :]) for k in range(KB)]), PE)
                    until(pe, DV, "y", i)

            @block.scalar
            def _(act):
                a = nc.scalar
                act.wait_ge(s["loaded"], 16 * len(loads))
                with act.Fori(0, GROUPS) as i:
                    for g in range(KB):
                        until(act, PE, f"q{g}", i)
                        mark(a.activation(dense(qT[:, g, :]), slices(fb[g]), ACT.Identity, bias=bq[:, g:g + 1]), AC)
                    until(act, PE, "turn", i)
                    mark(a.copy(rT[:].rearrange("p k (j x) -> p (k j) x", x=R), turned(wide[:])), AC)
                    for g in range(KB):
                        until(act, PE, f"h{g}", i)
                        mark(a.activation(dense(hT[:, g, :]), slices(fb[g]), ACT.Gelu, bias=b1[:, g:g + 1]), AC)

            @block.vector
            def _(dve):
                v = nc.vector
                dve.wait_ge(s["loaded"], 16 * len(loads))
                with dve.Fori(0, GROUPS) as i:
                    own = Chain(dve, s["chain"], i, 7)
                    x, xn = m["X"][:, bass.ds(i * GT, GT), :], m["XN"][:, bass.ds(i * GT, GT), :]
                    dve.wait_ge(s["acc_in"], i * (16 * ACCS) + 16 * ACCS)
                    a = sum_accumulators(v, own, b)
                    own(v.tensor_scalar(b["z"][:], a[:, :, D], 0.5, None, ALU.max))
                    own(v.reciprocal(b["z"][:], b["z"][:]))
                    own(v.tensor_tensor(b["t"][:], a[:, :, 0:D], col_of(b["z"][:], D), ALU.mult))
                    own(v.tensor_tensor(b["t"][:], b["t"][:], xn, ALU.add))
                    mark(v.tensor_tensor(x, x, b["t"][:], ALU.add), DV)
                    until(dve, PE, "mix", i)
                    mark(v.tensor_tensor(ret[:], rows, xn, ALU.add), DV)
                    until(dve, PE, "y", i)
                    until(dve, DV, "ret", i)
                    own(v.tensor_tensor(b["t"][:], rows, row_of(b2[:], GT), ALU.add))
                    mark(v.tensor_tensor(x, x, b["t"][:], ALU.add), DV)
                    until(dve, DV, "y", i)
                    own.end()


def close1(nc, c, m, acc):
    tag = "close1"
    with ExitStack() as ctx:
        sb = lambda n, sh, d=F32: ctx.enter_context(nc.sbuf_tensor(f"{tag}_{n}", sh, d))
        b = {"acc": sb("acc", [R, ACCS, GT, D + 1]), "t": sb("t", [R, GT, D])}
        xT = sb("xT", [128, KB, GN])
        wide = ctx.enter_context(nc.psum_tensor(f"{tag}_wide", [128, 1536], F32))
        rows = wide[0:R, 0:GT * D].rearrange("p (j x) -> p j x", j=GT)
        with phase(nc, tag, "acc_in", "sp_passed", "pe", "dve", "act", "chain") as s, nc.Block() as block:
            PE, DV, AC = Steps(s["pe"], ["mix"]), Steps(s["dve"], ["acc_used", "x"]), Steps(s["act"], ["x"])

            @block.sync
            def _(sp):
                with sp.Fori(0, GROUPS) as i:
                    load_accumulators(sp, acc, b, i, s["acc_in"])
                    until(sp, DV, "acc_used", i)
                    sp.sem_inc(s["sp_passed"], 1)

            @block.tensor
            def _(pe):
                with pe.Fori(0, GROUPS) as i:
                    until(pe, AC, "x", i)
                    mark(heads_product(nc, rows, xT, m["KV"]), PE)
                    until(pe, DV, "x", i)

            @block.scalar
            def _(act):
                with act.Fori(0, GROUPS) as i:
                    mark(nc.scalar.copy(xT[:], m["XNT"][:, :, bass.ds(i * GN, GN)]), AC)
                    until(act, PE, "mix", i)

            @block.vector
            def _(dve):
                v = nc.vector
                with dve.Fori(0, GROUPS) as i:
                    own = Chain(dve, s["chain"], i, 3)
                    x, xn = m["X"][:, bass.ds(i * GT, GT), :], m["XN"][:, bass.ds(i * GT, GT), :]
                    dve.wait_ge(s["acc_in"], i * (16 * ACCS) + 16 * ACCS)
                    a = sum_accumulators(v, own, b)
                    own(v.tensor_tensor(x, x, xn, ALU.add))
                    mark(v.tensor_tensor(b["t"][:], a[:, :, 0:D], x, ALU.add), DV)
                    until(dve, DV, "acc_used", i)
                    until(dve, PE, "mix", i)
                    mark(v.tensor_tensor(x, rows, b["t"][:], ALU.add), DV)
                    until(dve, DV, "x", i)
                    own.end()


def build_experts(nc, c, tag, XT, target, table, experts, dims, weights, last_bias, gate, func, layer_bias, layer_scale=None, affine=None):
    L = len(dims) - 1
    blocks = [max(d // 128, 1) for d in dims]
    part = [min(d, 128) for d in dims]
    P = min(experts, 2)
    with ExitStack() as ctx:
        sb = lambda n, sh, d=F32: ctx.enter_context(nc.sbuf_tensor(f"{tag}_{n}", sh, d))
        ps = lambda n, sh: ctx.enter_context(nc.psum_tensor(f"{tag}_{n}", sh, F32))
        wt = [[sb(f"w{l}_{p}", [part[l], blocks[l], dims[l + 1]]) for l in range(L)] for p in range(P)]
        h = [sb(f"h{l}", [part[l], blocks[l], GN]) for l in range(1, L)]
        xe = sb("xe", [128, KB, GN]) if affine else None
        brow, t = sb("brow", [R, experts, D]), sb("t", [R, GT, D])
        wide, fb = ps("wide", [128, 1536]), [ps(f"fb{n}", [128, 1024]) for n in range(2)]
        rows = wide[0:R, 0:GT * D].rearrange("p (j x) -> p j x", j=GT)
        jobs = [(l, g) for l in range(L - 1) for g in range(blocks[l + 1])]
        names = [f"h{l}_{g}" for l, g in jobs]
        NL = sum(blocks[:L])
        with phase(nc, tag, "loaded", "w_in0", "w_in1", "pe", "dve", "act", "chain", "pe_passed", "sp_passed") as s, nc.Block() as block:
            PE = Steps(s["pe"], names + ["rows"])
            AC = Steps(s["act"], (["xe"] if affine else []) + names)
            DV = Steps(s["dve"], ["rows_used", "x"], before=1)

            def each_expert(eng, body):
                if experts <= 2:
                    for e in range(experts):
                        body(e, e, e * GROUPS)
                else:
                    with eng.Fori(0, experts // 2) as n:
                        for p in range(2):
                            body(n * 2 + p, p, (n * 2 + p) * GROUPS)

            @block.sync
            def _(sp):
                sp.dma_start(brow[:], last_bias).then_inc(s["loaded"], 16)

                def load(e, p, first):
                    if not first:
                        until(sp, DV, "x", (e - 1) * GROUPS - 1)
                        sp.sem_inc(s["sp_passed"], 1)
                    for l in range(L):
                        for k in range(blocks[l]):
                            sp.dma_start(wt[p][l][:, k, :], weights[l][bass.ds(e * dims[l] + k * 128, part[l])]).then_inc(s[f"w_in{p}"], 16)
                for p in range(P):
                    load(p, p, True)
                if experts > 2:
                    with sp.Fori(1, experts // 2) as n:
                        for p in range(2):
                            load(n * 2 + p, p, False)

            @block.tensor
            def _(pe):
                def body(e, p, before):
                    pe.wait_ge(s[f"w_in{p}"], (e - p) * (8 * NL) + 16 * NL)
                    pe.sem_inc(s["pe_passed"], 1)
                    with pe.Fori(0, GROUPS) as i:
                        turn = i + before
                        if affine:
                            until(pe, AC, "xe", turn)
                            src = [xe[:, k, :] for k in range(KB)]
                        else:
                            src = [XT[:, k, bass.ds(i * GN, GN)] for k in range(KB)]
                        for n, (l, g) in enumerate(jobs):
                            if n >= 2:
                                until(pe, AC, names[n - 2], turn)
                            if l >= 1 and g == 0:
                                until(pe, AC, names[n - 1], turn)
                            ins = src if l == 0 else [h[l - 1][:, k, :] for k in range(blocks[l])]
                            m_ = part[l + 1]
                            mark(product_t(nc, fb[n % 2], m_, [(wt[p][l][:, k, g * 128:g * 128 + m_], ins[k]) for k in range(blocks[l])]), PE)
                        until(pe, AC, names[-1], turn)
                        until(pe, DV, "x", turn - 1)
                        mark(product_rows(nc, rows, [(h[-1][:, k, :], wt[p][L - 1][:, k, :]) for k in range(blocks[L - 1])]), PE)

                each_expert(pe, body)

            @block.scalar
            def _(act):
                a = nc.scalar

                def body(e, p, before):
                    with act.Fori(0, GROUPS) as i:
                        turn = i + before
                        if affine:
                            for k in range(KB):
                                last = a.activation(xe[:, k, :], XT[:, k, bass.ds(i * GN, GN)], ACT.Identity, bias=affine[1][:, bass.ds(e * KB + k, 1)],
                                                    scale=affine[0][:, bass.ds(e * KB + k, 1)])
                            mark(last, AC)
                        for n, (l, g) in enumerate(jobs):
                            until(act, PE, names[n], turn)
                            at = bass.ds(e * blocks[l + 1] + g, 1)
                            scale = layer_scale[l][0:part[l + 1], at] if layer_scale else 1.0
                            mark(a.activation(dense(h[l][:, g, :]), slices(fb[n % 2][0:part[l + 1], :]), func,
                                              bias=layer_bias[l][0:part[l + 1], at], scale=scale), AC)
                each_expert(act, body)

            @block.vector
            def _(dve):
                v = nc.vector
                dve.wait_ge(s["loaded"], 16)
                dve.sem_inc(s["dve"], 1)

                def body(e, p, before):
                    with dve.Fori(0, GROUPS) as i:
                        turn = i + before
                        own = Chain(dve, s["chain"], turn, 1 if gate is not None else 0)
                        x = target[:, bass.ds(i * GT, GT), :]
                        until(dve, PE, "rows", turn)
                        v.tensor_tensor(t[:], rows, brow[:, bass.ds(e, 1), :].to_broadcast([R, GT, D]), ALU.add).then_inc(s["dve"], 1)
                        until(dve, DV, "rows_used", turn)
                        if gate is not None:
                            own(v.tensor_tensor(t[:], t[:], col_of(gate[:, bass.ds(e * TILES + i * GT, GT)], D), ALU.mult))
                        mark(v.tensor_tensor(x, x, t[:], ALU.add), DV)
                        until(dve, DV, "x", turn)
                        own.end()
                each_expert(dve, body)


def put_in(nc, tag, pairs, fill=()):
    with phase(nc, tag, "loaded") as s, nc.Block() as block:
        @block.sync
        def _(sp):
            for to, frm in pairs:
                sp.dma_start(to, frm).then_inc(s["loaded"], 16)
            if pairs:
                sp.wait_ge(s["loaded"], 16 * len(pairs))

        @block.vector
        def _(dve):
            for to, value in fill:
                nc.vector.memset(to, value)


def top_two(v, own, b, E, n_=GT):
    for n, src in ((1, "g"), (2, "g2")):
        own(v.tensor_reduce(b[f"v{n}"][:], b[src][:], AX, ALU.max))
        own(v.tensor_tensor(b[f"o{n}"][:], b[src][:], col_of(b[f"v{n}"][:], E), ALU.is_equal))
        own(v.tensor_tensor(b["k"][:], b[f"o{n}"][:], row_of(b["rev"][:, 0:E], n_), ALU.mult))
        own(v.tensor_reduce(b["k1"][:], b["k"][:], AX, ALU.max))
        own(v.tensor_tensor(b[f"o{n}"][:], b["k"][:], col_of(b["k1"][:], E), ALU.is_equal))
        if n == 1:
            own(v.scalar_tensor_tensor(b["g2"][:].rearrange("p j e -> p (j e)"), b["o1"][:].rearrange("p j e -> p (j e)"), -4.0,
                                       b["g"][:].rearrange("p j e -> p (j e)"), ALU.mult, ALU.add))


TOP_TWO_STEPS = 11


def gate_buffers(sb, E, n=GT):
    return ({k: sb(k, [R, n, E]) for k in ("g", "g2", "o1", "o2", "k", "ex")} | {k: sb(k, [R, n]) for k in ("v1", "v2", "k1", "r")}
            | {"rev": sb("rev", [R, 8])})


def build_gated_open(nc, c, layer, m, router, router_bias, E, mode):
    def loads(sb):
        w = gate_buffers(sb, E) | {"wr": sb("wr", [128, KB, E]), "br": sb("br", [R, E])}
        w["hand_in"], w["hand_out"] = w["g2"][:], w["ex"][:]
        return w, [(w["wr"][:, k, :], blocked(router, k)) for k in range(KB)] + [(w["br"][:], everywhere(router_bias))]

    def units(w):
        return [(w and [w["wr"][:, k, :] for k in range(KB)], E)]

    def post(v, own, hand_over, b, grp):
        own(v.tensor_scalar(b["rev"][:], c["iota"][0:R, 0:8], -1.0, 8.0, ALU.mult, ALU.add))
        own(v.tensor_tensor(b["g"][:], b["st"][:], row_of(b["br"][:], GT), ALU.add))
        own(v.tensor_reduce(b["r"][:], b["g"][:], AX, ALU.max))
        hand_over(v.tensor_tensor(b["g2"][:], b["g"][:], col_of(b["r"][:], E), ALU.subtract))
        own(v.tensor_reduce(b["r"][:], b["ex"][:], AX, ALU.add))
        own(v.reciprocal(b["r"][:], b["r"][:]))
        own(v.tensor_tensor(b["g"][:], b["ex"][:], col_of(b["r"][:], E), ALU.mult))
        out = m["gate"][:, 0:E * TILES].rearrange("p (e t) -> p t e", e=E)[:, grp, :]
        if mode == "all":
            return v.tensor_copy(out, b["g"][:])
        top_two(v, own, b, E)
        if mode == "top_ratio":
            own(v.tensor_tensor(b["r"][:], b["v1"][:], b["v2"][:], ALU.add))
        else:
            hand_over(v.tensor_tensor(b["g2"][:], b["g"][:], col_of(b["v1"][:], E), ALU.subtract))
            own(v.tensor_tensor(b["k"][:], b["o2"][:], b["ex"][:], ALU.mult))
            own(v.tensor_reduce(b["v2"][:], b["k"][:], AX, ALU.add))
            own(v.tensor_scalar(b["r"][:], b["v2"][:], 1.0, None, ALU.add))
            own(v.memset(b["v1"][:], 1.0))
        own(v.reciprocal(b["r"][:], b["r"][:]))
        own(v.tensor_tensor(b["v1"][:], b["v1"][:], b["r"][:], ALU.mult))
        own(v.tensor_tensor(b["v2"][:], b["v2"][:], b["r"][:], ALU.mult))
        own(v.tensor_tensor(b["o1"][:], b["o1"][:], col_of(b["v1"][:], E), ALU.mult))
        own(v.tensor_tensor(b["o2"][:], b["o2"][:], col_of(b["v2"][:], E), ALU.mult))
        return v.tensor_tensor(out, b["o1"][:], b["o2"][:], ALU.add)

    steps = {"all": 6, "top_ratio": 6 + TOP_TWO_STEPS + 6, "top_softmax": 6 + TOP_TWO_STEPS + 9}[mode]
    hand = (ACT.Exp,) * (2 if mode == "top_softmax" else 1)
    build_open(nc, c, f"{layer}g", m["X"], m["XN"], m["XNT"], loads, units, post, lambda sp, b, i, sem=None: 0, None, None, steps, hand=hand)


def experts0(nc, c, m, I):
    build_gated_open(nc, c, 0, m, I["L0_ffn_gW"], I["L0_ffn_gb"], 4, "top_softmax")
    with ExitStack() as ctx:
        sb = lambda n, sh, d=F32: ctx.enter_context(nc.sbuf_tensor(f"ffn0_{n}", sh, d))
        s1, s2, e1, e2 = sb("s1", [128, 2]), sb("s2", [128, 1]), sb("e1", [128, 4]), sb("e2", [64, 4])
        put_in(nc, "ffn0_in", [(s1[:], columns(I["L0_ffn_sb1"])), (s2[:], columns(I["L0_ffn_sb2"])),
                               (e1[:], I["L0_ffn_eb1"].rearrange("e p -> p e")), (e2[:], I["L0_ffn_eb2"].rearrange("e p -> p e"))])
        flat = lambda n: I[n].rearrange("e r o -> (e r) o")
        build_experts(nc, c, "ffn0s", m["XNT"], m["X"], None, 1, [256, 256, 128, 256], [I["L0_ffn_sW1"], I["L0_ffn_sW2"], I["L0_ffn_sW3"]],
                      everywhere(I["L0_ffn_sb3"]).unsqueeze(1), None, ACT.Relu, [s1, s2])
        build_experts(nc, c, "ffn0e", m["XNT"], m["X"], None, 4, [256, 128, 64, 256], [flat("L0_ffn_eW1"), flat("L0_ffn_eW2"), flat("L0_ffn_eW3")],
                      everywhere(I["L0_ffn_eb3"]), m["gate"], ACT.Relu, [e1, e2])


def experts1(nc, c, m, I):
    ENT = 8
    with ExitStack() as ctx:
        sb = lambda n, sh, d=F32: ctx.enter_context(nc.sbuf_tensor(f"ffn1_{n}", sh, d))
        mean, mean_b, wr, br = sb("mean", [128, KB]), sb("mean_b", [128, KB, R]), sb("wr", [128, KB, ENT]), sb("br", [R, ENT])
        b1 = sb("b1", [128, ENT * 4])

        def add_up(t, kv_p, b):
            for j in range(GT):
                for k in range(KB):
                    last = t.matmul(kv_p[:, k, 0:1], b["xn_s"][:, j, k * 128:(k + 1) * 128], c["ones"][0:R, 0:1], start=False, stop=False, skip_group_check=True)
            return last

        def to_mean(v, own, kv_p, b):
            own(v.tensor_scalar(mean[:], kv_p[:, :, 0], 1.0 / NODES, None, ALU.mult))
            own(v.tensor_copy(mean_b[:], col_of(mean[:], R)))

        build_open(nc, c, "1g", m["X"], m["XN"], m["XNT"], lambda sb: ({}, []), lambda w: [], lambda v, own, hand_over, b, grp: v.memset(b["st"][:], 0.0),
                   lambda sp, b, i, sem=None: 0, add_up, to_mean, 0)
        put_in(nc, "ffn1_in", [(wr[:, k, :], blocked(I["L1_ffn_Wr"], k)) for k in range(KB)] + [(br[:], everywhere(I["L1_ffn_br"]))]
               + [(b1[:, e * 4:(e + 1) * 4], columns(I["L1_ffn_b1"][e])) for e in range(ENT)])
        b = gate_buffers(lambda n, sh: sb("r_" + n, sh), ENT, 1)
        lp = ctx.enter_context(nc.psum_tensor("ffn1_logits", [R, 1, ENT], F32))
        with phase(nc, "route", "pe", "dve", "act", "chain") as s, nc.Block() as block:
            @block.tensor
            def _(pe):
                for k in range(KB):
                    last = nc.tensor.matmul(lp[:, 0, :], mean_b[:, k, :], wr[:, k, :], start=(k == 0), stop=(k == KB - 1))
                last.then_inc(s["pe"], 1)

            @block.scalar
            def _(act):
                for n in range(3):
                    act.wait_ge(s["dve"], n + 1)
                    nc.scalar.activation(b["ex"][:], b["g2"][:], ACT.Exp).then_inc(s["act"], 1)

            @block.vector
            def _(dve):
                v = nc.vector
                own = Chain(dve, s["chain"])
                capacity = float(-(-NODES * 5 // (4 * ENT)))
                exps = iter(range(1, 4))

                def exp(ins):
                    ins.then_inc(s["dve"], 1)
                    dve.wait_ge(s["act"], next(exps))

                def softmax():
                    own(v.tensor_reduce(b["r"][:], b["g"][:], AX, ALU.max))
                    exp(v.tensor_tensor(b["g2"][:], b["g"][:], col_of(b["r"][:], ENT), ALU.subtract))
                    own(v.tensor_reduce(b["r"][:], b["ex"][:], AX, ALU.add))
                    own(v.reciprocal(b["r"][:], b["r"][:]))
                    own(v.tensor_tensor(b["g"][:], b["ex"][:], col_of(b["r"][:], ENT), ALU.mult))

                own(v.tensor_scalar(b["rev"][:], c["iota"][0:R, 0:8], -1.0, 8.0, ALU.mult, ALU.add))
                dve.wait_ge(s["pe"], 1)
                own(v.tensor_tensor(b["g"][:], lp[:], row_of(br[:], 1), ALU.add))
                softmax()
                own(v.tensor_scalar(b["k"][:], b["g"][:], float(NODES), capacity, ALU.mult, ALU.max))
                own(v.reciprocal(b["k"][:], b["k"][:]))
                own(v.tensor_scalar(b["k"][:], b["k"][:], capacity, None, ALU.mult))
                own(v.tensor_tensor(b["g"][:], b["g"][:], b["k"][:], ALU.mult))
                softmax()
                top_two(v, own, b, ENT, 1)
                exp(v.tensor_tensor(b["g2"][:], b["g"][:], col_of(b["v1"][:], ENT), ALU.subtract))
                own(v.tensor_tensor(b["k"][:], b["o2"][:], b["ex"][:], ALU.mult))
                own(v.tensor_reduce(b["r"][:], b["k"][:], AX, ALU.add))
                own(v.tensor_scalar(b["r"][:], b["r"][:], 1.0, None, ALU.add))
                own(v.reciprocal(b["r"][:], b["r"][:]))
                own(v.tensor_tensor(b["k"][:], b["k"][:], b["o1"][:], ALU.add))
                own(v.tensor_tensor(b["k"][:], b["k"][:], col_of(b["r"][:], ENT), ALU.mult))
                own(v.tensor_copy(m["gate"][:].rearrange("p (e t) -> p e t", e=ENT), col_of(b["k"][:, 0, :], TILES)))
        flat = lambda n: I[n].rearrange("e r o -> (e r) o")
        build_experts(nc, c, "ffn1e", m["XNT"], m["XN"], None, ENT, [256, 512, 256], [flat("L1_ffn_W1"), flat("L1_ffn_W2")],
                      everywhere(I["L1_ffn_b2"]), m["gate"], ACT.Gelu, [b1])
    with ExitStack() as ctx:
        sb = lambda n, sh, d=F32: ctx.enter_context(nc.sbuf_tensor(f"norm1_{n}", sh, d))
        b = norm_buffers(sb)
        t, gamma, beta = sb("t", [R, GT, D]), sb("gamma", [R, D]), sb("beta", [R, D])
        put_in(nc, "norm1_in", [(gamma[:], everywhere(I["L1_ffn_gamma"])), (beta[:], everywhere(I["L1_ffn_beta"]))])
        with phase(nc, "norm1", "dve", "act", "chain", "passed") as s, nc.Block() as block:
            DV, AC = Steps(s["dve"], ["var", "x"]), Steps(s["act"], ["std"])

            @block.vector
            def _(dve):
                v = nc.vector
                with dve.Fori(0, GROUPS) as i:
                    own = Chain(dve, s["chain"], i, VARIANCE_STEPS + STANDARDIZE_STEPS + 3)
                    x, y = m["X"][:, bass.ds(i * GT, GT), :], m["XN"][:, bass.ds(i * GT, GT), :]
                    mark(variance(v, own, y, b, 1e-5, s["passed"]), DV)
                    until(dve, AC, "std", i)
                    own(standardize(v, own, y, t, b))
                    own(v.tensor_tensor(t[:], t[:], row_of(gamma[:], GT), ALU.mult))
                    own(v.tensor_tensor(t[:], t[:], row_of(beta[:], GT), ALU.add))
                    mark(v.tensor_tensor(x, x, t[:], ALU.add), DV)
                    until(dve, DV, "x", i)
                    own.end()

            @block.scalar
            def _(act):
                with act.Fori(0, GROUPS) as i:
                    until(act, DV, "var", i)
                    mark(nc.scalar.activation(b["std"][:], b["var"][:], ACT.Sqrt), AC)


def build_transposed(nc, c, tag, parts, out):
    n = sum(w.shape[0] for w in parts) // 128
    with ExitStack() as ctx:
        w = ctx.enter_context(nc.sbuf_tensor(f"{tag}_w", [128, n, D], F32))
        tp = [ctx.enter_context(nc.psum_tensor(f"{tag}_p{q}", [128, KB, 128], F32)) for q in range(2)]
        with phase(nc, tag, "loaded", "pe", "act") as s, nc.Block() as block:
            @block.sync
            def _(sp):
                at = 0
                for part in parts:
                    k = part.shape[0] // 128
                    sp.dma_start(w[:, at:at + k, :], part.rearrange("(b p) x -> p b x", p=128)).then_inc(s["loaded"], 16)
                    at += k

            @block.tensor
            def _(pe):
                pe.wait_ge(s["loaded"], 16 * len(parts))
                for b in range(n):
                    if b >= 2:
                        pe.wait_ge(s["act"], b - 1)
                    for k in range(KB):
                        last = nc.tensor.transpose(tp[b % 2][:, k, :], w[:, b, k * 128:(k + 1) * 128], c["ident"][:])
                    last.then_inc(s["pe"], 1)

            @block.scalar
            def _(act):
                for b in range(n):
                    act.wait_ge(s["pe"], b + 1)
                    nc.scalar.copy(out[:, :, b * 128:(b + 1) * 128], tp[b % 2][:]).then_inc(s["act"], 1)


def close2(nc, c, m, I, acc):
    tag = "close2"
    with ExitStack() as ctx:
        sb = lambda n, sh, d=F32: ctx.enter_context(nc.sbuf_tensor(f"{tag}_{n}", sh, d))
        ps = lambda n, sh: ctx.enter_context(nc.psum_tensor(f"{tag}_{n}", sh, F32))
        b = {"acc": sb("acc", [R, ACCS, GT, D + 1]), "t": sb("t", [R, GT, D]), "u": sb("u", [R, GT, D]), "z": sb("z", [R, GT, 8])} | norm_buffers(sb)
        w = sb("w", [128, KB, D])
        rowv = {n: sb(n, [R, D]) for n in ("bias", "gamma", "beta", "ln1_g", "ln1_b", "b2", "ln2_g", "ln2_b")}
        b1 = sb("b1", [128, KB])
        aT, qT, hT, low, ex = [sb(n, [128, KB, GN]) for n in ("aT", "qT", "hT", "low", "ex")]
        wide, fb = ps("wide", [128, 1536]), [ps(f"fb{n}", [128, 1024]) for n in range(2)]
        small = ps("small", [R, GT, 8])
        rows = wide[0:R, 0:GT * D].rearrange("p (j x) -> p j x", j=GT)
        loads = [(w[:, k, :], blocked(I["L2_gnn_W"], k)) for k in range(KB)] + [(b1[:], columns(I["L2_mix_b1"]))]
        loads += [(rowv[n][:], everywhere(I[("L2_gnn_" if n in ("bias", "gamma", "beta") else "L2_mix_") + n])) for n in rowv]
        W1, W2 = 3 * D, 4 * D
        with phase(nc, tag, "loaded", "acc_in", "sp_passed", "pe", "dve", "act", "chain", "passed") as s, nc.Block() as block:
            PE = Steps(s["pe"], ["agg", "gcn", "q0", "q1", "mix", "x1", "h0", "h1", "y"])
            DV = Steps(s["dve"], ["agg", "gcn_var", "gcn_x", "low0", "low1", "q0", "q1", "x1_var", "x1", "y_var", "x"])
            AC = Steps(s["act"], ["agg", "gcn_std", "ex0", "ex1", "x1_std", "x1", "h0", "h1", "y_std"])

            @block.sync
            def _(sp):
                for to, frm in loads:
                    sp.dma_start(to, frm).then_inc(s["loaded"], 16)
                with sp.Fori(0, GROUPS) as i:
                    load_accumulators(sp, acc, b, i, s["acc_in"])
                    until(sp, DV, "agg", i)
                    sp.sem_inc(s["sp_passed"], 1)

            @block.tensor
            def _(pe):
                pe.wait_ge(s["loaded"], 16 * len(loads))
                with pe.Fori(0, GROUPS) as i:
                    xt = [m["XNT"][:, k, bass.ds(i * GN, GN)] for k in range(KB)]
                    until(pe, DV, "agg", i)
                    mark(turn_tiles(nc, c, wide, b["t"]), PE)
                    until(pe, AC, "agg", i)
                    mark(product_rows(nc, rows, [(aT[:, k, :], w[:, k, :]) for k in range(KB)]), PE)
                    for g in range(KB):
                        mark(product_t(nc, fb[g], 128, [(m["WT"][:, k, g * 128:(g + 1) * 128], xt[k]) for k in range(KB)]), PE)
                    until(pe, DV, "q1", i)
                    until(pe, DV, "gcn_x", i)
                    mark(heads_product(nc, rows, qT, m["KV"], small), PE)
                    until(pe, DV, "x1", i)
                    mark(turn_tiles(nc, c, wide, b["u"]), PE)
                    until(pe, AC, "x1", i)
                    for g in range(KB):
                        mark(product_t(nc, fb[g], 128, [(m["WT"][:, k, W1 + g * 128:W1 + (g + 1) * 128], aT[:, k, :]) for k in range(KB)]), PE)
                    until(pe, AC, "h1", i)
                    mark(product_rows(nc, rows, [(hT[:, k, :], m["WT"][:, k, W2:W2 + D]) for k in range(KB)]), PE)
                    until(pe, DV, "x", i)

            @block.scalar
            def _(act):
                a = nc.scalar
                act.wait_ge(s["loaded"], 16 * len(loads))

                def std(name, i):
                    until(act, DV, name + "_var", i)
                    mark(a.activation(b["std"][:], b["var"][:], ACT.Sqrt), AC)

                def turn(name, i):
                    until(act, PE, name, i)
                    mark(a.copy(aT[:].rearrange("p k (j x) -> p (k j) x", x=R), turned(wide[:])), AC)

                with act.Fori(0, GROUPS) as i:
                    turn("agg", i)
                    std("gcn", i)
                    for g in range(KB):
                        until(act, DV, f"low{g}", i)
                        mark(a.activation(ex[:, g, :], low[:, g, :], ACT.Exp), AC)
                    std("x1", i)
                    turn("x1", i)
                    for g in range(KB):
                        until(act, PE, f"h{g}", i)
                        mark(a.activation(dense(hT[:, g, :]), slices(fb[g]), ACT.Gelu, bias=b1[:, g:g + 1]), AC)
                    std("y", i)

            @block.vector
            def _(dve):
                v = nc.vector
                dve.wait_ge(s["loaded"], 16 * len(loads))
                with dve.Fori(0, GROUPS) as i:
                    own = Chain(dve, s["chain"], i, 29)
                    grp = bass.ds(i * GT, GT)
                    x, xn = m["X"][:, grp, :], m["XN"][:, grp, :]
                    t, u = b["t"][:], b["u"][:]

                    def norm(name, src, gain, shift):
                        mark(variance(v, own, src, b, 1e-5, s["passed"]), DV)
                        until(dve, AC, name + "_std", i)
                        own(standardize(v, own, src, src, b))
                        own(v.tensor_tensor(src, src, row_of(rowv[gain][:], GT), ALU.mult))
                        return v.tensor_tensor(src, src, row_of(rowv[shift][:], GT), ALU.add)

                    dve.wait_ge(s["acc_in"], i * (16 * ACCS) + 16 * ACCS)
                    a = sum_accumulators(v, own, b)
                    own(v.tensor_tensor(u, xn, col_of(m["dinv"][:, grp], D), ALU.mult))
                    own(v.tensor_tensor(u, u, a[:, :, 0:D], ALU.add))
                    mark(v.tensor_tensor(t, u, col_of(m["dinv"][:, grp], D), ALU.mult), DV)
                    until(dve, PE, "gcn", i)
                    own(v.tensor_tensor(u, rows, row_of(rowv["bias"][:], GT), ALU.add))
                    own(v.tensor_tensor(u, u, xn, ALU.add))
                    own(norm("gcn", u, "gamma", "beta"))
                    mark(v.tensor_tensor(x, x, u, ALU.add), DV)
                    for g in range(KB):
                        until(dve, PE, f"q{g}", i)
                        mark(v.tensor_scalar(dense(low[:, g, :]), slices(fb[g]), 0.0, None, ALU.min), DV)
                    for g in range(KB):
                        until(dve, AC, f"ex{g}", i)
                        mark(v.scalar_tensor_tensor(dense(qT[:, g, :]), slices(fb[g]), 0.0, dense(ex[:, g, :]), ALU.max, ALU.add), DV)
                    until(dve, PE, "mix", i)
                    own(v.tensor_scalar(b["z"][:], small[:], 1e-6, None, ALU.add))
                    own(v.reciprocal(b["z"][:], b["z"][:]))
                    u4 = u.rearrange("p j (h x) -> p j h x", x=32)
                    own(v.tensor_tensor(u4, rows.rearrange("p j (h x) -> p j h x", x=32), b["z"][:].unsqueeze(3).to_broadcast([R, GT, 8, 32]), ALU.mult))
                    own(v.tensor_tensor(u, u, xn, ALU.add))
                    mark(norm("x1", u, "ln1_g", "ln1_b"), DV)
                    until(dve, PE, "y", i)
                    own(v.tensor_tensor(t, rows, row_of(rowv["b2"][:], GT), ALU.add))
                    own(v.tensor_tensor(t, t, u, ALU.add))
                    own(norm("y", t, "ln2_g", "ln2_b"))
                    mark(v.tensor_tensor(x, x, t, ALU.add), DV)
                    until(dve, DV, "x", i)
                    own.end()


def build_key_sums(nc, c, m, wkv):
    tag = "keys3"
    with ExitStack() as ctx:
        sb = lambda n, sh, d=F32: ctx.enter_context(nc.sbuf_tensor(f"{tag}_{n}", sh, d))
        ps = lambda n, sh: ctx.enter_context(nc.psum_tensor(f"{tag}_{n}", sh, F32))
        w, xT, st = sb("w", [128, KB, 512]), sb("xT", [128, KB, GN]), sb("st", [R, GT, 512])
        topc, diag, topr, inv = sb("topc", [128, KB]), sb("diag", [128, KB, 128]), sb("topr", [R, D]), sb("inv", [128, KB])
        tp, unit_p, kv_p = ps("tp", [128, KB, 128]), [ps(f"unit{n}", [R, 512]) for n in range(4)], ps("kv_p", [128, KB, 256])
        with phase(nc, tag, "loaded", "pe0", "dve0", "pe", "dve", "act", "chain") as s, nc.Block() as block:
            UNITS = [f"u{j}" for j in range(GT)]
            PE, DV = Steps(s["pe"], UNITS + ["kv"]), Steps(s["dve"], ["low"])
            AC = Steps(s["act"], ["x"] + UNITS + ["exp"])

            @block.sync
            def _(sp):
                for k in range(KB):
                    sp.dma_start(w[:, k, :], blocked(wkv, k)[:, D:3 * D]).then_inc(s["loaded"], 16)

            @block.tensor
            def _(pe):
                t = nc.tensor
                for k in range(KB):
                    last = t.transpose(tp[:, k, 0:R], m["key_top"][:, k * 128:(k + 1) * 128], c["ident"][0:R, 0:R])
                last.then_inc(s["pe0"], 1)
                pe.wait_ge(s["dve0"], 1)
                for k in range(KB):
                    last = t.matmul(tp[0:R, k, :], c["ones"][:, 0:R], diag[:, k, :], start=True, stop=True)
                last.then_inc(s["pe0"], 1)
                for k in range(KB):
                    t.matmul(kv_p[:, k, :], c["zeros"][:, 0:128], c["zeros"][:, 0:256], start=(k == 0), stop=False, skip_group_check=True)
                pe.wait_ge(s["loaded"], 16 * KB)
                with pe.Fori(0, GROUPS) as i:
                    until(pe, AC, "x", i)
                    for j, name in enumerate(UNITS):
                        if j >= 4:
                            until(pe, AC, UNITS[j - 4], i)
                        for k in range(KB):
                            last = t.matmul(unit_p[j % 4][:], xT[:, k, j * R:(j + 1) * R], w[:, k, :], start=(k == 0), stop=(k == KB - 1))
                        mark(last, PE)
                    until(pe, AC, "exp", i)
                    for j in range(GT):
                        for k in range(KB):
                            key = st[:, j, k * 128:(k + 1) * 128]
                            t.matmul(kv_p[:, k, 0:128], key, st[:, j, D + k * 128:D + (k + 1) * 128], start=False, stop=False, skip_group_check=True)
                            last = t.matmul(kv_p[:, k, 128:129], key, c["ones"][0:R, 0:1], start=False, stop=False, skip_group_check=True)
                    mark(last, PE)
                for k in range(KB):
                    last = t.matmul(kv_p[:, k, :], c["zeros"][:, 0:128], c["zeros"][:, 0:256], start=False, stop=True, skip_group_check=True)
                last.then_inc(s["pe0"], 1)

            @block.scalar
            def _(act):
                a = nc.scalar
                with act.Fori(0, GROUPS) as i:
                    mark(a.copy(xT[:], m["XNT"][:, :, bass.ds(i * GN, GN)]), AC)
                    for j, name in enumerate(UNITS):
                        until(act, PE, name, i)
                        mark(a.copy(st[:, j, :], unit_p[j % 4][:]), AC)
                    until(act, DV, "low", i)
                    mark(a.activation(st[:, :, 0:D], st[:, :, 0:D], ACT.Exp), AC)
                    until(act, PE, "kv", i)

            @block.vector
            def _(dve):
                v = nc.vector
                own = Chain(dve, s["chain"])
                dve.wait_ge(s["pe0"], 1)
                own(v.tensor_reduce(topc[:], tp[:, :, 0:R], AX, ALU.max))
                for k in range(KB):
                    last = v.tensor_scalar(diag[:, k, :], c["ident"][:], topc[:, k:k + 1], None, ALU.mult)
                last.then_inc(s["dve0"], 1)
                dve.wait_ge(s["pe0"], 2)
                own(v.tensor_copy(topr[:].rearrange("p (k x) -> p k x", k=KB), tp[0:R, :, :]))
                with dve.Fori(0, GROUPS) as i:
                    until(dve, AC, UNITS[-1], i)
                    mark(v.tensor_tensor(st[:, :, 0:D], st[:, :, 0:D], row_of(topr[:], GT), ALU.subtract), DV)
                dve.wait_ge(s["pe0"], 3)
                own(v.reciprocal(inv[:], kv_p[:, :, 128]))
                for k in range(KB):
                    own(v.scalar_tensor_tensor(m["KV"][:, k, 0:128], kv_p[:, k, 0:128], inv[:, k:k + 1], c["block"][:], ALU.mult, ALU.mult))


def close3(nc, c, m, I, acc, xp_table):
    tag = "close3"
    H, C, GH = 4, D // 4, 64
    with ExitStack() as ctx:
        sb = lambda n, sh, d=F32: ctx.enter_context(nc.sbuf_tensor(f"{tag}_{n}", sh, d))
        ps = lambda n, sh: ctx.enter_context(nc.psum_tensor(f"{tag}_{n}", sh, F32))
        b = {"acc": sb("acc", [R, ACCS, GT, D + H]), "xp": sb("xp", [R, GT, D]), "t": sb("t", [R, GT, D]), "u": sb("u", [R, GT, D]),
             "z": sb("z", [R, GT, H])} | norm_buffers(sb)
        out, gate = sb("out", [R, GT, D]), sb("gate", [R, GT, D])
        wq, wp, wg1, wg2 = sb("wq", [128, KB, D]), sb("wp", [128, KB, D]), sb("wg1", [128, KB, GH]), sb("wg2", [GH, D])
        rowv = {n: sb(n, [R, D]) for n in ("bias", "gamma", "beta", "ln_g", "ln_b", "bg2", "bproj")}
        bg1 = sb("bg1", [GH, 1])
        qT, rT, hT = sb("qT", [128, KB, GN]), sb("rT", [128, KB, GN]), sb("hT", [GH, GN])
        wide, fb = ps("wide", [128, 1536]), [ps(f"fb{n}", [128, 1024]) for n in range(2)]
        rows = wide[0:R, 0:GT * D].rearrange("p (j x) -> p j x", j=GT)
        loads = [(wg2[:], I["L3_mix_Wg2"]), (bg1[:], columns(I["L3_mix_bg1"], GH))]
        for k in range(KB):
            loads += [(wq[:, k, :], blocked(I["L3_mix_Wqkv"], k)[:, 0:D]), (wp[:, k, :], blocked(I["L3_mix_Wproj"], k)), (wg1[:, k, :], blocked(I["L3_mix_Wg1"], k))]
        loads += [(rowv[n][:], everywhere(I[("L3_gnn_" if n in ("bias", "gamma", "beta") else "L3_mix_") + n])) for n in rowv]
        with phase(nc, tag, "loaded", "acc_in", "sp_passed", "pe", "dve", "act", "chain", "passed") as s, nc.Block() as block:
            PE = Steps(s["pe"], ["q0", "q1", "mix", "xg", "h", "gate", "prod", "y"])
            DV = Steps(s["dve"], ["acc_used", "gat_var", "gat_x", "mix", "xg_var", "xg", "pre", "prod", "x"])
            AC = Steps(s["act"], ["q0", "q1", "gat_std", "xg_std", "xg", "h", "gate", "prod"])

            @block.sync
            def _(sp):
                for to, frm in loads:
                    sp.dma_start(to, frm).then_inc(s["loaded"], 16)
                with sp.Fori(0, GROUPS) as i:
                    load_accumulators(sp, acc, b, i, s["acc_in"], [(b["xp"], xp_table)])
                    until(sp, DV, "acc_used", i)
                    sp.sem_inc(s["sp_passed"], 1)

            @block.tensor
            def _(pe):
                pe.wait_ge(s["loaded"], 16 * len(loads))
                with pe.Fori(0, GROUPS) as i:
                    xt = [m["XNT"][:, k, bass.ds(i * GN, GN)] for k in range(KB)]
                    for g in range(KB):
                        mark(product_t(nc, fb[g], 128, [(wq[:, k, g * 128:(g + 1) * 128], xt[k]) for k in range(KB)]), PE)
                    until(pe, AC, "q1", i)
                    mark(heads_product(nc, rows, qT, m["KV"]), PE)
                    until(pe, DV, "xg", i)
                    mark(turn_tiles(nc, c, wide, b["u"]), PE)
                    until(pe, AC, "xg", i)
                    mark(product_t(nc, fb[0], GH, [(wg1[:, k, :], rT[:, k, :]) for k in range(KB)]), PE)
                    until(pe, AC, "h", i)
                    mark(product_rows(nc, rows, [(hT[:], wg2[:])]), PE)
                    until(pe, DV, "prod", i)
                    mark(turn_tiles(nc, c, wide, out), PE)
                    until(pe, AC, "prod", i)
                    mark(product_rows(nc, rows, [(rT[:, k, :], wp[:, k, :]) for k in range(KB)]), PE)
                    until(pe, DV, "x", i)

            @block.scalar
            def _(act):
                a = nc.scalar
                act.wait_ge(s["loaded"], 16 * len(loads))

                def std(name, i):
                    until(act, DV, name + "_var", i)
                    mark(a.activation(b["std"][:], b["var"][:], ACT.Sqrt), AC)

                def turn(name, i):
                    until(act, PE, name, i)
                    mark(a.copy(rT[:].rearrange("p k (j x) -> p (k j) x", x=R), turned(wide[:])), AC)

                with act.Fori(0, GROUPS) as i:
                    for g in range(KB):
                        until(act, PE, f"q{g}", i)
                        mark(a.copy(dense(qT[:, g, :]), slices(fb[g])), AC)
                    std("gat", i)
                    std("xg", i)
                    turn("xg", i)
                    until(act, PE, "h", i)
                    mark(a.activation(dense(hT[:]), slices(fb[0][0:GH, :]), ACT.Gelu, bias=bg1[:]), AC)
                    until(act, DV, "pre", i)
                    mark(a.activation(gate[:], gate[:], ACT.Sigmoid), AC)
                    turn("prod", i)

            @block.vector
            def _(dve):
                v = nc.vector
                dve.wait_ge(s["loaded"], 16 * len(loads))
                with dve.Fori(0, GROUPS) as i:
                    own = Chain(dve, s["chain"], i, 22)
                    grp = bass.ds(i * GT, GT)
                    x, xn = m["X"][:, grp, :], m["XN"][:, grp, :]
                    t, u = b["t"][:], b["u"][:]
                    heads = lambda ap: ap.rearrange("p j (h x) -> p j h x", x=C)
                    each = lambda ap: ap.unsqueeze(3).to_broadcast([R, GT, H, C])
                    dve.wait_ge(s["acc_in"], i * (16 * (ACCS + 1)) + 16 * (ACCS + 1))
                    a = sum_accumulators(v, own, b)
                    own(v.tensor_tensor(heads(t), heads(b["xp"][:]), each(m["p_self"][:, grp, :]), ALU.mult))
                    own(v.tensor_tensor(t, t, a[:, :, 0:D], ALU.add))
                    own(v.tensor_tensor(b["z"][:], a[:, :, D:D + H], m["p_self"][:, grp, :], ALU.add))
                    own(v.tensor_scalar(b["z"][:], b["z"][:], 1e-16, None, ALU.add))
                    own(v.reciprocal(b["z"][:], b["z"][:]))
                    own(v.tensor_tensor(heads(t), heads(t), each(b["z"][:]), ALU.mult))
                    mark(v.tensor_tensor(t, t, row_of(rowv["bias"][:], GT), ALU.add), DV)
                    until(dve, DV, "acc_used", i)
                    mark(variance(v, own, t, b, 1e-5, s["passed"]), DV)
                    until(dve, AC, "gat_std", i)
                    own(standardize(v, own, t, t, b))
                    own(v.tensor_tensor(t, t, row_of(rowv["gamma"][:], GT), ALU.mult))
                    own(v.tensor_tensor(t, t, row_of(rowv["beta"][:], GT), ALU.add))
                    own(v.tensor_tensor(t, t, xn, ALU.add))
                    own(v.tensor_scalar(t, t, 0.0, None, ALU.max))
                    mark(v.tensor_tensor(x, x, t, ALU.add), DV)
                    until(dve, PE, "mix", i)
                    mark(v.tensor_copy(out[:], rows), DV)
                    mark(variance(v, own, xn, b, 1e-5, s["passed"]), DV)
                    until(dve, AC, "xg_std", i)
                    own(standardize(v, own, xn, u, b))
                    own(v.tensor_tensor(u, u, row_of(rowv["ln_g"][:], GT), ALU.mult))
                    mark(v.tensor_tensor(u, u, row_of(rowv["ln_b"][:], GT), ALU.add), DV)
                    until(dve, PE, "gate", i)
                    mark(v.tensor_tensor(gate[:], rows, row_of(rowv["bg2"][:], GT), ALU.add), DV)
                    until(dve, AC, "gate", i)
                    mark(v.tensor_tensor(out[:], out[:], gate[:], ALU.mult), DV)
                    until(dve, PE, "y", i)
                    own(v.tensor_tensor(t, rows, row_of(rowv["bproj"][:], GT), ALU.add))
                    mark(v.tensor_tensor(x, x, t, ALU.add), DV)
                    until(dve, DV, "x", i)
                    own.end()


def alloc_all(nc, ctx, dbg=False):
    sb = lambda n, sh, d=F32: ctx.enter_context(nc.sbuf_tensor(n, sh, d))
    c = {"iota_i": sb("iota_i", [128, 256], I32), "part_i": sb("part_i", [128, 1], I32), "iota": sb("iota", [128, 256]), "part": sb("part", [128, 1]),
         "ones": sb("ones", [128, 128]), "zeros": sb("zeros", [128, 256]), "ident": sb("ident", [128, 128]), "lower": sb("lower", [128, 128]),
         "block": sb("block", [128, 128]), "block4": sb("block4", [128, 4]), "tmp1": sb("tmp1", [128, 1])}
    m = {"X": sb("X", [R, TILES, D]), "XN": sb("XN", [R, TILES, D]), "XNT": sb("XNT", [128, KB, NODES]), "KV": sb("KV", [128, KB, 132]),
         "gate": sb("gate", [R, 8 * TILES]), "deg3": sb("deg3", [R, 3, TILES]), "relcnt": sb("relcnt", [R, TILES * TYPES])}
    e = {n: sb("e_" + n, [R, CHUNKS]) for n in ("src", "dst", "src_lo", "dst_lo", "dst_hi", "slot", "weight", "attr", "dst_dup")}
    return c, m, e


def edge_setup(nc, c, m, e, I, dram):
    build_constants(nc, c)
    with ExitStack() as ctx:
        temps = ("src_i", "dst_i", "typ_i", "rel_i", "tmp_i", "tmp", "src_hi", "src_dup")
        e = e | {n: ctx.enter_context(nc.sbuf_tensor("e_" + n, [R, CHUNKS], I32 if n.endswith("_i") else F32)) for n in temps}
        build_edge_numbers(nc, c, e, I["src"], I["dst"], I["edge_type_7"], I["edge_weight"], I["edge_weight1"])
        build_edge_rows(nc, c, e, dram)
        build_scatter_rows(nc, c, e, dram)
        build_degrees(nc, c, e, m["deg3"][:].rearrange("p k t -> p (k t)"), m["relcnt"][:])


def as_chunks(v):
    return v.rearrange("(p c) -> p c", p=R)


def bulk(nc, tag, steps):
    with phase(nc, tag, "chain", "dve", "act") as s, nc.Block() as block:
        todo = []

        @block.vector
        def _(dve):
            def act_step(ins, *args, **kw):
                ins.then_inc(s["dve"], 1)
                todo.append((args, kw))
                dve.wait_ge(s["act"], len(todo))
            steps(nc.vector, Chain(dve, s["chain"]), act_step)

        @block.scalar
        def _(act):
            for n, (args, kw) in enumerate(todo):
                act.wait_ge(s["dve"], n + 1)
                nc.scalar.activation(*args, **kw).then_inc(s["act"], 1)


def layer0(nc, c, m, e, I, dram):
    open0(nc, c, m, I, dram)
    src, dst = as_chunks(I["src"]), as_chunks(I["dst"])
    with ExitStack() as ctx:
        sb = lambda n, sh, d=F32: ctx.enter_context(nc.sbuf_tensor(f"gnn0_{n}", sh, d))
        score, top = sb("score", [R, CHUNKS, 1]), sb("top", [R, 1, TILES])
        build_score0(nc, c, e, src, dst, dram, I["L0_gnn_attn"], score, top[:])
        look = {"table": top[:, 0, :], "ids": dram["dst_lo_ids"], "slot": e["dst_hi"][:], "slots": TILES}
        build_messages(nc, c, e, "msg0", dram["el"], src, dram["dst_row"], e["dst"], dram["dst_ids"], score, 1, dram["acc"], look)
    close0(nc, c, m, I, dram["acc"])
    experts0(nc, c, m, I)


def layer1(nc, c, m, e, I, dram):
    open1(nc, c, m, I, dram)

    def inverse(v, own, act_step):
        own(v.tensor_scalar(m["relcnt"][:], m["relcnt"][:], 1.0, None, ALU.max))
        own(v.reciprocal(m["relcnt"][:], m["relcnt"][:]))
    bulk(nc, "share1", inverse)
    look = {"table": m["relcnt"][:], "ids": dram["src_lo_ids"], "slot": e["slot"][:], "slots": TILES * TYPES}
    build_messages(nc, c, e, "msg1", dram["rel_table"], dram["rel"], dram["src_row"], e["src"], dram["src_ids"], None, 1, dram["acc"], look)
    close1(nc, c, m, dram["acc"])
    experts1(nc, c, m, I)


def layer2(nc, c, m, e, I, dram):
    with ExitStack() as ctx:
        sb = lambda n, sh, d=F32: ctx.enter_context(nc.sbuf_tensor(f"layer2_{n}", sh, d))
        m["WT"], m["dinv"], live = sb("WT", [128, KB, 5 * D]), sb("dinv", [R, TILES]), sb("live", [R, TILES])
        build_transposed(nc, c, "turn2", [I["L2_mix_Wqkv"], I["L2_mix_W1"], I["L2_mix_W2"]], m["WT"])

        def degree(v, own, act_step):
            d = m["dinv"][:]
            own(v.tensor_scalar(d, m["deg3"][:, 1, :], 1.0, None, ALU.add))
            own(v.tensor_scalar(live[:], d, 0.0, None, ALU.is_gt))
            own(v.tensor_scalar(d, d, 1e-30, None, ALU.max))
            act_step(v.tensor_copy(d, d), d, d, ACT.Sqrt)
            own(v.reciprocal(d, d))
            own(v.tensor_tensor(d, d, live[:], ALU.mult))
        bulk(nc, "degree2", degree)
        open2(nc, c, m, I, dram)
        build_messages(nc, c, e, "msg2", dram["el"], as_chunks(I["src"]), dram["dst_row"], e["dst"], dram["dst_ids"],
                       e["weight"][:].unsqueeze(2), 1, dram["acc"])
        close2(nc, c, m, I, dram["acc"])
    experts2(nc, c, m, I)


def experts2(nc, c, m, I):
    ENT, F = 8, 1024
    build_gated_open(nc, c, 2, m, I["L2_ffn_Wr"], I["L2_ffn_br"], ENT, "top_ratio")
    build_open(nc, c, "2n", m["XN"], m["XN"], m["XNT"], lambda sb: ({}, []), lambda w: [], lambda v, own, hand_over, b, grp: v.memset(b["st"][:], 0.0),
               lambda sp, b, i, sem=None: 0, None, None, 0)
    with ExitStack() as ctx:
        sb = lambda n, sh, d=F32: ctx.enter_context(nc.sbuf_tensor(f"ffn2_{n}", sh, d))
        b1, gain, shift = sb("b1", [128, ENT * F // 128]), sb("gain", [128, ENT * KB]), sb("shift", [128, ENT * KB])
        put_in(nc, "ffn2_in", [(b1[:, e * 8:(e + 1) * 8], columns(I["L2_ffn_b1"][e])) for e in range(ENT)]
               + [(t[:, e * KB:(e + 1) * KB], columns(I[n][e])) for t, n in ((gain, "L2_ffn_ln_g"), (shift, "L2_ffn_ln_b")) for e in range(ENT)])
        flat = lambda n: I[n].rearrange("e r o -> (e r) o")
        build_experts(nc, c, "ffn2e", m["XNT"], m["X"], None, ENT, [256, F, 256], [flat("L2_ffn_W1"), flat("L2_ffn_W2")],
                      everywhere(I["L2_ffn_b2"]), m["gate"], ACT.Gelu, [b1], affine=(gain, shift))


def layer3(nc, c, m, e, I, dram):
    H = 4
    with ExitStack() as ctx:
        sb = lambda n, sh, d=F32: ctx.enter_context(nc.sbuf_tensor(f"layer3_{n}", sh, d))
        m["p_self"], top = sb("p_self", [R, TILES, H]), sb("top", [R, H, TILES])
        top_t, self_ = sb("top_t", [R, TILES, H]), sb("self", [R, TILES, H])
        we, att, slope, mean = sb("we", [R, D]), sb("att", [R, D]), sb("slope", [R, H]), sb("mean", [R, TILES])
        m["a_src"], m["a_dst"], m["key_top"] = sb("a_src", [R, TILES, H]), sb("a_dst", [R, TILES, H]), sb("key_top", [R, D])
        put_in(nc, "layer3_in", [(we[:], everywhere(I["L3_gnn_We"].rearrange("o x -> (o x)"))), (att[:], everywhere(I["L3_gnn_att_edge"].rearrange("h x -> (h x)")))],
               [(m["key_top"][:], -HUGE)])
        open3(nc, c, m, I, dram)
        build_key_sums(nc, c, m, I["L3_mix_Wqkv"])

        def own_loops(v, own, act_step):
            own(v.tensor_tensor(we[:], we[:], att[:], ALU.mult))
            own(v.tensor_reduce(slope[:], we[:].rearrange("p (h x) -> p h x", h=H), AX, ALU.add))
            own(v.tensor_scalar(mean[:], m["deg3"][:, 0, :], 1.0, None, ALU.max))
            own(v.reciprocal(mean[:], mean[:]))
            own(v.tensor_tensor(mean[:], mean[:], m["deg3"][:, 2, :], ALU.mult))
            own(v.tensor_tensor(self_[:], col_of(mean[:], H), row_of(slope[:], TILES), ALU.mult))
            own(v.tensor_tensor(self_[:], self_[:], m["a_src"][:], ALU.add))
            own(v.tensor_tensor(self_[:], self_[:], m["a_dst"][:], ALU.add))
            own(leaky(v, self_[:]))
        bulk(nc, "loops3", own_loops)
        with ExitStack() as inner:
            sb = lambda n, sh, d=F32: inner.enter_context(nc.sbuf_tensor(f"gnn3_{n}", sh, d))
            logit = sb("logit", [R, CHUNKS, H])
            whole = lambda t: t[:].rearrange("p t h -> p (t h)")
            src_hi = sb("src_hi", [R, CHUNKS])

            def high(v, own, act_step):
                own(v.tensor_tensor(src_hi[:], e["src"][:], e["src_lo"][:], ALU.subtract))
                own(v.tensor_scalar(src_hi[:], src_hi[:], 1.0 / R, None, ALU.mult))
                own(v.tensor_scalar(src_hi[:], src_hi[:], 8388608.0 * 1.5, -8388608.0 * 1.5, ALU.add, ALU.add))
            bulk(nc, "high3", high)
            build_logits3(nc, c, e, dram, whole(m["a_src"]), whole(m["a_dst"]), src_hi, slope[:], logit, top[:])

            def with_loops(v, own, act_step):
                own(v.tensor_tensor(top_t[:], top[:].rearrange("p h t -> p t h"), self_[:], ALU.max))
                act_step(v.tensor_tensor(self_[:], self_[:], top_t[:], ALU.subtract), m["p_self"][:], self_[:], ACT.Exp)
            bulk(nc, "tops3", with_loops)
            look = {"table": whole(top_t), "ids": dram["dst_lo_ids"], "slot": e["dst_hi"][:], "slots": TILES}
            build_messages(nc, c, e, "msg3", dram["el"], as_chunks(I["src"]), dram["dst_row"], e["dst"], dram["dst_ids"], logit, H, dram["acc4"], look)
        close3(nc, c, m, I, dram["acc4"], dram["el"])
    experts3(nc, c, m, I)


def leaky(v, x):
    flat = x.rearrange("p a b -> p (a b)")
    return v.scalar_tensor_tensor(flat, flat, 0.2, flat, ALU.mult, ALU.max)


def experts3(nc, c, m, I):
    ENT = 8
    build_gated_open(nc, c, 3, m, I["L3_ffn_Wr"], I["L3_ffn_br"], ENT, "all")
    with ExitStack() as ctx:
        sb = lambda n, sh, d=F32: ctx.enter_context(nc.sbuf_tensor(f"ffn3_{n}", sh, d))
        t = {f"{n}{l}": sb(f"{n}{l}", [128, ENT * KB]) for n in ("b", "g", "be", "m", "v") for l in (1, 2)}
        put_in(nc, "ffn3_in", [(t[n][:, e * KB:(e + 1) * KB], columns(I["L3_ffn_" + n][e])) for n in t for e in range(ENT)])

        def fold(v, own, act_step):
            for l in "12":
                own(v.tensor_scalar(t["v" + l][:], t["v" + l][:], 1e-3, None, ALU.add))
                act_step(v.tensor_tensor(t["b" + l][:], t["b" + l][:], t["m" + l][:], ALU.subtract), t["m" + l][:], t["v" + l][:], ACT.Sqrt)
                own(v.reciprocal(t["v" + l][:], t["m" + l][:]))
                own(v.tensor_tensor(t["g" + l][:], t["g" + l][:], t["v" + l][:], ALU.mult))
                own(v.tensor_tensor(t["b" + l][:], t["b" + l][:], t["g" + l][:], ALU.mult))
                own(v.tensor_tensor(t["b" + l][:], t["b" + l][:], t["be" + l][:], ALU.add))
        bulk(nc, "fold3", fold)
        flat = lambda n: I[n].rearrange("e r o -> (e r) o")
        build_experts(nc, c, "ffn3e", m["XNT"], m["X"], None, ENT, [256, 256, 256, 256], [flat("L3_ffn_W1"), flat("L3_ffn_W2"), flat("L3_ffn_Wo")],
                      everywhere(I["L3_ffn_bo"]), m["gate"], ACT.Relu, [t["b1"], t["b2"]], layer_scale=[t["g1"], t["g2"]])


def build(nc, I, out):
    def scratch(name, shape, dt=F32):
        return nc.dram_tensor(name, shape, dt, kind="Internal").ap()

    dram = {"el": scratch("el_table", [NODES, D]), "er": scratch("er_table", [NODES, D]), "rel_table": scratch("rel_table", [NODES * TYPES, D]),
            "acc": [scratch(f"acc{k}", [NODES + R, D + 1]) for k in range(ACCS)], "acc4": [scratch(f"acc_heads{k}", [NODES + R, D + 4]) for k in range(ACCS)],
            "src_row": scratch("src_row", [R, CHUNKS], I32), "dst_row": scratch("dst_row", [R, CHUNKS], I32), "rel": scratch("rel_row", [R, CHUNKS], I32)}
    for name in ("src", "dst", "src_lo", "dst_lo"):
        dram[name + "_ids"] = scratch(name + "_ids", [EDGES], I16)
    with ExitStack() as ctx:
        ctx.enter_context(nc.allow_non_contiguous_dma(reason="bias vectors as columns"))
        c, m, e = alloc_all(nc, ctx)
        edge_setup(nc, c, m, e, I, dram)
        put_in(nc, "x_in", [(m["X"][:], by_tile(I["x"]))])
        layer0(nc, c, m, e, I, dram)
        layer1(nc, c, m, e, I, dram)
        layer2(nc, c, m, e, I, dram)
        layer3(nc, c, m, e, I, dram)
        with phase(nc, "x_out", "stored") as s, nc.Block() as block:
            @block.sync
            def _(sp):
                sp.dma_start(by_tile(out), m["X"][:]).then_inc(s["stored"], 16)
                sp.wait_ge(s["stored"], 16)


def kernel(**inputs):
    import numpy as _np
    import concourse.bacc as _bacc
    from concourse import mybir as _mybir
    from concourse.bass_utils import run_bass_kernel_spmd as _run

    nc = _bacc.Bacc("TRN2", target_bir_lowering=False, num_devices=1)
    arrays, aps = {}, {}
    for name, value in inputs.items():
        a = _np.ascontiguousarray(value)
        arrays[f"in_{name}_dram"] = a
        aps[name] = nc.dram_tensor(f"in_{name}_dram", a.shape, _mybir.dt.from_np(a.dtype), kind="ExternalInput").ap()
    out = nc.dram_tensor("out_0_dram", [NODES, D], _mybir.dt.float32, kind="ExternalOutput").ap()
    build(nc, aps, out)
    r = _run(nc, [arrays], core_ids=[0])
    return r.results[0]["out_0_dram"]
```

```python
from contextlib import ExitStack, contextmanager

import concourse.bass as bass
from concourse import mybir

F32 = mybir.dt.float32
I32 = mybir.dt.int32
I16 = mybir.dt.int16
BF16 = mybir.dt.bfloat16
ALU = mybir.AluOpType
ACT = mybir.ActivationFunctionType
AX = mybir.AxisListType.X

NODES, EDGES, D = 3125, 100000, 256
R = 125
TILES = NODES // R
CHUNKS = EDGES // R
G = 4
LANES = 2
UNIT = G * LANES
TURNS = CHUNKS // UNIT
GT = 5
GROUPS = TILES // GT
GN = GT * R
KB = D // 128
HUGE = 3.0e38
TYPES = 7
ACCS = G



class Chain:

    def __init__(self, eng, sem, turn=None, per_turn=0, before=0):
        self.eng, self.sem, self.turn, self.per_turn, self.before, self.n = eng, sem, turn, per_turn, before, 0

    def __call__(self, ins):
        self.n += 1
        ins.then_inc(self.sem, 1)
        n = self.before + self.n
        self.eng.wait_ge(self.sem, n if self.turn is None else self.turn * self.per_turn + n)

    def pause(self, passed):
        self.eng.sem_inc(passed, 1)

    def end(self):
        assert self.turn is None or self.n == self.per_turn, f"this loop's turn has {self.n} steps"


class Steps:

    def __init__(self, sem, names, before=0):
        self.sem, self.names, self.before, self.order = sem, names, before, {n: k for k, n in enumerate(names)}
        assert len(self.order) == len(names)

    def at(self, name, turn=None):
        k = self.before + self.order[name] + 1
        return k if turn is None else turn * len(self.names) + k


@contextmanager
def phase(nc, tag, *names):
    sems = {n: nc.alloc_semaphore(f"{tag}_{n}") for n in names}
    yield sems
    nc.clear_and_free_semaphores(list(sems.values()))
    nc.all_engine_barrier()


def row_of(ap, k):
    return ap.unsqueeze(1).to_broadcast([ap.shape[0], k, ap.shape[1]])


def col_of(ap, n):
    return ap.unsqueeze(2).to_broadcast([ap.shape[0], ap.shape[1], n])


def build_constants(nc, c):
    with phase(nc, "constants", "pool_made", "chain") as s:
        with nc.Block() as block:
            @block.gpsimd
            def _(pool):
                own = Chain(pool, s["pool_made"])
                own(nc.gpsimd.iota(c["iota_i"][:], [[1, 256]], base=0, channel_multiplier=0))
                own(nc.gpsimd.iota(c["part_i"][:], [[0, 1]], base=0, channel_multiplier=1))

            @block.vector
            def _(dve):
                own = Chain(dve, s["chain"])
                dve.wait_ge(s["pool_made"], 2)
                own(nc.vector.tensor_copy(c["iota"][:], c["iota_i"][:]))
                own(nc.vector.tensor_copy(c["part"][:], c["part_i"][:]))
                own(nc.vector.memset(c["ones"][:], 1.0))
                own(nc.vector.memset(c["zeros"][:], 0.0))
                own(nc.vector.tensor_scalar(c["ident"][:], c["iota"][:, 0:128], c["part"][:], None, ALU.is_equal))
                own(nc.vector.tensor_scalar(c["lower"][:], c["iota"][:, 0:128], c["part"][:], None, ALU.is_lt))
                for h in range(4):
                    own(nc.vector.tensor_scalar(c["block4"][:, h:h + 1], c["part"][:], h * 32 - 0.5, None, ALU.is_gt))
                    own(nc.vector.tensor_scalar(c["tmp1"][:], c["part"][:], h * 32 + 31.5, None, ALU.is_lt))
                    own(nc.vector.tensor_tensor(c["block4"][:, h:h + 1], c["block4"][:, h:h + 1], c["tmp1"][:], ALU.mult))
                own(nc.vector.tensor_copy(c["block"][:].rearrange("p (h x) -> p h x", x=32), col_of(c["block4"][:], 32)))


def build_edge_numbers(nc, c, e, src, dst, edge_type, edge_weight, edge_attr):
    with phase(nc, "numbers", "edges_in", "chain") as s, nc.Block() as block:
        @block.sync
        def _(sp):
            for to, frm in ((e["src_i"], src), (e["dst_i"], dst), (e["typ_i"], edge_type)):
                sp.dma_start(to[:], frm.rearrange("(p c) -> p c", p=R)).then_inc(s["edges_in"], 16)
            sp.dma_start(e["weight"][:], edge_weight.rearrange("(p c) -> p c", p=R)).then_inc(s["edges_in"], 16)
            sp.dma_start(e["attr"][:], edge_attr.rearrange("(p c) k -> p (c k)", p=R)).then_inc(s["edges_in"], 16)

        @block.vector
        def _(dve):
            own = Chain(dve, s["chain"])
            dve.wait_ge(s["edges_in"], 80)
            v = nc.vector
            for side in ("src", "dst"):
                ids, lo, hi, cmp, it = e[side][:], e[side + "_lo"][:], e[side + "_hi"][:], e["tmp"][:], e["tmp_i"][:]
                own(v.tensor_copy(ids, e[side + "_i"][:]))
                own(v.tensor_scalar(hi, ids, 1.0 / R, None, ALU.mult))
                own(v.tensor_copy(it, hi))
                own(v.tensor_copy(hi, it))
                own(v.scalar_tensor_tensor(lo, hi, -float(R), ids, ALU.mult, ALU.add))
                own(v.tensor_scalar(cmp, lo, 0.0, None, ALU.is_lt))
                own(v.scalar_tensor_tensor(lo, cmp, float(R), lo, ALU.mult, ALU.add))
                own(v.scalar_tensor_tensor(hi, cmp, -1.0, hi, ALU.mult, ALU.add))
                own(v.tensor_scalar(cmp, lo, float(R), None, ALU.is_ge))
                own(v.scalar_tensor_tensor(lo, cmp, -float(R), lo, ALU.mult, ALU.add))
                own(v.tensor_tensor(hi, cmp, hi, ALU.add))
            own(v.tensor_copy(e["tmp"][:], e["typ_i"][:]))
            own(v.scalar_tensor_tensor(e["slot"][:], e["src_hi"][:], float(TYPES), e["tmp"][:], ALU.mult, ALU.add))
            own(v.scalar_tensor_tensor(e["tmp"][:], e["dst"][:], float(TYPES), e["tmp"][:], ALU.mult, ALU.add))
            own(v.tensor_copy(e["rel_i"][:], e["tmp"][:]))


def build_edge_rows(nc, c, e, dram):
    names = ("src", "dst", "src_lo", "dst_lo")
    B = 100
    with ExitStack() as ctx:
        turned_p = [ctx.enter_context(nc.psum_tensor(f"edge_rows_p{k}", [B, CHUNKS // B, 128], F32)) for k in range(len(names))]
        rows = [ctx.enter_context(nc.sbuf_tensor(f"edge_rows{k}", [B, CHUNKS // B, R], I16)) for k in range(len(names))]
        with phase(nc, "edge_rows", "turned", "copied", "stored") as s, nc.Block() as block:
            @block.tensor
            def _(pe):
                for k, name in enumerate(names):
                    for b in range(CHUNKS // B):
                        last = nc.tensor.transpose(turned_p[k][:, b, 0:R], e[name][:, b * B:(b + 1) * B], c["ident"][0:R, 0:R])
                    last.then_inc(s["turned"], 1)

            @block.scalar
            def _(act):
                for k in range(len(names)):
                    act.wait_ge(s["turned"], k + 1)
                    nc.scalar.copy(rows[k][:], turned_p[k][:, :, 0:R]).then_inc(s["copied"], 1)

            @block.sync
            def _(sp):
                for k, name in enumerate(names):
                    sp.wait_ge(s["copied"], k + 1)
                    sp.dma_start(dram[name + "_ids"].rearrange("(b p r) -> p b r", p=B, r=R), rows[k][:]).then_inc(s["stored"], 16)
                sp.wait_ge(s["stored"], 16 * len(names))


def spread(ids, i, lane):
    return ids[bass.ds((i * UNIT + lane * G) * R, G * R)].partition_broadcast(R)


def flat(t):
    return t.rearrange("p g j -> p (g j)")


def in_chunks(t):
    return t.rearrange("p (g j) -> p g j", g=G)


def build_earlier(nc, c, e, dram):
    AHEAD = 4
    turns = CHUNKS // (G * AHEAD)
    with ExitStack() as ctx:
        ids = [ctx.enter_context(nc.sbuf_tensor(f"ids_dst{l}", [R, G * R], I16)) for l in range(AHEAD)]
        earlier = ctx.enter_context(nc.sbuf_tensor("earlier", [R, AHEAD, G, R], F32))
        with phase(nc, "earlier", *[f"ids_in{l}" for l in range(AHEAD)], "ids_used") as s, nc.Block() as block:
            @block.vector
            def _(dve):
                with dve.Fori(0, turns) as i:
                    for l in range(AHEAD):
                        dve.wait_ge(s[f"ids_in{l}"], i * 16 + 16)
                        count_earlier(nc, c, earlier[:, l], ids[l], e["dst"], e["dst_dup"], (i * AHEAD + l) * G).then_inc(s["ids_used"], 1)
                    dve.wait_ge(s["ids_used"], (i + 1) * AHEAD)

            @block.sync
            def _(sp):
                def loads(i, first=False):
                    for l in range(AHEAD):
                        if not first:
                            sp.wait_ge(s["ids_used"], (i - 1) * AHEAD + l + 1)
                        at = (i * AHEAD + l) * G * R
                        sp.dma_start(ids[l][:], dram["dst_ids"][bass.ds(at, G * R)].partition_broadcast(R)).then_inc(s[f"ids_in{l}"], 16)
                loads(0, first=True)
                with sp.Fori(1, turns) as i:
                    loads(i)


def count_earlier(nc, c, out, ids, node, count, chunk):
    for g in range(G):
        at = bass.ds(chunk + g, 1)
        last = nc.vector.scalar_tensor_tensor(out[:, g, :], ids[:, g * R:(g + 1) * R], node[:, at], c["lower"][0:R, 0:R],
                                              ALU.is_equal, ALU.mult, accum_out=count[:, at])
    return last


def build_scatter_rows(nc, c, tag, node, count, out):
    with (nc.sbuf_tensor(f"{tag}_t", [R, CHUNKS], F32) as t, nc.sbuf_tensor(f"{tag}_row", [R, CHUNKS], I32) as row,
          phase(nc, tag, "chain", "stored") as s, nc.Block() as block):
        @block.vector
        def _(dve):
            v = nc.vector
            own = Chain(dve, s["chain"])
            own(v.tensor_scalar(count, count, 1.0, None, ALU.min))
            own(v.tensor_scalar(t[:], node, c["part"][0:R, :], -float(NODES), ALU.subtract, ALU.add))
            own(v.tensor_tensor(t[:], t[:], count, ALU.mult))
            own(v.tensor_tensor(t[:], node, t[:], ALU.subtract))
            own(v.tensor_copy(row[:], t[:]))
            own(v.tensor_scalar(count, count, -1.0, 1.0, ALU.mult, ALU.add))

        @block.sync
        def _(sp):
            sp.wait_ge(s["chain"], 6)
            sp.dma_start(out, row[:]).then_inc(s["stored"], 16)
            sp.wait_ge(s["stored"], 16)


class EdgeCounts:

    names = ("hots_ready", "counted", "src_in0", "src_in1", "src_used", "pay_chain")

    def __init__(self, c, e, ids, deg3, relcnt, src_dup):
        self.c, self.e, self.ids, self.deg3, self.relcnt, self.src_dup = c, e, ids, deg3, relcnt, src_dup
        self.KD, self.KT = 3 * TILES, TILES * TYPES

    def allocate(self, sb, ps):
        lanes = range(LANES)
        self.hot_d = [sb(f"hot_d{l}", [R, G, R]) for l in lanes]
        self.hot_s = [sb(f"hot_s{l}", [R, G, R], BF16) for l in lanes]
        self.pay_d = [sb(f"pay_d{l}", [R, G, 3, TILES]) for l in lanes]
        self.pay_s = [sb(f"pay_s{l}", [R, G, self.KT], BF16) for l in lanes]
        self.src_b = [sb(f"src_b{l}", [R, G * R], I16) for l in lanes]
        self.earlier = [sb(f"earlier{l}", [R, G, R]) for l in lanes]
        self.acc_d, self.acc_s = ps("acc_d", [R, self.KD]), ps("acc_s", [R, self.KT])

    def load(self, sp, s, i, l, first=False):
        if not first:
            sp.wait_ge(s["src_used"], i * LANES + l + 1)
        sp.dma_start(self.src_b[l][:], spread(self.ids, i, l)).then_inc(s[f"src_in{l}"], 16)

    def vector(self, nc, dve, s, i, l):
        v, c, e = nc.vector, self.c, self.e
        cs = bass.ds(i * UNIT + l * G, G)
        hot_d, hot_s, pay_d, pay_s = self.hot_d[l], self.hot_s[l], self.pay_d[l], self.pay_s[l]
        dve.wait_ge(s["counted"], i * LANES + l + 1)
        v.tensor_tensor(hot_d[:], row_of(c["iota"][0:R, 0:R], G), col_of(e["dst_lo"][:, cs], R), ALU.is_equal)
        v.tensor_tensor(hot_s[:], row_of(c["iota"][0:R, 0:R], G), col_of(e["src_lo"][:, cs], R), ALU.is_equal)
        v.tensor_tensor(pay_s[:], row_of(c["iota"][0:R, 0:self.KT], G), col_of(e["slot"][:, cs], self.KT), ALU.is_equal)
        v.tensor_tensor(pay_d[:, :, 0, :], row_of(c["iota"][0:R, 0:TILES], G), col_of(e["dst_hi"][:, cs], TILES),
                        ALU.is_equal).then_inc(s["pay_chain"], 1)
        dve.wait_ge(s["pay_chain"], i * LANES + l + 1)
        v.tensor_tensor(pay_d[:, :, 1, :], pay_d[:, :, 0, :], col_of(e["weight"][:, cs], TILES), ALU.mult)
        v.tensor_tensor(pay_d[:, :, 2, :], pay_d[:, :, 0, :], col_of(e["attr"][:, cs], TILES), ALU.mult).then_inc(s["hots_ready"], 1)
        dve.wait_ge(s[f"src_in{l}"], i * 16 + 16)
        dve.wait_ge(s["src_used"], i * LANES + l + 1)
        count_earlier(nc, c, self.earlier[l], self.src_b[l], e["src"], self.src_dup, i * UNIT + l * G).then_inc(s["src_used"], 1)

    def tensor(self, t, pe, s, i, l):
        pe.wait_ge(s["hots_ready"], i * LANES + l + 1)
        for g in range(G):
            t.matmul(self.acc_d[:], self.hot_d[l][:, g, :], self.pay_d[l][:, g].rearrange("p k t -> p (k t)"),
                     start=False, stop=False, skip_group_check=True)
            last = t.matmul(self.acc_s[:], self.hot_s[l][:, g, :], self.pay_s[l][:, g, :], start=False, stop=False, skip_group_check=True)
        last.then_inc(s["counted"], 1)

    def edge_of_sums(self, t, s, first):
        zeros = self.c["zeros"]
        t.matmul(self.acc_d[:], zeros[0:R, 0:R], zeros[0:R, 0:self.KD], start=first, stop=not first, skip_group_check=True)
        t.matmul(self.acc_s[:], zeros[0:R, 0:R], zeros[0:R, 0:self.KT], start=first, stop=not first,
                 skip_group_check=True).then_inc(s["counted"], LANES if first else 1)

    def finish(self, v, dve, s):
        dve.wait_ge(s["counted"], LANES * (TURNS + 1) + 1)
        v.tensor_copy(self.deg3, self.acc_d[:])
        v.tensor_copy(self.relcnt, self.acc_s[:])


class Tops:

    names = ("scores_ready", "spread_ready", "spread_used", "dve_passed", "pay_ready", "apart_ready", "places_ready", "placed_ready", "ids_in0", "ids_in1", "ids_used", "chain")

    def __init__(self, nc, c, e, s, sb, ps, ids, sc, top, heads):
        self.c, self.e, self.s, self.ids, self.sc, self.top, self.heads = c, e, s, ids, sc, top, heads
        lanes = range(LANES)
        self.other = [sb(f"other{l}", [R, G, R]) for l in lanes]
        self.masked = [sb(f"masked{h}", [R, G, R]) for h in range(heads)]
        self.hot = [sb(f"place{l}", [R, G, R]) for l in lanes]
        self.best = [sb(f"best{l}", [R, heads, G]) for l in lanes]
        self.pay = [sb(f"pay{l}", [R, G, heads + 1, TILES]) for l in lanes]
        self.cand = [sb(f"cand{l}", [R, G, heads + 1, TILES]) for l in lanes]
        self.most = [sb(f"most{l}", [R, heads, TILES]) for l in lanes]
        self.spread_p = [ps(f"spread{h}", [R, 512]) for h in range(heads)]
        self.placed = [ps(f"placed{l}", [R, G, 128]) for l in lanes]

    def prepare(self, dve, v, own, l, i):
        e, c, heads = self.e, self.c, self.heads
        cs = bass.ds(i * UNIT + l * G, G)
        ids = self.ids[l]
        dve.wait_ge(self.s[f"ids_in{l}"], i * 16 + 16)
        for g in range(G):
            last = v.tensor_scalar(self.other[l][:, g, :], ids[:, g * R:(g + 1) * R], e["dst"][:, bass.ds(i * UNIT + l * G + g, 1)], -HUGE, ALU.not_equal, ALU.mult)
        last.then_inc(self.s["ids_used"], 1)
        own(v.tensor_tensor(self.cand[l][:, :, heads, :], row_of(c["iota"][0:R, 0:TILES], G), col_of(e["dst_hi"][:, cs], TILES), ALU.is_equal))
        own(v.tensor_tensor(self.pay[l][:, :, heads, :], self.cand[l][:, :, heads, :], col_of(e["dst_dup"][:, cs], TILES), ALU.mult))

    def find_places(self, act, a, i, l):
        s, n = self.s, i * LANES + l
        act.wait_ge(s["placed_ready"], n + 1)
        for g in range(G):
            last = a.activation(self.hot[l][:, g, :], self.c["iota"][0:R, 0:R], ACT.Abs, scale=-1.0,
                                bias=self.e["dst_lo"][:, bass.ds(i * UNIT + l * G + g, 1)])
        last.then_inc(s["apart_ready"], 1)
        act.wait_ge(s["apart_ready"], n + 1)
        a.activation(flat(self.hot[l][:]), flat(self.hot[l][:]), ACT.Relu, bias=self.c["ones"][0:R, 0:1], scale=-1.0).then_inc(s["places_ready"], 1)

    def rank(self, dve, v, l, i):
        s, heads = self.s, self.heads
        for h in range(heads):
            dve.wait_ge(s["spread_ready"], (i * LANES + l) * heads + h + 1)
            dve.sem_inc(s["dve_passed"], 1)
            for g in range(G):
                last = v.tensor_tensor_reduce(self.masked[h][:, g, :], self.other[l][:, g, :], self.spread_p[h][:, g * R:(g + 1) * R],
                                              1.0, -HUGE, ALU.add, ALU.max, self.best[l][:, h, g:g + 1])
            last.then_inc(s["spread_used"], 1)
        dve.wait_ge(s["spread_used"], (i * LANES + l + 2) * heads)
        v.tensor_tensor(self.pay[l][:, :, 0:heads, :], self.pay[l][:, :, heads, :].unsqueeze(2).to_broadcast([R, G, heads, TILES]),
                        self.best[l][:].rearrange("p h g -> p g h").unsqueeze(3).to_broadcast([R, G, heads, TILES]), ALU.mult).then_inc(s["pay_ready"], 1)

    def raise_tops(self, dve, v, own, l, i):
        heads, cand, placed = self.heads, self.cand, self.placed
        dve.wait_ge(self.s["placed_ready"], (i + 1) * LANES + l + 1)
        there = cand[l][:, :, heads, :]
        own(v.tensor_scalar(there, placed[l][:, :, heads * TILES:(heads + 1) * TILES], 1.0, HUGE, ALU.subtract, ALU.mult))
        own(v.tensor_tensor(cand[l][:, :, 0:heads, :], placed[l][:, :, 0:heads * TILES].rearrange("p g (h t) -> p g h t", h=heads),
                            there.unsqueeze(2).to_broadcast([R, G, heads, TILES]), ALU.add))
        own(v.tensor_reduce(self.most[l][:], cand[l][:, :, 0:heads, :].rearrange("p g h t -> p h t g"), AX, ALU.max))
        own(v.tensor_tensor(self.top, self.top, self.most[l][:], ALU.max))

    def spread_scores(self, pe, t, l, i):
        s, heads = self.s, self.heads
        pe.wait_ge(s["scores_ready"], i * LANES + l + 1)
        for h in range(heads):
            pe.wait_ge(s["spread_used"], (i * LANES + l) * heads + h + 1)
            for g in range(G):
                last = t.matmul(self.spread_p[h][:, g * R:(g + 1) * R], self.sc[l][:, g, h:h + 1].to_broadcast([R, R]),
                                self.c["ident"][0:R, 0:R], start=True, stop=True)
            last.then_inc(s["spread_ready"], 1)

    def place(self, pe, t, l, i):
        pe.wait_ge(self.s["places_ready"], i * LANES + l + 1)
        pe.wait_ge(self.s["pay_ready"], i * LANES + l + 1)
        for g in range(G):
            last = t.matmul(self.placed[l][:, g, 0:(self.heads + 1) * TILES], self.hot[l][:, g, :], self.pay[l][:, g].rearrange("p h t -> p (h t)"),
                            start=True, stop=True)
        last.then_inc(self.s["placed_ready"], 1)


    def run_vector(self, dve, v, score, steps, look=None):
        look = look or (lambda i, l: None)
        chain, PREPARE, RAISE = self.s["chain"], 2, 4
        start, turn = 1 + LANES * (steps + PREPARE), LANES * (steps + PREPARE + RAISE)
        own = Chain(dve, chain)
        own(v.memset(self.top, -HUGE))
        look(0, 0)
        score(own, 0, 0)
        self.prepare(dve, v, own, 0, 0)
        look(0, 1)
        score(own, 0, 1)
        self.prepare(dve, v, own, 1, 0)
        look(1, 0)
        self.rank(dve, v, 0, 0)

        def whole_turn(own, i, last=False):
            score(own, i, 0)
            self.raise_tops(dve, v, own, 0, i - 1)
            self.prepare(dve, v, own, 0, i)
            look(i, 1)
            self.rank(dve, v, 1, i - 1)
            score(own, i, 1)
            self.raise_tops(dve, v, own, 1, i - 1)
            self.prepare(dve, v, own, 1, i)
            if not last:
                look(i + 1, 0)
            self.rank(dve, v, 0, i)

        with dve.Fori(1, TURNS - 1) as i:
            own = Chain(dve, chain, i, turn, before=start - turn)
            whole_turn(own, i)
            own.end()
        own = Chain(dve, chain, before=start + (TURNS - 2) * turn)
        whole_turn(own, TURNS - 1, last=True)
        self.rank(dve, v, 1, TURNS - 1)
        self.raise_tops(dve, v, own, 0, TURNS - 1)
        self.raise_tops(dve, v, own, 1, TURNS - 1)

    def run_tensor(self, pe, t, find=None):
        find = find or (lambda i, l: None)
        pe.sem_inc(self.s["spread_used"], self.heads)
        pe.sem_inc(self.s["placed_ready"], LANES)
        find(0, 0)
        find(0, 1)
        self.spread_scores(pe, t, 0, 0)
        find(1, 0)
        self.spread_scores(pe, t, 1, 0)
        self.place(pe, t, 0, 0)

        def whole_turn(i, last=False):
            find(i, 1)
            self.spread_scores(pe, t, 0, i)
            self.place(pe, t, 1, i - 1)
            if not last:
                find(i + 1, 0)
            self.spread_scores(pe, t, 1, i)
            self.place(pe, t, 0, i)

        with pe.Fori(1, TURNS - 1) as i:
            whole_turn(i)
        whole_turn(TURNS - 1, last=True)
        self.place(pe, t, 1, TURNS - 1)


def build_logits3(nc, c, e, dram, a_src, a_dst, src_hi, logit, top):
    heads = logit.shape[2]
    K = TILES * heads
    with ExitStack() as ctx:
        sb = lambda n, sh, d=F32: ctx.enter_context(nc.sbuf_tensor(f"logits3_{n}", sh, d))
        ps = lambda n, sh: ctx.enter_context(nc.psum_tensor(f"logits3_{n}", sh, F32))
        per_lane = lambda n, sh, d=F32: [sb(f"{n}{l}", sh, d) for l in range(LANES)]
        sides = ("src", "dst")
        table, high = {"src": a_src, "dst": a_dst}, {"src": src_hi, "dst": e["dst_hi"][:]}
        ids = per_lane("ids", [R, G * R], I16)
        lo = {n: per_lane(f"lo_{n}", [R, G * R], I16) for n in sides}
        hot = {n: per_lane(f"hot_{n}", [R, G, R]) for n in sides}
        mask = {n: sb(f"mask_{n}", [R, G, TILES]) for n in sides}
        picked = {n: sb(f"picked_{n}", [R, G, TILES, heads]) for n in sides}
        found = {n: ps(f"found_{n}", [R, G, 128]) for n in sides}
        sc, apart = per_lane("sc", [R, G, heads]), per_lane("apart", [R, G, R])
        minus_part, one = sb("minus_part", [R, 1]), c["ones"][0:R, 0:1]
        names = ["lo_in0", "lo_in1", "act_chain", "hot_ready", "found_ready", "found_used", "kept"] + list(Tops.names)
        with phase(nc, "logits3", *names) as s, nc.Block() as block:
            tops = Tops(nc, c, e, s, sb, ps, ids, sc, top, heads)

            @block.sync
            def _(sp):
                def loads(i, first=False):
                    for l in range(LANES):
                        if not first:
                            sp.wait_ge(s["hot_ready"], (i * LANES + l - LANES + 1) * 2)
                        for n in sides:
                            sp.dma_start(lo[n][l][:], spread(dram[n + "_lo_ids"], i, l)).then_inc(s[f"lo_in{l}"], 16)
                        if not first:
                            sp.wait_ge(s["ids_used"], i * LANES + l - LANES + 1)
                        sp.dma_start(ids[l][:], spread(dram["dst_ids"], i, l)).then_inc(s[f"ids_in{l}"], 16)
                loads(0, first=True)
                with sp.Fori(1, TURNS) as i:
                    loads(i)

            @block.vector
            def _(dve):
                v = nc.vector

                def make(own, i, l):
                    cs = bass.ds(i * UNIT + l * G, G)
                    for n in sides:
                        last = v.tensor_tensor(mask[n][:], row_of(c["iota"][0:R, 0:TILES], G), col_of(high[n][:, cs], TILES), ALU.is_equal)
                    own(last)
                    for k, n in enumerate(sides):
                        dve.wait_ge(s["found_ready"], (i * LANES + l) * 2 + k + 1)
                        v.tensor_tensor(picked[n][:], found[n][:, :, 0:K].rearrange("p g (k h) -> p g k h", h=heads),
                                        mask[n][:].unsqueeze(3).to_broadcast([R, G, TILES, heads]), ALU.mult).then_inc(s["found_used"], 1)
                    dve.wait_ge(s["found_used"], (i * LANES + l + 2) * 2)
                    own(v.tensor_tensor(picked["src"][:], picked["src"][:], picked["dst"][:], ALU.add))
                    dve.wait_ge(s["kept"], i * LANES + l + 1)
                    own(v.tensor_reduce(sc[l][:], picked["src"][:].rearrange("p g k h -> p g h k"), AX, ALU.add))
                    own(v.tensor_tensor(sc[l][:], sc[l][:], logit[:, cs, :], ALU.add))
                    v.scalar_tensor_tensor(flat(sc[l][:]), flat(sc[l][:]), 0.2, flat(sc[l][:]), ALU.mult, ALU.max).then_inc(s["scores_ready"], 1)

                tops.run_vector(dve, v, make, 4)

            @block.scalar
            def _(act):
                a = nc.scalar

                def look(i, l):
                    act.wait_ge(s[f"lo_in{l}"], i * 32 + 32)
                    for k, n in enumerate(sides):
                        a.activation(flat(hot[n][l][:]), lo[n][l][:], ACT.Abs, bias=minus_part[:]).then_inc(s["act_chain"], 1)
                        act.wait_ge(s["act_chain"], (i * LANES + l) * 2 + k + 2)
                        a.activation(flat(hot[n][l][:]), flat(hot[n][l][:]), ACT.Relu, bias=one, scale=-1.0).then_inc(s["hot_ready"], 1)

                def keep(i, l):
                    act.wait_ge(s["scores_ready"], i * LANES + l + 1)
                    a.copy(logit[:, bass.ds(i * UNIT + l * G, G), :], sc[l][:]).then_inc(s["kept"], 1)

                act.sem_inc(s["kept"], LANES)
                a.mul(minus_part[:], c["part"][0:R, :], -1.0).then_inc(s["act_chain"], 1)
                act.wait_ge(s["act_chain"], 1)
                look(0, 0)
                with act.Fori(0, TURNS - 1) as i:
                    look(i, 1)
                    tops.find_places(act, a, i, 0)
                    keep(i, 0)
                    look(i + 1, 0)
                    tops.find_places(act, a, i, 1)
                    keep(i, 1)
                look(TURNS - 1, 1)
                for l in range(LANES):
                    tops.find_places(act, a, TURNS - 1, l)
                    keep(TURNS - 1, l)

            @block.tensor
            def _(pe):
                t = nc.tensor

                def find(i, l):
                    for k, n in enumerate(sides):
                        pe.wait_ge(s["hot_ready"], (i * LANES + l) * 2 + k + 1)
                        pe.wait_ge(s["found_used"], (i * LANES + l) * 2 + k + 1)
                        for g in range(G):
                            last = t.matmul(found[n][:, g, 0:K], hot[n][l][:, g, :], table[n], start=True, stop=True)
                        last.then_inc(s["found_ready"], 1)

                pe.sem_inc(s["found_used"], 2)
                tops.run_tensor(pe, t, find)


def build_messages(nc, c, e, tag, table, take, put, node, ids, weight, heads, acc, look=None, beside=None):
    W = D + heads
    C = D // heads
    with ExitStack() as ctx:
        sb = lambda n, sh, d=F32: ctx.enter_context(nc.sbuf_tensor(f"{tag}_{n}", sh, d))
        per_lane = lambda n, sh, d=F32: [sb(f"{n}{l}", sh, d) for l in range(LANES)]
        take_b, put_b = per_lane("take", [R, G], I32), per_lane("put", [R, G], I32)
        rows, sent = per_lane("rows", [R, G, W]), per_lane("sent", [R, G, W])
        id_b, same = per_lane("ids", [R, G * R], I16), per_lane("same", [R, G, R])
        sum_p = [ctx.enter_context(nc.psum_tensor(f"{tag}_sum{g}", [R, 512], F32)) for g in range(G)]
        if look:
            slots = look["slots"]
            K = slots * heads
            lo_b, hot, mask = per_lane("lo", [R, G * R], I16), per_lane("hot", [R, G, R]), per_lane("mask", [R, G, slots])
            picked, w = per_lane("picked", [R, G, slots, heads]), per_lane("w", [R, G, heads])
            diff = per_lane("diff", [R, G, heads])
            found = [ctx.enter_context(nc.psum_tensor(f"{tag}_found{l}", [R, G, 128 if K <= 128 else 256], F32)) for l in range(LANES)]
        if beside:
            beside.allocate(sb, lambda n, sh: ctx.enter_context(nc.psum_tensor(f"{tag}_{n}", sh, F32)))
        ids_bytes = 32 if look else 16
        names = ([f"{n}{l}" for n in ("take_in", "put_in", "rows_in", "ids_in") for l in range(LANES)]
                 + [f"acc_done{g}" for g in range(G)]
                 + ["same_ready", "hot_ready", "found_ready", "diff_ready", "exp_ready", "scaled", "summed", "moved", "chain", "pool_passed", "sp_passed"] + list(beside.names if beside else ()))
        with phase(nc, tag, *names) as s, nc.Block() as block:
            @block.sync
            def _(sp):
                def load_ids(i, l):
                    sp.dma_start(id_b[l][:], spread(ids, i, l)).then_inc(s[f"ids_in{l}"], 16)
                    if look:
                        sp.dma_start(lo_b[l][:], spread(look["ids"], i, l)).then_inc(s[f"ids_in{l}"], 16)

                def load_numbers(i, l):
                    cs = bass.ds(i * UNIT + l * G, G)
                    sp.dma_start(take_b[l][:], take[:, cs]).then_inc(s[f"take_in{l}"], 16)
                    return cs

                for l in range(LANES):
                    sp.dma_start(put_b[l][:], put[:, load_numbers(0, l)]).then_inc(s[f"put_in{l}"], 16)
                    load_ids(0, l)
                    if beside:
                        beside.load(sp, s, 0, l, first=True)
                with sp.Fori(1, TURNS) as i:
                    for l in range(LANES):
                        sp.wait_ge(s["same_ready"], i * LANES + l - LANES + 1)
                        if look:
                            sp.wait_ge(s["hot_ready"], i * LANES + l - LANES + 1)
                        load_ids(i, l)
                    for l in range(LANES):
                        sp.wait_ge(s[f"rows_in{l}"], i * (16 * G))
                        sp.sem_inc(s["sp_passed"], 1)
                        cs = load_numbers(i, l)
                        for g in range(G):
                            sp.wait_ge(s[f"acc_done{g}"], i * (16 * LANES) + 16 * (l - LANES + 1))
                        sp.dma_start(put_b[l][:], put[:, cs]).then_inc(s[f"put_in{l}"], 16)
                        if beside:
                            beside.load(sp, s, i, l)

            @block.vector
            def _(dve):
                v = nc.vector
                if beside:
                    dve.sem_inc(s["src_used"], LANES)
                with dve.Fori(0, TURNS) as i:
                    own = Chain(dve, s["chain"], i, LANES * (2 if weight is None else 3))
                    cs = [bass.ds(i * UNIT + l * G, G) for l in range(LANES)]
                    for l in range(LANES):
                        dve.wait_ge(s[f"ids_in{l}"], i * ids_bytes + ids_bytes)
                        if look:
                            v.tensor_scalar(flat(hot[l][:]), lo_b[l][:], c["part"][0:R, :], None, ALU.is_equal).then_inc(s["hot_ready"], 1)
                            own(v.tensor_tensor(mask[l][:], row_of(c["iota"][0:R, 0:slots], G), col_of(look["slot"][:, cs[l]], slots), ALU.is_equal))
                        dve.wait_ge(s["summed"], i * UNIT + (l + 1) * G)
                        v.tensor_tensor(same[l][:], in_chunks(id_b[l][:]), col_of(node[:, cs[l]], R), ALU.is_equal).then_inc(s["same_ready"], 1)
                    for l in range(LANES if look else 0):
                        dve.wait_ge(s["found_ready"], i * LANES + l + 1)
                        own(v.tensor_tensor(picked[l][:], found[l][:, :, 0:K].rearrange("p g (k h) -> p g k h", h=heads),
                                            mask[l][:].unsqueeze(3).to_broadcast([R, G, slots, heads]), ALU.mult))
                        to = w[l] if weight is None else diff[l]
                        last = v.tensor_reduce(to[:], picked[l][:].rearrange("p g k h -> p g h k"), AX, ALU.add)
                        if weight is None:
                            last.then_inc(s["exp_ready"], 1)
                        else:
                            own(last)
                            v.tensor_tensor(diff[l][:], weight[:, cs[l], :], diff[l][:], ALU.subtract).then_inc(s["diff_ready"], 1)
                    for l in range(LANES):
                        weigh = w[l][:] if look else weight[:, cs[l], :]
                        if look:
                            dve.wait_ge(s["exp_ready"], i * LANES + l + 1)
                        dve.wait_ge(s[f"rows_in{l}"], i * (16 * G) + 16 * G)
                        v.tensor_copy(rows[l][:, :, D:W], weigh)
                        vw = rows[l][:, :, 0:D].rearrange("p g (h x) -> p g h x", h=heads)
                        v.tensor_tensor(vw, vw, weigh.unsqueeze(3).to_broadcast([R, G, heads, C]), ALU.mult).then_inc(s["scaled"], 1)
                        if beside:
                            beside.vector(nc, dve, s, i, l)
                    if look:
                        own.end()
                if beside:
                    beside.finish(v, dve, s)

            @block.tensor
            def _(pe):
                t = nc.tensor
                pe.sem_inc(s["summed"], UNIT)
                if beside:
                    beside.edge_of_sums(t, s, first=True)
                with pe.Fori(0, TURNS) as i:
                    for l in range(LANES if look else 0):
                        pe.wait_ge(s["hot_ready"], i * LANES + l + 1)
                        for g in range(G):
                            last = t.matmul(found[l][:, g, 0:K], hot[l][:, g, :], look["table"], start=True, stop=True)
                        last.then_inc(s["found_ready"], 1)
                    for l in range(LANES):
                        pe.wait_ge(s["same_ready"], i * LANES + l + 1)
                        pe.wait_ge(s["scaled"], i * LANES + l + 1)
                        for g in range(G):
                            pe.wait_ge(s["moved"], i * UNIT + l * G + g + 1)
                            t.matmul(sum_p[g][:, 0:W], same[l][:, g, :], rows[l][:, g, :], start=True, stop=True).then_inc(s["summed"], 1)
                        if beside:
                            beside.tensor(t, pe, s, i, l)
                if beside:
                    beside.edge_of_sums(t, s, first=False)

            @block.scalar
            def _(act):
                act.sem_inc(s["moved"], G)

                def move(i, first=False):
                    if look and weight is not None:
                        for l in range(LANES):
                            act.wait_ge(s["diff_ready"], i * LANES + l + 1)
                            nc.scalar.activation(w[l][:], diff[l][:], ACT.Exp).then_inc(s["exp_ready"], 1)
                    for l in range(LANES):
                        for g in range(G):
                            act.wait_ge(s["summed"], i * UNIT + UNIT + l * G + g + 1)
                            if not first:
                                act.wait_ge(s[f"acc_done{g}"], i * (16 * LANES))
                            nc.scalar.copy(sent[l][:, g, :], sum_p[g][:, 0:W]).then_inc(s["moved"], 1)

                move(0, first=True)
                with act.Fori(1, TURNS) as i:
                    move(i)

            @block.gpsimd
            def _(pool):
                def gather(i, l):
                    pool.wait_ge(s[f"take_in{l}"], i * 16 + 16)
                    pool.wait_ge(s["summed"], i * UNIT + (l + 1) * G)
                    pool.sem_inc(s["pool_passed"], 1)
                    for g in range(G):
                        nc.gpsimd.indirect_dma_start(rows[l][:, g, 0:D], None, table, bass.IndirectOffsetOnAxis(ap=take_b[l][:, g:g + 1], axis=0)
                                                     ).then_inc(s[f"rows_in{l}"], 16)

                def scatter(i, l, first=False):
                    pool.wait_ge(s[f"put_in{l}"], i * 16 + 16)
                    for g in range(G):
                        pool.wait_ge(s["moved"], i * UNIT + (l + 1) * G + g + 1)
                        if not first:
                            pool.wait_ge(s[f"acc_done{g}"], i * (16 * LANES) + 16 * l)
                        pool.sem_inc(s["pool_passed"], 1)
                        nc.gpsimd.indirect_dma_start(acc[g], bass.IndirectOffsetOnAxis(ap=put_b[l][:, g:g + 1], axis=0), sent[l][:, g, :], None,
                                                     compute_op=ALU.add).then_inc(s[f"acc_done{g}"], 16)

                gather(0, 0)
                gather(0, 1)
                scatter(0, 0, first=True)
                gather(1, 0)
                scatter(0, 1)
                with pool.Fori(1, TURNS - 1) as i:
                    gather(i, 1)
                    scatter(i, 0)
                    gather(i + 1, 0)
                    scatter(i, 1)
                gather(TURNS - 1, 1)
                scatter(TURNS - 1, 0)
                scatter(TURNS - 1, 1)
                for g in range(G):
                    pool.wait_ge(s[f"acc_done{g}"], 16 * LANES * TURNS)



def until(eng, steps, name, turn=None):
    eng.wait_ge(steps.sem, steps.at(name, turn))


def mark(ins, steps):
    ins.then_inc(steps.sem, 1)


def by_tile(ap):
    return ap.rearrange("(t r) w -> r t w", r=R)


def slices(ap):
    return ap[:, 0:GT * 128].rearrange("p (s x) -> p s x", x=128)[:, :, 0:R]


def dense(ap):
    return ap.rearrange("p (s x) -> p s x", x=R)


def turn_tiles(nc, c, to, tile, blocks=KB):
    for k in range(blocks):
        for j in range(GT):
            q = k * GT + j
            last = nc.tensor.transpose(to[:, q * 128:q * 128 + R], tile[:, j, k * 128:(k + 1) * 128], c["ident"][0:R, 0:R])
    return last


def turned(ap, blocks=KB):
    return ap[:, 0:blocks * GT * 128].rearrange("p (q x) -> p q x", x=128)[:, :, 0:R]


def product_t(nc, to, m, pairs):
    first, second = to[0:m, 0:512].rearrange("p (s x) -> p s x", x=128)[:, :, 0:R], to[0:m, 512:512 + R]
    n = len(pairs)
    for a, (w, f) in enumerate(pairs):
        nc.tensor.matmul(first, w, f[:, 0:4 * R].rearrange("p (s x) -> p s x", x=R), start=(a == 0), stop=(a == n - 1))
    for a, (w, f) in enumerate(pairs):
        last = nc.tensor.matmul(second, w, f[:, 4 * R:GN], start=(a == 0), stop=(a == n - 1))
    return last


def product_rows(nc, to, pairs):
    n = len(pairs)
    for j in range(GT):
        for a, (f, w) in enumerate(pairs):
            last = nc.tensor.matmul(to[:, j, :], f[:, j * R:(j + 1) * R], w, start=(a == 0), stop=(a == n - 1))
    return last


def variance(v, own, x, b, eps, passed):
    for j in range(GT):
        last = v.bn_stats(b["stats"][:, j, :], x[:, j, :])
    own(last)
    own.pause(passed)
    for j in range(GT):
        last = v.bn_aggr(b["mv"][:, j, :], b["stats"][:, j, :])
    own(last)
    return v.tensor_scalar(b["var"][:], b["mv"][:, :, 1], eps, None, ALU.add)


VARIANCE_STEPS = 2


def standardize(v, own, x, out, b):
    own(v.reciprocal(b["rstd"][:], b["std"][:]))
    for j in range(GT):
        last = v.tensor_scalar(out[:, j, :], x[:, j, :], b["mv"][:, j, 0:1], b["rstd"][:, j:j + 1], ALU.subtract, ALU.mult)
    return last


STANDARDIZE_STEPS = 1


def norm_buffers(sb):
    return {"stats": sb("stats", [R, GT, 6]), "mv": sb("mv", [R, GT, 2]), "var": sb("var", [R, GT]),
            "std": sb("std", [R, GT]), "rstd": sb("rstd", [R, GT])}


def build_open(nc, c, layer, X, XN, XNT, loads, units, post, stores, kv, kv_cols, per_turn, hand=(), clear=()):
    tag = f"open{layer}"
    NU = len(units(None))
    UNITS = [f"u{n}" for n in range(NU * GT)]
    with ExitStack() as ctx:
        sb = lambda n, sh, d=F32: ctx.enter_context(nc.sbuf_tensor(f"{tag}_{n}", sh, d))
        ps = lambda n, sh: ctx.enter_context(nc.psum_tensor(f"{tag}_{n}", sh, F32))
        b = norm_buffers(sb)
        xn_s, xT = sb("xn_s", [R, GT, D]), sb("xT", [128, KB, GN])
        st = sb("st", [R, GT, max(sum(n for _, n in units(None)), 1)])
        b["st"], b["xn_s"] = st, xn_s
        wide, unit_p, kv_p = ps("wide", [128, 1536]), [ps(f"unit{n}", [R, 512]) for n in range(4)], ps("kv_p", [128, KB, 256])
        w, w_loads = loads(sb)
        b.update(w)
        with phase(nc, tag, "loaded", "pe", "dve", "act", "stored", "cleared", "chain", "passed", "sp_passed") as s, nc.Block() as block:
            PE = Steps(s["pe"], ["turn"] + UNITS + ["kv_added"])
            HANDS = [f"hand{n}" for n in range(len(hand))]
            DV = Steps(s["dve"], ["var", "xn"] + HANDS + ["post"])
            AC = Steps(s["act"], ["std", "keep", "turned", "all_turned"] + UNITS + HANDS)
            NS = stores(None, b, None)

            @block.sync
            def _(sp):
                for to, frm in w_loads:
                    sp.dma_start(to, frm).then_inc(s["loaded"], 16)
                for table in clear:
                    rows = table.rearrange("(p n) d -> p n d", p=R)
                    sp.dma_start(rows, row_of(c["zeros"][0:R, 0:rows.shape[2]], rows.shape[1])).then_inc(s["cleared"], 16)
                with sp.Fori(0, GROUPS) as i:
                    until(sp, DV, "post", i)
                    sp.sem_inc(s["sp_passed"], 1)
                    if NS:
                        stores(sp, b, i, s["stored"])
                if NS:
                    sp.wait_ge(s["stored"], 16 * NS * GROUPS)
                if clear:
                    sp.wait_ge(s["cleared"], 16 * len(clear))

            @block.vector
            def _(dve):
                v = nc.vector
                dve.wait_ge(s["loaded"], 16 * len(w_loads))
                with dve.Fori(0, GROUPS) as i:
                    own = Chain(dve, s["chain"], i, VARIANCE_STEPS + STANDARDIZE_STEPS + per_turn)
                    grp = bass.ds(i * GT, GT)
                    mark(variance(v, own, X[:, grp, :], b, 1e-5, s["passed"]), DV)
                    until(dve, AC, "std", i)
                    mark(standardize(v, own, X[:, grp, :], xn_s, b), DV)
                    until(dve, DV, "xn", i)
                    until(dve, AC, (UNITS or ["all_turned"])[-1], i)
                    handed = iter(HANDS)

                    def hand_over(ins):
                        mark(ins, DV)
                        until(dve, AC, next(handed), i)

                    mark(post(v, own, hand_over, b, grp), DV)
                    own.end()
                    until(dve, PE, "kv_added", i)
                    until(dve, AC, "all_turned", i)
                    if NS:
                        dve.wait_ge(s["stored"], i * (16 * NS) + 16 * NS)

            @block.scalar
            def _(act):
                a = nc.scalar
                with act.Fori(0, GROUPS) as i:
                    grp = bass.ds(i * GT, GT)
                    until(act, DV, "var", i)
                    mark(a.activation(b["std"][:], b["var"][:], ACT.Sqrt), AC)
                    until(act, DV, "xn", i)
                    mark(a.copy(XN[:, grp, :], xn_s[:]), AC)
                    until(act, PE, "turn", i)
                    mark(a.copy(xT[:].rearrange("p k (j x) -> p (k j) x", x=R), turned(wide[:])), AC)
                    until(act, AC, "turned", i)
                    mark(a.copy(XNT[:, :, bass.ds(i * GN, GN)], xT[:]), AC)
                    at = 0
                    for u, name in enumerate(UNITS):
                        n = units(None)[u % NU][1]
                        until(act, PE, name, i)
                        mark(a.copy(st[:, u // NU, at:at + n], unit_p[u % 4][:, 0:n]), AC)
                        at = (at + n) % st.shape[2]
                    for n, name in enumerate(HANDS):
                        until(act, DV, name, i)
                        mark(a.activation(b["hand_out"], b["hand_in"], hand[n]), AC)
                    until(act, DV, "post", i)
                    until(act, PE, "kv_added", i)
                    if NS:
                        act.wait_ge(s["stored"], i * (16 * NS) + 16 * NS)

            @block.tensor
            def _(pe):
                t = nc.tensor
                pe.wait_ge(s["loaded"], 16 * len(w_loads))
                for k in range(KB):
                    t.matmul(kv_p[:, k, :], c["zeros"][:, 0:128], c["zeros"][:, 0:256], start=(k == 0), stop=False, skip_group_check=True)
                with pe.Fori(0, GROUPS) as i:
                    until(pe, DV, "xn", i)
                    mark(turn_tiles(nc, c, wide, xn_s), PE)
                    until(pe, AC, "turned", i)
                    for u, name in enumerate(UNITS):
                        if u >= 4:
                            until(pe, AC, UNITS[u - 4], i)
                        j, (wk, n) = u // NU, units(w)[u % NU]
                        for k in range(KB):
                            last = t.matmul(unit_p[u % 4][:, 0:n], xT[:, k, j * R:(j + 1) * R], wk[k], start=(k == 0), stop=(k == KB - 1))
                        mark(last, PE)
                    until(pe, DV, "post", i)
                    if kv is None:
                        mark(t.matmul(kv_p[:, 0, :], c["zeros"][:, 0:128], c["zeros"][:, 0:256], start=False, stop=False, skip_group_check=True), PE)
                    else:
                        mark(kv(t, kv_p, b), PE)
                for k in range(KB):
                    last = t.matmul(kv_p[:, k, :], c["zeros"][:, 0:128], c["zeros"][:, 0:256], start=False, stop=True, skip_group_check=True)
        if kv_cols is None:
            return
        with phase(nc, tag + "_end", "chain") as s, nc.Block() as block:
            @block.vector
            def _(dve):
                v = nc.vector
                own = Chain(dve, s["chain"])
                kv_cols(v, own, kv_p, b)


def blocked(w, k):
    return w[k * 128:(k + 1) * 128]


def everywhere(vec, p=R):
    return vec.partition_broadcast(p)


def center_heads(v, own, x3, b, div, eps):
    n = x3.shape[1]
    own(v.tensor_reduce(b["hm"][:, 0:n], x3, AX, ALU.add))
    own(v.tensor_scalar(b["hm"][:, 0:n], b["hm"][:, 0:n], 1.0 / 32, None, ALU.mult))
    own(v.tensor_tensor(x3, x3, col_of(b["hm"][:, 0:n], 32), ALU.subtract))
    own(v.tensor_tensor(b["sq"][:, 0:n, :], x3, x3, ALU.mult))
    own(v.tensor_reduce(b["hm"][:, 0:n], b["sq"][:, 0:n, :], AX, ALU.add))
    return v.tensor_scalar(b["hand_in"], b["hm"][:, 0:n], 1.0 / div, eps, ALU.mult, ALU.add)


CENTER_STEPS = 5


def keep_blocks(c, scale, out, ones=False):
    def cols(v, own, kv_p, b):
        for k in range(KB):
            own(v.scalar_tensor_tensor(out[:, k, 0:128], kv_p[:, k, 0:128], scale, c["block"][:], ALU.mult, ALU.mult))
            if ones:
                own(v.tensor_scalar(out[:, k, 128:132], c["block4"][:], kv_p[:, k, 128:129], None, ALU.mult))
    return cols


def open0(nc, c, m, I, dram):
    def loads(sb):
        w = {"el": sb("w_el", [128, KB, 512]), "kv": sb("w_kv", [128, KB, 512]), "bias": sb("bias", [R, 1024]),
             "gain": sb("gain", [R, 512]), "shift": sb("shift", [R, 512]), "hm": sb("hm", [R, 16 * GT]), "sq": sb("sq", [R, 16 * GT, 32]),
             "hv": sb("hv", [R, 16 * GT]), "hs": sb("hs", [R, 16 * GT])}
        w["hand_in"], w["hand_out"] = w["hv"][:], w["hs"][:]
        l = []
        for k in range(KB):
            l += [(w["el"][:, k, 0:D], blocked(I["L0_gnn_W_src"], k)), (w["el"][:, k, D:512], blocked(I["L0_gnn_W_dst"], k)),
                  ] + [(w["kv"][:, k, n * D:(n + 1) * D].rearrange("p (h x) -> p h x", x=32),
                        blocked(I["L0_mix_w_qkv"], k).rearrange("p (h x) -> p h x", x=96)[:, :, 32 * n + 32:32 * n + 64]) for n in range(2)]
        l += [(w["bias"][:, 0:D], everywhere(I["L0_gnn_b_src"])), (w["bias"][:, D:512], everywhere(I["L0_gnn_b_dst"])),
              ] + [(w["bias"][:, 512 + n * D:512 + (n + 1) * D].rearrange("p (h x) -> p h x", x=32),
                    everywhere(I["L0_mix_b_qkv"]).rearrange("p (h x) -> p h x", x=96)[:, :, 32 * n + 32:32 * n + 64]) for n in range(2)]
        for to, kind in (("gain", "g"), ("shift", "b")):
            for n, of in enumerate("kv"):
                l.append((w[to][:, n * D:(n + 1) * D].rearrange("p (h x) -> p h x", x=32),
                          everywhere(I[f"L0_mix_{of}ln_{kind}"]).unsqueeze(1).to_broadcast([R, 8, 32])))
        return w, l

    def units(w):
        return [(w and [w[n][:, k, :] for k in range(KB)], 512) for n in ("el", "kv")]

    def post(v, own, hand_over, b, grp):
        own(v.tensor_tensor(b["st"][:], b["st"][:], row_of(b["bias"][:], GT), ALU.add))
        own(v.tensor_copy(b["sq"][:].rearrange("p (j h) x -> p j (h x)", j=GT), b["st"][:, :, 512:1024]))
        kv3 = b["st"][:, :, 512:1024].rearrange("p j (h x) -> p j h x", x=32)
        sq3, hm3 = b["sq"][:].rearrange("p (j h) x -> p j h x", j=GT), b["hm"][:].rearrange("p (j h) -> p j h", j=GT)
        own(v.tensor_reduce(b["hm"][:], b["sq"][:], AX, ALU.add))
        own(v.tensor_scalar(b["hm"][:], b["hm"][:], 1.0 / 32, None, ALU.mult))
        own(v.tensor_tensor(kv3, kv3, hm3.unsqueeze(3).to_broadcast([R, GT, 16, 32]), ALU.subtract))
        own(v.tensor_tensor(sq3, kv3, kv3, ALU.mult))
        own(v.tensor_reduce(b["hm"][:], b["sq"][:], AX, ALU.add))
        hand_over(v.tensor_scalar(b["hand_in"], b["hm"][:], 1.0 / 32, 1e-5, ALU.mult, ALU.add))
        own(v.reciprocal(b["hm"][:], b["hand_out"]))
        own(v.tensor_tensor(kv3, kv3, hm3.unsqueeze(3).to_broadcast([R, GT, 16, 32]), ALU.mult))
        own(v.tensor_tensor(b["st"][:, :, 512:1024], b["st"][:, :, 512:1024], row_of(b["gain"][:], GT), ALU.mult))
        return v.tensor_tensor(b["st"][:, :, 512:1024], b["st"][:, :, 512:1024], row_of(b["shift"][:], GT), ALU.add)

    def stores(sp, b, i, sem=None):
        if sp is not None:
            grp = bass.ds(i * GT, GT)
            sp.dma_start(by_tile(dram["el"])[:, grp], b["st"][:, :, 0:D]).then_inc(sem, 16)
            sp.dma_start(by_tile(dram["er"])[:, grp], b["st"][:, :, D:512]).then_inc(sem, 16)
        return 2

    def kv(t, kv_p, b):
        for j in range(GT):
            for k in range(KB):
                at = 512 + k * 128
                last = t.matmul(kv_p[:, k, 0:128], b["st"][:, j, at:at + 128], b["st"][:, j, at + D:at + D + 128], start=False, stop=False, skip_group_check=True)
        return last

    build_open(nc, c, 0, m["X"], m["XN"], m["XNT"], loads, units, post, stores, kv, keep_blocks(c, 1.0 / NODES, m["KV"]), 10, hand=(ACT.Sqrt,), clear=dram["acc"])


def open1(nc, c, m, I, dram):
    def loads(sb):
        w = {"rel": sb("w_rel", [128, KB, TYPES * D]), "hm": sb("hm", [R, 8 * GT]), "sq": sb("sq", [R, 8 * GT, 32]),
             "hv": sb("hv", [R, 8 * GT]), "hs": sb("hs", [R, 8 * GT]), "val": sb("val", [R, GT, D])}
        w["hand_in"], w["hand_out"] = w["hv"][:], w["hs"][:]
        l = [(w["rel"][:, k, :].rearrange("p (t o) -> p t o", t=TYPES),
              I["L1_gnn_weights"].rearrange("(t k p) o -> k p t o", t=TYPES, k=KB)[k]) for k in range(KB)]
        for n in ("kln_weight", "kln_bias", "vln_weight", "vln_bias"):
            w[n] = sb(n, [R, D])
            l.append((w[n][:], everywhere(I["L1_mix_" + n].rearrange("h o x -> (h o x)"))))
        return w, l

    def units(w):
        at = list(range(0, TYPES * D, 512))
        return [(w and [w["rel"][:, k, a:min(a + 512, TYPES * D)] for k in range(KB)], min(512, TYPES * D - a)) for a in at]

    def post(v, own, hand_over, b, grp):
        heads = b["xn_s"][:].rearrange("p j (h x) -> p (j h) x", x=32)
        hand_over(center_heads(v, own, heads, b, 31.0, 0.0))
        own(v.tensor_scalar(b["hm"][:], b["hand_out"], 1e-5, None, ALU.add))
        own(v.reciprocal(b["hm"][:], b["hm"][:]))
        own(v.tensor_tensor(heads, heads, col_of(b["hm"][:], 32), ALU.mult))
        own(v.tensor_tensor(b["val"][:], b["xn_s"][:], row_of(b["vln_weight"][:], GT), ALU.mult))
        own(v.tensor_tensor(b["val"][:], b["val"][:], row_of(b["vln_bias"][:], GT), ALU.add))
        own(v.tensor_tensor(b["xn_s"][:], b["xn_s"][:], row_of(b["kln_weight"][:], GT), ALU.mult))
        return v.tensor_tensor(b["xn_s"][:], b["xn_s"][:], row_of(b["kln_bias"][:], GT), ALU.add)

    def stores(sp, b, i, sem=None):
        if sp is not None:
            sp.dma_start(dram["rel_table"].rearrange("(t r s) d -> r t (s d)", r=R, s=TYPES)[:, bass.ds(i * GT, GT)], b["st"][:]).then_inc(sem, 16)
        return 1

    def kv(t, kv_p, b):
        for j in range(GT):
            for k in range(KB):
                cs = slice(k * 128, (k + 1) * 128)
                last = t.matmul(kv_p[:, k, 0:128], b["xn_s"][:, j, cs], b["val"][:, j, cs], start=False, stop=False, skip_group_check=True)
        return last

    build_open(nc, c, 1, m["X"], m["XN"], m["XNT"], loads, units, post, stores, kv, keep_blocks(c, 1.0 / NODES, m["KV"]), CENTER_STEPS + 6, hand=(ACT.Sqrt,), clear=dram["acc"])


def open2(nc, c, m, I, dram):
    def loads(sb):
        w = {"low": sb("low", [R, GT, D]), "exp": sb("exp", [R, GT, D]), "scaled": sb("scaled", [R, GT, D])}
        w["hand_in"], w["hand_out"] = w["low"][:], w["exp"][:]
        return w, []

    def units(w):
        return [([m["WT"][:, k, D:3 * D] for k in range(KB)], 512)]

    def post(v, own, hand_over, b, grp):
        own(v.tensor_tensor(b["scaled"][:], b["xn_s"][:], col_of(m["dinv"][:, grp], D), ALU.mult))
        hand_over(v.tensor_scalar(b["low"][:], b["st"][:, :, 0:D], 0.0, None, ALU.min))
        own(v.tensor_scalar(b["low"][:], b["st"][:, :, 0:D], 0.0, None, ALU.max))
        return v.tensor_tensor(b["low"][:], b["low"][:], b["exp"][:], ALU.add)

    def stores(sp, b, i, sem=None):
        if sp is not None:
            sp.dma_start(by_tile(dram["el"])[:, bass.ds(i * GT, GT)], b["scaled"][:]).then_inc(sem, 16)
        return 1

    def kv(t, kv_p, b):
        for j in range(GT):
            for k in range(KB):
                key = b["low"][:, j, k * 128:(k + 1) * 128]
                t.matmul(kv_p[:, k, 0:128], key, b["st"][:, j, D + k * 128:D + (k + 1) * 128], start=False, stop=False, skip_group_check=True)
                last = t.matmul(kv_p[:, k, 128:129], key, c["ones"][0:R, 0:1], start=False, stop=False, skip_group_check=True)
        return last

    build_open(nc, c, 2, m["X"], m["XN"], m["XNT"], loads, units, post, stores, kv, keep_blocks(c, 1.0, m["KV"], ones=True), 2, hand=(ACT.Exp,), clear=dram["acc"])


def open3(nc, c, m, I, dram):
    def loads(sb):
        w = {"xk": sb("w_xk", [128, KB, 512]), "att_src": sb("att_src", [R, D]), "att_dst": sb("att_dst", [R, D]), "prod": sb("prod", [R, GT, D]),
             "most": sb("most", [R, D])}
        l = []
        for k in range(KB):
            l += [(w["xk"][:, k, 0:D], blocked(I["L3_gnn_W"], k)), (w["xk"][:, k, D:512], blocked(I["L3_mix_Wqkv"], k)[:, D:2 * D])]
        for n in ("att_src", "att_dst"):
            l.append((w[n][:], everywhere(I["L3_gnn_" + n].rearrange("h x -> (h x)"))))
        return w, l

    def units(w):
        return [(w and [w["xk"][:, k, :] for k in range(KB)], 512)]

    def post(v, own, hand_over, b, grp):
        for n in ("src", "dst"):
            own(v.tensor_tensor(b["prod"][:], b["st"][:, :, 0:D], row_of(b["att_" + n][:], GT), ALU.mult))
            own(v.tensor_reduce(m["a_" + n][:, grp, :], b["prod"][:].rearrange("p j (h x) -> p j h x", h=4), AX, ALU.add))
        own(v.tensor_reduce(b["most"][:], b["st"][:, :, D:512].rearrange("p j x -> p x j"), AX, ALU.max))
        return v.tensor_tensor(m["key_top"][:], m["key_top"][:], b["most"][:], ALU.max)

    def stores(sp, b, i, sem=None):
        if sp is not None:
            sp.dma_start(by_tile(dram["el"])[:, bass.ds(i * GT, GT)], b["st"][:, :, 0:D]).then_inc(sem, 16)
        return 1

    build_open(nc, c, 3, m["X"], m["XN"], m["XNT"], loads, units, post, stores, None, None, 5, clear=dram["acc4"])


def build_score0(nc, c, e, src, dst, dram, attn, score, top):
    with ExitStack() as ctx:
        sb = lambda n, sh, d=F32: ctx.enter_context(nc.sbuf_tensor(f"score0_{n}", sh, d))
        ps = lambda n, sh: ctx.enter_context(nc.psum_tensor(f"score0_{n}", sh, F32))
        per_lane = lambda n, sh, d=F32: [sb(f"{n}{l}", sh, d) for l in range(LANES)]
        ends = ("src", "dst")
        idx = {n: per_lane(f"idx_{n}", [R, G], I32) for n in ends}
        rows = {n: per_lane(f"rows_{n}", [R, G, D]) for n in ends}
        ids, sc, att = per_lane("ids", [R, G * R], I16), per_lane("sc", [R, G, 1]), sb("att", [R, D])
        names = [f"{n}{l}" for n in ("idx_in", "rows_in") for l in range(LANES)] + ["loaded", "pool_passed", "sp_passed", "kept", "passed"]
        with phase(nc, "score0", *names, *Tops.names) as s, nc.Block() as block:
            tops = Tops(nc, c, e, s, sb, ps, ids, sc, top, 1)

            @block.sync
            def _(sp):
                sp.dma_start(att[:], everywhere(attn)).then_inc(s["loaded"], 16)

                def loads(i, first=False):
                    for l in range(LANES):
                        if not first:
                            sp.wait_ge(s[f"rows_in{l}"], i * (2 * 16 * G))
                            sp.sem_inc(s["sp_passed"], 1)
                        for n, frm in (("src", src), ("dst", dst)):
                            sp.dma_start(idx[n][l][:], frm[:, bass.ds(i * UNIT + l * G, G)]).then_inc(s[f"idx_in{l}"], 16)
                        if not first:
                            sp.wait_ge(s["ids_used"], i * LANES + l - LANES + 1)
                            sp.sem_inc(s["sp_passed"], 1)
                        sp.dma_start(ids[l][:], spread(dram["dst_ids"], i, l)).then_inc(s[f"ids_in{l}"], 16)
                loads(0, first=True)
                with sp.Fori(1, TURNS) as i:
                    loads(i)

            @block.gpsimd
            def _(pool):
                def gather(i, first=False):
                    for l in range(LANES):
                        pool.wait_ge(s[f"idx_in{l}"], i * 32 + 32)
                        if not first:
                            pool.wait_ge(s["scores_ready"], i * LANES + l - LANES + 1)
                        pool.sem_inc(s["pool_passed"], 1)
                        for g in range(G):
                            for n, table in (("src", dram["el"]), ("dst", dram["er"])):
                                nc.gpsimd.indirect_dma_start(rows[n][l][:, g, :], None, table, bass.IndirectOffsetOnAxis(ap=idx[n][l][:, g:g + 1], axis=0)
                                                             ).then_inc(s[f"rows_in{l}"], 16)
                gather(0, first=True)
                with pool.Fori(1, TURNS) as i:
                    gather(i)

            @block.vector
            def _(dve):
                v = nc.vector
                dve.wait_ge(s["loaded"], 16)

                def make(own, i, l):
                    a, b = rows["src"][l], rows["dst"][l]
                    dve.wait_ge(s[f"rows_in{l}"], i * (2 * 16 * G) + 2 * 16 * G)
                    own(v.tensor_tensor(a[:], a[:], b[:], ALU.add))
                    own(v.scalar_tensor_tensor(flat(b[:]), flat(a[:]), 0.2, flat(a[:]), ALU.mult, ALU.max))
                    dve.wait_ge(s["kept"], i * LANES + l + 1)
                    dve.sem_inc(s["passed"], 1)
                    for g in range(G):
                        last = v.tensor_tensor_reduce(a[:, g, :], b[:, g, :], att[:], 1.0, 0.0, ALU.mult, ALU.add, sc[l][:, g, :])
                    last.then_inc(s["scores_ready"], 1)

                tops.run_vector(dve, v, make, 2)

            @block.scalar
            def _(act):
                act.sem_inc(s["kept"], LANES)
                with act.Fori(0, TURNS) as i:
                    for l in range(LANES):
                        tops.find_places(act, nc.scalar, i, l)
                        act.wait_ge(s["scores_ready"], i * LANES + l + 1)
                        nc.scalar.copy(score[:, bass.ds(i * UNIT + l * G, G), :], sc[l][:]).then_inc(s["kept"], 1)

            @block.tensor
            def _(pe):
                tops.run_tensor(pe, nc.tensor)


def columns(vec, p=128):
    return vec.rearrange("(k p) -> p k", p=p)


def heads_product(nc, to, features, kv, small=None):
    for j in range(GT):
        for k in range(KB):
            f = features[:, k, j * R:(j + 1) * R]
            last = nc.tensor.matmul(to[:, j, k * 128:(k + 1) * 128], f, kv[:, k, 0:128], start=True, stop=True)
            if small is not None:
                last = nc.tensor.matmul(small[:, j, k * 4:(k + 1) * 4], f, kv[:, k, 128:132], start=True, stop=True)
    return last


def sum_accumulators(v, own, b):
    a = b["acc"]
    own(v.tensor_tensor(a[:, 0:2], a[:, 0:2], a[:, 2:4], ALU.add))
    own(v.tensor_tensor(a[:, 0], a[:, 0], a[:, 1], ALU.add))
    return a[:, 0]


def load_accumulators(sp, acc, b, i, sem, extra=()):
    for k in range(ACCS):
        sp.dma_start(b["acc"][:, k], by_tile(acc[k][0:NODES])[:, bass.ds(i * GT, GT)]).then_inc(sem, 16)
    for to, frm in extra:
        sp.dma_start(to[:], by_tile(frm)[:, bass.ds(i * GT, GT)]).then_inc(sem, 16)


def close0(nc, c, m, I, acc):
    tag = "close0"
    with ExitStack() as ctx:
        sb = lambda n, sh, d=F32: ctx.enter_context(nc.sbuf_tensor(f"{tag}_{n}", sh, d))
        ps = lambda n, sh: ctx.enter_context(nc.psum_tensor(f"{tag}_{n}", sh, F32))
        b = {"acc": sb("acc", [R, ACCS, GT, D + 1]), "t": sb("t", [R, GT, D]), "z": sb("z", [R, GT])}
        wq, w1, w2 = sb("wq", [128, KB, D]), sb("w1", [128, KB, D]), sb("w2", [128, KB, D])
        bq, b1, b2 = sb("bq", [128, KB]), sb("b1", [128, KB]), sb("b2", [R, D])
        qT, rT, hT, ret = sb("qT", [128, KB, GN]), sb("rT", [128, KB, GN]), sb("hT", [128, KB, GN]), sb("ret", [R, GT, D])
        wide, fb = ps("wide", [128, 1536]), [ps(f"fb{n}", [128, 1024]) for n in range(2)]
        rows = wide[0:R, 0:GT * D].rearrange("p (j x) -> p j x", j=GT)
        loads = [(b1[:], columns(I["L0_mix_b1"])), (b2[:], everywhere(I["L0_mix_b2"]))]
        for k in range(KB):
            loads += [(wq[:, k, :].rearrange("p (h x) -> p h x", x=32), blocked(I["L0_mix_w_qkv"], k).rearrange("p (h x) -> p h x", x=96)[:, :, 0:32]),
                      (w1[:, k, :], blocked(I["L0_mix_w1"], k)), (w2[:, k, :], blocked(I["L0_mix_w2"], k))]
            for h in range(4):
                at = (k * 4 + h) * 96
                loads.append((bq[h * 32:(h + 1) * 32, k:k + 1], I["L0_mix_b_qkv"][at:at + 32].unsqueeze(1)))
        with phase(nc, tag, "loaded", "acc_in", "sp_passed", "pe", "dve", "act", "chain") as s, nc.Block() as block:
            PE = Steps(s["pe"], ["q0", "q1", "mix", "turn", "h0", "h1", "y"])
            DV = Steps(s["dve"], ["acc_used", "ret", "y"])
            AC = Steps(s["act"], ["q0", "q1", "turn", "h0", "h1"])

            @block.sync
            def _(sp):
                for to, frm in loads:
                    sp.dma_start(to, frm).then_inc(s["loaded"], 16)
                with sp.Fori(0, GROUPS) as i:
                    load_accumulators(sp, acc, b, i, s["acc_in"])
                    until(sp, DV, "acc_used", i)
                    sp.sem_inc(s["sp_passed"], 1)

            @block.tensor
            def _(pe):
                pe.wait_ge(s["loaded"], 16 * len(loads))
                with pe.Fori(0, GROUPS) as i:
                    xt = [m["XNT"][:, k, bass.ds(i * GN, GN)] for k in range(KB)]
                    for g in range(KB):
                        mark(product_t(nc, fb[g], 128, [(wq[:, k, g * 128:(g + 1) * 128], xt[k]) for k in range(KB)]), PE)
                    until(pe, AC, "q1", i)
                    mark(heads_product(nc, rows, qT, m["KV"]), PE)
                    until(pe, DV, "ret", i)
                    mark(turn_tiles(nc, c, wide, ret), PE)
                    until(pe, AC, "turn", i)
                    for g in range(KB):
                        mark(product_t(nc, fb[g], 128, [(w1[:, k, g * 128:(g + 1) * 128], rT[:, k, :]) for k in range(KB)]), PE)
                    until(pe, AC, "h1", i)
                    mark(product_rows(nc, rows, [(hT[:, k, :], w2[:, k, :]) for k in range(KB)]), PE)
                    until(pe, DV, "y", i)

            @block.scalar
            def _(act):
                a = nc.scalar
                act.wait_ge(s["loaded"], 16 * len(loads))
                with act.Fori(0, GROUPS) as i:
                    for g in range(KB):
                        until(act, PE, f"q{g}", i)
                        mark(a.activation(dense(qT[:, g, :]), slices(fb[g]), ACT.Identity, bias=bq[:, g:g + 1]), AC)
                    until(act, PE, "turn", i)
                    mark(a.copy(rT[:].rearrange("p k (j x) -> p (k j) x", x=R), turned(wide[:])), AC)
                    for g in range(KB):
                        until(act, PE, f"h{g}", i)
                        mark(a.activation(dense(hT[:, g, :]), slices(fb[g]), ACT.Gelu, bias=b1[:, g:g + 1]), AC)

            @block.vector
            def _(dve):
                v = nc.vector
                dve.wait_ge(s["loaded"], 16 * len(loads))
                with dve.Fori(0, GROUPS) as i:
                    own = Chain(dve, s["chain"], i, 7)
                    x, xn = m["X"][:, bass.ds(i * GT, GT), :], m["XN"][:, bass.ds(i * GT, GT), :]
                    dve.wait_ge(s["acc_in"], i * (16 * ACCS) + 16 * ACCS)
                    a = sum_accumulators(v, own, b)
                    own(v.tensor_scalar(b["z"][:], a[:, :, D], 0.5, None, ALU.max))
                    own(v.reciprocal(b["z"][:], b["z"][:]))
                    own(v.tensor_tensor(b["t"][:], a[:, :, 0:D], col_of(b["z"][:], D), ALU.mult))
                    own(v.tensor_tensor(b["t"][:], b["t"][:], xn, ALU.add))
                    mark(v.tensor_tensor(x, x, b["t"][:], ALU.add), DV)
                    until(dve, PE, "mix", i)
                    mark(v.tensor_tensor(ret[:], rows, xn, ALU.add), DV)
                    until(dve, PE, "y", i)
                    until(dve, DV, "ret", i)
                    own(v.tensor_tensor(b["t"][:], rows, row_of(b2[:], GT), ALU.add))
                    mark(v.tensor_tensor(x, x, b["t"][:], ALU.add), DV)
                    until(dve, DV, "y", i)
                    own.end()


def close1(nc, c, m, acc):
    tag = "close1"
    with ExitStack() as ctx:
        sb = lambda n, sh, d=F32: ctx.enter_context(nc.sbuf_tensor(f"{tag}_{n}", sh, d))
        b = {"acc": sb("acc", [R, ACCS, GT, D + 1]), "t": sb("t", [R, GT, D])}
        xT = sb("xT", [128, KB, GN])
        wide = ctx.enter_context(nc.psum_tensor(f"{tag}_wide", [128, 1536], F32))
        rows = wide[0:R, 0:GT * D].rearrange("p (j x) -> p j x", j=GT)
        with phase(nc, tag, "acc_in", "sp_passed", "pe", "dve", "act", "chain") as s, nc.Block() as block:
            PE, DV, AC = Steps(s["pe"], ["mix"]), Steps(s["dve"], ["acc_used", "x"]), Steps(s["act"], ["x"])

            @block.sync
            def _(sp):
                with sp.Fori(0, GROUPS) as i:
                    load_accumulators(sp, acc, b, i, s["acc_in"])
                    until(sp, DV, "acc_used", i)
                    sp.sem_inc(s["sp_passed"], 1)

            @block.tensor
            def _(pe):
                with pe.Fori(0, GROUPS) as i:
                    until(pe, AC, "x", i)
                    mark(heads_product(nc, rows, xT, m["KV"]), PE)
                    until(pe, DV, "x", i)

            @block.scalar
            def _(act):
                with act.Fori(0, GROUPS) as i:
                    mark(nc.scalar.copy(xT[:], m["XNT"][:, :, bass.ds(i * GN, GN)]), AC)
                    until(act, PE, "mix", i)

            @block.vector
            def _(dve):
                v = nc.vector
                with dve.Fori(0, GROUPS) as i:
                    own = Chain(dve, s["chain"], i, 3)
                    x, xn = m["X"][:, bass.ds(i * GT, GT), :], m["XN"][:, bass.ds(i * GT, GT), :]
                    dve.wait_ge(s["acc_in"], i * (16 * ACCS) + 16 * ACCS)
                    a = sum_accumulators(v, own, b)
                    own(v.tensor_tensor(x, x, xn, ALU.add))
                    mark(v.tensor_tensor(b["t"][:], a[:, :, 0:D], x, ALU.add), DV)
                    until(dve, DV, "acc_used", i)
                    until(dve, PE, "mix", i)
                    mark(v.tensor_tensor(x, rows, b["t"][:], ALU.add), DV)
                    until(dve, DV, "x", i)
                    own.end()


def build_experts(nc, tag, XT, target, experts, dims, weights, last_bias, gate, func, layer_bias, layer_scale=None, affine=None):
    L = len(dims) - 1
    blocks = [max(d // 128, 1) for d in dims]
    part = [min(d, 128) for d in dims]
    P = min(experts, 2)
    with ExitStack() as ctx:
        sb = lambda n, sh, d=F32: ctx.enter_context(nc.sbuf_tensor(f"{tag}_{n}", sh, d))
        ps = lambda n, sh: ctx.enter_context(nc.psum_tensor(f"{tag}_{n}", sh, F32))
        wt = [[sb(f"w{l}_{p}", [part[l], blocks[l], dims[l + 1]]) for l in range(L)] for p in range(P)]
        h = [sb(f"h{l}", [part[l], blocks[l], GN]) for l in range(1, L)]
        xe = sb("xe", [128, KB, GN]) if affine else None
        brow, t = sb("brow", [R, experts, D]), sb("t", [R, GT, D])
        wide, fb = ps("wide", [128, 1536]), [ps(f"fb{n}", [128, 1024]) for n in range(2)]
        rows = wide[0:R, 0:GT * D].rearrange("p (j x) -> p j x", j=GT)
        jobs = [(l, g) for l in range(L - 1) for g in range(blocks[l + 1])]
        names = [f"h{l}_{g}" for l, g in jobs]
        NL = sum(blocks[:L])
        with phase(nc, tag, "loaded", "w_in0", "w_in1", "pe", "dve", "act", "chain", "pe_passed", "sp_passed") as s, nc.Block() as block:
            PE = Steps(s["pe"], names + ["rows"])
            AC = Steps(s["act"], (["xe"] if affine else []) + names)
            DV = Steps(s["dve"], ["rows_used", "x"], before=1)

            def each_expert(eng, body):
                if experts <= 2:
                    for e in range(experts):
                        body(e, e, e * GROUPS)
                else:
                    with eng.Fori(0, experts // 2) as n:
                        for p in range(2):
                            body(n * 2 + p, p, (n * 2 + p) * GROUPS)

            @block.sync
            def _(sp):
                sp.dma_start(brow[:], last_bias).then_inc(s["loaded"], 16)

                def load(e, p, first):
                    if not first:
                        until(sp, DV, "x", (e - 1) * GROUPS - 1)
                        sp.sem_inc(s["sp_passed"], 1)
                    for l in range(L):
                        for k in range(blocks[l]):
                            sp.dma_start(wt[p][l][:, k, :], weights[l][bass.ds(e * dims[l] + k * 128, part[l])]).then_inc(s[f"w_in{p}"], 16)
                for p in range(P):
                    load(p, p, True)
                if experts > 2:
                    with sp.Fori(1, experts // 2) as n:
                        for p in range(2):
                            load(n * 2 + p, p, False)

            @block.tensor
            def _(pe):
                def body(e, p, before):
                    pe.wait_ge(s[f"w_in{p}"], (e - p) * (8 * NL) + 16 * NL)
                    pe.sem_inc(s["pe_passed"], 1)
                    with pe.Fori(0, GROUPS) as i:
                        turn = i + before
                        if affine:
                            until(pe, AC, "xe", turn)
                            src = [xe[:, k, :] for k in range(KB)]
                        else:
                            src = [XT[:, k, bass.ds(i * GN, GN)] for k in range(KB)]
                        for n, (l, g) in enumerate(jobs):
                            if n >= 2:
                                until(pe, AC, names[n - 2], turn)
                            if l >= 1 and g == 0:
                                until(pe, AC, names[n - 1], turn)
                            ins = src if l == 0 else [h[l - 1][:, k, :] for k in range(blocks[l])]
                            m_ = part[l + 1]
                            mark(product_t(nc, fb[n % 2], m_, [(wt[p][l][:, k, g * 128:g * 128 + m_], ins[k]) for k in range(blocks[l])]), PE)
                        until(pe, AC, names[-1], turn)
                        until(pe, DV, "x", turn - 1)
                        mark(product_rows(nc, rows, [(h[-1][:, k, :], wt[p][L - 1][:, k, :]) for k in range(blocks[L - 1])]), PE)

                each_expert(pe, body)

            @block.scalar
            def _(act):
                a = nc.scalar

                def body(e, p, before):
                    with act.Fori(0, GROUPS) as i:
                        turn = i + before
                        if affine:
                            for k in range(KB):
                                last = a.activation(xe[:, k, :], XT[:, k, bass.ds(i * GN, GN)], ACT.Identity, bias=affine[1][:, bass.ds(e * KB + k, 1)],
                                                    scale=affine[0][:, bass.ds(e * KB + k, 1)])
                            mark(last, AC)
                        for n, (l, g) in enumerate(jobs):
                            until(act, PE, names[n], turn)
                            at = bass.ds(e * blocks[l + 1] + g, 1)
                            scale = layer_scale[l][0:part[l + 1], at] if layer_scale else 1.0
                            mark(a.activation(dense(h[l][:, g, :]), slices(fb[n % 2][0:part[l + 1], :]), func,
                                              bias=layer_bias[l][0:part[l + 1], at], scale=scale), AC)
                each_expert(act, body)

            @block.vector
            def _(dve):
                v = nc.vector
                dve.wait_ge(s["loaded"], 16)
                dve.sem_inc(s["dve"], 1)

                def body(e, p, before):
                    with dve.Fori(0, GROUPS) as i:
                        turn = i + before
                        own = Chain(dve, s["chain"], turn, 1 if gate is not None else 0)
                        x = target[:, bass.ds(i * GT, GT), :]
                        until(dve, PE, "rows", turn)
                        v.tensor_tensor(t[:], rows, brow[:, bass.ds(e, 1), :].to_broadcast([R, GT, D]), ALU.add).then_inc(s["dve"], 1)
                        until(dve, DV, "rows_used", turn)
                        if gate is not None:
                            own(v.tensor_tensor(t[:], t[:], col_of(gate[:, bass.ds(e * TILES + i * GT, GT)], D), ALU.mult))
                        mark(v.tensor_tensor(x, x, t[:], ALU.add), DV)
                        until(dve, DV, "x", turn)
                        own.end()
                each_expert(dve, body)


def put_in(nc, tag, pairs, fill=()):
    with phase(nc, tag, "loaded") as s, nc.Block() as block:
        @block.sync
        def _(sp):
            for to, frm in pairs:
                sp.dma_start(to, frm).then_inc(s["loaded"], 16)
            if pairs:
                sp.wait_ge(s["loaded"], 16 * len(pairs))

        @block.vector
        def _(dve):
            for to, value in fill:
                nc.vector.memset(to, value)


def top_two(v, own, b, E, n_=GT):
    for n, src in ((1, "g"), (2, "g2")):
        own(v.tensor_reduce(b[f"v{n}"][:], b[src][:], AX, ALU.max))
        own(v.tensor_tensor(b[f"o{n}"][:], b[src][:], col_of(b[f"v{n}"][:], E), ALU.is_equal))
        own(v.tensor_tensor(b["k"][:], b[f"o{n}"][:], row_of(b["rev"][:, 0:E], n_), ALU.mult))
        own(v.tensor_reduce(b["k1"][:], b["k"][:], AX, ALU.max))
        own(v.tensor_tensor(b[f"o{n}"][:], b["k"][:], col_of(b["k1"][:], E), ALU.is_equal))
        if n == 1:
            own(v.scalar_tensor_tensor(b["g2"][:].rearrange("p j e -> p (j e)"), b["o1"][:].rearrange("p j e -> p (j e)"), -4.0,
                                       b["g"][:].rearrange("p j e -> p (j e)"), ALU.mult, ALU.add))


TOP_TWO_STEPS = 11


def gate_buffers(sb, E, n=GT):
    return ({k: sb(k, [R, n, E]) for k in ("g", "g2", "o1", "o2", "k", "ex")} | {k: sb(k, [R, n]) for k in ("v1", "v2", "k1", "r")}
            | {"rev": sb("rev", [R, 8])})


def build_gated_open(nc, c, layer, m, router, router_bias, E, mode):
    def loads(sb):
        w = gate_buffers(sb, E) | {"wr": sb("wr", [128, KB, E]), "br": sb("br", [R, E])}
        w["hand_in"], w["hand_out"] = w["g2"][:], w["ex"][:]
        return w, [(w["wr"][:, k, :], blocked(router, k)) for k in range(KB)] + [(w["br"][:], everywhere(router_bias))]

    def units(w):
        return [(w and [w["wr"][:, k, :] for k in range(KB)], E)]

    def post(v, own, hand_over, b, grp):
        own(v.tensor_scalar(b["rev"][:], c["iota"][0:R, 0:8], -1.0, 8.0, ALU.mult, ALU.add))
        own(v.tensor_tensor(b["g"][:], b["st"][:], row_of(b["br"][:], GT), ALU.add))
        own(v.tensor_reduce(b["r"][:], b["g"][:], AX, ALU.max))
        hand_over(v.tensor_tensor(b["g2"][:], b["g"][:], col_of(b["r"][:], E), ALU.subtract))
        own(v.tensor_reduce(b["r"][:], b["ex"][:], AX, ALU.add))
        own(v.reciprocal(b["r"][:], b["r"][:]))
        own(v.tensor_tensor(b["g"][:], b["ex"][:], col_of(b["r"][:], E), ALU.mult))
        out = m["gate"][:, 0:E * TILES].rearrange("p (e t) -> p t e", e=E)[:, grp, :]
        if mode == "all":
            return v.tensor_copy(out, b["g"][:])
        top_two(v, own, b, E)
        if mode == "top_ratio":
            own(v.tensor_tensor(b["r"][:], b["v1"][:], b["v2"][:], ALU.add))
        else:
            hand_over(v.tensor_tensor(b["g2"][:], b["g"][:], col_of(b["v1"][:], E), ALU.subtract))
            own(v.tensor_tensor(b["k"][:], b["o2"][:], b["ex"][:], ALU.mult))
            own(v.tensor_reduce(b["v2"][:], b["k"][:], AX, ALU.add))
            own(v.tensor_scalar(b["r"][:], b["v2"][:], 1.0, None, ALU.add))
            own(v.memset(b["v1"][:], 1.0))
        own(v.reciprocal(b["r"][:], b["r"][:]))
        own(v.tensor_tensor(b["v1"][:], b["v1"][:], b["r"][:], ALU.mult))
        own(v.tensor_tensor(b["v2"][:], b["v2"][:], b["r"][:], ALU.mult))
        own(v.tensor_tensor(b["o1"][:], b["o1"][:], col_of(b["v1"][:], E), ALU.mult))
        own(v.tensor_tensor(b["o2"][:], b["o2"][:], col_of(b["v2"][:], E), ALU.mult))
        return v.tensor_tensor(out, b["o1"][:], b["o2"][:], ALU.add)

    steps = {"all": 6, "top_ratio": 6 + TOP_TWO_STEPS + 6, "top_softmax": 6 + TOP_TWO_STEPS + 9}[mode]
    hand = (ACT.Exp,) * (2 if mode == "top_softmax" else 1)
    build_open(nc, c, f"{layer}g", m["X"], m["XN"], m["XNT"], loads, units, post, lambda sp, b, i, sem=None: 0, None, None, steps, hand=hand)


def experts0(nc, c, m, I):
    build_gated_open(nc, c, 0, m, I["L0_ffn_gW"], I["L0_ffn_gb"], 4, "top_softmax")
    with ExitStack() as ctx:
        sb = lambda n, sh, d=F32: ctx.enter_context(nc.sbuf_tensor(f"ffn0_{n}", sh, d))
        s1, s2, e1, e2 = sb("s1", [128, 2]), sb("s2", [128, 1]), sb("e1", [128, 4]), sb("e2", [64, 4])
        put_in(nc, "ffn0_in", [(s1[:], columns(I["L0_ffn_sb1"])), (s2[:], columns(I["L0_ffn_sb2"])),
                               (e1[:], I["L0_ffn_eb1"].rearrange("e p -> p e")), (e2[:], I["L0_ffn_eb2"].rearrange("e p -> p e"))])
        flat = lambda n: I[n].rearrange("e r o -> (e r) o")
        build_experts(nc, "ffn0s", m["XNT"], m["X"], 1, [256, 256, 128, 256], [I["L0_ffn_sW1"], I["L0_ffn_sW2"], I["L0_ffn_sW3"]],
                      everywhere(I["L0_ffn_sb3"]).unsqueeze(1), None, ACT.Relu, [s1, s2])
        build_experts(nc, "ffn0e", m["XNT"], m["X"], 4, [256, 128, 64, 256], [flat("L0_ffn_eW1"), flat("L0_ffn_eW2"), flat("L0_ffn_eW3")],
                      everywhere(I["L0_ffn_eb3"]), m["gate"], ACT.Relu, [e1, e2])


def experts1(nc, c, m, I):
    ENT = 8
    with ExitStack() as ctx:
        sb = lambda n, sh, d=F32: ctx.enter_context(nc.sbuf_tensor(f"ffn1_{n}", sh, d))
        mean, mean_b, wr, br = sb("mean", [128, KB]), sb("mean_b", [128, KB, R]), sb("wr", [128, KB, ENT]), sb("br", [R, ENT])
        b1 = sb("b1", [128, ENT * 4])

        def add_up(t, kv_p, b):
            for j in range(GT):
                for k in range(KB):
                    last = t.matmul(kv_p[:, k, 0:1], b["xn_s"][:, j, k * 128:(k + 1) * 128], c["ones"][0:R, 0:1], start=False, stop=False, skip_group_check=True)
            return last

        def to_mean(v, own, kv_p, b):
            own(v.tensor_scalar(mean[:], kv_p[:, :, 0], 1.0 / NODES, None, ALU.mult))
            own(v.tensor_copy(mean_b[:], col_of(mean[:], R)))

        build_open(nc, c, "1g", m["X"], m["XN"], m["XNT"], lambda sb: ({}, []), lambda w: [], lambda v, own, hand_over, b, grp: v.memset(b["st"][:], 0.0),
                   lambda sp, b, i, sem=None: 0, add_up, to_mean, 0)
        put_in(nc, "ffn1_in", [(wr[:, k, :], blocked(I["L1_ffn_Wr"], k)) for k in range(KB)] + [(br[:], everywhere(I["L1_ffn_br"]))]
               + [(b1[:, e * 4:(e + 1) * 4], columns(I["L1_ffn_b1"][e])) for e in range(ENT)])
        b = gate_buffers(lambda n, sh: sb("r_" + n, sh), ENT, 1)
        lp = ctx.enter_context(nc.psum_tensor("ffn1_logits", [R, 1, ENT], F32))
        with phase(nc, "route", "pe", "dve", "act", "chain") as s, nc.Block() as block:
            @block.tensor
            def _(pe):
                for k in range(KB):
                    last = nc.tensor.matmul(lp[:, 0, :], mean_b[:, k, :], wr[:, k, :], start=(k == 0), stop=(k == KB - 1))
                last.then_inc(s["pe"], 1)

            @block.scalar
            def _(act):
                for n in range(3):
                    act.wait_ge(s["dve"], n + 1)
                    nc.scalar.activation(b["ex"][:], b["g2"][:], ACT.Exp).then_inc(s["act"], 1)

            @block.vector
            def _(dve):
                v = nc.vector
                own = Chain(dve, s["chain"])
                capacity = float(-(-NODES * 5 // (4 * ENT)))
                exps = iter(range(1, 4))

                def exp(ins):
                    ins.then_inc(s["dve"], 1)
                    dve.wait_ge(s["act"], next(exps))

                def softmax():
                    own(v.tensor_reduce(b["r"][:], b["g"][:], AX, ALU.max))
                    exp(v.tensor_tensor(b["g2"][:], b["g"][:], col_of(b["r"][:], ENT), ALU.subtract))
                    own(v.tensor_reduce(b["r"][:], b["ex"][:], AX, ALU.add))
                    own(v.reciprocal(b["r"][:], b["r"][:]))
                    own(v.tensor_tensor(b["g"][:], b["ex"][:], col_of(b["r"][:], ENT), ALU.mult))

                own(v.tensor_scalar(b["rev"][:], c["iota"][0:R, 0:8], -1.0, 8.0, ALU.mult, ALU.add))
                dve.wait_ge(s["pe"], 1)
                own(v.tensor_tensor(b["g"][:], lp[:], row_of(br[:], 1), ALU.add))
                softmax()
                own(v.tensor_scalar(b["k"][:], b["g"][:], float(NODES), capacity, ALU.mult, ALU.max))
                own(v.reciprocal(b["k"][:], b["k"][:]))
                own(v.tensor_scalar(b["k"][:], b["k"][:], capacity, None, ALU.mult))
                own(v.tensor_tensor(b["g"][:], b["g"][:], b["k"][:], ALU.mult))
                softmax()
                top_two(v, own, b, ENT, 1)
                exp(v.tensor_tensor(b["g2"][:], b["g"][:], col_of(b["v1"][:], ENT), ALU.subtract))
                own(v.tensor_tensor(b["k"][:], b["o2"][:], b["ex"][:], ALU.mult))
                own(v.tensor_reduce(b["r"][:], b["k"][:], AX, ALU.add))
                own(v.tensor_scalar(b["r"][:], b["r"][:], 1.0, None, ALU.add))
                own(v.reciprocal(b["r"][:], b["r"][:]))
                own(v.tensor_tensor(b["k"][:], b["k"][:], b["o1"][:], ALU.add))
                own(v.tensor_tensor(b["k"][:], b["k"][:], col_of(b["r"][:], ENT), ALU.mult))
                own(v.tensor_copy(m["gate"][:].rearrange("p (e t) -> p e t", e=ENT), col_of(b["k"][:, 0, :], TILES)))
        flat = lambda n: I[n].rearrange("e r o -> (e r) o")
        build_experts(nc, "ffn1e", m["XNT"], m["XN"], ENT, [256, 512, 256], [flat("L1_ffn_W1"), flat("L1_ffn_W2")],
                      everywhere(I["L1_ffn_b2"]), m["gate"], ACT.Gelu, [b1])
    with ExitStack() as ctx:
        sb = lambda n, sh, d=F32: ctx.enter_context(nc.sbuf_tensor(f"norm1_{n}", sh, d))
        b = norm_buffers(sb)
        t, gamma, beta = sb("t", [R, GT, D]), sb("gamma", [R, D]), sb("beta", [R, D])
        put_in(nc, "norm1_in", [(gamma[:], everywhere(I["L1_ffn_gamma"])), (beta[:], everywhere(I["L1_ffn_beta"]))])
        with phase(nc, "norm1", "dve", "act", "chain", "passed") as s, nc.Block() as block:
            DV, AC = Steps(s["dve"], ["var", "x"]), Steps(s["act"], ["std"])

            @block.vector
            def _(dve):
                v = nc.vector
                with dve.Fori(0, GROUPS) as i:
                    own = Chain(dve, s["chain"], i, VARIANCE_STEPS + STANDARDIZE_STEPS + 3)
                    x, y = m["X"][:, bass.ds(i * GT, GT), :], m["XN"][:, bass.ds(i * GT, GT), :]
                    mark(variance(v, own, y, b, 1e-5, s["passed"]), DV)
                    until(dve, AC, "std", i)
                    own(standardize(v, own, y, t, b))
                    own(v.tensor_tensor(t[:], t[:], row_of(gamma[:], GT), ALU.mult))
                    own(v.tensor_tensor(t[:], t[:], row_of(beta[:], GT), ALU.add))
                    mark(v.tensor_tensor(x, x, t[:], ALU.add), DV)
                    until(dve, DV, "x", i)
                    own.end()

            @block.scalar
            def _(act):
                with act.Fori(0, GROUPS) as i:
                    until(act, DV, "var", i)
                    mark(nc.scalar.activation(b["std"][:], b["var"][:], ACT.Sqrt), AC)


def build_transposed(nc, c, tag, parts, out):
    n = sum(w.shape[0] for w in parts) // 128
    with ExitStack() as ctx:
        w = ctx.enter_context(nc.sbuf_tensor(f"{tag}_w", [128, n, D], F32))
        tp = [ctx.enter_context(nc.psum_tensor(f"{tag}_p{q}", [128, KB, 128], F32)) for q in range(2)]
        with phase(nc, tag, "loaded", "pe", "act") as s, nc.Block() as block:
            @block.sync
            def _(sp):
                at = 0
                for part in parts:
                    k = part.shape[0] // 128
                    sp.dma_start(w[:, at:at + k, :], part.rearrange("(b p) x -> p b x", p=128)).then_inc(s["loaded"], 16)
                    at += k

            @block.tensor
            def _(pe):
                pe.wait_ge(s["loaded"], 16 * len(parts))
                for b in range(n):
                    if b >= 2:
                        pe.wait_ge(s["act"], b - 1)
                    for k in range(KB):
                        last = nc.tensor.transpose(tp[b % 2][:, k, :], w[:, b, k * 128:(k + 1) * 128], c["ident"][:])
                    last.then_inc(s["pe"], 1)

            @block.scalar
            def _(act):
                for b in range(n):
                    act.wait_ge(s["pe"], b + 1)
                    nc.scalar.copy(out[:, :, b * 128:(b + 1) * 128], tp[b % 2][:]).then_inc(s["act"], 1)


def close2(nc, c, m, I, acc):
    tag = "close2"
    with ExitStack() as ctx:
        sb = lambda n, sh, d=F32: ctx.enter_context(nc.sbuf_tensor(f"{tag}_{n}", sh, d))
        ps = lambda n, sh: ctx.enter_context(nc.psum_tensor(f"{tag}_{n}", sh, F32))
        b = {"acc": sb("acc", [R, ACCS, GT, D + 1]), "t": sb("t", [R, GT, D]), "u": sb("u", [R, GT, D]), "z": sb("z", [R, GT, 8])} | norm_buffers(sb)
        w = sb("w", [128, KB, D])
        rowv = {n: sb(n, [R, D]) for n in ("bias", "gamma", "beta", "ln1_g", "ln1_b", "b2", "ln2_g", "ln2_b")}
        b1 = sb("b1", [128, KB])
        aT, qT, hT, low, ex = [sb(n, [128, KB, GN]) for n in ("aT", "qT", "hT", "low", "ex")]
        wide, fb = ps("wide", [128, 1536]), [ps(f"fb{n}", [128, 1024]) for n in range(2)]
        small = ps("small", [R, GT, 8])
        rows = wide[0:R, 0:GT * D].rearrange("p (j x) -> p j x", j=GT)
        loads = [(w[:, k, :], blocked(I["L2_gnn_W"], k)) for k in range(KB)] + [(b1[:], columns(I["L2_mix_b1"]))]
        loads += [(rowv[n][:], everywhere(I[("L2_gnn_" if n in ("bias", "gamma", "beta") else "L2_mix_") + n])) for n in rowv]
        W1, W2 = 3 * D, 4 * D
        with phase(nc, tag, "loaded", "acc_in", "sp_passed", "pe", "dve", "act", "chain", "passed") as s, nc.Block() as block:
            PE = Steps(s["pe"], ["agg", "gcn", "q0", "q1", "mix", "x1", "h0", "h1", "y"])
            DV = Steps(s["dve"], ["agg", "gcn_var", "gcn_x", "low0", "low1", "q0", "q1", "x1_var", "x1", "y_var", "x"])
            AC = Steps(s["act"], ["agg", "gcn_std", "ex0", "ex1", "x1_std", "x1", "h0", "h1", "y_std"])

            @block.sync
            def _(sp):
                for to, frm in loads:
                    sp.dma_start(to, frm).then_inc(s["loaded"], 16)
                with sp.Fori(0, GROUPS) as i:
                    load_accumulators(sp, acc, b, i, s["acc_in"])
                    until(sp, DV, "agg", i)
                    sp.sem_inc(s["sp_passed"], 1)

            @block.tensor
            def _(pe):
                pe.wait_ge(s["loaded"], 16 * len(loads))
                with pe.Fori(0, GROUPS) as i:
                    xt = [m["XNT"][:, k, bass.ds(i * GN, GN)] for k in range(KB)]
                    until(pe, DV, "agg", i)
                    mark(turn_tiles(nc, c, wide, b["t"]), PE)
                    until(pe, AC, "agg", i)
                    mark(product_rows(nc, rows, [(aT[:, k, :], w[:, k, :]) for k in range(KB)]), PE)
                    for g in range(KB):
                        mark(product_t(nc, fb[g], 128, [(m["WT"][:, k, g * 128:(g + 1) * 128], xt[k]) for k in range(KB)]), PE)
                    until(pe, DV, "q1", i)
                    until(pe, DV, "gcn_x", i)
                    mark(heads_product(nc, rows, qT, m["KV"], small), PE)
                    until(pe, DV, "x1", i)
                    mark(turn_tiles(nc, c, wide, b["u"]), PE)
                    until(pe, AC, "x1", i)
                    for g in range(KB):
                        mark(product_t(nc, fb[g], 128, [(m["WT"][:, k, W1 + g * 128:W1 + (g + 1) * 128], aT[:, k, :]) for k in range(KB)]), PE)
                    until(pe, AC, "h1", i)
                    mark(product_rows(nc, rows, [(hT[:, k, :], m["WT"][:, k, W2:W2 + D]) for k in range(KB)]), PE)
                    until(pe, DV, "x", i)

            @block.scalar
            def _(act):
                a = nc.scalar
                act.wait_ge(s["loaded"], 16 * len(loads))

                def std(name, i):
                    until(act, DV, name + "_var", i)
                    mark(a.activation(b["std"][:], b["var"][:], ACT.Sqrt), AC)

                def turn(name, i):
                    until(act, PE, name, i)
                    mark(a.copy(aT[:].rearrange("p k (j x) -> p (k j) x", x=R), turned(wide[:])), AC)

                with act.Fori(0, GROUPS) as i:
                    turn("agg", i)
                    std("gcn", i)
                    for g in range(KB):
                        until(act, DV, f"low{g}", i)
                        mark(a.activation(ex[:, g, :], low[:, g, :], ACT.Exp), AC)
                    std("x1", i)
                    turn("x1", i)
                    for g in range(KB):
                        until(act, PE, f"h{g}", i)
                        mark(a.activation(dense(hT[:, g, :]), slices(fb[g]), ACT.Gelu, bias=b1[:, g:g + 1]), AC)
                    std("y", i)

            @block.vector
            def _(dve):
                v = nc.vector
                dve.wait_ge(s["loaded"], 16 * len(loads))
                with dve.Fori(0, GROUPS) as i:
                    own = Chain(dve, s["chain"], i, 29)
                    grp = bass.ds(i * GT, GT)
                    x, xn = m["X"][:, grp, :], m["XN"][:, grp, :]
                    t, u = b["t"][:], b["u"][:]

                    def norm(name, src, gain, shift):
                        mark(variance(v, own, src, b, 1e-5, s["passed"]), DV)
                        until(dve, AC, name + "_std", i)
                        own(standardize(v, own, src, src, b))
                        own(v.tensor_tensor(src, src, row_of(rowv[gain][:], GT), ALU.mult))
                        return v.tensor_tensor(src, src, row_of(rowv[shift][:], GT), ALU.add)

                    dve.wait_ge(s["acc_in"], i * (16 * ACCS) + 16 * ACCS)
                    a = sum_accumulators(v, own, b)
                    own(v.tensor_tensor(u, xn, col_of(m["dinv"][:, grp], D), ALU.mult))
                    own(v.tensor_tensor(u, u, a[:, :, 0:D], ALU.add))
                    mark(v.tensor_tensor(t, u, col_of(m["dinv"][:, grp], D), ALU.mult), DV)
                    until(dve, PE, "gcn", i)
                    own(v.tensor_tensor(u, rows, row_of(rowv["bias"][:], GT), ALU.add))
                    own(v.tensor_tensor(u, u, xn, ALU.add))
                    own(norm("gcn", u, "gamma", "beta"))
                    mark(v.tensor_tensor(x, x, u, ALU.add), DV)
                    for g in range(KB):
                        until(dve, PE, f"q{g}", i)
                        mark(v.tensor_scalar(dense(low[:, g, :]), slices(fb[g]), 0.0, None, ALU.min), DV)
                    for g in range(KB):
                        until(dve, AC, f"ex{g}", i)
                        mark(v.scalar_tensor_tensor(dense(qT[:, g, :]), slices(fb[g]), 0.0, dense(ex[:, g, :]), ALU.max, ALU.add), DV)
                    until(dve, PE, "mix", i)
                    own(v.tensor_scalar(b["z"][:], small[:], 1e-6, None, ALU.add))
                    own(v.reciprocal(b["z"][:], b["z"][:]))
                    u4 = u.rearrange("p j (h x) -> p j h x", x=32)
                    own(v.tensor_tensor(u4, rows.rearrange("p j (h x) -> p j h x", x=32), b["z"][:].unsqueeze(3).to_broadcast([R, GT, 8, 32]), ALU.mult))
                    own(v.tensor_tensor(u, u, xn, ALU.add))
                    mark(norm("x1", u, "ln1_g", "ln1_b"), DV)
                    until(dve, PE, "y", i)
                    own(v.tensor_tensor(t, rows, row_of(rowv["b2"][:], GT), ALU.add))
                    own(v.tensor_tensor(t, t, u, ALU.add))
                    own(norm("y", t, "ln2_g", "ln2_b"))
                    mark(v.tensor_tensor(x, x, t, ALU.add), DV)
                    until(dve, DV, "x", i)
                    own.end()


def build_key_sums(nc, c, m, wkv):
    tag = "keys3"
    with ExitStack() as ctx:
        sb = lambda n, sh, d=F32: ctx.enter_context(nc.sbuf_tensor(f"{tag}_{n}", sh, d))
        ps = lambda n, sh: ctx.enter_context(nc.psum_tensor(f"{tag}_{n}", sh, F32))
        w, xT, st = sb("w", [128, KB, 512]), sb("xT", [128, KB, GN]), sb("st", [R, GT, 512])
        topc, diag, topr, inv = sb("topc", [128, KB]), sb("diag", [128, KB, 128]), sb("topr", [R, D]), sb("inv", [128, KB])
        tp, unit_p, kv_p = ps("tp", [128, KB, 128]), [ps(f"unit{n}", [R, 512]) for n in range(4)], ps("kv_p", [128, KB, 256])
        with phase(nc, tag, "loaded", "pe0", "dve0", "pe", "dve", "act", "chain") as s, nc.Block() as block:
            UNITS = [f"u{j}" for j in range(GT)]
            PE, DV = Steps(s["pe"], UNITS + ["kv"]), Steps(s["dve"], ["low"])
            AC = Steps(s["act"], ["x"] + UNITS + ["exp"])

            @block.sync
            def _(sp):
                for k in range(KB):
                    sp.dma_start(w[:, k, :], blocked(wkv, k)[:, D:3 * D]).then_inc(s["loaded"], 16)

            @block.tensor
            def _(pe):
                t = nc.tensor
                for k in range(KB):
                    last = t.transpose(tp[:, k, 0:R], m["key_top"][:, k * 128:(k + 1) * 128], c["ident"][0:R, 0:R])
                last.then_inc(s["pe0"], 1)
                pe.wait_ge(s["dve0"], 1)
                for k in range(KB):
                    last = t.matmul(tp[0:R, k, :], c["ones"][:, 0:R], diag[:, k, :], start=True, stop=True)
                last.then_inc(s["pe0"], 1)
                for k in range(KB):
                    t.matmul(kv_p[:, k, :], c["zeros"][:, 0:128], c["zeros"][:, 0:256], start=(k == 0), stop=False, skip_group_check=True)
                pe.wait_ge(s["loaded"], 16 * KB)
                with pe.Fori(0, GROUPS) as i:
                    until(pe, AC, "x", i)
                    for j, name in enumerate(UNITS):
                        if j >= 4:
                            until(pe, AC, UNITS[j - 4], i)
                        for k in range(KB):
                            last = t.matmul(unit_p[j % 4][:], xT[:, k, j * R:(j + 1) * R], w[:, k, :], start=(k == 0), stop=(k == KB - 1))
                        mark(last, PE)
                    until(pe, AC, "exp", i)
                    for j in range(GT):
                        for k in range(KB):
                            key = st[:, j, k * 128:(k + 1) * 128]
                            t.matmul(kv_p[:, k, 0:128], key, st[:, j, D + k * 128:D + (k + 1) * 128], start=False, stop=False, skip_group_check=True)
                            last = t.matmul(kv_p[:, k, 128:129], key, c["ones"][0:R, 0:1], start=False, stop=False, skip_group_check=True)
                    mark(last, PE)
                for k in range(KB):
                    last = t.matmul(kv_p[:, k, :], c["zeros"][:, 0:128], c["zeros"][:, 0:256], start=False, stop=True, skip_group_check=True)
                last.then_inc(s["pe0"], 1)

            @block.scalar
            def _(act):
                a = nc.scalar
                with act.Fori(0, GROUPS) as i:
                    mark(a.copy(xT[:], m["XNT"][:, :, bass.ds(i * GN, GN)]), AC)
                    for j, name in enumerate(UNITS):
                        until(act, PE, name, i)
                        mark(a.copy(st[:, j, :], unit_p[j % 4][:]), AC)
                    until(act, DV, "low", i)
                    mark(a.activation(st[:, :, 0:D], st[:, :, 0:D], ACT.Exp), AC)
                    until(act, PE, "kv", i)

            @block.vector
            def _(dve):
                v = nc.vector
                own = Chain(dve, s["chain"])
                dve.wait_ge(s["pe0"], 1)
                own(v.tensor_reduce(topc[:], tp[:, :, 0:R], AX, ALU.max))
                for k in range(KB):
                    last = v.tensor_scalar(diag[:, k, :], c["ident"][:], topc[:, k:k + 1], None, ALU.mult)
                last.then_inc(s["dve0"], 1)
                dve.wait_ge(s["pe0"], 2)
                own(v.tensor_copy(topr[:].rearrange("p (k x) -> p k x", k=KB), tp[0:R, :, :]))
                with dve.Fori(0, GROUPS) as i:
                    until(dve, AC, UNITS[-1], i)
                    mark(v.tensor_tensor(st[:, :, 0:D], st[:, :, 0:D], row_of(topr[:], GT), ALU.subtract), DV)
                dve.wait_ge(s["pe0"], 3)
                own(v.reciprocal(inv[:], kv_p[:, :, 128]))
                for k in range(KB):
                    own(v.scalar_tensor_tensor(m["KV"][:, k, 0:128], kv_p[:, k, 0:128], inv[:, k:k + 1], c["block"][:], ALU.mult, ALU.mult))


def close3(nc, c, m, I, acc, xp_table):
    tag = "close3"
    H, C, GH = 4, D // 4, 64
    with ExitStack() as ctx:
        sb = lambda n, sh, d=F32: ctx.enter_context(nc.sbuf_tensor(f"{tag}_{n}", sh, d))
        ps = lambda n, sh: ctx.enter_context(nc.psum_tensor(f"{tag}_{n}", sh, F32))
        b = {"acc": sb("acc", [R, ACCS, GT, D + H]), "xp": sb("xp", [R, GT, D]), "t": sb("t", [R, GT, D]), "u": sb("u", [R, GT, D]),
             "z": sb("z", [R, GT, H])} | norm_buffers(sb)
        out, gate = sb("out", [R, GT, D]), sb("gate", [R, GT, D])
        wq, wp, wg1, wg2 = sb("wq", [128, KB, D]), sb("wp", [128, KB, D]), sb("wg1", [128, KB, GH]), sb("wg2", [GH, D])
        rowv = {n: sb(n, [R, D]) for n in ("bias", "gamma", "beta", "ln_g", "ln_b", "bg2", "bproj")}
        bg1 = sb("bg1", [GH, 1])
        qT, rT, hT = sb("qT", [128, KB, GN]), sb("rT", [128, KB, GN]), sb("hT", [GH, GN])
        wide, fb = ps("wide", [128, 1536]), [ps(f"fb{n}", [128, 1024]) for n in range(2)]
        rows = wide[0:R, 0:GT * D].rearrange("p (j x) -> p j x", j=GT)
        loads = [(wg2[:], I["L3_mix_Wg2"]), (bg1[:], columns(I["L3_mix_bg1"], GH))]
        for k in range(KB):
            loads += [(wq[:, k, :], blocked(I["L3_mix_Wqkv"], k)[:, 0:D]), (wp[:, k, :], blocked(I["L3_mix_Wproj"], k)), (wg1[:, k, :], blocked(I["L3_mix_Wg1"], k))]
        loads += [(rowv[n][:], everywhere(I[("L3_gnn_" if n in ("bias", "gamma", "beta") else "L3_mix_") + n])) for n in rowv]
        with phase(nc, tag, "loaded", "acc_in", "sp_passed", "pe", "dve", "act", "chain", "passed") as s, nc.Block() as block:
            PE = Steps(s["pe"], ["q0", "q1", "mix", "xg", "h", "gate", "prod", "y"])
            DV = Steps(s["dve"], ["acc_used", "gat_var", "gat_x", "mix", "xg_var", "xg", "pre", "prod", "x"])
            AC = Steps(s["act"], ["q0", "q1", "gat_std", "xg_std", "xg", "h", "gate", "prod"])

            @block.sync
            def _(sp):
                for to, frm in loads:
                    sp.dma_start(to, frm).then_inc(s["loaded"], 16)
                with sp.Fori(0, GROUPS) as i:
                    load_accumulators(sp, acc, b, i, s["acc_in"], [(b["xp"], xp_table)])
                    until(sp, DV, "acc_used", i)
                    sp.sem_inc(s["sp_passed"], 1)

            @block.tensor
            def _(pe):
                pe.wait_ge(s["loaded"], 16 * len(loads))
                with pe.Fori(0, GROUPS) as i:
                    xt = [m["XNT"][:, k, bass.ds(i * GN, GN)] for k in range(KB)]
                    for g in range(KB):
                        mark(product_t(nc, fb[g], 128, [(wq[:, k, g * 128:(g + 1) * 128], xt[k]) for k in range(KB)]), PE)
                    until(pe, AC, "q1", i)
                    mark(heads_product(nc, rows, qT, m["KV"]), PE)
                    until(pe, DV, "xg", i)
                    mark(turn_tiles(nc, c, wide, b["u"]), PE)
                    until(pe, AC, "xg", i)
                    mark(product_t(nc, fb[0], GH, [(wg1[:, k, :], rT[:, k, :]) for k in range(KB)]), PE)
                    until(pe, AC, "h", i)
                    mark(product_rows(nc, rows, [(hT[:], wg2[:])]), PE)
                    until(pe, DV, "prod", i)
                    mark(turn_tiles(nc, c, wide, out), PE)
                    until(pe, AC, "prod", i)
                    mark(product_rows(nc, rows, [(rT[:, k, :], wp[:, k, :]) for k in range(KB)]), PE)
                    until(pe, DV, "x", i)

            @block.scalar
            def _(act):
                a = nc.scalar
                act.wait_ge(s["loaded"], 16 * len(loads))

                def std(name, i):
                    until(act, DV, name + "_var", i)
                    mark(a.activation(b["std"][:], b["var"][:], ACT.Sqrt), AC)

                def turn(name, i):
                    until(act, PE, name, i)
                    mark(a.copy(rT[:].rearrange("p k (j x) -> p (k j) x", x=R), turned(wide[:])), AC)

                with act.Fori(0, GROUPS) as i:
                    for g in range(KB):
                        until(act, PE, f"q{g}", i)
                        mark(a.copy(dense(qT[:, g, :]), slices(fb[g])), AC)
                    std("gat", i)
                    std("xg", i)
                    turn("xg", i)
                    until(act, PE, "h", i)
                    mark(a.activation(dense(hT[:]), slices(fb[0][0:GH, :]), ACT.Gelu, bias=bg1[:]), AC)
                    until(act, DV, "pre", i)
                    mark(a.activation(gate[:], gate[:], ACT.Sigmoid), AC)
                    turn("prod", i)

            @block.vector
            def _(dve):
                v = nc.vector
                dve.wait_ge(s["loaded"], 16 * len(loads))
                with dve.Fori(0, GROUPS) as i:
                    own = Chain(dve, s["chain"], i, 22)
                    grp = bass.ds(i * GT, GT)
                    x, xn = m["X"][:, grp, :], m["XN"][:, grp, :]
                    t, u = b["t"][:], b["u"][:]
                    heads = lambda ap: ap.rearrange("p j (h x) -> p j h x", x=C)
                    each = lambda ap: ap.unsqueeze(3).to_broadcast([R, GT, H, C])
                    dve.wait_ge(s["acc_in"], i * (16 * (ACCS + 1)) + 16 * (ACCS + 1))
                    a = sum_accumulators(v, own, b)
                    own(v.tensor_tensor(heads(t), heads(b["xp"][:]), each(m["p_self"][:, grp, :]), ALU.mult))
                    own(v.tensor_tensor(t, t, a[:, :, 0:D], ALU.add))
                    own(v.tensor_tensor(b["z"][:], a[:, :, D:D + H], m["p_self"][:, grp, :], ALU.add))
                    own(v.tensor_scalar(b["z"][:], b["z"][:], 1e-16, None, ALU.add))
                    own(v.reciprocal(b["z"][:], b["z"][:]))
                    own(v.tensor_tensor(heads(t), heads(t), each(b["z"][:]), ALU.mult))
                    mark(v.tensor_tensor(t, t, row_of(rowv["bias"][:], GT), ALU.add), DV)
                    until(dve, DV, "acc_used", i)
                    mark(variance(v, own, t, b, 1e-5, s["passed"]), DV)
                    until(dve, AC, "gat_std", i)
                    own(standardize(v, own, t, t, b))
                    own(v.tensor_tensor(t, t, row_of(rowv["gamma"][:], GT), ALU.mult))
                    own(v.tensor_tensor(t, t, row_of(rowv["beta"][:], GT), ALU.add))
                    own(v.tensor_tensor(t, t, xn, ALU.add))
                    own(v.tensor_scalar(t, t, 0.0, None, ALU.max))
                    mark(v.tensor_tensor(x, x, t, ALU.add), DV)
                    until(dve, PE, "mix", i)
                    mark(v.tensor_copy(out[:], rows), DV)
                    mark(variance(v, own, xn, b, 1e-5, s["passed"]), DV)
                    until(dve, AC, "xg_std", i)
                    own(standardize(v, own, xn, u, b))
                    own(v.tensor_tensor(u, u, row_of(rowv["ln_g"][:], GT), ALU.mult))
                    mark(v.tensor_tensor(u, u, row_of(rowv["ln_b"][:], GT), ALU.add), DV)
                    until(dve, PE, "gate", i)
                    mark(v.tensor_tensor(gate[:], rows, row_of(rowv["bg2"][:], GT), ALU.add), DV)
                    until(dve, AC, "gate", i)
                    mark(v.tensor_tensor(out[:], out[:], gate[:], ALU.mult), DV)
                    until(dve, PE, "y", i)
                    own(v.tensor_tensor(t, rows, row_of(rowv["bproj"][:], GT), ALU.add))
                    mark(v.tensor_tensor(x, x, t, ALU.add), DV)
                    until(dve, DV, "x", i)
                    own.end()


def alloc_all(nc, ctx):
    sb = lambda n, sh, d=F32: ctx.enter_context(nc.sbuf_tensor(n, sh, d))
    c = {"iota_i": sb("iota_i", [128, 256], I32), "part_i": sb("part_i", [128, 1], I32), "iota": sb("iota", [128, 256]), "part": sb("part", [128, 1]),
         "ones": sb("ones", [128, 128]), "zeros": sb("zeros", [128, D + 4]), "ident": sb("ident", [128, 128]), "lower": sb("lower", [128, 128]),
         "block": sb("block", [128, 128]), "block4": sb("block4", [128, 4]), "tmp1": sb("tmp1", [128, 1])}
    m = {"X": sb("X", [R, TILES, D]), "XN": sb("XN", [R, TILES, D]), "XNT": sb("XNT", [128, KB, NODES]), "KV": sb("KV", [128, KB, 132]),
         "gate": sb("gate", [R, 8 * TILES]), "deg3": sb("deg3", [R, 3, TILES]), "relcnt": sb("relcnt", [R, TILES * TYPES])}
    e = {n: sb("e_" + n, [R, CHUNKS]) for n in ("src", "dst", "src_lo", "dst_lo", "dst_hi", "slot", "weight", "attr", "dst_dup")}
    return c, m, e


def edge_setup(nc, c, m, e, I, dram):
    build_constants(nc, c)
    with ExitStack() as ctx:
        temps = ("src_i", "dst_i", "typ_i", "rel_i", "tmp_i", "tmp", "src_hi")
        e = e | {n: ctx.enter_context(nc.sbuf_tensor("e_" + n, [R, CHUNKS], I32 if n.endswith("_i") else F32)) for n in temps}
        build_edge_numbers(nc, c, e, I["src"], I["dst"], I["edge_type_7"], I["edge_weight"], I["edge_weight1"])
        build_edge_rows(nc, c, e, dram)
        put_out(nc, "rel_out", dram["rel"], e["rel_i"][:])
        build_earlier(nc, c, e, dram)
        build_scatter_rows(nc, c, "dst_rows", e["dst"][:], e["dst_dup"][:], dram["dst_row"])


def put_out(nc, tag, to, frm):
    with phase(nc, tag, "stored") as s, nc.Block() as block:
        @block.sync
        def _(sp):
            sp.dma_start(to, frm).then_inc(s["stored"], 16)
            sp.wait_ge(s["stored"], 16)


def as_chunks(v):
    return v.rearrange("(p c) -> p c", p=R)


def bulk(nc, tag, steps):
    with phase(nc, tag, "chain", "dve", "act") as s, nc.Block() as block:
        todo = []

        @block.vector
        def _(dve):
            def act_step(ins, *args, **kw):
                ins.then_inc(s["dve"], 1)
                todo.append((args, kw))
                dve.wait_ge(s["act"], len(todo))
            steps(nc.vector, Chain(dve, s["chain"]), act_step)

        @block.scalar
        def _(act):
            for n, (args, kw) in enumerate(todo):
                act.wait_ge(s["dve"], n + 1)
                nc.scalar.activation(*args, **kw).then_inc(s["act"], 1)


def layer0(nc, c, m, e, I, dram):
    open0(nc, c, m, I, dram)
    src, dst = as_chunks(I["src"]), as_chunks(I["dst"])
    with ExitStack() as ctx:
        sb = lambda n, sh, d=F32: ctx.enter_context(nc.sbuf_tensor(f"gnn0_{n}", sh, d))
        score, top = sb("score", [R, CHUNKS, 1]), sb("top", [R, 1, TILES])
        build_score0(nc, c, e, src, dst, dram, I["L0_gnn_attn"], score, top[:])
        look = {"table": top[:, 0, :], "ids": dram["dst_lo_ids"], "slot": e["dst_hi"][:], "slots": TILES}
        src_dup = sb("src_dup", [R, CHUNKS])
        counts = EdgeCounts(c, e, dram["src_ids"], m["deg3"][:].rearrange("p k t -> p (k t)"), m["relcnt"][:], src_dup)
        build_messages(nc, c, e, "msg0", dram["el"], src, dram["dst_row"], e["dst"], dram["dst_ids"], score, 1, dram["acc"], look, counts)
        build_scatter_rows(nc, c, "src_rows", e["src"][:], src_dup[:], dram["src_row"])
    close0(nc, c, m, I, dram["acc"])
    experts0(nc, c, m, I)


def layer1(nc, c, m, e, I, dram):
    open1(nc, c, m, I, dram)

    def inverse(v, own, act_step):
        own(v.tensor_scalar(m["relcnt"][:], m["relcnt"][:], 1.0, None, ALU.max))
        own(v.reciprocal(m["relcnt"][:], m["relcnt"][:]))
    bulk(nc, "share1", inverse)
    look = {"table": m["relcnt"][:], "ids": dram["src_lo_ids"], "slot": e["slot"][:], "slots": TILES * TYPES}
    build_messages(nc, c, e, "msg1", dram["rel_table"], dram["rel"], dram["src_row"], e["src"], dram["src_ids"], None, 1, dram["acc"], look)
    close1(nc, c, m, dram["acc"])
    experts1(nc, c, m, I)


def layer2(nc, c, m, e, I, dram):
    with ExitStack() as ctx:
        sb = lambda n, sh, d=F32: ctx.enter_context(nc.sbuf_tensor(f"layer2_{n}", sh, d))
        m["WT"], m["dinv"], live = sb("WT", [128, KB, 5 * D]), sb("dinv", [R, TILES]), sb("live", [R, TILES])
        build_transposed(nc, c, "turn2", [I["L2_mix_Wqkv"], I["L2_mix_W1"], I["L2_mix_W2"]], m["WT"])

        def degree(v, own, act_step):
            d = m["dinv"][:]
            own(v.tensor_scalar(d, m["deg3"][:, 1, :], 1.0, None, ALU.add))
            own(v.tensor_scalar(live[:], d, 0.0, None, ALU.is_gt))
            own(v.tensor_scalar(d, d, 1e-30, None, ALU.max))
            act_step(v.tensor_copy(d, d), d, d, ACT.Sqrt)
            own(v.reciprocal(d, d))
            own(v.tensor_tensor(d, d, live[:], ALU.mult))
        bulk(nc, "degree2", degree)
        open2(nc, c, m, I, dram)
        build_messages(nc, c, e, "msg2", dram["el"], as_chunks(I["src"]), dram["dst_row"], e["dst"], dram["dst_ids"],
                       e["weight"][:].unsqueeze(2), 1, dram["acc"])
        close2(nc, c, m, I, dram["acc"])
    experts2(nc, c, m, I)


def experts2(nc, c, m, I):
    ENT, F = 8, 1024
    build_gated_open(nc, c, 2, m, I["L2_ffn_Wr"], I["L2_ffn_br"], ENT, "top_ratio")
    build_open(nc, c, "2n", m["XN"], m["XN"], m["XNT"], lambda sb: ({}, []), lambda w: [], lambda v, own, hand_over, b, grp: v.memset(b["st"][:], 0.0),
               lambda sp, b, i, sem=None: 0, None, None, 0)
    with ExitStack() as ctx:
        sb = lambda n, sh, d=F32: ctx.enter_context(nc.sbuf_tensor(f"ffn2_{n}", sh, d))
        b1, gain, shift = sb("b1", [128, ENT * F // 128]), sb("gain", [128, ENT * KB]), sb("shift", [128, ENT * KB])
        put_in(nc, "ffn2_in", [(b1[:, e * 8:(e + 1) * 8], columns(I["L2_ffn_b1"][e])) for e in range(ENT)]
               + [(t[:, e * KB:(e + 1) * KB], columns(I[n][e])) for t, n in ((gain, "L2_ffn_ln_g"), (shift, "L2_ffn_ln_b")) for e in range(ENT)])
        flat = lambda n: I[n].rearrange("e r o -> (e r) o")
        build_experts(nc, "ffn2e", m["XNT"], m["X"], ENT, [256, F, 256], [flat("L2_ffn_W1"), flat("L2_ffn_W2")],
                      everywhere(I["L2_ffn_b2"]), m["gate"], ACT.Gelu, [b1], affine=(gain, shift))


def layer3(nc, c, m, e, I, dram):
    H = 4
    with ExitStack() as ctx:
        sb = lambda n, sh, d=F32: ctx.enter_context(nc.sbuf_tensor(f"layer3_{n}", sh, d))
        m["p_self"], top = sb("p_self", [R, TILES, H]), sb("top", [R, H, TILES])
        top_t, self_ = sb("top_t", [R, TILES, H]), sb("self", [R, TILES, H])
        we, att, slope, mean = sb("we", [R, D]), sb("att", [R, D]), sb("slope", [R, H]), sb("mean", [R, TILES])
        m["a_src"], m["a_dst"], m["key_top"] = sb("a_src", [R, TILES, H]), sb("a_dst", [R, TILES, H]), sb("key_top", [R, D])
        put_in(nc, "layer3_in", [(we[:], everywhere(I["L3_gnn_We"].rearrange("o x -> (o x)"))), (att[:], everywhere(I["L3_gnn_att_edge"].rearrange("h x -> (h x)")))],
               [(m["key_top"][:], -HUGE)])
        open3(nc, c, m, I, dram)
        build_key_sums(nc, c, m, I["L3_mix_Wqkv"])

        def own_loops(v, own, act_step):
            own(v.tensor_tensor(we[:], we[:], att[:], ALU.mult))
            own(v.tensor_reduce(slope[:], we[:].rearrange("p (h x) -> p h x", h=H), AX, ALU.add))
            own(v.tensor_scalar(mean[:], m["deg3"][:, 0, :], 1.0, None, ALU.max))
            own(v.reciprocal(mean[:], mean[:]))
            own(v.tensor_tensor(mean[:], mean[:], m["deg3"][:, 2, :], ALU.mult))
            own(v.tensor_tensor(self_[:], col_of(mean[:], H), row_of(slope[:], TILES), ALU.mult))
            own(v.tensor_tensor(self_[:], self_[:], m["a_src"][:], ALU.add))
            own(v.tensor_tensor(self_[:], self_[:], m["a_dst"][:], ALU.add))
            own(leaky(v, self_[:]))
        bulk(nc, "loops3", own_loops)
        with ExitStack() as inner:
            sb = lambda n, sh, d=F32: inner.enter_context(nc.sbuf_tensor(f"gnn3_{n}", sh, d))
            logit = sb("logit", [R, CHUNKS, H])
            whole = lambda t: t[:].rearrange("p t h -> p (t h)")
            src_hi = sb("src_hi", [R, CHUNKS])

            def high(v, own, act_step):
                own(v.tensor_tensor(src_hi[:], e["src"][:], e["src_lo"][:], ALU.subtract))
                own(v.tensor_scalar(src_hi[:], src_hi[:], 1.0 / R, None, ALU.mult))
                own(v.tensor_scalar(src_hi[:], src_hi[:], 8388608.0 * 1.5, -8388608.0 * 1.5, ALU.add, ALU.add))
                own(v.tensor_tensor(logit[:], col_of(e["attr"][:], H), row_of(slope[:], CHUNKS), ALU.mult))
            bulk(nc, "high3", high)
            build_logits3(nc, c, e, dram, whole(m["a_src"]), whole(m["a_dst"]), src_hi, logit, top[:])

            def with_loops(v, own, act_step):
                own(v.tensor_tensor(top_t[:], top[:].rearrange("p h t -> p t h"), self_[:], ALU.max))
                act_step(v.tensor_tensor(self_[:], self_[:], top_t[:], ALU.subtract), m["p_self"][:], self_[:], ACT.Exp)
            bulk(nc, "tops3", with_loops)
            look = {"table": whole(top_t), "ids": dram["dst_lo_ids"], "slot": e["dst_hi"][:], "slots": TILES}
            build_messages(nc, c, e, "msg3", dram["el"], as_chunks(I["src"]), dram["dst_row"], e["dst"], dram["dst_ids"], logit, H, dram["acc4"], look)
        close3(nc, c, m, I, dram["acc4"], dram["el"])
    experts3(nc, c, m, I)


def leaky(v, x):
    flat = x.rearrange("p a b -> p (a b)")
    return v.scalar_tensor_tensor(flat, flat, 0.2, flat, ALU.mult, ALU.max)


def experts3(nc, c, m, I):
    ENT = 8
    build_gated_open(nc, c, 3, m, I["L3_ffn_Wr"], I["L3_ffn_br"], ENT, "all")
    with ExitStack() as ctx:
        sb = lambda n, sh, d=F32: ctx.enter_context(nc.sbuf_tensor(f"ffn3_{n}", sh, d))
        t = {f"{n}{l}": sb(f"{n}{l}", [128, ENT * KB]) for n in ("b", "g", "be", "m", "v") for l in (1, 2)}
        put_in(nc, "ffn3_in", [(t[n][:, e * KB:(e + 1) * KB], columns(I["L3_ffn_" + n][e])) for n in t for e in range(ENT)])

        def fold(v, own, act_step):
            for l in "12":
                own(v.tensor_scalar(t["v" + l][:], t["v" + l][:], 1e-3, None, ALU.add))
                act_step(v.tensor_tensor(t["b" + l][:], t["b" + l][:], t["m" + l][:], ALU.subtract), t["m" + l][:], t["v" + l][:], ACT.Sqrt)
                own(v.reciprocal(t["v" + l][:], t["m" + l][:]))
                own(v.tensor_tensor(t["g" + l][:], t["g" + l][:], t["v" + l][:], ALU.mult))
                own(v.tensor_tensor(t["b" + l][:], t["b" + l][:], t["g" + l][:], ALU.mult))
                own(v.tensor_tensor(t["b" + l][:], t["b" + l][:], t["be" + l][:], ALU.add))
        bulk(nc, "fold3", fold)
        flat = lambda n: I[n].rearrange("e r o -> (e r) o")
        build_experts(nc, "ffn3e", m["XNT"], m["X"], ENT, [256, 256, 256, 256], [flat("L3_ffn_W1"), flat("L3_ffn_W2"), flat("L3_ffn_Wo")],
                      everywhere(I["L3_ffn_bo"]), m["gate"], ACT.Relu, [t["b1"], t["b2"]], layer_scale=[t["g1"], t["g2"]])


def build(nc, I, out):
    def scratch(name, shape, dt=F32):
        return nc.dram_tensor(name, shape, dt, kind="Internal").ap()

    dram = {"el": scratch("el_table", [NODES, D]), "er": scratch("er_table", [NODES, D]), "rel_table": scratch("rel_table", [NODES * TYPES, D]),
            "acc": [scratch(f"acc{k}", [NODES + R, D + 1]) for k in range(ACCS)], "acc4": [scratch(f"acc_heads{k}", [NODES + R, D + 4]) for k in range(ACCS)],
            "src_row": scratch("src_row", [R, CHUNKS], I32), "dst_row": scratch("dst_row", [R, CHUNKS], I32), "rel": scratch("rel_row", [R, CHUNKS], I32)}
    for name in ("src", "dst", "src_lo", "dst_lo"):
        dram[name + "_ids"] = scratch(name + "_ids", [EDGES], I16)
    with ExitStack() as ctx:
        ctx.enter_context(nc.allow_non_contiguous_dma(reason="bias vectors as columns"))
        c, m, e = alloc_all(nc, ctx)
        edge_setup(nc, c, m, e, I, dram)
        put_in(nc, "x_in", [(m["X"][:], by_tile(I["x"]))])
        layer0(nc, c, m, e, I, dram)
        layer1(nc, c, m, e, I, dram)
        layer2(nc, c, m, e, I, dram)
        layer3(nc, c, m, e, I, dram)
        with phase(nc, "x_out", "stored") as s, nc.Block() as block:
            @block.sync
            def _(sp):
                sp.dma_start(by_tile(out), m["X"][:]).then_inc(s["stored"], 16)
                sp.wait_ge(s["stored"], 16)


def kernel(**inputs):
    import numpy as _np
    import concourse.bacc as _bacc
    from concourse import mybir as _mybir
    from concourse.bass_utils import run_bass_kernel_spmd as _run

    nc = _bacc.Bacc("TRN2", target_bir_lowering=False, num_devices=1)
    arrays, aps = {}, {}
    for name, value in inputs.items():
        a = _np.ascontiguousarray(value)
        arrays[f"in_{name}_dram"] = a
        aps[name] = nc.dram_tensor(f"in_{name}_dram", a.shape, _mybir.dt.from_np(a.dtype), kind="ExternalInput").ap()
    out = nc.dram_tensor("out_0_dram", [NODES, D], _mybir.dt.float32, kind="ExternalOutput").ap()
    build(nc, aps, out)
    r = _run(nc, [arrays], core_ids=[0])
    return r.results[0]["out_0_dram"]
```
